# Optimizing a Trainium2 kernel written in Bass

```python
import numpy as np
import jax
import jax.numpy as jnp

def _softmax(x, axis=-1):
    return jax.nn.softmax(x, axis=axis)

def _gelu(x):
    return jax.nn.gelu(x, approximate=True)

def _silu(x):
    return jax.nn.silu(x)

def _sigmoid(x):
    return jax.nn.sigmoid(x)

def _layernorm(x, axis=-1, eps=1e-05):
    m = jnp.mean(x, axis=axis, keepdims=True)
    v = jnp.var(x, axis=axis, keepdims=True)
    return (x - m) / jnp.sqrt(v + eps)

def _scatter_add(tgt, idx, src, axis=0):
    return tgt.at[idx].add(src)

def _segment_sum(src, seg, n):
    return jax.ops.segment_sum(src, seg, n)
kernel_name = 'mk_perceiver_d4_seqx_r4_dc8f76'

def setup_inputs(seed: int=0):
    np.random.seed(seed)
    _w = jnp.asarray

    def _rec_inputs():
        import jax
        import jax.numpy as jnp
        _rk = jax.random.key(seed)
        x = 7.22e-05 + 1 * jax.random.normal(jax.random.fold_in(_rk, 1), (32, 64, 256), jnp.float32)
        _lenS = 64 - jax.random.randint(jax.random.fold_in(_rk, 7), (32,), 0, max(1, 64 // 4) + 1, jnp.int32)
        _lenS2 = 256 - jax.random.randint(jax.random.fold_in(_rk, 8), (32,), 0, max(1, 256 // 4) + 1, jnp.int32)
        _ctx_1024P = jax.random.normal(jax.random.fold_in(_rk, 11), (32, 16, 256), jnp.float32)
        _ctx_1024c = jax.random.dirichlet(jax.random.fold_in(_rk, 511), 0.3 * jnp.ones((16,), jnp.float32), (32, 256))
        _ctx_1024t = jnp.einsum('bsk,bkd->bsd', _ctx_1024c, _ctx_1024P)
        _ctx_1024t = _ctx_1024t * jax.lax.rsqrt(jnp.mean(jnp.square(_ctx_1024t)) + 1e-12) * 0.953939
        ctx_1024 = 4.13588e-05 + 0.999923 * (_ctx_1024t + 0.3 * jax.random.normal(jax.random.fold_in(_rk, 611), (32, 256, 256), jnp.float32))
        _validS = jnp.arange(64)[None, :] < _lenS[:, None]
        _validS2 = jnp.arange(256)[None, :] < _lenS2[:, None]
        _causal = jnp.tril(jnp.ones((64, 64), dtype=bool))
        mask_Bx1x1xS2_fk0 = jnp.where(jnp.broadcast_to(_validS2[:, None, None, :], (32, 1, 1, 256)), 0.0, 1.0).astype(jnp.float32)
        return (x, ctx_1024, mask_Bx1x1xS2_fk0)
    x, ctx_1024, mask_Bx1x1xS2_fk0 = _rec_inputs()

    def _L0_xattn_setup():
        import jax, jax.numpy as jnp
        import numpy as np
        B, S, D, H = (4, 512, 256, 16)
        HD = D // H
        key = jax.random.key(seed)
        ks = jax.random.split(key, 11)
        s = 1.0 / np.sqrt(D)
        return {'query': jax.random.normal(ks[0], (B, S, D), jnp.float32), 'key': jax.random.normal(ks[1], (B, S, D), jnp.float32), 'value': jax.random.normal(ks[2], (B, S, D), jnp.float32), 'Wq': jax.random.normal(ks[3], (D, D), jnp.float32) * s, 'bq': jnp.zeros((D,), jnp.float32), 'Wk': jax.random.normal(ks[4], (D, D), jnp.float32) * s, 'bk': jnp.zeros((D,), jnp.float32), 'Wv': jax.random.normal(ks[5], (D, D), jnp.float32) * s, 'bv': jnp.zeros((D,), jnp.float32), 'Wo': jax.random.normal(ks[6], (D, D), jnp.float32) * s, 'bo': jnp.zeros((D,), jnp.float32)}
    _L0_xattn_all = _L0_xattn_setup()
    _L0_xattn_in = {k: v for k, v in _L0_xattn_all.items() if k in ('Wq', 'bq', 'Wk', 'bk', 'Wv', 'bv', 'Wo', 'bo')}
    del _L0_xattn_all

    def _L0_attn_setup():
        import jax, jax.numpy as jnp
        import numpy as np
        LN_EPS = 1e-05
        DENOM_EPS = 1e-06
        NUM_HEADS = 16

        def _layer_norm(x, gamma, beta):
            mu = jnp.mean(x, axis=-1, keepdims=True)
            var = jnp.mean(jnp.square(x - mu), axis=-1, keepdims=True)
            return (x - mu) * jax.lax.rsqrt(var + LN_EPS) * gamma + beta
        key = jax.random.key(seed)
        k1, k2, k3 = jax.random.split(key, 3)
        B, L, D = (4, 1024, 256)
        x = jax.random.normal(k1, (B, L, D), dtype=jnp.float32)
        gamma = jnp.ones((D,), dtype=jnp.float32)
        beta = jnp.zeros((D,), dtype=jnp.float32)
        Wqkv = jax.random.normal(k2, (D, 3 * D), dtype=jnp.float32) / np.sqrt(D)
        Wout = jax.random.normal(k3, (D, D), dtype=jnp.float32) / np.sqrt(D)
        return {'x': x, 'gamma': gamma, 'beta': beta, 'Wqkv': Wqkv, 'Wout': Wout}
    _L0_attn_all = _L0_attn_setup()
    _L0_attn_in = {k: v for k, v in _L0_attn_all.items() if k in ('gamma', 'beta', 'Wqkv', 'Wout')}
    del _L0_attn_all

    def _L0_ffn_setup():
        import jax, jax.numpy as jnp
        import numpy as np
        H = 256
        DFF = 1024
        E = 8
        B = 8
        S = 128
        INIT_LAMBDA = 0.2
        key = jax.random.key(seed)
        ks = jax.random.split(key, 9)
        hidden_states = jax.random.normal(ks[0], (S, B, H), dtype=jnp.float32)
        gW1 = 0.01 * jax.random.normal(ks[1], (H, H), dtype=jnp.float32)
        gb1 = jnp.zeros((H,), dtype=jnp.float32)
        gW2 = 0.01 * jax.random.normal(ks[2], (E, H), dtype=jnp.float32)
        gb2 = jnp.full((E,), INIT_LAMBDA, dtype=jnp.float32)
        sc1 = 1.0 / np.sqrt(H)
        sc2 = 1.0 / np.sqrt(DFF)
        eW1 = sc1 * jax.random.normal(ks[3], (E, DFF, H), dtype=jnp.float32)
        eb1 = sc1 * jax.random.normal(ks[4], (E, DFF), dtype=jnp.float32)
        eW2 = sc2 * jax.random.normal(ks[5], (E, H, DFF), dtype=jnp.float32)
        eb2 = sc2 * jax.random.normal(ks[6], (E, H), dtype=jnp.float32)
        return {'hidden_states': hidden_states, 'gW1': gW1, 'gb1': gb1, 'gW2': gW2, 'gb2': gb2, 'eW1': eW1, 'eb1': eb1, 'eW2': eW2, 'eb2': eb2}
    _L0_ffn_all = _L0_ffn_setup()
    _L0_ffn_in = {k: v for k, v in _L0_ffn_all.items() if k in ('gW1', 'gb1', 'gW2', 'gb2', 'eW1', 'eb1', 'eW2', 'eb2')}
    del _L0_ffn_all

    def _L1_xattn_setup():
        import jax, jax.numpy as jnp
        import numpy as np
        DIM = 256
        H = 16
        D = 64
        INNER = H * D
        EPS = 1e-05

        def layernorm(x, w, b):
            mu = jnp.mean(x, axis=-1, keepdims=True)
            var = jnp.var(x, axis=-1, keepdims=True)
            return (x - mu) * jax.lax.rsqrt(var + EPS) * w + b
        key = jax.random.key(seed)
        ks = jax.random.split(key, 8)
        B, N, S = (4, 64, 2048)
        s = 1.0 / np.sqrt(DIM)
        return {'latents': jax.random.normal(ks[0], (B, N, DIM), jnp.float32), 'context': jax.random.normal(ks[1], (B, S, DIM), jnp.float32), 'ln_l_w': jnp.ones((DIM,), jnp.float32), 'ln_l_b': jnp.zeros((DIM,), jnp.float32), 'ln_c_w': jnp.ones((DIM,), jnp.float32), 'ln_c_b': jnp.zeros((DIM,), jnp.float32), 'Wq': jax.random.normal(ks[2], (DIM, INNER), jnp.float32) * s, 'Wkv': jax.random.normal(ks[3], (DIM, 2 * INNER), jnp.float32) * s, 'Wo': jax.random.normal(ks[4], (INNER, DIM), jnp.float32) * (1.0 / np.sqrt(INNER)), 'bo': jnp.zeros((DIM,), jnp.float32)}
    _L1_xattn_all = _L1_xattn_setup()
    _L1_xattn_in = {k: v for k, v in _L1_xattn_all.items() if k in ('ln_l_w', 'ln_l_b', 'ln_c_w', 'ln_c_b', 'Wq', 'Wkv', 'Wo', 'bo')}
    del _L1_xattn_all

    def _L1_attn_setup():
        import jax, jax.numpy as jnp
        import numpy as np
        N_HEAD = 16
        GAMMA_MIN = 0.9
        GAMMA_MAX = 0.999
        GN_EPS = 1e-05

        def _gammas(n_head):
            lo = float(np.log(1.0 - GAMMA_MAX))
            hi = float(np.log(1.0 - GAMMA_MIN))
            return 1.0 - jnp.exp(jnp.linspace(lo, hi, n_head, dtype=jnp.float32))
        key = jax.random.key(seed)
        ks = jax.random.split(key, 5)
        B, T, C = (2, 512, 256)
        scale = 0.02
        return {'x': jax.random.normal(ks[0], (B, T, C), dtype=jnp.float32), 'wq': jax.random.normal(ks[1], (C, C), dtype=jnp.float32) * scale, 'wk': jax.random.normal(ks[2], (C, C), dtype=jnp.float32) * scale, 'wv': jax.random.normal(ks[3], (C, C), dtype=jnp.float32) * scale, 'wo': jax.random.normal(ks[4], (C, C), dtype=jnp.float32) * scale, 'gn_w': jnp.ones((C,), dtype=jnp.float32), 'gn_b': jnp.zeros((C,), dtype=jnp.float32)}
    _L1_attn_all = _L1_attn_setup()
    _L1_attn_in = {k: v for k, v in _L1_attn_all.items() if k in ('wq', 'wk', 'wv', 'wo', 'gn_w', 'gn_b')}
    del _L1_attn_all

    def _L1_ffn_setup():
        import math
        import jax, jax.numpy as jnp
        import numpy as np
        B, T, H = (4, 512, 256)
        E, K, F = (8, 2, 512)
        CAP_FACTOR = 1.25

        def _moe_forward(x, Wg, W_in, W_out):
            b, t, h = x.shape
            xf = x.reshape(-1, h)
            S = xf.shape[0]
            C = int(math.ceil(K * S / E * CAP_FACTOR))
            logits = xf @ Wg
            probs = jax.nn.softmax(logits, axis=-1)
            top_vals, top_idx = jax.lax.top_k(probs, K)
            flat_idx = top_idx.T.reshape(-1)
            onehot = jax.nn.one_hot(flat_idx, E, dtype=jnp.int32)
            cum = jnp.cumsum(onehot, axis=0) - 1
            loc = jnp.take_along_axis(cum, flat_idx[:, None], axis=1)[:, 0]
            loc = loc.reshape(K, S).T
            keep = loc < C
            gates = top_vals * keep.astype(top_vals.dtype)
            denom = jnp.maximum(gates.sum(-1, keepdims=True), 1e-09)
            gates = gates / denom
            loc_c = jnp.where(keep, loc, C)
            e_flat = top_idx.reshape(-1)
            l_flat = loc_c.reshape(-1)
            xk = jnp.broadcast_to(xf[:, None, :], (S, K, h)).reshape(-1, h)
            xk = jnp.where(keep.reshape(-1, 1), xk, 0.0)
            buf = jnp.zeros((E, C + 1, h), x.dtype).at[e_flat, l_flat].set(xk)
            inp = buf[:, :C]
            hid = jnp.einsum('ech,ehf->ecf', inp, W_in)
            a, g = jnp.split(hid, 2, axis=-1)
            hid = jax.nn.gelu(a, approximate=False) * g
            out_e = jnp.einsum('ecf,efh->ech', hid, W_out)
            out_pad = jnp.concatenate([out_e, jnp.zeros((E, 1, h), out_e.dtype)], axis=1)
            gathered = out_pad[e_flat, l_flat].reshape(S, K, h)
            y = (gathered * gates[..., None]).sum(axis=1)
            return y.reshape(b, t, h)
        key = jax.random.key(seed)
        k1, k2, k3, k4 = jax.random.split(key, 4)
        x = jax.random.normal(k1, (B, T, H), dtype=jnp.float32)
        Wg = jax.random.normal(k2, (H, E), dtype=jnp.float32) * 0.02
        W_in = jax.random.normal(k3, (E, H, 2 * F), dtype=jnp.float32) * (1.0 / math.sqrt(H))
        W_out = jax.random.normal(k4, (E, F, H), dtype=jnp.float32) * (1.0 / math.sqrt(F))
        return {'x': x, 'Wg': Wg, 'W_in': W_in, 'W_out': W_out}
    _L1_ffn_all = _L1_ffn_setup()
    _L1_ffn_in = {k: v for k, v in _L1_ffn_all.items() if k in ('Wg', 'W_in', 'W_out')}
    del _L1_ffn_all

    def _L2_xattn_setup():
        import jax, jax.numpy as jnp
        import numpy as np
        HIDDEN = 256
        HEADS = 16
        CHUNK = 512
        OVERLAP = 128
        HEAD_DIM = HIDDEN // HEADS
        SCALE = 1.0 / np.sqrt(HEAD_DIM)

        def _attn(q, k, v):
            B, Lq, _ = q.shape
            Lk = k.shape[1]
            qh = q.reshape(B, Lq, HEADS, HEAD_DIM)
            kh = k.reshape(B, Lk, HEADS, HEAD_DIM)
            vh = v.reshape(B, Lk, HEADS, HEAD_DIM)
            scores = jnp.einsum('bqhd,bkhd->bhqk', qh, kh) * SCALE
            probs = jax.nn.softmax(scores, axis=-1)
            out = jnp.einsum('bhqk,bkhd->bqhd', probs, vh)
            return out.reshape(B, Lq, HIDDEN)

        def _chunked_attention(query, key, value):
            B, S, _ = query.shape
            if S <= CHUNK:
                return _attn(query, key, value)
            step = CHUNK - OVERLAP
            chunks = []
            for start in range(0, S, step):
                end = min(start + CHUNK, S)
                ks = max(0, start - OVERLAP)
                ke = min(S, end + OVERLAP)
                chunks.append(_attn(query[:, start:end], key[:, ks:ke], value[:, ks:ke]))
            out = jnp.zeros((B, S, HIDDEN), dtype=query.dtype)
            wsum = jnp.zeros((B, S, 1), dtype=query.dtype)
            n = len(chunks)
            pos = 0
            for i, ch in enumerate(chunks):
                L = ch.shape[1]
                w = np.ones(L, dtype=np.float32)
                f = min(OVERLAP, L)
                if i > 0:
                    w[:f] = np.linspace(0.0, 1.0, f)
                if i < n - 1:
                    w[-f:] = np.linspace(1.0, 0.0, f)
                end = min(pos + L, S)
                a = end - pos
                wj = jnp.asarray(w[:a], dtype=query.dtype)[None, :, None]
                out = out.at[:, pos:end].add(ch[:, :a] * wj)
                wsum = wsum.at[:, pos:end].add(jnp.broadcast_to(wj, (B, a, 1)))
                pos += step
            return out / (wsum + 1e-10)
        key = jax.random.key(seed)
        kq, kk, kv = jax.random.split(key, 3)
        B, S = (2, 2048)
        return {'query': jax.random.normal(kq, (B, S, HIDDEN), dtype=jnp.float32), 'key': jax.random.normal(kk, (B, S, HIDDEN), dtype=jnp.float32), 'value': jax.random.normal(kv, (B, S, HIDDEN), dtype=jnp.float32)}
    _L2_xattn_all = _L2_xattn_setup()
    _L2_xattn_in = {k: v for k, v in _L2_xattn_all.items() if k in ()}
    del _L2_xattn_all

    def _L2_attn_setup():
        import jax, jax.numpy as jnp
        import numpy as np
        D_MODEL = 256
        N_HEADS = 16
        D_HEAD = D_MODEL // N_HEADS

        def _rmsnorm(x, w):
            xf = x.astype(jnp.float32)
            rms = jnp.mean(xf * xf, axis=-1, keepdims=True)
            return (xf / jnp.sqrt(rms + 1e-06) * w.astype(jnp.float32)).astype(x.dtype)
        key = jax.random.key(seed)
        ks = jax.random.split(key, 7)
        x = jax.random.normal(ks[0], (1, 1024, D_MODEL), dtype=jnp.float32)
        Wqkv = jax.random.normal(ks[1], (3 * D_MODEL, D_MODEL), dtype=jnp.float32) * (1.0 / np.sqrt(D_MODEL))
        bqkv = jax.random.normal(ks[2], (3 * D_MODEL,), dtype=jnp.float32) * 0.01
        Wo = jax.random.normal(ks[3], (D_MODEL, D_MODEL), dtype=jnp.float32) * (1.0 / np.sqrt(D_MODEL))
        bo = jax.random.normal(ks[4], (D_MODEL,), dtype=jnp.float32) * 0.01
        wq = jnp.ones((D_HEAD,), dtype=jnp.float32)
        wk = jnp.ones((D_HEAD,), dtype=jnp.float32)
        return {'x': x, 'Wqkv': Wqkv, 'bqkv': bqkv, 'Wo': Wo, 'bo': bo, 'wq': wq, 'wk': wk}
    _L2_attn_all = _L2_attn_setup()
    _L2_attn_in = {k: v for k, v in _L2_attn_all.items() if k in ('Wqkv', 'bqkv', 'Wo', 'bo', 'wq', 'wk')}
    del _L2_attn_all

    def _L2_ffn_setup():
        import math
        import jax, jax.numpy as jnp
        import numpy as np
        D_CONTENT = 256
        D_POSITION = 32
        NUM_TILES = 8
        BATCH = 8
        SEQ = 512

        def make_pe(seq_len, d_pos):
            pos = jnp.arange(seq_len, dtype=jnp.float32)[:, None]
            div = jnp.exp(jnp.arange(0, d_pos, 2, dtype=jnp.float32) * (-math.log(10000.0) / d_pos))
            ang = pos * div
            pe = jnp.zeros((seq_len, d_pos), dtype=jnp.float32)
            pe = pe.at[:, 0::2].set(jnp.sin(ang))
            pe = pe.at[:, 1::2].set(jnp.cos(ang))
            return pe
        key = jax.random.key(seed)
        k1, k2, k3, k4 = jax.random.split(key, 4)
        x = jax.random.normal(k1, (BATCH, SEQ, D_CONTENT), dtype=jnp.float32)
        tile_sigs = jax.random.normal(k2, (NUM_TILES, D_POSITION), dtype=jnp.float32)
        lim = 1.0 / math.sqrt(D_CONTENT)
        W = jax.random.uniform(k3, (NUM_TILES, D_CONTENT, D_CONTENT), minval=-lim, maxval=lim, dtype=jnp.float32)
        b = jax.random.uniform(k4, (NUM_TILES, D_CONTENT), minval=-lim, maxval=lim, dtype=jnp.float32)
        return {'x': x, 'tile_sigs': tile_sigs, 'W': W, 'b': b}
    _L2_ffn_all = _L2_ffn_setup()
    _L2_ffn_in = {k: v for k, v in _L2_ffn_all.items() if k in ('tile_sigs', 'W', 'b')}
    del _L2_ffn_all

    def _L3_xattn_setup():
        import jax, jax.numpy as jnp
        import numpy as np
        B, S, DIM, H = (4, 512, 256, 16)
        DEPTH = DIM // H

        def _split_heads(x):
            return x.reshape(x.shape[0], x.shape[1], H, DEPTH).transpose(0, 2, 1, 3)
        key = jax.random.key(seed)
        ks = jax.random.split(key, 12)
        s = 0.02
        return {'Q': jax.random.normal(ks[0], (B, S, DIM), jnp.float32), 'K': jax.random.normal(ks[1], (B, S, DIM), jnp.float32), 'V': jax.random.normal(ks[2], (B, S, DIM), jnp.float32), 'mask': jax.random.randint(ks[3], (B, 1, 1, S), 0, 2).astype(jnp.float32), 'Wq': jax.random.normal(ks[4], (DIM, DIM), jnp.float32) * s, 'bq': jnp.zeros((DIM,), jnp.float32), 'Wk': jax.random.normal(ks[5], (DIM, DIM), jnp.float32) * s, 'bk': jnp.zeros((DIM,), jnp.float32), 'Wv': jax.random.normal(ks[6], (DIM, DIM), jnp.float32) * s, 'bv': jnp.zeros((DIM,), jnp.float32), 'Wo': jax.random.normal(ks[7], (DIM, DIM), jnp.float32) * s, 'bo': jnp.zeros((DIM,), jnp.float32)}
    _L3_xattn_all = _L3_xattn_setup()
    _L3_xattn_in = {k: v for k, v in _L3_xattn_all.items() if k in ('Wq', 'bq', 'Wk', 'bk', 'Wv', 'bv', 'Wo', 'bo')}
    del _L3_xattn_all

    def _L3_attn_setup():
        import jax, jax.numpy as jnp
        import numpy as np
        from jax import lax
        B, S, D_IN = (4, 1024, 256)
        D_FAST, D_SLOW = (128, 128)
        Z_BIAS_FAST, Z_BIAS_SLOW = (2.0, -2.0)

        def _binop(q_i, q_j):
            a_i, b_i = q_i
            a_j, b_j = q_j
            return (a_i * a_j, a_j * b_i + b_j)

        def parallel_scan(a, b):
            _, h = lax.associative_scan(_binop, (a, b), axis=1)
            return h
        key = jax.random.key(seed)
        ks = jax.random.split(key, 6)
        scale = 0.02
        x = jax.random.normal(ks[0], (B, S, D_IN), dtype=jnp.float32)
        W_zf = jax.random.normal(ks[1], (D_IN, D_FAST), dtype=jnp.float32) * scale
        b_zf = jnp.full((D_FAST,), Z_BIAS_FAST, dtype=jnp.float32)
        W_hf = jax.random.normal(ks[2], (D_IN, D_FAST), dtype=jnp.float32) * scale
        b_hf = jnp.zeros((D_FAST,), dtype=jnp.float32)
        W_zs = jax.random.normal(ks[3], (D_IN, D_SLOW), dtype=jnp.float32) * scale
        b_zs = jnp.full((D_SLOW,), Z_BIAS_SLOW, dtype=jnp.float32)
        W_hs = jax.random.normal(ks[4], (D_IN, D_SLOW), dtype=jnp.float32) * scale
        b_hs = jnp.zeros((D_SLOW,), dtype=jnp.float32)
        W_g = jax.random.normal(ks[5], (D_FAST + D_SLOW, D_FAST + D_SLOW), dtype=jnp.float32) * scale
        b_g = jnp.zeros((D_FAST + D_SLOW,), dtype=jnp.float32)
        return {'x': x, 'W_zf': W_zf, 'b_zf': b_zf, 'W_hf': W_hf, 'b_hf': b_hf, 'W_zs': W_zs, 'b_zs': b_zs, 'W_hs': W_hs, 'b_hs': b_hs, 'W_g': W_g, 'b_g': b_g}
    _L3_attn_all = _L3_attn_setup()
    _L3_attn_in = {k: v for k, v in _L3_attn_all.items() if k in ('W_zf', 'b_zf', 'W_hf', 'b_hf', 'W_zs', 'b_zs', 'W_hs', 'b_hs', 'W_g', 'b_g')}
    del _L3_attn_all

    def _L3_ffn_setup():
        import jax, jax.numpy as jnp
        import numpy as np
        DIM = 256
        HIDDEN = 768
        SCALE = 1.0 / 127.0

        def _dequant(w_int, dtype):
            return w_int.astype(dtype) * jnp.asarray(SCALE, dtype)
        key = jax.random.key(seed)
        k_x, k_g, k_u, k_d = jax.random.split(key, 4)
        x = jax.random.normal(k_x, (4, 512, DIM), dtype=jnp.float32)
        w_gate = jax.random.randint(k_g, (HIDDEN, DIM), -127, 128, dtype=jnp.int32)
        w_up = jax.random.randint(k_u, (HIDDEN, DIM), -127, 128, dtype=jnp.int32)
        w_down = jax.random.randint(k_d, (DIM, HIDDEN), -127, 128, dtype=jnp.int32)
        return {'x': x, 'w_gate': w_gate, 'w_up': w_up, 'w_down': w_down}
    _L3_ffn_all = _L3_ffn_setup()
    _L3_ffn_in = {k: v for k, v in _L3_ffn_all.items() if k in ('w_gate', 'w_up', 'w_down')}
    del _L3_ffn_all
    return {'x': x, 'ctx_1024': ctx_1024, 'mask_Bx1x1xS2_fk0': mask_Bx1x1xS2_fk0, 'L0_xattn_Wq': _L0_xattn_in['Wq'], 'L0_xattn_bq': _L0_xattn_in['bq'], 'L0_xattn_Wk': _L0_xattn_in['Wk'], 'L0_xattn_bk': _L0_xattn_in['bk'], 'L0_xattn_Wv': _L0_xattn_in['Wv'], 'L0_xattn_bv': _L0_xattn_in['bv'], 'L0_xattn_Wo': _L0_xattn_in['Wo'], 'L0_xattn_bo': _L0_xattn_in['bo'], 'L0_attn_gamma': _L0_attn_in['gamma'], 'L0_attn_beta': _L0_attn_in['beta'], 'L0_attn_Wqkv': _L0_attn_in['Wqkv'], 'L0_attn_Wout': _L0_attn_in['Wout'], 'L0_ffn_gW1': _L0_ffn_in['gW1'], 'L0_ffn_gb1': _L0_ffn_in['gb1'], 'L0_ffn_gW2': _L0_ffn_in['gW2'], 'L0_ffn_gb2': _L0_ffn_in['gb2'], 'L0_ffn_eW1': _L0_ffn_in['eW1'], 'L0_ffn_eb1': _L0_ffn_in['eb1'], 'L0_ffn_eW2': _L0_ffn_in['eW2'], 'L0_ffn_eb2': _L0_ffn_in['eb2'], 'L1_xattn_ln_l_w': _L1_xattn_in['ln_l_w'], 'L1_xattn_ln_l_b': _L1_xattn_in['ln_l_b'], 'L1_xattn_ln_c_w': _L1_xattn_in['ln_c_w'], 'L1_xattn_ln_c_b': _L1_xattn_in['ln_c_b'], 'L1_xattn_Wq': _L1_xattn_in['Wq'], 'L1_xattn_Wkv': _L1_xattn_in['Wkv'], 'L1_xattn_Wo': _L1_xattn_in['Wo'], 'L1_xattn_bo': _L1_xattn_in['bo'], 'L1_attn_wq': _L1_attn_in['wq'], 'L1_attn_wk': _L1_attn_in['wk'], 'L1_attn_wv': _L1_attn_in['wv'], 'L1_attn_wo': _L1_attn_in['wo'], 'L1_attn_gn_w': _L1_attn_in['gn_w'], 'L1_attn_gn_b': _L1_attn_in['gn_b'], 'L1_ffn_Wg': _L1_ffn_in['Wg'], 'L1_ffn_W_in': _L1_ffn_in['W_in'], 'L1_ffn_W_out': _L1_ffn_in['W_out'], 'L2_attn_Wqkv': _L2_attn_in['Wqkv'], 'L2_attn_bqkv': _L2_attn_in['bqkv'], 'L2_attn_Wo': _L2_attn_in['Wo'], 'L2_attn_bo': _L2_attn_in['bo'], 'L2_attn_wq': _L2_attn_in['wq'], 'L2_attn_wk': _L2_attn_in['wk'], 'L2_ffn_tile_sigs': _L2_ffn_in['tile_sigs'], 'L2_ffn_W': _L2_ffn_in['W'], 'L2_ffn_b': _L2_ffn_in['b'], 'L3_xattn_Wq': _L3_xattn_in['Wq'], 'L3_xattn_bq': _L3_xattn_in['bq'], 'L3_xattn_Wk': _L3_xattn_in['Wk'], 'L3_xattn_bk': _L3_xattn_in['bk'], 'L3_xattn_Wv': _L3_xattn_in['Wv'], 'L3_xattn_bv': _L3_xattn_in['bv'], 'L3_xattn_Wo': _L3_xattn_in['Wo'], 'L3_xattn_bo': _L3_xattn_in['bo'], 'L3_attn_W_zf': _L3_attn_in['W_zf'], 'L3_attn_b_zf': _L3_attn_in['b_zf'], 'L3_attn_W_hf': _L3_attn_in['W_hf'], 'L3_attn_b_hf': _L3_attn_in['b_hf'], 'L3_attn_W_zs': _L3_attn_in['W_zs'], 'L3_attn_b_zs': _L3_attn_in['b_zs'], 'L3_attn_W_hs': _L3_attn_in['W_hs'], 'L3_attn_b_hs': _L3_attn_in['b_hs'], 'L3_attn_W_g': _L3_attn_in['W_g'], 'L3_attn_b_g': _L3_attn_in['b_g'], 'L3_ffn_w_gate': _L3_ffn_in['w_gate'], 'L3_ffn_w_up': _L3_ffn_in['w_up'], 'L3_ffn_w_down': _L3_ffn_in['w_down']}

def reference(x, ctx_1024, mask_Bx1x1xS2_fk0, L0_xattn_Wq, L0_xattn_bq, L0_xattn_Wk, L0_xattn_bk, L0_xattn_Wv, L0_xattn_bv, L0_xattn_Wo, L0_xattn_bo, L0_attn_gamma, L0_attn_beta, L0_attn_Wqkv, L0_attn_Wout, L0_ffn_gW1, L0_ffn_gb1, L0_ffn_gW2, L0_ffn_gb2, L0_ffn_eW1, L0_ffn_eb1, L0_ffn_eW2, L0_ffn_eb2, L1_xattn_ln_l_w, L1_xattn_ln_l_b, L1_xattn_ln_c_w, L1_xattn_ln_c_b, L1_xattn_Wq, L1_xattn_Wkv, L1_xattn_Wo, L1_xattn_bo, L1_attn_wq, L1_attn_wk, L1_attn_wv, L1_attn_wo, L1_attn_gn_w, L1_attn_gn_b, L1_ffn_Wg, L1_ffn_W_in, L1_ffn_W_out, L2_attn_Wqkv, L2_attn_bqkv, L2_attn_Wo, L2_attn_bo, L2_attn_wq, L2_attn_wk, L2_ffn_tile_sigs, L2_ffn_W, L2_ffn_b, L3_xattn_Wq, L3_xattn_bq, L3_xattn_Wk, L3_xattn_bk, L3_xattn_Wv, L3_xattn_bv, L3_xattn_Wo, L3_xattn_bo, L3_attn_W_zf, L3_attn_b_zf, L3_attn_W_hf, L3_attn_b_hf, L3_attn_W_zs, L3_attn_b_zs, L3_attn_W_hs, L3_attn_b_hs, L3_attn_W_g, L3_attn_b_g, L3_ffn_w_gate, L3_ffn_w_up, L3_ffn_w_down):
    import jax
    import jax.numpy as jnp

    def _L0_xattn_ref(query, key, value, Wq, bq, Wk, bk, Wv, bv, Wo, bo):
        import jax, jax.numpy as jnp
        import numpy as np
        B, S, D, H = (4, 512, 256, 16)
        HD = D // H
        b = query.shape[0]
        Q = (query @ Wq + bq).reshape(b, -1, H, HD).transpose(0, 2, 1, 3)
        K = (key @ Wk + bk).reshape(b, -1, H, HD).transpose(0, 2, 1, 3)
        V = (value @ Wv + bv).reshape(b, -1, H, HD).transpose(0, 2, 1, 3)
        energy = jnp.einsum('bhqd,bhkd->bhqk', Q, K) / np.sqrt(HD)
        attn = jax.nn.softmax(energy, axis=-1)
        x = jnp.einsum('bhqk,bhkd->bhqd', attn, V)
        x = x.transpose(0, 2, 1, 3).reshape(b, -1, H * HD)
        return x @ Wo + bo

    def _L0_attn_ref(x, gamma, beta, Wqkv, Wout):
        import jax, jax.numpy as jnp
        import numpy as np
        LN_EPS = 1e-05
        DENOM_EPS = 1e-06
        NUM_HEADS = 16

        def _layer_norm(x, gamma, beta):
            mu = jnp.mean(x, axis=-1, keepdims=True)
            var = jnp.mean(jnp.square(x - mu), axis=-1, keepdims=True)
            return (x - mu) * jax.lax.rsqrt(var + LN_EPS) * gamma + beta
        B, L, D = x.shape
        H = NUM_HEADS
        HD = D // H
        residual = x
        xn = _layer_norm(x, gamma, beta)
        qkv = (xn @ Wqkv).reshape(B, L, 3, H, HD)
        qkv = jnp.transpose(qkv, (2, 0, 3, 1, 4))
        q, k, v = (qkv[0], qkv[1], qkv[2])
        q = jax.nn.elu(q) + 1.0
        k = jax.nn.elu(k) + 1.0
        kv = jnp.einsum('bhld,bhle->bhde', k, v)
        qkv_out = jnp.einsum('bhld,bhde->bhle', q, kv)
        denom = jnp.einsum('bhld,bhd->bhl', q, k.sum(axis=2)) + DENOM_EPS
        out = qkv_out / denom[..., None]
        out = jnp.transpose(out, (0, 2, 1, 3)).reshape(B, L, D)
        return residual + out @ Wout

    def _L0_ffn_ref(hidden_states, gW1, gb1, gW2, gb2, eW1, eb1, eW2, eb2):
        import jax, jax.numpy as jnp
        import numpy as np
        H = 256
        DFF = 1024
        E = 8
        B = 8
        S = 128
        INIT_LAMBDA = 0.2
        x = jnp.transpose(hidden_states, (1, 0, 2))
        h = jax.nn.relu(jnp.einsum('bsh,oh->bso', x, gW1) + gb1)
        gate = jnp.einsum('bsh,eh->bse', h, gW2) + gb2
        g = gate.mean(axis=1)
        W1 = jnp.einsum('be,eoi->boi', g, eW1)
        b1 = g @ eb1
        W2 = jnp.einsum('be,eoi->boi', g, eW2)
        b2 = g @ eb2
        y = jax.nn.relu(jnp.einsum('bsi,boi->bso', x, W1) + b1[:, None, :])
        y = jnp.einsum('bsi,boi->bso', y, W2) + b2[:, None, :]
        return jnp.transpose(y, (1, 0, 2))

    def _L1_xattn_ref(latents, context, ln_l_w, ln_l_b, ln_c_w, ln_c_b, Wq, Wkv, Wo, bo):
        import jax, jax.numpy as jnp
        import numpy as np
        DIM = 256
        H = 16
        D = 64
        INNER = H * D
        EPS = 1e-05

        def layernorm(x, w, b):
            mu = jnp.mean(x, axis=-1, keepdims=True)
            var = jnp.var(x, axis=-1, keepdims=True)
            return (x - mu) * jax.lax.rsqrt(var + EPS) * w + b
        b, n, _ = latents.shape
        s = context.shape[1]
        lat = layernorm(latents, ln_l_w, ln_l_b)
        ctx = layernorm(context, ln_c_w, ln_c_b)
        q = (lat @ Wq).reshape(b, n, H, D).transpose(0, 2, 1, 3)
        kv = ctx @ Wkv
        k, v = jnp.split(kv, 2, axis=-1)
        k = k.reshape(b, s, H, D).transpose(0, 2, 1, 3)
        v = v.reshape(b, s, H, D).transpose(0, 2, 1, 3)
        scale = D ** (-0.5)
        attn = jnp.einsum('bhnd,bhsd->bhns', q, k) * scale
        attn = jnp.clip(attn, -11.0, 11.0)
        attn = jax.nn.softmax(attn, axis=-1)
        out = jnp.einsum('bhns,bhsd->bhnd', attn, v)
        out = out.transpose(0, 2, 1, 3).reshape(b, n, INNER)
        return out @ Wo + bo

    def _L1_attn_ref(x, wq, wk, wv, wo, gn_w, gn_b):
        import jax, jax.numpy as jnp
        import numpy as np
        N_HEAD = 16
        GAMMA_MIN = 0.9
        GAMMA_MAX = 0.999
        GN_EPS = 1e-05

        def _gammas(n_head):
            lo = float(np.log(1.0 - GAMMA_MAX))
            hi = float(np.log(1.0 - GAMMA_MIN))
            return 1.0 - jnp.exp(jnp.linspace(lo, hi, n_head, dtype=jnp.float32))
        B, T, C = x.shape
        H = N_HEAD
        d = C // H
        gammas = _gammas(H)
        q = (x @ wq.T).reshape(B, T, H, d).transpose(0, 2, 1, 3)
        k = (x @ wk.T).reshape(B, T, H, d).transpose(0, 2, 1, 3)
        v = (x @ wv.T).reshape(B, T, H, d).transpose(0, 2, 1, 3)
        pos = jnp.arange(T, dtype=jnp.float32)
        dist = pos[:, None] - pos[None, :]
        causal = dist >= 0
        safe_dist = jnp.where(causal, dist, 0.0)
        D = jnp.where(causal, gammas[:, None, None] ** safe_dist, 0.0)
        scores = jnp.einsum('bhid,bhjd->bhij', q, k) * D
        y = jnp.einsum('bhij,bhjd->bhid', scores, v)
        y = y.transpose(0, 2, 1, 3)
        mean = y.mean(axis=(1, 3), keepdims=True)
        var = y.var(axis=(1, 3), keepdims=True)
        y = (y - mean) * jax.lax.rsqrt(var + GN_EPS)
        y = y.reshape(B, T, C) * gn_w + gn_b
        return y @ wo.T

    def _L1_ffn_ref(x, Wg, W_in, W_out):
        import math
        import jax, jax.numpy as jnp
        import numpy as np
        B, T, H = (4, 512, 256)
        E, K, F = (8, 2, 512)
        CAP_FACTOR = 1.25

        def _moe_forward(x, Wg, W_in, W_out):
            b, t, h = x.shape
            xf = x.reshape(-1, h)
            S = xf.shape[0]
            C = int(math.ceil(K * S / E * CAP_FACTOR))
            logits = xf @ Wg
            probs = jax.nn.softmax(logits, axis=-1)
            top_vals, top_idx = jax.lax.top_k(probs, K)
            flat_idx = top_idx.T.reshape(-1)
            onehot = jax.nn.one_hot(flat_idx, E, dtype=jnp.int32)
            cum = jnp.cumsum(onehot, axis=0) - 1
            loc = jnp.take_along_axis(cum, flat_idx[:, None], axis=1)[:, 0]
            loc = loc.reshape(K, S).T
            keep = loc < C
            gates = top_vals * keep.astype(top_vals.dtype)
            denom = jnp.maximum(gates.sum(-1, keepdims=True), 1e-09)
            gates = gates / denom
            loc_c = jnp.where(keep, loc, C)
            e_flat = top_idx.reshape(-1)
            l_flat = loc_c.reshape(-1)
            xk = jnp.broadcast_to(xf[:, None, :], (S, K, h)).reshape(-1, h)
            xk = jnp.where(keep.reshape(-1, 1), xk, 0.0)
            buf = jnp.zeros((E, C + 1, h), x.dtype).at[e_flat, l_flat].set(xk)
            inp = buf[:, :C]
            hid = jnp.einsum('ech,ehf->ecf', inp, W_in)
            a, g = jnp.split(hid, 2, axis=-1)
            hid = jax.nn.gelu(a, approximate=False) * g
            out_e = jnp.einsum('ecf,efh->ech', hid, W_out)
            out_pad = jnp.concatenate([out_e, jnp.zeros((E, 1, h), out_e.dtype)], axis=1)
            gathered = out_pad[e_flat, l_flat].reshape(S, K, h)
            y = (gathered * gates[..., None]).sum(axis=1)
            return y.reshape(b, t, h)
        return _moe_forward(x, Wg, W_in, W_out)

    def _L2_xattn_ref(query, key, value):
        import jax, jax.numpy as jnp
        import numpy as np
        HIDDEN = 256
        HEADS = 16
        CHUNK = 512
        OVERLAP = 128
        HEAD_DIM = HIDDEN // HEADS
        SCALE = 1.0 / np.sqrt(HEAD_DIM)

        def _attn(q, k, v):
            B, Lq, _ = q.shape
            Lk = k.shape[1]
            qh = q.reshape(B, Lq, HEADS, HEAD_DIM)
            kh = k.reshape(B, Lk, HEADS, HEAD_DIM)
            vh = v.reshape(B, Lk, HEADS, HEAD_DIM)
            scores = jnp.einsum('bqhd,bkhd->bhqk', qh, kh) * SCALE
            probs = jax.nn.softmax(scores, axis=-1)
            out = jnp.einsum('bhqk,bkhd->bqhd', probs, vh)
            return out.reshape(B, Lq, HIDDEN)

        def _chunked_attention(query, key, value):
            B, S, _ = query.shape
            if S <= CHUNK:
                return _attn(query, key, value)
            step = CHUNK - OVERLAP
            chunks = []
            for start in range(0, S, step):
                end = min(start + CHUNK, S)
                ks = max(0, start - OVERLAP)
                ke = min(S, end + OVERLAP)
                chunks.append(_attn(query[:, start:end], key[:, ks:ke], value[:, ks:ke]))
            out = jnp.zeros((B, S, HIDDEN), dtype=query.dtype)
            wsum = jnp.zeros((B, S, 1), dtype=query.dtype)
            n = len(chunks)
            pos = 0
            for i, ch in enumerate(chunks):
                L = ch.shape[1]
                w = np.ones(L, dtype=np.float32)
                f = min(OVERLAP, L)
                if i > 0:
                    w[:f] = np.linspace(0.0, 1.0, f)
                if i < n - 1:
                    w[-f:] = np.linspace(1.0, 0.0, f)
                end = min(pos + L, S)
                a = end - pos
                wj = jnp.asarray(w[:a], dtype=query.dtype)[None, :, None]
                out = out.at[:, pos:end].add(ch[:, :a] * wj)
                wsum = wsum.at[:, pos:end].add(jnp.broadcast_to(wj, (B, a, 1)))
                pos += step
            return out / (wsum + 1e-10)
        return _chunked_attention(query, key, value)

    def _L2_attn_ref(x, Wqkv, bqkv, Wo, bo, wq, wk):
        import jax, jax.numpy as jnp
        import numpy as np
        D_MODEL = 256
        N_HEADS = 16
        D_HEAD = D_MODEL // N_HEADS

        def _rmsnorm(x, w):
            xf = x.astype(jnp.float32)
            rms = jnp.mean(xf * xf, axis=-1, keepdims=True)
            return (xf / jnp.sqrt(rms + 1e-06) * w.astype(jnp.float32)).astype(x.dtype)
        b, s, d = x.shape
        qkv = x @ Wqkv.T + bqkv
        q, k, v = jnp.split(qkv, 3, axis=-1)
        q = q.reshape(b, s, N_HEADS, D_HEAD)
        k = k.reshape(b, s, N_HEADS, D_HEAD)
        v = v.reshape(b, s, N_HEADS, D_HEAD)
        q = _rmsnorm(q, wq)
        k = _rmsnorm(k, wk)
        qf = q.astype(jnp.float32)
        kf = k.astype(jnp.float32)
        vf = v.astype(jnp.float32)
        attn = jnp.einsum('bqhd,bkhd->bhqk', qf, kf)
        attn = jax.nn.softmax(attn, axis=-1)
        z = jnp.einsum('bhqk,bkhd->bqhd', attn, vf).astype(x.dtype)
        z = z.reshape(b, s, d)
        return z @ Wo.T + bo

    def _L2_ffn_ref(x, tile_sigs, W, b):
        import math
        import jax, jax.numpy as jnp
        import numpy as np
        D_CONTENT = 256
        D_POSITION = 32
        NUM_TILES = 8
        BATCH = 8
        SEQ = 512

        def make_pe(seq_len, d_pos):
            pos = jnp.arange(seq_len, dtype=jnp.float32)[:, None]
            div = jnp.exp(jnp.arange(0, d_pos, 2, dtype=jnp.float32) * (-math.log(10000.0) / d_pos))
            ang = pos * div
            pe = jnp.zeros((seq_len, d_pos), dtype=jnp.float32)
            pe = pe.at[:, 0::2].set(jnp.sin(ang))
            pe = pe.at[:, 1::2].set(jnp.cos(ang))
            return pe
        B, S, D = x.shape
        P = tile_sigs.shape[1]
        pe = make_pe(S, P)
        scores = jnp.einsum('sp,tp->st', pe, jnp.sign(tile_sigs))
        idx = jnp.argmax(scores, axis=-1)
        y_all = jnp.einsum('bsd,tod->bsto', x, W) + b
        idx4 = jnp.broadcast_to(idx[None, :, None, None], (B, S, 1, D))
        out = jnp.take_along_axis(y_all, idx4, axis=2)[:, :, 0]
        return out

    def _L3_xattn_ref(Q, K, V, mask, Wq, bq, Wk, bk, Wv, bv, Wo, bo):
        import jax, jax.numpy as jnp
        import numpy as np
        B, S, DIM, H = (4, 512, 256, 16)
        DEPTH = DIM // H

        def _split_heads(x):
            return x.reshape(x.shape[0], x.shape[1], H, DEPTH).transpose(0, 2, 1, 3)
        q = _split_heads(Q @ Wq + bq)
        k = _split_heads(K @ Wk + bk)
        v = _split_heads(V @ Wv + bv)
        logits = jnp.einsum('bhqd,bhkd->bhqk', q, k) / jnp.sqrt(jnp.float32(DEPTH))
        logits = logits + mask * -1000000000.0
        attn = jax.nn.softmax(logits, axis=-1)
        ctx = jnp.einsum('bhqk,bhkd->bhqd', attn, v)
        ctx = ctx.transpose(0, 2, 1, 3).reshape(Q.shape[0], Q.shape[1], DIM)
        return ctx @ Wo + bo

    def _L3_attn_ref(x, W_zf, b_zf, W_hf, b_hf, W_zs, b_zs, W_hs, b_hs, W_g, b_g):
        import jax, jax.numpy as jnp
        import numpy as np
        from jax import lax
        B, S, D_IN = (4, 1024, 256)
        D_FAST, D_SLOW = (128, 128)
        Z_BIAS_FAST, Z_BIAS_SLOW = (2.0, -2.0)

        def _binop(q_i, q_j):
            a_i, b_i = q_i
            a_j, b_j = q_j
            return (a_i * a_j, a_j * b_i + b_j)

        def parallel_scan(a, b):
            _, h = lax.associative_scan(_binop, (a, b), axis=1)
            return h
        z_fast = jax.nn.sigmoid(jnp.einsum('bsd,df->bsf', x, W_zf) + b_zf)
        h_tilde_fast = jnp.einsum('bsd,df->bsf', x, W_hf) + b_hf
        h_fast = parallel_scan(1.0 - z_fast, z_fast * h_tilde_fast)
        z_slow = jax.nn.sigmoid(jnp.einsum('bsd,df->bsf', x, W_zs) + b_zs)
        h_tilde_slow = jnp.einsum('bsd,df->bsf', x, W_hs) + b_hs
        h_slow = parallel_scan(1.0 - z_slow, z_slow * h_tilde_slow)
        h_combined = jnp.concatenate([h_fast, h_slow], axis=-1)
        gate = jax.nn.sigmoid(jnp.einsum('bsc,cd->bsd', h_combined, W_g) + b_g)
        return gate * h_combined

    def _L3_ffn_ref(x, w_gate, w_up, w_down):
        import jax, jax.numpy as jnp
        import numpy as np
        DIM = 256
        HIDDEN = 768
        SCALE = 1.0 / 127.0

        def _dequant(w_int, dtype):
            return w_int.astype(dtype) * jnp.asarray(SCALE, dtype)
        wg = _dequant(w_gate, x.dtype)
        wu = _dequant(w_up, x.dtype)
        wd = _dequant(w_down, x.dtype)
        gate = jnp.einsum('bsd,hd->bsh', x, wg)
        up = jnp.einsum('bsd,hd->bsh', x, wu)
        h = jax.nn.silu(gate) * up
        return jnp.einsum('bsh,dh->bsd', h, wd)
    x = x + _L0_xattn_ref(_layernorm(x, axis=-1), ctx_1024, ctx_1024, L0_xattn_Wq, L0_xattn_bq, L0_xattn_Wk, L0_xattn_bk, L0_xattn_Wv, L0_xattn_bv, L0_xattn_Wo, L0_xattn_bo)
    x = x + _L0_attn_ref(_layernorm(x, axis=-1), L0_attn_gamma, L0_attn_beta, L0_attn_Wqkv, L0_attn_Wout)
    x = x + _L0_ffn_ref(_layernorm(x, axis=-1), L0_ffn_gW1, L0_ffn_gb1, L0_ffn_gW2, L0_ffn_gb2, L0_ffn_eW1, L0_ffn_eb1, L0_ffn_eW2, L0_ffn_eb2)
    x = x + _L1_xattn_ref(_layernorm(x, axis=-1), ctx_1024, L1_xattn_ln_l_w, L1_xattn_ln_l_b, L1_xattn_ln_c_w, L1_xattn_ln_c_b, L1_xattn_Wq, L1_xattn_Wkv, L1_xattn_Wo, L1_xattn_bo)
    x = x + _L1_attn_ref(_layernorm(x, axis=-1), L1_attn_wq, L1_attn_wk, L1_attn_wv, L1_attn_wo, L1_attn_gn_w, L1_attn_gn_b)
    x = x + _L1_ffn_ref(_layernorm(x, axis=-1), L1_ffn_Wg, L1_ffn_W_in, L1_ffn_W_out)
    x = x + _L2_xattn_ref(_layernorm(x, axis=-1), ctx_1024, ctx_1024)
    x = x + _L2_attn_ref(_layernorm(x, axis=-1), L2_attn_Wqkv, L2_attn_bqkv, L2_attn_Wo, L2_attn_bo, L2_attn_wq, L2_attn_wk)
    x = x + _L2_ffn_ref(_layernorm(x, axis=-1), L2_ffn_tile_sigs, L2_ffn_W, L2_ffn_b)
    x = x + _L3_xattn_ref(_layernorm(x, axis=-1), ctx_1024, ctx_1024, mask_Bx1x1xS2_fk0, L3_xattn_Wq, L3_xattn_bq, L3_xattn_Wk, L3_xattn_bk, L3_xattn_Wv, L3_xattn_bv, L3_xattn_Wo, L3_xattn_bo)
    x = x + _L3_attn_ref(_layernorm(x, axis=-1), L3_attn_W_zf, L3_attn_b_zf, L3_attn_W_hf, L3_attn_b_hf, L3_attn_W_zs, L3_attn_b_zs, L3_attn_W_hs, L3_attn_b_hs, L3_attn_W_g, L3_attn_b_g)
    x = x + _L3_ffn_ref(_layernorm(x, axis=-1), L3_ffn_w_gate, L3_ffn_w_up, L3_ffn_w_down)
    return x

_drawn_inputs = setup_inputs


def setup_inputs(seed=0):
    import zlib

    import numpy as np

    out = dict(_drawn_inputs(seed))
    spreads = {'L0_xattn_bq': (0.0, 0.1),
     'L0_xattn_bk': (0.0, 2.0),
     'L0_xattn_bv': (0.0, 0.1),
     'L0_xattn_bo': (0.0, 0.1),
     'L0_attn_gamma': (1.0, 0.2),
     'L0_attn_beta': (0.0, 0.1),
     'L0_ffn_gb1': (0.0, 0.314),
     'L0_ffn_gb2': (0.20000000298023224, 0.2),
     'L1_xattn_ln_l_w': (1.0, 0.2),
     'L1_xattn_ln_l_b': (0.0, 0.1),
     'L1_xattn_ln_c_w': (1.0, 0.2),
     'L1_xattn_ln_c_b': (0.0, 0.1),
     'L1_xattn_bo': (0.0, 0.1),
     'L1_attn_gn_w': (1.0, 0.2),
     'L1_attn_gn_b': (0.0, 0.1),
     'L2_attn_wq': (1.0, 0.2),
     'L2_attn_wk': (1.0, 0.2),
     'L3_xattn_bq': (0.0, 2.0),
     'L3_xattn_bk': (0.0, 2.0),
     'L3_xattn_bv': (0.0, 0.505),
     'L3_xattn_bo': (0.0, 0.1),
     'L3_attn_b_zf': (2.0, 0.6),
     'L3_attn_b_hf': (0.0, 0.473),
     'L3_attn_b_zs': (-2.0, 0.6),
     'L3_attn_b_hs': (0.0, 0.457),
     'L3_attn_b_g': (0.0, 0.8)}
    factors = {'L0_ffn_gW1': 4.31,
     'L2_attn_bqkv': 6.664,
     'L2_attn_bo': 8.0,
     'L2_ffn_b': 3.009,
     'L3_xattn_Wq': 8.0,
     'L3_xattn_Wk': 8.0,
     'L3_attn_W_zf': 8.0,
     'L3_attn_W_zs': 8.0,
     'L3_attn_W_g': 8.0}
    for name, (base, spread) in spreads.items():
        noise = np.random.default_rng([zlib.crc32(name.encode()), seed]).standard_normal(out[name].shape)
        drawn = base * np.exp(spread * noise) if base else spread * noise
        out[name] = jnp.asarray(drawn.astype(out[name].dtype))
    for name, factor in factors.items():
        out[name] = (out[name] * factor).astype(out[name].dtype)
    return out
```

```python
from contextlib import ExitStack, contextmanager

import concourse.bass as bass
from concourse import mybir

ALU = mybir.AluOpType
ACT = mybir.ActivationFunctionType
F32 = mybir.dt.float32
I32 = mybir.dt.int32
AX_X = mybir.AxisListType.X

P = 128
BATCH = 32
SEQ = 64
DIM = 256
KC = DIM // P
TOKENS = BATCH * SEQ
TILES = TOKENS // P
NKEY = 256
HEADS = 16
EPS = 1e-5


_stages, _names = [], {}


@contextmanager
def stage(nc):
    sems = []
    _stages.append(len(_stages))
    tag = f"s{len(_stages)}"

    def unique(name):
        _names[name] = _names.get(name, 0) + 1
        return f"{tag}_{name}_{_names[name]}"

    with ExitStack() as ctx:
        def sb(name, shape, dt=F32):
            return ctx.enter_context(nc.sbuf_tensor(unique(name), shape, dt))

        def ps(name, shape, dt=F32):
            return ctx.enter_context(nc.psum_tensor(unique(name), shape, dt))

        def sem(name):
            s = nc.alloc_semaphore(unique(name))
            sems.append(s)
            return s

        yield sb, ps, sem
    nc.clear_and_free_semaphores(sems)
    nc.all_engine_barrier()


class Chain:

    def __init__(self, eng, sem, base=0):
        self.eng, self.sem, self.base, self.n = eng, sem, base, 0

    def __call__(self, ins):
        self.n += 1
        ins.then_inc(self.sem, 1)
        self.eng.wait_ge(self.sem, self.base + self.n)


def rows_to_sbuf(w):
    return w.rearrange("(c p) n -> p c n", p=P)


def row(v):
    return v.rearrange("(a n) -> a n", a=1)


def layernorm_transposed(nc, X, XNT, ident, passes=1, affine=None, residual=False, load=None, store=None):
    with stage(nc) as (sb, ps, sem):
        XN = sb("ln_xn", [P, TILES, DIM])
        stats = sb("ln_stats", [P, TILES, 6])
        diff = sb("ln_diff", [P, TILES])
        mean = sb("ln_mean", [P, TILES])
        var = sb("ln_var", [P, TILES])
        std = sb("ln_std", [P, TILES])
        rstd = sb("ln_rstd", [P, TILES])
        col = sb("ln_col", [P, 2, KC])
        flip = [[ps("ln_flip", [P, 512]) for _ in range(KC)] for _ in range(2)]
        s_var, s_std, s_dve, s_stat = sem("ln_var_ready"), sem("ln_std_ready"), sem("ln_dve_step"), sem("ln_stats_done")
        s_norm, s_flip, s_out, s_col = sem("ln_normed"), sem("ln_flipped"), sem("ln_stored"), sem("ln_columns_loaded")
        s_norm2, s_in, s_dram = sem("ln_pass_normed"), sem("ln_rows_loaded"), sem("ln_dram_stored")
        with nc.Block() as block:
            @block.sync
            def _(sp):
                if load is not None:
                    sp.dma_start(X[:, :, :], load).then_inc(s_in, 16)
                if affine:
                    for n, v in enumerate(affine):
                        sp.dma_start(col[:, n, :], v).then_inc(s_col, 16)
                if store is not None:
                    sp.wait_ge(s_out, TILES * KC)
                    for c in range(KC):
                        sp.dma_start(store[:, c], XNT[:, c, :].rearrange("p (b s) -> p b s", s=NKEY)).then_inc(s_dram, 16)
                    sp.wait_ge(s_dram, 16 * KC)

            @block.vector
            def _(dve):
                link = Chain(dve, s_dve)
                if load is not None:
                    dve.wait_ge(s_in, 16)
                for n in range(passes):
                    src = XN if n else X
                    with dve.Fori(0, TILES) as t:
                        nc.vector.bn_stats(stats[:, t, :], src[:, t, :]).then_inc(s_stat, 1)
                    dve.wait_ge(s_stat, TILES * (n + 1))
                    link(nc.vector.tensor_tensor(mean[:, :], stats[:, :, 1], stats[:, :, 4], ALU.add))
                    link(nc.vector.tensor_scalar(mean[:, :], mean[:, :], 0.5, None, ALU.mult))
                    link(nc.vector.tensor_tensor(diff[:, :], stats[:, :, 1], stats[:, :, 4], ALU.subtract))
                    link(nc.vector.tensor_tensor(diff[:, :], diff[:, :], diff[:, :], ALU.mult))
                    link(nc.vector.tensor_scalar(diff[:, :], diff[:, :], DIM / 4.0, None, ALU.mult))
                    link(nc.vector.tensor_tensor(var[:, :], stats[:, :, 2], stats[:, :, 5], ALU.add))
                    link(nc.vector.tensor_tensor(var[:, :], var[:, :], diff[:, :], ALU.add))
                    nc.vector.tensor_scalar(var[:, :], var[:, :], 1.0 / DIM, EPS, ALU.mult, ALU.add).then_inc(s_var, 1)
                    dve.wait_ge(s_std, n + 1)
                    link(nc.vector.reciprocal(rstd[:, :], std[:, :]))
                    done = s_norm if n == passes - 1 else s_norm2
                    with dve.Fori(0, TILES) as t:
                        nc.vector.tensor_scalar(XN[:, t, :], src[:, t, :], mean[:, bass.ds(t, 1)],
                                                rstd[:, bass.ds(t, 1)], ALU.subtract, ALU.mult).then_inc(done, 1)
                    if n < passes - 1:
                        dve.wait_ge(s_norm2, TILES)
                        if residual:
                            for h in range(2):
                                half = slice(h * TILES // 2, (h + 1) * TILES // 2)
                                link(nc.vector.tensor_tensor(X[:, half, :], X[:, half, :], XN[:, half, :], ALU.add))

            @block.tensor
            def _(pe):
                for t in range(TILES):
                    pe.wait_ge(s_norm, t + 1)
                    if t >= 2:
                        pe.wait_ge(s_out, KC * (t - 1))
                    for c in range(KC):
                        last = nc.tensor.transpose(flip[t % 2][c][:, 0:P], XN[:, t, c * P:(c + 1) * P], ident[:, :])
                    last.then_inc(s_flip, 1)

            @block.scalar
            def _(act):
                for n in range(passes):
                    act.wait_ge(s_var, n + 1)
                    nc.scalar.activation(std[:, :], var[:, :], ACT.Sqrt).then_inc(s_std, 1)
                if affine:
                    act.wait_ge(s_col, 32)
                with act.Fori(0, TILES // 2) as i:
                    for u in range(2):
                        act.wait_ge(s_flip, i * 2 + (u + 1))
                        for c in range(KC):
                            dst = XNT[:, c, bass.ds(i * 2 * P + u * P, P)]
                            if affine:
                                nc.scalar.activation(dst, flip[u][c][:, 0:P], ACT.Identity, bias=col[:, 1, c:c + 1],
                                                     scale=col[:, 0, c:c + 1]).then_inc(s_out, 1)
                            else:
                                nc.scalar.copy(dst, flip[u][c][:, 0:P]).then_inc(s_out, 1)


def project_transposed(nc, XNT, dst, w, bias, chunks):
    TC = 512
    with stage(nc) as (sb, ps, sem):
        W = sb("pj_w", [P, KC, chunks * P])
        B = sb("pj_b", [P, chunks])
        out = [ps("pj_out", [P, TC]) for _ in range(4)]
        s_w, s_mm, s_st = sem("pj_w_loaded"), sem("pj_multiplied"), sem("pj_stored")
        jobs = [(m, t) for m in range(chunks) for t in range(TOKENS // TC)]
        with nc.Block() as block:
            @block.sync
            def _(sp):
                sp.dma_start(W[:, :, :], rows_to_sbuf(w)).then_inc(s_w, 16)
                if bias is not None:
                    sp.dma_start(B[:, :], bias).then_inc(s_w, 16)

            @block.tensor
            def _(pe):
                pe.wait_ge(s_w, 16 if bias is None else 32)
                for n, (m, t) in enumerate(jobs):
                    if n >= 4:
                        pe.wait_ge(s_st, n - 3)
                    for c in range(KC):
                        last = nc.tensor.matmul(out[n % 4][:, :], W[:, c, m * P:(m + 1) * P],
                                                XNT[:, c, t * TC:(t + 1) * TC], start=(c == 0), stop=(c == KC - 1))
                    last.then_inc(s_mm, 1)

            @block.vector
            def _(dve):
                if bias is not None:
                    dve.wait_ge(s_w, 32)
                for n, (m, t) in enumerate(jobs):
                    dve.wait_ge(s_mm, n + 1)
                    if bias is not None:
                        last = nc.vector.tensor_scalar(dst[:, m, t * TC:(t + 1) * TC], out[n % 4][:, :], B[:, m:m + 1],
                                                       None, ALU.add)
                    else:
                        last = nc.vector.tensor_copy(dst[:, m, t * TC:(t + 1) * TC], out[n % 4][:, :])
                    last.then_inc(s_st, 1)


def cross_attention(nc, X, QT, ident, ones, spread_mask, ctxT, head, wkv=None, bk=None, bv=None, ctx=None,
                    wo=None, bo=None, mask=None, clip=None):
    inner = HEADS * head
    chunks = inner // P
    PAIR = 2 * head
    HPC = P // head
    STEPS = 4
    MV = bool(clip or mask is not None)
    with stage(nc) as (sb, ps, sem):
        CT = [sb("ca_ctxT", [P, KC, NKEY]) for _ in range(2)]
        KT = [sb("ca_kT", [P, chunks, NKEY]) for _ in range(2)] if wkv is not None else CT
        V = [sb("ca_v", [P, 2, 8, PAIR + 1]) for _ in range(2)]
        CN = [sb("ca_ctx", [P, 2, NKEY]) for _ in range(2)] if wkv is None else None
        QB = [sb("ca_q_spread", [P, 4, 2, SEQ]) for _ in range(STEPS)]
        PR = [sb("ca_probs", [P, 4, NKEY]) for _ in range(2)]
        SC = [sb("ca_scores_moved", [P, 4, NKEY]) for _ in range(2)] if MV else None
        PT = [sb("ca_probsT", [P, 8, P]) for _ in range(2)]
        nmax = [sb("ca_neg_max", [P, 4]) for _ in range(2)]
        rsum = [sb("ca_inv_sum", [P, 4]) for _ in range(2)]
        A = sb("ca_attended", [P, inner])
        AT = sb("ca_attendedT", [P, chunks, P])
        SM = sb("ca_spread_mask", [P, HPC])
        if wkv is not None:
            W = sb("ca_wkv", [P, KC, 2 * inner])
        if bk is not None:
            BK = sb("ca_bk", [P, chunks])
            BV = sb("ca_bv", [P, chunks])
        if wo is not None:
            WO = sb("ca_wo", [P, chunks, DIM])
            BO = sb("ca_bo", [1, DIM])
        if mask is not None:
            MK = [sb("ca_mask", [P, NKEY]) for _ in range(2)]
            MV9 = sb("ca_mask_factor", [P, 1])
            MB = [sb("ca_mask_added", [P, NKEY]) for _ in range(2)]
        psS = [ps("ca_scores", [P, 4, NKEY]) for _ in range(2)]
        psT = ps("ca_probs_flipped", [P, 8, P])
        psA = ps("ca_projected", [P, 2, NKEY])
        WIDE = PAIR + 1 <= 64
        psO = ps("ca_out", [P, 512])
        OP = 4 if WIDE else 2
        OR = 4 // OP

        s_w = sem("weights_loaded")
        s_ct = [sem(f"ctx{u}_loaded") for u in range(2)]
        s_mk = [sem(f"mask{u}_loaded") for u in range(2)]
        s_mb = sem("mask_scaled")
        s_kp, s_kr, s_vp, s_vr = sem("k_projected"), sem("k_ready"), sem("v_projected"), sem("v_ready")
        s_one = sem("v_ones_set")
        s_q, s_s, s_mv, s_mx = sem("queries_spread"), sem("scores_ready"), sem("scores_moved"), sem("max_ready")
        s_e, s_t, s_tc = sem("probs_ready"), sem("probs_flipped"), sem("probsT_ready")
        s_pv, s_rs, s_o = sem("attended"), sem("inv_sum_ready"), sem("attended_stored")
        s_at, s_atc, s_y, s_x = sem("attended_flipped"), sem("attendedT_ready"), sem("out_projected"), sem("x_updated")
        s_vp2, s_pv2 = sem("v_part_projected"), sem("attended_part")
        s_free = s_mv if MV else s_e
        KB = chunks * NKEY // 512
        assert chunks in (2, 8)

        with nc.Block() as block:
            @block.sync
            def _(sp):
                nw = 1
                sp.dma_start(SM[:, :], spread_mask).then_inc(s_w, 16)
                if wkv is not None:
                    sp.dma_start(W[:, :, :], rows_to_sbuf(wkv)).then_inc(s_w, 16)
                if bk is not None:
                    sp.dma_start(BK[:, :], bk).then_inc(s_w, 16)
                    sp.dma_start(BV[:, :], bv).then_inc(s_w, 16)
                if wo is not None:
                    sp.dma_start(WO[:, :, :], rows_to_sbuf(wo)).then_inc(s_w, 16)
                    sp.dma_start(BO[:, :], row(bo)).then_inc(s_w, 16)
                sp.sem_inc(s_vp, 2)
                if mask is not None:
                    sp.sem_inc(s_mb, 2)
                with sp.Fori(0, TILES) as i:
                    for u in range(2):
                        if wkv is not None:
                            sp.wait_ge(s_vp, i * 2 + (u + 1))
                        else:
                            sp.wait_ge(s_s, i * STEPS + (2 * u + 2))
                        sp.dma_start(CT[u][:, :, :], ctxT[i, u].rearrange("(c p) s -> p c s", p=P)).then_inc(s_ct[u], 16)
                        if wkv is None:
                            sp.dma_start(CN[u][:, :, :], ctx[i, u].rearrange("(c p) d -> p c d", p=P)).then_inc(s_ct[u], 16)
                        if mask is not None:
                            sp.wait_ge(s_mb, i * 2 + (u + 1))
                            sp.dma_start(MK[u][:, :], mask[i, u].partition_broadcast(P)).then_inc(s_mk[u], 16)

            NW = 16 * (1 + (wkv is not None) + 2 * (bk is not None) + 2 * (wo is not None))
            CL = 16 * (2 if wkv is None else 1)

            @block.gpsimd
            def _(pool):
                for u in range(2):
                    nc.gpsimd.memset(V[u][:, :, :, PAIR:PAIR + 1], 1.0).then_inc(s_one, 1)
                if mask is not None:
                    nc.gpsimd.memset(MV9[:, :], -1e9).then_inc(s_one, 1)
                    pool.wait_ge(s_one, 3)
                pool.wait_ge(s_w, NW)
                pool.sem_inc(s_s, STEPS)
                if MV:
                    pool.sem_inc(s_mv, 2)
                with pool.Fori(0, TILES) as i:
                    for u in range(2):
                        if wkv is None:
                            pool.wait_ge(s_ct[u], (i + 1) * CL)
                            pool.wait_ge(s_pv, i * STEPS + (2 * u + 2))
                            for c in range(2):
                                last = nc.gpsimd.tensor_tensor(V[u][:, c, :, 0:PAIR],
                                                               CN[u][:, c, :].rearrange("p (a d) -> p a d", a=8),
                                                               ones[:, 0:1].unsqueeze(2).broadcast_to([P, 8, PAIR]), ALU.mult)
                            last.then_inc(s_vr, 1)
                        if mask is not None:
                            pool.wait_ge(s_mk[u], (i + 1) * 16)
                            pool.wait_ge(s_mv, i * STEPS + 2)
                            nc.gpsimd.tensor_tensor(MB[u][:, :], MK[u][:, :], MV9[:, :].broadcast_to([P, NKEY]), ALU.mult).then_inc(s_mb, 1)
                        for g in range(2):
                            n = 2 * u + g
                            pool.wait_ge(s_s, i * STEPS + (n + 1))
                            tok = bass.ds(i * P + u * SEQ, SEQ)
                            if chunks == 2:
                                q = QT[:, g, tok].unsqueeze(1).broadcast_to([P, 8, SEQ])
                                m = SM[:, :].unsqueeze(2).broadcast_to([P, 8, SEQ])
                                o = QB[n][:, :, :, :].rearrange("p a b q -> p (a b) q")
                                nc.gpsimd.tensor_tensor(o, q, m, ALU.mult).then_inc(s_q, 1)
                            else:
                                for h in range(2):
                                    q = QT[:, 4 * g:4 * g + 4, tok]
                                    m = SM[:, h:h + 1].unsqueeze(2).broadcast_to([P, 4, SEQ])
                                    last = nc.gpsimd.tensor_tensor(QB[n][:, :, h, :], q, m, ALU.mult)
                                last.then_inc(s_q, 1)

            @block.tensor
            def _(pe):
                pe.wait_ge(s_w, NW)
                pe.wait_ge(s_one, 2)
                pe.sem_inc(s_x, 1)
                pe.sem_inc(s_e, 2)
                pe.sem_inc(s_tc, 1)
                pe.sem_inc(s_o, 1)
                with pe.Fori(0, TILES) as i:
                    pe.wait_ge(s_x, i + 1)
                    def project(u):
                        pe.wait_ge(s_ct[u], (i + 1) * 16)
                        for k in range(KB):
                            if u or k:
                                if k:
                                    pe.wait_ge(s_kr, i * 2 * KB + (u * KB + k))
                                else:
                                    pe.wait_ge(s_vr, i * 2 * KB + u * KB)
                            for j in range(2):
                                m = 2 * k + j
                                for c in range(KC):
                                    last = nc.tensor.matmul(psA[:, j, :], W[:, c, m * P:(m + 1) * P], CT[u][:, c, :],
                                                            start=(c == 0), stop=(c == KC - 1))
                            last.then_inc(s_kp, 1)
                        for k in range(KB):
                            if k:
                                pe.wait_ge(s_vr, i * 2 * KB + (u * KB + k))
                            else:
                                pe.wait_ge(s_kr, i * 2 * KB + (u + 1) * KB)
                            if chunks == 2:
                                for j in range(2):
                                    for c in range(KC):
                                        last = nc.tensor.matmul(psA[:, j, :], CT[u][:, c, j * P:(j + 1) * P],
                                                                W[:, c, inner:2 * inner], start=(c == 0), stop=(c == KC - 1))
                            else:
                                j, hf = k // 2, k % 2
                                for c in range(KC):
                                    last = nc.tensor.matmul(psA[:, :, :].rearrange("p a b -> p (a b)"),
                                                            CT[u][:, c, j * P:(j + 1) * P],
                                                            W[:, c, inner + hf * 512:inner + (hf + 1) * 512],
                                                            start=(c == 0), stop=(c == KC - 1))
                            if k < KB - 1:
                                last.then_inc(s_vp2, 1)
                            else:
                                last.then_inc(s_vp, 1)

                    def scores(n):
                        u, g = n // 2, n % 2
                        pe.wait_ge(s_q, i * STEPS + (n + 1))
                        if wkv is not None:
                            pe.wait_ge(s_kr, i * 2 * KB + (u + 1) * KB)
                        pe.wait_ge(s_free, i * STEPS + (n + 1))
                        for a in range(4):
                            k = KT[u][:, g, :] if chunks == 2 else KT[u][:, 4 * g + a, :]
                            last = nc.tensor.matmul(psS[n % 2][:, a, :], QB[n][:, a, :, :].rearrange("p b q -> p (b q)"), k,
                                                    start=True, stop=True)
                        last.then_inc(s_s, 1)

                    def flip(n):
                        pe.wait_ge(s_e, i * STEPS + (n + 3))
                        pe.wait_ge(s_tc, i * STEPS + (n + 1))
                        for a in range(4):
                            for c in range(2):
                                last = nc.tensor.transpose(psT[:, 2 * a + c, :], PR[n % 2][:, a, c * P:(c + 1) * P], ident[:, :])
                        last.then_inc(s_t, 1)

                    def attend(n):
                        u, g = n // 2, n % 2
                        pe.wait_ge(s_tc, i * STEPS + (n + 2))
                        if g == 0:
                            pe.wait_ge(s_vr, (i * 2 * KB + (u + 1) * KB) if wkv is not None else (i * 2 + (u + 1)))
                        for r in range(OR):
                            pe.wait_ge(s_o, i * STEPS * OR + (n * OR + r + 1))
                            for a in range(OP):
                                pr = r * OP + a
                                for c in range(2):
                                    last = nc.tensor.matmul(psO[:, a * (PAIR + 1):(a + 1) * (PAIR + 1)], PT[n % 2][:, 2 * pr + c, :],
                                                            V[u][:, c, 4 * g + pr, :], start=(c == 0), stop=(c == 1))
                            last.then_inc(s_pv if r == OR - 1 else s_pv2, 1)

                    if wkv is not None:
                        project(0)
                        project(1)
                    else:
                        for u in range(2):
                            pe.wait_ge(s_ct[u], (i + 1) * CL)
                    scores(0)
                    for n in range(STEPS):
                        if n + 1 < STEPS:
                            scores(n + 1)
                        flip(n)
                        attend(n)
                    if wo is not None:
                        pe.wait_ge(s_o, (i + 1) * STEPS * OR + 1)
                        pa = psA[:, :, :].rearrange("p a b -> p (a b)")
                        for r in range(chunks // 4 or 1):
                            nn = min(4, chunks)
                            if r:
                                pe.wait_ge(s_atc, i * (chunks // 4 or 1) + r)
                            for c in range(nn):
                                last = nc.tensor.transpose(pa[:, c * P:(c + 1) * P], A[:, (r * nn + c) * P:(r * nn + c + 1) * P], ident[:, :])
                            last.then_inc(s_at, 1)
                        pe.wait_ge(s_atc, (i + 1) * (chunks // 4 or 1))
                        for c in range(chunks):
                            nc.tensor.matmul(pa[:, 0:DIM], AT[:, c, :], WO[:, c, :], start=(c == 0), stop=False)
                        nc.tensor.matmul(pa[:, 0:DIM], ones[0:1, :], BO[:, :], start=False, stop=True).then_inc(s_y, 1)

            @block.scalar
            def _(act):
                act.wait_ge(s_w, NW)
                act.sem_inc(s_t, 2)
                with act.Fori(0, TILES) as i:
                    def keys(u):
                        for k in range(KB):
                            act.wait_ge(s_kp, i * 2 * KB + (u * KB + k + 1))
                            if bk is not None:
                                for j in range(2):
                                    last = nc.scalar.activation(KT[u][:, 2 * k + j, :], psA[:, j, :], ACT.Identity,
                                                                bias=BK[:, 2 * k + j:2 * k + j + 1])
                            else:
                                last = nc.scalar.copy(KT[u][:, 2 * k:2 * k + 2, :], psA[:, :, :])
                            last.then_inc(s_kr, 1)

                    if wkv is not None:
                        keys(0)
                        keys(1)
                    for n in range(STEPS):
                        act.wait_ge(s_t, i * STEPS + (n + 1))
                        if clip:
                            act.wait_ge(s_mv, i * STEPS + (n + 3))
                            nc.scalar.activation(PR[n % 2][:, :, :], SC[n % 2][:, :, :], ACT.Exp).then_inc(s_e, 1)
                        else:
                            act.wait_ge(s_mx, i * STEPS + (n + 1))
                            for a in range(4):
                                src = SC[n % 2] if MV else psS[n % 2]
                                last = nc.scalar.activation(PR[n % 2][:, a, :], src[:, a, :], ACT.Exp,
                                                            bias=nmax[n % 2][:, a:a + 1])
                            last.then_inc(s_e, 1)
                        if mask is not None:
                            act.wait_ge(s_t, i * STEPS + (n + 3))
                            act.wait_ge(s_pv, i * STEPS + (n + 1))
                            nc.scalar.copy(PT[n % 2][:, :, :], psT[:, :, :]).then_inc(s_tc, 1)
                    if wo is not None:
                        for r in range(chunks // 4 or 1):
                            nn = min(4, chunks)
                            act.wait_ge(s_at, i * (chunks // 4 or 1) + (r + 1))
                            if bk is not None:
                                for c in range(nn):
                                    last = nc.scalar.activation(AT[:, c, :], psA[:, :, :].rearrange("p a b -> p (a b)")[:, c * P:(c + 1) * P],
                                                                ACT.Identity, bias=BV[:, c:c + 1])
                            else:
                                last = nc.scalar.copy(AT[:, r * nn:(r + 1) * nn, :].rearrange("p a b -> p (a b)"),
                                                      psA[:, :, :].rearrange("p a b -> p (a b)")[:, 0:nn * P])
                            last.then_inc(s_atc, 1)

            @block.vector
            def _(dve):
                dve.sem_inc(s_pv, 2 if wkv is not None else STEPS)
                PC = 2 if wkv is not None else STEPS
                with dve.Fori(0, TILES) as i:
                    def values(u):
                        for k in range(KB):
                            if k < KB - 1:
                                dve.wait_ge(s_vp2, i * 2 * (KB - 1) + (u * (KB - 1) + k + 1))
                            else:
                                dve.wait_ge(s_vp, i * 2 + (u + 3))
                            if chunks == 2:
                                for c in range(2):
                                    last = nc.vector.tensor_copy(V[u][:, c, :, 0:PAIR], psA[:, c, :].rearrange("p (a d) -> p a d", a=8))
                            else:
                                j, hf = k // 2, k % 2
                                last = nc.vector.tensor_copy(V[u][:, j, 4 * hf:4 * hf + 4, 0:PAIR],
                                                             psA[:, :, :].rearrange("p a b -> p (a b)").rearrange("p (a d) -> p a d", a=4))
                            last.then_inc(s_vr, 1)

                    def take(n):
                        dve.wait_ge(s_s, i * STEPS + (n + 1) + STEPS)
                        if MV:
                            dve.wait_ge(s_e, i * STEPS + (n + 1))
                        if clip:
                            nc.vector.tensor_scalar(SC[n % 2][:, :, :], psS[n % 2][:, :, :], -clip, clip, ALU.max,
                                                    ALU.min).then_inc(s_mv, 1)
                            return
                        if mask is not None:
                            if n % 2 == 0:
                                dve.wait_ge(s_mb, i * 2 + (n // 2 + 3))
                            nc.vector.tensor_tensor(SC[n % 2][:, :, :], psS[n % 2][:, :, :],
                                                    MB[n // 2][:, :].unsqueeze(1).broadcast_to([P, 4, NKEY]), ALU.add).then_inc(s_mv, 1)
                            dve.wait_ge(s_mv, i * STEPS + (n + 3))
                        src = SC[n % 2] if MV else psS[n % 2]
                        nc.vector.tensor_reduce(nmax[n % 2][:, :], src[:, :, :], AX_X, ALU.max, negate=True).then_inc(s_mx, 1)

                    def copy_flipped(n):
                        dve.wait_ge(s_t, i * STEPS + (n + 3))
                        dve.wait_ge(s_pv, i * STEPS + (n + 1) + PC - 2)
                        nc.vector.tensor_copy(PT[n % 2][:, :, :], psT[:, :, :]).then_inc(s_tc, 1)

                    def store(n):
                        u, g = n // 2, n % 2
                        for r in range(OR):
                            if r < OR - 1:
                                dve.wait_ge(s_pv2, i * STEPS * (OR - 1) + (n * (OR - 1) + r + 1))
                            else:
                                dve.wait_ge(s_pv, i * STEPS + (n + 1) + PC)
                            O = psO[:, 0:OP * (PAIR + 1)].rearrange("p (a w) -> p a w", a=OP)
                            R = rsum[n % 2][:, r * OP:(r + 1) * OP]
                            nc.vector.reciprocal(R, O[:, :, PAIR]).then_inc(s_rs, 1)
                            dve.wait_ge(s_rs, i * STEPS * OR + (n * OR + r + 1))
                            for h in range(2):
                                dst = A[u * SEQ:(u + 1) * SEQ, :].rearrange("p (a b d) -> p a b d", a=8, b=2)[
                                    :, 4 * g + r * OP:4 * g + (r + 1) * OP, h, :]
                                last = nc.vector.tensor_tensor(
                                    dst, O[h * SEQ:(h + 1) * SEQ, :, h * head:(h + 1) * head],
                                    R[h * SEQ:(h + 1) * SEQ, :].unsqueeze(2).broadcast_to([SEQ, OP, head]), ALU.mult)
                            last.then_inc(s_o, 1)

                    if wkv is not None:
                        values(0)
                        values(1)
                    take(0)
                    for n in range(STEPS):
                        if n + 1 < STEPS:
                            take(n + 1)
                        if mask is None:
                            copy_flipped(n)
                        store(n)
                    if wo is not None:
                        dve.wait_ge(s_y, i + 1)
                        nc.vector.tensor_tensor(X[:, i, :], psA[:, :, :].rearrange("p a b -> p (a b)")[:, 0:DIM], X[:, i, :],
                                                ALU.add).then_inc(s_x, 1)
                    else:
                        dve.wait_ge(s_o, (i + 1) * STEPS * OR + 1)
                        nc.vector.tensor_tensor(X[:, i, :], A[:, :], X[:, i, :], ALU.add).then_inc(s_x, 1)


def linear_attention(nc, X, XNT, ident, d):
    with stage(nc) as (sb, ps, sem):
        W = sb("la_wqkv", [P, KC, 3 * DIM])
        WO = sb("la_wout", [P, KC, DIM])
        SH = sb("la_same_head", [P, P])
        H8 = sb("la_heads", [P, 8])
        XS = sb("la_x", [P, KC, P])
        low = sb("la_below_zero", [P, 2, DIM])
        ex = sb("la_exp", [P, 2, DIM])
        QS = sb("la_qT", [P, KC, P])
        KS = sb("la_k", [P, DIM])
        VS = sb("la_v", [P, 2, P + 1])
        KV = sb("la_kv", [P, 2, 2, P + 8])
        rden = sb("la_inv_denominator", [P, 2, 8])
        A = sb("la_attended", [P, DIM])
        AT = sb("la_attendedT", [P, KC, P])
        psQ, psK = ps("la_psq", [P, 512]), ps("la_pskv", [P, 512])
        psM = [ps("la_psm", [P, 512]) for _ in range(2)]
        psO, psT, psY = ps("la_pso", [P, 512]), ps("la_pst", [P, 512]), ps("la_psy", [P, 512])
        s_w, s_one, s_xs = sem("weights_loaded"), sem("v_ones_set"), sem("x_tile_ready")
        s_p, s_low, s_ex, s_f = sem("qkv_projected"), sem("below_zero_ready"), sem("exp_ready"), sem("features_ready")
        s_m, s_kv, s_o, s_d, s_a = sem("kv_summed"), sem("kv_ready"), sem("out_ready"), sem("dve_step"), sem("attended_ready")
        s_at, s_atc, s_y, s_x = sem("attended_flipped"), sem("attendedT_ready"), sem("out_projected"), sem("x_updated")
        with nc.Block() as block:
            @block.sync
            def _(sp):
                sp.dma_start(W[:, :, :], rows_to_sbuf(d["L0_attn_Wqkv"])).then_inc(s_w, 16)
                sp.dma_start(WO[:, :, :], rows_to_sbuf(d["L0_attn_Wout"])).then_inc(s_w, 16)
                sp.dma_start(SH[:, :], d["same_head"]).then_inc(s_w, 16)
                sp.dma_start(H8[:, :], d["heads8"]).then_inc(s_w, 16)

            @block.gpsimd
            def _(pool):
                nc.gpsimd.memset(VS[:, :, P:P + 1], 1.0).then_inc(s_one, 1)

            @block.tensor
            def _(pe):
                pe.wait_ge(s_w, 64)
                pe.wait_ge(s_one, 1)
                with pe.Fori(0, TILES) as i:
                    pe.wait_ge(s_xs, i + 1)
                    for m in range(KC):
                        for c in range(KC):
                            nc.tensor.matmul(psQ[:, m * P:(m + 1) * P], W[:, c, m * P:(m + 1) * P], XS[:, c, :],
                                             start=(c == 0), stop=(c == KC - 1))
                    for c in range(KC):
                        last = nc.tensor.matmul(psK[:, :], XS[:, c, :], W[:, c, DIM:3 * DIM], start=(c == 0),
                                                stop=(c == KC - 1))
                    last.then_inc(s_p, 1)
                    pe.wait_ge(s_f, i + 1)
                    for b in range(2):
                        r = slice(b * SEQ, (b + 1) * SEQ)
                        for g in range(2):
                            last = nc.tensor.matmul(psM[b][:, g * (P + 1):(g + 1) * (P + 1)], KS[r, g * P:(g + 1) * P],
                                                    VS[r, g, :], start=True, stop=True)
                    last.then_inc(s_m, 1)
                    pe.wait_ge(s_kv, i + 1)
                    for b in range(2):
                        for g in range(2):
                            last = nc.tensor.matmul(psO[b * SEQ:(b + 1) * SEQ, g * (P + 8):(g + 1) * (P + 8)],
                                                    QS[:, g, b * SEQ:(b + 1) * SEQ], KV[:, b, g, :], start=True, stop=True)
                    last.then_inc(s_o, 1)
                    pe.wait_ge(s_a, i + 1)
                    for c in range(KC):
                        last = nc.tensor.transpose(psT[:, c * P:(c + 1) * P], A[:, c * P:(c + 1) * P], ident[:, :])
                    last.then_inc(s_at, 1)
                    pe.wait_ge(s_atc, i + 1)
                    for c in range(KC):
                        last = nc.tensor.matmul(psY[:, 0:DIM], AT[:, c, :], WO[:, c, :], start=(c == 0), stop=(c == KC - 1))
                    last.then_inc(s_y, 1)

            @block.scalar
            def _(act):
                act.sem_inc(s_x, 1)
                with act.Fori(0, TILES) as i:
                    act.wait_ge(s_x, i + 1)
                    nc.scalar.copy(XS[:, :, :], XNT[:, :, bass.ds(i * P, P)]).then_inc(s_xs, 1)
                    act.wait_ge(s_low, i + 1)
                    nc.scalar.activation(ex[:, :, :], low[:, :, :], ACT.Exp).then_inc(s_ex, 1)
                    act.wait_ge(s_at, i + 1)
                    nc.scalar.copy(AT[:, :, :].rearrange("p a b -> p (a b)"), psT[:, 0:DIM]).then_inc(s_atc, 1)

            @block.vector
            def _(dve):
                dve.wait_ge(s_w, 64)
                with dve.Fori(0, TILES) as i:
                    link = Chain(dve, s_d, i * 2)
                    dve.wait_ge(s_p, i + 1)
                    nc.vector.tensor_scalar(low[:, 0, :], psQ[:, 0:DIM], 0.0, None, ALU.min)
                    nc.vector.tensor_scalar(low[:, 1, :], psK[:, 0:DIM], 0.0, None, ALU.min).then_inc(s_low, 1)
                    for g in range(2):
                        nc.vector.tensor_copy(VS[:, g, 0:P], psK[:, DIM + g * P:DIM + (g + 1) * P])
                    dve.wait_ge(s_ex, i + 1)
                    nc.vector.scalar_tensor_tensor(QS[:, :, :].rearrange("p a b -> p (a b)"), psQ[:, 0:DIM], 0.0,
                                                   ex[:, 0, :], ALU.max, ALU.add)
                    nc.vector.scalar_tensor_tensor(KS[:, :], psK[:, 0:DIM], 0.0, ex[:, 1, :], ALU.max,
                                                   ALU.add).then_inc(s_f, 1)
                    dve.wait_ge(s_m, i + 1)
                    for b in range(2):
                        for g in range(2):
                            o = g * (P + 1)
                            nc.vector.tensor_tensor(KV[:, b, g, 0:P], psM[b][:, o:o + P], SH[:, :], ALU.mult)
                            last = nc.vector.tensor_scalar(KV[:, b, g, P:P + 8], H8[:, :], psM[b][:, o + P:o + P + 1], None,
                                                           ALU.mult)
                    last.then_inc(s_kv, 1)
                    dve.wait_ge(s_o, i + 1)
                    O = psO[:, 0:2 * (P + 8)].rearrange("p (g w) -> p g w", g=2)
                    link(nc.vector.tensor_scalar(rden[:, :, :], O[:, :, P:P + 8], 1e-6, None, ALU.add))
                    link(nc.vector.reciprocal(rden[:, :, :], rden[:, :, :]))
                    for g in range(2):
                        last = nc.vector.tensor_tensor(A[:, g * P:(g + 1) * P].rearrange("p (h d) -> p h d", h=8),
                                                       O[:, g, 0:P].rearrange("p (h d) -> p h d", h=8),
                                                       rden[:, g, :].unsqueeze(2).broadcast_to([P, 8, 16]), ALU.mult)
                    last.then_inc(s_a, 1)
                    dve.wait_ge(s_y, i + 1)
                    nc.vector.tensor_tensor(X[:, i, :], psY[:, 0:DIM], X[:, i, :], ALU.add).then_inc(s_x, 1)


def mixed_experts(nc, X, XNT, ident, ones, d):
    E, DFF, TC = 8, 1024, 512
    NM = DFF // P
    NT = TOKENS // TC
    BPC = TC // SEQ
    with ExitStack() as outer:
        def keep(name, shape):
            return outer.enter_context(nc.sbuf_tensor(name, shape, F32))

        GT = keep("me_gateT", [E, P])
        GTOK = keep("me_gate", [P, E])
        GB = keep("me_gate_rows", [P, E, SEQ])
        with stage(nc) as (sb, ps, sem):
            W1 = sb("mg_w1", [P, KC, DIM])
            B1 = sb("mg_b1", [P, KC])
            W2 = sb("mg_w2", [P, KC, E])
            B2 = sb("mg_b2", [1, E])
            hid = [sb("mg_hidden", [P, TC]) for _ in range(2)]
            part = sb("mg_batch_sums", [P, KC, NT, SEQ])
            HM = sb("mg_hidden_mean", [P, KC, 2, SEQ])
            DG = sb("mg_gate_diagonals", [SEQ, E, SEQ])
            psH = [ps("mg_psh", [P, 512]) for _ in range(2)]
            psG, psGT, psB = ps("mg_psg", [P, 512]), ps("mg_psgt", [P, 512]), ps("mg_psb", [P, 512])
            s_w, s_h, s_r, s_p = sem("weights_loaded"), sem("hidden_projected"), sem("hidden_ready"), sem("batch_sums_ready")
            s_d, s_m, s_g, s_gt, s_dg, s_gb = (sem("dve_step"), sem("mean_ready"), sem("gates_projected"), sem("gates_ready"),
                                               sem("diagonals_ready"), sem("gate_rows_projected"))
            jobs = [(m, t) for m in range(KC) for t in range(NT)]
            with nc.Block() as block:
                @block.sync
                def _(sp):
                    sp.dma_start(W1[:, :, :], rows_to_sbuf(d["L0_ffn_gW1T"])).then_inc(s_w, 16)
                    sp.dma_start(B1[:, :], d["L0_ffn_gb1_col"]).then_inc(s_w, 16)
                    sp.dma_start(W2[:, :, :], rows_to_sbuf(d["L0_ffn_gW2T"])).then_inc(s_w, 16)
                    sp.dma_start(B2[:, :], row(d["L0_ffn_gb2"])).then_inc(s_w, 16)

                @block.tensor
                def _(pe):
                    pe.wait_ge(s_w, 64)
                    for n, (m, t) in enumerate(jobs):
                        if n >= 2:
                            pe.wait_ge(s_r, n - 1)
                        for c in range(KC):
                            last = nc.tensor.matmul(psH[n % 2][:, :], W1[:, c, m * P:(m + 1) * P],
                                                    XNT[:, c, t * TC:(t + 1) * TC], start=(c == 0), stop=(c == KC - 1))
                        last.then_inc(s_h, 1)
                    pe.wait_ge(s_m, 1)
                    for c in range(KC):
                        nc.tensor.matmul(psG[:, 0:E], HM[:, c, :, :].rearrange("p a s -> p (a s)"), W2[:, c, :],
                                         start=(c == 0), stop=False)
                    nc.tensor.matmul(psG[:, 0:E], ones[0:1, :], B2[:, :], start=False, stop=True)
                    for c in range(KC):
                        nc.tensor.matmul(psGT[0:E, 0:P], W2[:, c, :], HM[:, c, :, :].rearrange("p a s -> p (a s)"),
                                         start=(c == 0), stop=False)
                    nc.tensor.matmul(psGT[0:E, 0:P], B2[:, :], ones[0:1, :], start=False, stop=True).then_inc(s_g, 1)
                    pe.wait_ge(s_dg, 1)
                    nc.tensor.matmul(psB[:, :], ones[0:SEQ, :], DG[:, :, :].rearrange("p e s -> p (e s)"),
                                     start=True, stop=True).then_inc(s_gb, 1)

                @block.scalar
                def _(act):
                    act.wait_ge(s_w, 64)
                    for n, (m, t) in enumerate(jobs):
                        act.wait_ge(s_h, n + 1)
                        if n >= 2:
                            act.wait_ge(s_p, n - 1)
                        nc.scalar.activation(hid[n % 2][:, :], psH[n % 2][:, :], ACT.Relu, bias=B1[:, m:m + 1]).then_inc(s_r, 1)

                @block.vector
                def _(dve):
                    link = Chain(dve, s_d)
                    for n, (m, t) in enumerate(jobs):
                        dve.wait_ge(s_r, n + 1)
                        nc.vector.tensor_reduce(part[:, m, t, :], hid[n % 2][:, :].rearrange("p (b s) -> p s b", s=SEQ), AX_X,
                                                ALU.add).then_inc(s_p, 1)
                    dve.wait_ge(s_p, len(jobs))
                    for m in range(KC):
                        link(nc.vector.tensor_reduce(HM[:, m, 0, :], part[:, m, :, :].rearrange("p t s -> p s t"), AX_X, ALU.add))
                    link(nc.vector.tensor_scalar(HM[:, :, 1, :], HM[:, :, 0, :], 1.0 / BATCH, None, ALU.mult))
                    nc.vector.tensor_copy(HM[:, :, 0, :], HM[:, :, 1, :]).then_inc(s_m, 1)
                    dve.wait_ge(s_g, 1)
                    nc.vector.tensor_copy(GT[:, :], psGT[0:E, 0:P])
                    link(nc.vector.tensor_copy(GTOK[:, :], psG[:, 0:E]))
                    for e in range(E):
                        last = nc.vector.tensor_scalar(DG[:, e, :], ident[0:SEQ, 0:SEQ], GTOK[0:SEQ, e:e + 1], None, ALU.mult)
                    last.then_inc(s_dg, 1)
                    dve.wait_ge(s_gb, 1)
                    link(nc.vector.tensor_copy(GB[:, :, :].rearrange("p e s -> p (e s)"), psB[:, :]))

        Y1 = keep("me_hidden", [P, NM, TOKENS])
        with stage(nc) as (sb, ps, sem):
            W = sb("m1_w", [P, E, KC, DFF])
            B = sb("m1_b", [E, DFF])
            GTR = sb("m1_gateT", [E, BPC, SEQ])
            XG = sb("m1_x_gated", [P, E, KC, TC])
            out = [ps("m1_ps", [P, 512]) for _ in range(4)]
            s_b, s_gt = sem("biases_loaded"), sem("gateT_ready")
            s_we = [sem(f"expert{e}_loaded") for e in range(E)]
            s_xg, s_mm, s_y = sem("x_gated"), sem("multiplied"), sem("hidden_ready")
            with nc.Block() as block:
                @block.sync
                def _(sp):
                    sp.dma_start(B[:, :], d["L0_ffn_eb1"]).then_inc(s_b, 16)
                    for e in range(E):
                        sp.dma_start(W[:, e, :, :], rows_to_sbuf(d["L0_ffn_eW1T"][e])).then_inc(s_we[e], 16)

                @block.vector
                def _(dve):
                    nc.vector.tensor_copy(GTR[:, :, :], GT[:, 0:SEQ].unsqueeze(1).broadcast_to([E, BPC, SEQ])).then_inc(s_gt, 1)
                    dve.sem_inc(s_mm, NM)
                    with dve.Fori(0, NT) as t:
                        dve.wait_ge(s_mm, t * NM + NM)
                        for e in range(E):
                            for c in range(KC):
                                nc.vector.tensor_tensor(
                                    XG[:, e, c, :].rearrange("p (b s) -> p b s", s=SEQ),
                                    XNT[:, c, bass.ds(t * TC, TC)].rearrange("p (b s) -> p b s", s=SEQ),
                                    GB[:, e, :].unsqueeze(1).broadcast_to([P, BPC, SEQ]), ALU.mult).then_inc(s_xg, 1)

                @block.tensor
                def _(pe):
                    pe.wait_ge(s_b, 16)
                    pe.wait_ge(s_gt, 1)
                    for e in range(E):
                        pe.wait_ge(s_we[e], 16)
                    pe.sem_inc(s_y, 4)
                    with pe.Fori(0, NT) as t:
                        for m in range(NM):
                            pe.wait_ge(s_y, t * NM + (m + 1))
                            dst = out[m % 4][:, :]
                            nc.tensor.matmul(dst, B[:, m * P:(m + 1) * P], GTR[:, :, :].rearrange("p b s -> p (b s)"),
                                             start=True, stop=False)
                            for e in range(E):
                                for c in range(KC):
                                    if m == 0:
                                        pe.wait_ge(s_xg, t * E * KC + (e * KC + c + 1))
                                    last = nc.tensor.matmul(dst, W[:, e, c, m * P:(m + 1) * P], XG[:, e, c, :], start=False,
                                                            stop=(e == E - 1 and c == KC - 1))
                            last.then_inc(s_mm, 1)

                @block.scalar
                def _(act):
                    with act.Fori(0, NT) as t:
                        for m in range(NM):
                            act.wait_ge(s_mm, t * NM + (m + 1 + NM))
                            nc.scalar.activation(Y1[:, m, bass.ds(t * TC, TC)], out[m % 4][:, :], ACT.Relu).then_inc(s_y, 1)

        with stage(nc) as (sb, ps, sem):
            W = sb("m2_w", [P, E // 2, NM, 2, DIM])
            B = sb("m2_b", [E, DIM])
            BT = sb("m2_bias_rows", [P, DIM])
            out = [ps("m2_ps", [P, 2, DIM]) for _ in range(4)]
            psB = ps("m2_psb", [P, 512])
            s_b, s_bm, s_bt, s_bx = sem("bias_loaded"), sem("bias_projected"), sem("bias_rows_ready"), sem("bias_added")
            s_we = [sem(f"experts{e}_loaded") for e in range(E // 2)]
            s_mm, s_h, s_x = sem("multiplied"), sem("first_expert_added"), sem("second_expert_added")
            with nc.Block() as block:
                @block.sync
                def _(sp):
                    sp.dma_start(B[:, :], d["L0_ffn_eb2"]).then_inc(s_b, 16)
                    for j in range(E // 2):
                        for h in range(2):
                            sp.dma_start(W[:, j, :, h, :], rows_to_sbuf(d["L0_ffn_eW2T"][2 * j + h])).then_inc(s_we[j], 16)

                @block.tensor
                def _(pe):
                    pe.wait_ge(s_b, 16)
                    nc.tensor.matmul(psB[:, 0:DIM], GT[:, :], B[:, :], start=True, stop=True).then_inc(s_bm, 1)
                    for j in range(E // 2):
                        pe.wait_ge(s_we[j], 32)
                    pe.sem_inc(s_x, 4)
                    with pe.Fori(0, E // 2) as j:
                        for t in range(TILES):
                            pe.wait_ge(s_x, j * TILES + (t + 1))
                            for m in range(NM):
                                last = nc.tensor.matmul(out[t % 4][:, :, :].rearrange("p a b -> p (a b)"),
                                                        Y1[:, m, t * P:(t + 1) * P],
                                                        W[:, j, m, :, :].rearrange("p a b -> p (a b)"),
                                                        start=(m == 0), stop=(m == NM - 1))
                            last.then_inc(s_mm, 1)

                @block.vector
                def _(dve):
                    dve.wait_ge(s_bm, 1)
                    nc.vector.tensor_copy(BT[:, :], psB[:, 0:DIM]).then_inc(s_bt, 1)
                    dve.wait_ge(s_bt, 1)
                    nc.vector.tensor_tensor(X[:, :, :], X[:, :, :], BT[:, :].unsqueeze(1).broadcast_to([P, TILES, DIM]),
                                            ALU.add).then_inc(s_bx, 1)
                    dve.wait_ge(s_bx, 1)
                    with dve.Fori(0, E // 2) as j:
                        for t in range(TILES):
                            dve.wait_ge(s_mm, j * TILES + (t + 1))
                            nc.vector.scalar_tensor_tensor(X[:, t, :], out[t % 4][:, 0, :], GTOK[:, bass.ds(j * 2, 1)], X[:, t, :],
                                                           ALU.mult, ALU.add).then_inc(s_h, 1)
                            dve.wait_ge(s_h, j * TILES + (t + 1))
                            nc.vector.scalar_tensor_tensor(X[:, t, :], out[t % 4][:, 1, :], GTOK[:, bass.ds(j * 2 + 1, 1)],
                                                           X[:, t, :], ALU.mult, ALU.add).then_inc(s_x, 1)


def first_maximum(nc, link, onehot, top, scratch, values, order, shape):
    link(nc.vector.tensor_reduce(top, values, AX_X, ALU.max))
    link(nc.vector.tensor_tensor(onehot, values, top.unsqueeze(2).broadcast_to(shape), ALU.is_equal))
    link(nc.vector.tensor_tensor(onehot, onehot, order.unsqueeze(1).broadcast_to(shape), ALU.mult))
    link(nc.vector.tensor_reduce(scratch, onehot, AX_X, ALU.max))
    link(nc.vector.tensor_tensor(onehot, onehot, scratch.unsqueeze(2).broadcast_to(shape), ALU.is_equal))


def routed_experts(nc, X, XNT, ident, ones, d):
    E, F, TC = 8, 512, 512
    CAP = -(-2 * TOKENS * 5 // (E * 4))
    NF = F // P
    NT = TOKENS // TC
    with ExitStack() as outer:
        G = outer.enter_context(nc.sbuf_tensor("re_gate", [P, TILES, E], F32))
        with stage(nc) as (sb, ps, sem):
            WG = sb("rt_w", [P, KC, E])
            OR = sb("rt_order", [P, E])
            BE = sb("rt_before", [P, P])
            S = [P, TILES, E]
            L, PRB, P2, KM = sb("rt_logits", S), sb("rt_probs", S), sb("rt_probs_left", S), sb("rt_kept", [P, 2, TILES, E])
            OH = sb("rt_onehot", [P, 2, TILES, E])
            m, sm, v1, v2, sc = (sb("rt_max", [P, TILES]), sb("rt_sum", [P, TILES]), sb("rt_top1", [P, TILES]),
                                 sb("rt_top2", [P, TILES]), sb("rt_scratch", [P, TILES]))
            R = [sb("rt_running", [P, 2 * TILES, E]) for _ in range(2)]
            TOT = sb("rt_totals", [P, 2 * TILES, E])
            psL, psR, psT = ps("rt_psl", [P, 512]), ps("rt_psr", [P, 512]), ps("rt_pst", [P, 512])
            s_w, s_l, s_mx, s_e, s_d, s_oh, s_c = (sem("weights_loaded"), sem("logits_ready"), sem("logits_shifted"),
                                                   sem("exp_ready"), sem("dve_step"), sem("choices_ready"), sem("counts_ready"))
            with nc.Block() as block:
                @block.sync
                def _(sp):
                    sp.dma_start(WG[:, :, :], rows_to_sbuf(d["L1_ffn_Wg"])).then_inc(s_w, 16)
                    sp.dma_start(OR[:, :], d["expert_order"]).then_inc(s_w, 16)
                    sp.dma_start(BE[:, :], d["before"]).then_inc(s_w, 16)

                @block.tensor
                def _(pe):
                    pe.wait_ge(s_w, 48)
                    for t in range(TILES):
                        for c in range(KC):
                            last = nc.tensor.matmul(psL[:, t * E:(t + 1) * E], XNT[:, c, t * P:(t + 1) * P], WG[:, c, :],
                                                    start=(c == 0), stop=(c == KC - 1))
                    last.then_inc(s_l, 1)
                    pe.wait_ge(s_oh, 1)
                    flat = OH[:, :, :, :].rearrange("p k t e -> p (k t e)")
                    nc.tensor.matmul(psR[:, 0:2 * TILES * E], BE[:, :], flat, start=True, stop=True)
                    nc.tensor.matmul(psT[:, 0:2 * TILES * E], ones[:, :], flat, start=True, stop=True).then_inc(s_c, 1)

                @block.scalar
                def _(act):
                    act.wait_ge(s_mx, 1)
                    nc.scalar.activation(PRB[:, :, :], L[:, :, :], ACT.Exp).then_inc(s_e, 1)

                @block.vector
                def _(dve):
                    link = Chain(dve, s_d)
                    dve.wait_ge(s_w, 48)
                    dve.wait_ge(s_l, 1)
                    PL = psL[:, 0:TILES * E].rearrange("p (t e) -> p t e", e=E)
                    link(nc.vector.tensor_reduce(m[:, :], PL, AX_X, ALU.max))
                    nc.vector.tensor_tensor(L[:, :, :], PL, m[:, :].unsqueeze(2).broadcast_to(S), ALU.subtract).then_inc(s_mx, 1)
                    dve.wait_ge(s_e, 1)
                    link(nc.vector.tensor_reduce(sm[:, :], PRB[:, :, :], AX_X, ALU.add))
                    link(nc.vector.reciprocal(sm[:, :], sm[:, :]))
                    link(nc.vector.tensor_tensor(PRB[:, :, :], PRB[:, :, :], sm[:, :].unsqueeze(2).broadcast_to(S), ALU.mult))
                    first_maximum(nc, link, OH[:, 0, :, :], v1[:, :], sc[:, :], PRB[:, :, :], OR[:, :], S)
                    link(nc.vector.scalar_tensor_tensor(P2[:, :, :], OH[:, 0, :, :], -2.0, PRB[:, :, :], ALU.mult, ALU.add))
                    first_maximum(nc, link, OH[:, 1, :, :], v2[:, :], sc[:, :], P2[:, :, :], OR[:, :], S)
                    dve.sem_inc(s_oh, 1)
                    dve.wait_ge(s_c, 1)
                    W2 = 2 * TILES
                    PT = psT[:, 0:W2 * E].rearrange("p (t e) -> p t e", e=E)
                    link(nc.vector.tensor_copy(TOT[:, :, :], PT))
                    src, k, step = TOT, 0, 1
                    while step < W2:
                        dst = R[k % 2]
                        nc.vector.tensor_copy(dst[:, 0:step, :], src[:, 0:step, :])
                        link(nc.vector.tensor_tensor(dst[:, step:W2, :], src[:, step:W2, :], src[:, 0:W2 - step, :], ALU.add))
                        src, k, step = dst, k + 1, step * 2
                    dst = R[k % 2]
                    link(nc.vector.tensor_tensor(dst[:, :, :], src[:, :, :], TOT[:, :, :], ALU.subtract))
                    PR_ = psR[:, 0:W2 * E].rearrange("p (t e) -> p t e", e=E)
                    KF = KM[:, :, :, :].rearrange("p k t e -> p (k t) e")
                    link(nc.vector.tensor_tensor(KF, PR_, dst[:, :, :], ALU.add))
                    link(nc.vector.tensor_scalar(KF, KF, float(CAP), None, ALU.is_lt))
                    link(nc.vector.tensor_tensor(KF, KF, OH[:, :, :, :].rearrange("p k t e -> p (k t) e"), ALU.mult))
                    for n, v in enumerate((v1, v2)):
                        link(nc.vector.tensor_tensor(KM[:, n, :, :], KM[:, n, :, :], v[:, :].unsqueeze(2).broadcast_to(S), ALU.mult))
                    link(nc.vector.tensor_tensor(G[:, :, :], KM[:, 0, :, :], KM[:, 1, :, :], ALU.add))
                    link(nc.vector.tensor_reduce(sm[:, :], G[:, :, :], AX_X, ALU.add))
                    link(nc.vector.tensor_scalar(sm[:, :], sm[:, :], 1e-9, None, ALU.max))
                    link(nc.vector.reciprocal(sm[:, :], sm[:, :]))
                    link(nc.vector.tensor_tensor(G[:, :, :], G[:, :, :], sm[:, :].unsqueeze(2).broadcast_to(S), ALU.mult))

        with stage(nc) as (sb, ps, sem):
            WI = [sb("re_win", [P, KC, 2 * F]) for _ in range(2)]
            WO = [sb("re_wout", [P, NF, DIM]) for _ in range(2)]
            GE = [sb("re_gelu", [P, TC]) for _ in range(2)]
            HT = [sb("re_hidden", [P, NF, TC]) for _ in range(2)]
            psA = [ps("re_psa", [P, 512]) for _ in range(2)]
            psG = [ps("re_psg", [P, 512]) for _ in range(2)]
            psD = [ps("re_psd", [P, 512]) for _ in range(2)]
            s_w = [sem(f"expert{u}_loaded") for u in range(2)]
            s_up, s_ge, s_h, s_dn, s_x = sem("up_projected"), sem("gelu_ready"), sem("hidden_ready"), sem("down_projected"), sem("x_updated")
            NS = 2 * NT
            TPC = TC // P
            with nc.Block() as block:
                @block.sync
                def _(sp):
                    sp.sem_inc(s_dn, NS * TPC)
                    with sp.Fori(0, E // 2) as i:
                        for u in range(2):
                            sp.wait_ge(s_dn, i * NS * TPC + (u + 1) * NT * TPC)
                            sp.dma_start(WI[u][:, :, :], rows_to_sbuf(d["L1_ffn_W_in"].rearrange("(i u) k n -> i u k n", u=2)[i, u])).then_inc(s_w[u], 16)
                            sp.dma_start(WO[u][:, :, :], rows_to_sbuf(d["L1_ffn_W_out"].rearrange("(i u) k n -> i u k n", u=2)[i, u])).then_inc(s_w[u], 16)

                @block.tensor
                def _(pe):
                    pe.sem_inc(s_h, 2)
                    pe.sem_inc(s_x, 2)
                    with pe.Fori(0, E // 2) as i:
                        def up(n):
                            u, t = n // NT, n % NT
                            if t == 0:
                                pe.wait_ge(s_w[u], i * 32 + 32)
                            for f in range(NF):
                                k = n * NF + f
                                pe.wait_ge(s_h, i * NS * NF + (k + 1))
                                for dst, off in ((psA, 0), (psG, F)):
                                    for c in range(KC):
                                        last = nc.tensor.matmul(dst[k % 2][:, :], WI[u][:, c, off + f * P:off + (f + 1) * P],
                                                                XNT[:, c, t * TC:(t + 1) * TC], start=(c == 0), stop=(c == KC - 1))
                                last.then_inc(s_up, 1)

                        def down(n):
                            u, t = n // NT, n % NT
                            pe.wait_ge(s_h, i * NS * NF + ((n + 1) * NF + 2))
                            for j in range(TPC):
                                k = n * TPC + j
                                pe.wait_ge(s_x, i * NS * TPC + (k + 1))
                                for f in range(NF):
                                    last = nc.tensor.matmul(psD[k % 2][:, 0:DIM], HT[n % 2][:, f, j * P:(j + 1) * P], WO[u][:, f, :],
                                                            start=(f == 0), stop=(f == NF - 1))
                                last.then_inc(s_dn, 1)

                        up(0)
                        for n in range(NS):
                            if n + 1 < NS:
                                up(n + 1)
                            down(n)

                @block.scalar
                def _(act):
                    with act.Fori(0, E // 2) as i:
                        for k in range(NS * NF):
                            act.wait_ge(s_up, i * NS * NF + (k + 1))
                            act.wait_ge(s_h, i * NS * NF + (k + 1))
                            nc.scalar.activation(GE[k % 2][:, :], psA[k % 2][:, :], ACT.Gelu).then_inc(s_ge, 1)

                @block.vector
                def _(dve):
                    with dve.Fori(0, E // 2) as i:
                        def hidden(n):
                            for f in range(NF):
                                k = n * NF + f
                                dve.wait_ge(s_ge, i * NS * NF + (k + 1))
                                if f == 0:
                                    dve.wait_ge(s_dn, i * NS * TPC + (NS + n - 1) * TPC)
                                nc.vector.tensor_tensor(HT[n % 2][:, f, :], psG[k % 2][:, :], GE[k % 2][:, :], ALU.mult).then_inc(s_h, 1)

                        def add(n):
                            u, t = n // NT, n % NT
                            for j in range(TPC):
                                k = n * TPC + j
                                dve.wait_ge(s_dn, i * NS * TPC + (NS * TPC + k + 1))
                                tile = t * TPC + j
                                nc.vector.scalar_tensor_tensor(X[:, tile, :], psD[k % 2][:, 0:DIM], G[:, tile, bass.ds(i * 2 + u, 1)],
                                                               X[:, tile, :], ALU.mult, ALU.add).then_inc(s_x, 1)

                        hidden(0)
                        for n in range(NS):
                            if n + 1 < NS:
                                hidden(n + 1)
                            add(n)


def self_attention(nc, X, XNT, ident, ones, d, retention):
    NAME = "L1_attn" if retention else "L2_attn"
    VW = 32 if retention else 33
    with stage(nc) as (sb, ps, sem):
        W = sb("sa_wqkv", [P, KC, 3 * DIM])
        WO = sb("sa_wo", [P, KC, DIM])
        H8 = sb("sa_heads", [P, 8])
        if retention:
            DEC = sb("sa_decay", [P, 8, SEQ])
            BM = sb("sa_batch_mean", [P, P])
            GN = sb("sa_group_affine", [P, 2, KC])
            st = sb("sa_head_sums", [P, HEADS])
            mu = sb("sa_head_mean", [P, HEADS])
            A2 = sb("sa_centered", [P, DIM])
            std = sb("sa_head_std", [P, HEADS])
            rs16 = sb("sa_head_rstd", [P, HEADS])
        else:
            BQ = sb("sa_bqkv", [1, 3 * DIM])
            BO = sb("sa_bo", [1, DIM])
            WQK = sb("sa_rms_weights", [P, 2])
            rq = sb("sa_rms", [P, 32])
            rstd = sb("sa_inv_rms", [P, 32])
            nmax = sb("sa_max", [P, 16])
            QKN = sb("sa_qk_normed", [P, 2 * DIM])
        sq = sb("sa_squares", [P, 2 * DIM])
        XS = sb("sa_x", [P, KC, P])
        QK = sb("sa_qkT", [P, 4, P])
        V = sb("sa_v", [P, 8, VW])
        QB = sb("sa_q_spread", [P, 4, 8, SEQ])
        SC = sb("sa_scores", [P, 8, 2, SEQ])
        PR = sb("sa_probs", [P, 8, 2, SEQ])
        PT = sb("sa_probsT", [P, 8, P])
        rsum = sb("sa_inv_sum", [P, 2, 8])
        A = sb("sa_attended", [P, DIM])
        AT = sb("sa_attendedT", [P, KC, P])
        psF, psV = ps("sa_psf", [P, 512]), ps("sa_psv", [P, 512])
        psS = ps("sa_pss", [P, 2, 8, SEQ])
        psT = ps("sa_pst", [P, 8, P])
        psO = [ps("sa_pso", [P, 512]) for _ in range(2)]
        s_w, s_one, s_xs, s_p = sem("weights_loaded"), sem("v_ones_set"), sem("x_tile_ready"), sem("qkv_projected")
        s_sq, s_rms, s_sqrt, s_n, s_nf = sem("squares_ready"), sem("rms_ready"), sem("rms_root_ready"), sem("qk_normed"), sem("qk_flipped")
        s_qk, s_v, s_q, s_s = sem("qkT_ready"), sem("values_ready"), sem("queries_spread"), sem("scores_ready")
        s_mv, s_e, s_t, s_tc, s_pv = sem("scores_moved"), sem("probs_ready"), sem("probs_flipped"), sem("probsT_ready"), sem("attended")
        s_d, s_a = sem("dve_step"), sem("attended_ready")
        s_g, s_gm, s_gv, s_gs = sem("head_sums_ready"), sem("head_means_ready"), sem("head_var_ready"), sem("head_std_ready")
        s_at, s_atc, s_y, s_x = sem("attended_flipped"), sem("attendedT_ready"), sem("out_projected"), sem("x_updated")
        s_c2 = sem("centered_squares_ready")
        NW = 16 * 6
        with nc.Block() as block:
            @block.sync
            def _(sp):
                sp.dma_start(W[:, :, :], rows_to_sbuf(d["L1_attn_Wqkv"] if retention else d["L2_attn_WqkvT"])).then_inc(s_w, 16)
                sp.dma_start(WO[:, :, :], rows_to_sbuf(d[NAME + "_WoT"])).then_inc(s_w, 16)
                if retention:
                    sp.dma_start(H8[:, :], d["heads8"]).then_inc(s_w, 16)
                    sp.dma_start(DEC[:, :, :], d["decay"]).then_inc(s_w, 16)
                    sp.dma_start(BM[:, :], d["batch_mean"]).then_inc(s_w, 16)
                    sp.dma_start(GN[:, 0, :], d["L1_attn_gn_w_col"]).then_inc(s_w, 16)
                    sp.dma_start(GN[:, 1, :], d["L1_attn_gn_b_col"]).then_inc(s_w, 16)
                else:
                    sp.dma_start(H8[:, :], d["heads8"]).then_inc(s_w, 16)
                    sp.dma_start(BQ[:, :], row(d["L2_attn_bqkv"])).then_inc(s_w, 16)
                    sp.dma_start(BO[:, :], row(d["L2_attn_bo"])).then_inc(s_w, 16)
                    sp.dma_start(WQK[:, :], d["L2_attn_wqk_col"]).then_inc(s_w, 16)

            NW = 16 * (7 if retention else 6)

            @block.gpsimd
            def _(pool):
                if not retention:
                    nc.gpsimd.memset(V[:, :, 32:33], 1.0).then_inc(s_one, 1)
                pool.wait_ge(s_w, NW)
                with pool.Fori(0, TILES) as i:
                    pool.wait_ge(s_qk, i + 1)
                    for b in range(2):
                        for g in range(2):
                            q = QK[:, g, b * SEQ:(b + 1) * SEQ].unsqueeze(1).broadcast_to([P, 8, SEQ])
                            m = H8[:, :].unsqueeze(2).broadcast_to([P, 8, SEQ])
                            nc.gpsimd.tensor_tensor(QB[:, 2 * b + g, :, :], q, m, ALU.mult).then_inc(s_q, 1)

            @block.tensor
            def _(pe):
                pe.wait_ge(s_w, NW)
                if not retention:
                    pe.wait_ge(s_one, 1)
                with pe.Fori(0, TILES) as i:
                    pe.wait_ge(s_xs, i + 1)
                    if retention:
                        for m in range(4):
                            for c in range(KC):
                                nc.tensor.matmul(psF[:, m * P:(m + 1) * P], W[:, c, m * P:(m + 1) * P], XS[:, c, :],
                                                 start=(c == 0), stop=(c == KC - 1))
                        for c in range(KC):
                            last = nc.tensor.matmul(psV[:, 0:DIM], XS[:, c, :], W[:, c, 2 * DIM:3 * DIM], start=(c == 0),
                                                    stop=(c == KC - 1))
                        last.then_inc(s_p, 1)
                    else:
                        for dst, lo, hi in ((psF[:, :], 0, 2 * DIM), (psV[:, 0:DIM], 2 * DIM, 3 * DIM)):
                            for c in range(KC):
                                nc.tensor.matmul(dst, XS[:, c, :], W[:, c, lo:hi], start=(c == 0), stop=False)
                            last = nc.tensor.matmul(dst, ones[0:1, :], BQ[:, lo:hi], start=False, stop=True)
                        last.then_inc(s_p, 1)
                        pe.wait_ge(s_n, i + 1)
                        for m in range(4):
                            last = nc.tensor.transpose(psF[:, m * P:(m + 1) * P], QKN[:, m * P:(m + 1) * P], ident[:, :])
                        last.then_inc(s_nf, 1)
                    pe.wait_ge(s_qk, i + 1)
                    for b in range(2):
                        for g in range(2):
                            pe.wait_ge(s_q, i * 4 + (2 * b + g + 1))
                            for a in range(4):
                                last = nc.tensor.matmul(psS[:, b, 4 * g + a, :],
                                                        QB[:, 2 * b + g, 2 * a:2 * a + 2, :].rearrange("p b q -> p (b q)"),
                                                        QK[:, 2 + g, b * SEQ:(b + 1) * SEQ], start=True, stop=True)
                        last.then_inc(s_s, 1)
                    pe.wait_ge(s_e, (i + 1) * (2 if retention else 1))
                    for a in range(8):
                        last = nc.tensor.transpose(psT[:, a, :], PR[:, a, :, :].rearrange("p b j -> p (b j)"), ident[:, :])
                    last.then_inc(s_t, 1)
                    pe.wait_ge(s_tc, i + 1)
                    pe.wait_ge(s_v, i + 1)
                    for b in range(2):
                        r = slice(b * SEQ, (b + 1) * SEQ)
                        for a in range(8):
                            last = nc.tensor.matmul(psO[b][:, a * VW:(a + 1) * VW], PT[r, a, :], V[r, a, :], start=True, stop=True)
                    last.then_inc(s_pv, 1)
                    if retention:
                        pe.wait_ge(s_g, i + 1)
                        nc.tensor.matmul(psV[:, 0:HEADS], BM[:, :], st[:, :], start=True, stop=True).then_inc(s_gm, 1)
                        pe.wait_ge(s_c2, i + 1)
                        nc.tensor.matmul(psV[:, 0:HEADS], BM[:, :], mu[:, :], start=True, stop=True).then_inc(s_gv, 1)
                    pe.wait_ge(s_a, i + 1)
                    for c in range(KC):
                        last = nc.tensor.transpose(psF[:, c * P:(c + 1) * P], A[:, c * P:(c + 1) * P], ident[:, :])
                    last.then_inc(s_at, 1)
                    pe.wait_ge(s_atc, i + 1)
                    for c in range(KC):
                        last = nc.tensor.matmul(psV[:, 0:DIM], AT[:, c, :], WO[:, c, :], start=(c == 0),
                                                stop=(c == KC - 1 and retention))
                    if not retention:
                        last = nc.tensor.matmul(psV[:, 0:DIM], ones[0:1, :], BO[:, :], start=False, stop=True)
                    last.then_inc(s_y, 1)

            @block.scalar
            def _(act):
                act.wait_ge(s_w, NW)
                act.sem_inc(s_x, 1)
                with act.Fori(0, TILES) as i:
                    act.wait_ge(s_x, i + 1)
                    nc.scalar.copy(XS[:, :, :], XNT[:, :, bass.ds(i * P, P)]).then_inc(s_xs, 1)
                    if not retention:
                        act.wait_ge(s_p, i + 1)
                        nc.scalar.activation(sq[:, :], psF[:, :], ACT.Square).then_inc(s_sq, 1)
                        act.wait_ge(s_rms, i + 1)
                        nc.scalar.activation(rq[:, :], rq[:, :], ACT.Sqrt).then_inc(s_sqrt, 1)
                        act.wait_ge(s_nf, i + 1)
                        for m in range(2):
                            last = nc.scalar.activation(QK[:, 2 * m:2 * m + 2, :].rearrange("p a b -> p (a b)"),
                                                        psF[:, m * DIM:(m + 1) * DIM], ACT.Copy, scale=WQK[:, m:m + 1])
                        last.then_inc(s_qk, 1)
                        act.wait_ge(s_mv, i + 1)
                        nc.scalar.activation(PR[:, :, :, :].rearrange("p a b j -> p (a b j)"),
                                             SC[:, :, :, :].rearrange("p a b j -> p (a b j)"), ACT.Exp).then_inc(s_e, 1)
                    else:
                        act.wait_ge(s_p, i + 1)
                        nc.scalar.copy(QK[:, :, :].rearrange("p a b -> p (a b)"), psF[:, :]).then_inc(s_qk, 1)
                    act.wait_ge(s_t, i + 1)
                    nc.scalar.copy(PT[:, :, :], psT[:, :, :]).then_inc(s_tc, 1)
                    if retention:
                        act.wait_ge(s_gs, i + 1)
                        nc.scalar.activation(std[:, :], std[:, :], ACT.Sqrt).then_inc(s_sqrt, 1)
                    act.wait_ge(s_at, i + 1)
                    if retention:
                        for c in range(KC):
                            last = nc.scalar.activation(AT[:, c, :], psF[:, c * P:(c + 1) * P], ACT.Identity,
                                                        bias=GN[:, 1, c:c + 1], scale=GN[:, 0, c:c + 1])
                        last.then_inc(s_atc, 1)
                    else:
                        nc.scalar.copy(AT[:, :, :].rearrange("p a b -> p (a b)"), psF[:, 0:DIM]).then_inc(s_atc, 1)

            @block.vector
            def _(dve):
                dve.wait_ge(s_w, NW)
                NL = 7 if retention else 4
                with dve.Fori(0, TILES) as i:
                    link = Chain(dve, s_d, i * NL)
                    dve.wait_ge(s_p, i + 1)
                    nc.vector.tensor_copy(V[:, :, 0:32], psV[:, 0:DIM].rearrange("p (a w) -> p a w", a=8)).then_inc(s_v, 1)
                    if not retention:
                        dve.wait_ge(s_sq, i + 1)
                        link(nc.vector.tensor_reduce(rq[:, :], sq[:, :].rearrange("p (h d) -> p h d", d=16), AX_X, ALU.add))
                        nc.vector.tensor_scalar(rq[:, :], rq[:, :], 1.0 / 16, 1e-6, ALU.mult, ALU.add).then_inc(s_rms, 1)
                        dve.wait_ge(s_sqrt, i + 1)
                        link(nc.vector.reciprocal(rstd[:, :], rq[:, :]))
                        nc.vector.tensor_tensor(QKN[:, :].rearrange("p (h d) -> p h d", d=16),
                                                psF[:, :].rearrange("p (h d) -> p h d", d=16),
                                                rstd[:, :].unsqueeze(2).broadcast_to([P, 32, 16]), ALU.mult).then_inc(s_n, 1)
                        dve.wait_ge(s_s, (i + 1) * 2)
                        link(nc.vector.tensor_reduce(nmax[:, :], psS[:, :, :, :].rearrange("p b a j -> p (b a) j"), AX_X, ALU.max))
                        for b in range(2):
                            last = nc.vector.tensor_tensor(SC[:, :, b, :], psS[:, b, :, :],
                                                           nmax[:, 8 * b:8 * b + 8].unsqueeze(2).broadcast_to([P, 8, SEQ]),
                                                           ALU.subtract)
                        last.then_inc(s_mv, 1)
                    else:
                        for b in range(2):
                            dve.wait_ge(s_s, i * 2 + (b + 1))
                            nc.vector.tensor_tensor(PR[:, :, b, :], psS[:, b, :, :], DEC[:, :, :], ALU.mult).then_inc(s_e, 1)
                    dve.wait_ge(s_pv, i + 1)
                    for b in range(2):
                        O = psO[b][:, 0:8 * VW].rearrange("p (a w) -> p a w", a=8)
                        if not retention:
                            last = nc.vector.reciprocal(rsum[:, b, :], O[:, :, 32])
                            if b:
                                link(last)
                    for b in range(2):
                        O = psO[b][:, 0:8 * VW].rearrange("p (a w) -> p a w", a=8)
                        for h in range(2):
                            dst = A[b * SEQ:(b + 1) * SEQ, :].rearrange("p (a b d) -> p a b d", a=8, b=2)[:, :, h, :]
                            src = O[h * SEQ:(h + 1) * SEQ, :, 16 * h:16 * h + 16]
                            if retention:
                                last = nc.vector.tensor_copy(dst, src)
                            else:
                                last = nc.vector.tensor_tensor(
                                    dst, src, rsum[h * SEQ:(h + 1) * SEQ, b, :].unsqueeze(2).broadcast_to([SEQ, 8, 16]), ALU.mult)
                    A3 = A[:, :].rearrange("p (h d) -> p h d", d=16)
                    if retention:
                        link(last)
                        nc.vector.tensor_reduce(st[:, :], A3, AX_X, ALU.add).then_inc(s_g, 1)
                        dve.wait_ge(s_gm, i + 1)
                        C3 = A2[:, :].rearrange("p (h d) -> p h d", d=16)
                        link(nc.vector.tensor_copy(mu[:, :], psV[:, 0:HEADS]))
                        link(nc.vector.tensor_tensor(C3, A3, mu[:, :].unsqueeze(2).broadcast_to([P, HEADS, 16]), ALU.subtract))
                        link(nc.vector.tensor_tensor(sq[:, 0:DIM], A2[:, :], A2[:, :], ALU.mult))
                        nc.vector.tensor_reduce(mu[:, :], sq[:, 0:DIM].rearrange("p (h d) -> p h d", d=16), AX_X,
                                                ALU.add).then_inc(s_c2, 1)
                        dve.wait_ge(s_gv, i + 1)
                        nc.vector.tensor_scalar(std[:, :], psV[:, 0:HEADS], 1e-5, None, ALU.add).then_inc(s_gs, 1)
                        dve.wait_ge(s_sqrt, i + 1)
                        link(nc.vector.reciprocal(rs16[:, :], std[:, :]))
                        last = nc.vector.tensor_tensor(A3, C3, rs16[:, :].unsqueeze(2).broadcast_to([P, HEADS, 16]), ALU.mult)
                    last.then_inc(s_a, 1)
                    assert link.n <= NL
                    while link.n < NL:
                        link.n += 1
                        dve.sem_inc(s_d, 1)
                    dve.wait_ge(s_y, i + 1)
                    nc.vector.tensor_tensor(X[:, i, :], psV[:, 0:DIM], X[:, i, :], ALU.add).then_inc(s_x, 1)


def tiled_experts(nc, X, XNT, ident, ones, d):
    E = 8
    with stage(nc) as (sb, ps, sem):
        W = sb("te_w", [P, E, KC, DIM])
        B = sb("te_b", [E, DIM])
        PE_ = sb("te_position", [32, P])
        SG = sb("te_signatures", [32, E])
        lt = sb("te_negative", [32, E])
        SN = sb("te_signs", [32, E])
        OR = sb("te_order", [P, E])
        SCR = sb("te_scores", [P, 1, E])
        OH = sb("te_onehot", [P, 1, E])
        top, scr = sb("te_top", [P, 1]), sb("te_scratch", [P, 1])
        OHT = sb("te_onehotT", [E, P])
        DG = sb("te_diagonals", [SEQ, E, SEQ])
        OB = sb("te_onehot_rows", [P, E, SEQ])
        XG = [sb("te_x_picked", [P, KC, E, P]) for _ in range(2)]
        psS, psB, psT = ps("te_pss", [P, 512]), ps("te_psb", [P, 512]), ps("te_pst", [P, 512])
        out = [ps("te_psy", [P, 512]) for _ in range(2)]
        s_w, s_wb, s_sn, s_sc, s_d = sem("small_loaded"), sem("weights_loaded"), sem("signs_ready"), sem("scores_ready"), sem("dve_step")
        s_oh, s_tb, s_ob, s_xg, s_y, s_x = (sem("onehot_ready"), sem("onehot_spread"), sem("onehot_rows_ready"), sem("x_picked"),
                                            sem("multiplied"), sem("x_updated"))
        with nc.Block() as block:
            @block.sync
            def _(sp):
                sp.dma_start(PE_[:, :], d["positionT"]).then_inc(s_w, 16)
                sp.dma_start(SG[:, :], d["L2_ffn_tile_sigsT"]).then_inc(s_w, 16)
                sp.dma_start(OR[:, :], d["expert_order"]).then_inc(s_w, 16)
                sp.dma_start(B[:, :], d["L2_ffn_b"]).then_inc(s_wb, 16)
                for e in range(E):
                    sp.dma_start(W[:, e, :, :], rows_to_sbuf(d["L2_ffn_WT"][e])).then_inc(s_wb, 16)

            @block.tensor
            def _(pe):
                pe.wait_ge(s_sn, 1)
                nc.tensor.matmul(psS[:, 0:E], PE_[:, :], SN[:, :], start=True, stop=True).then_inc(s_sc, 1)
                pe.wait_ge(s_oh, 1)
                nc.tensor.transpose(psT[0:E, 0:P], OH[:, 0, :], ident[:, :])
                nc.tensor.matmul(psB[:, :], ones[0:SEQ, :], DG[:, :, :].rearrange("p e s -> p (e s)"), start=True,
                                 stop=True).then_inc(s_tb, 1)
                pe.wait_ge(s_wb, 16 * (1 + E))
                pe.sem_inc(s_x, 2)
                with pe.Fori(0, TILES // 2) as i:
                    for u in range(2):
                        pe.wait_ge(s_xg, i * 2 + (u + 1))
                        pe.wait_ge(s_x, i * 2 + (u + 1))
                        nc.tensor.matmul(out[u][:, 0:DIM], OHT[:, :], B[:, :], start=True, stop=False)
                        for e in range(E):
                            for c in range(KC):
                                last = nc.tensor.matmul(out[u][:, 0:DIM], XG[u][:, c, e, :], W[:, e, c, :], start=False,
                                                        stop=(e == E - 1 and c == KC - 1))
                        last.then_inc(s_y, 1)

            @block.vector
            def _(dve):
                link = Chain(dve, s_d)
                dve.wait_ge(s_w, 48)
                link(nc.vector.tensor_scalar(lt[:, :], SG[:, :], 0.0, None, ALU.is_lt))
                link(nc.vector.tensor_scalar(SN[:, :], SG[:, :], 0.0, None, ALU.is_gt))
                nc.vector.tensor_tensor(SN[:, :], SN[:, :], lt[:, :], ALU.subtract).then_inc(s_sn, 1)
                dve.wait_ge(s_sc, 1)
                link(nc.vector.tensor_copy(SCR[:, 0, :], psS[:, 0:E]))
                first_maximum(nc, link, OH[:, :, :], top[:, :], scr[:, :], SCR[:, :, :], OR[:, :], [P, 1, E])
                for e in range(E):
                    last = nc.vector.tensor_scalar(DG[:, e, :], ident[0:SEQ, 0:SEQ], OH[0:SEQ, 0, e:e + 1], None, ALU.mult)
                last.then_inc(s_oh, 1)
                dve.wait_ge(s_tb, 1)
                nc.vector.tensor_copy(OHT[:, :], psT[0:E, 0:P])
                nc.vector.tensor_copy(OB[:, :, :].rearrange("p e s -> p (e s)"), psB[:, :]).then_inc(s_ob, 1)
                dve.wait_ge(s_ob, 1)
                dve.sem_inc(s_y, 2)

                with dve.Fori(0, TILES // 2) as i:
                    for u in range(2):
                        dve.wait_ge(s_y, i * 2 + (u + 1))
                        for c in range(KC):
                            for b in range(2):
                                x = XNT[:, c, bass.ds(i * 2 * P + (u * P + b * SEQ), SEQ)].unsqueeze(1).broadcast_to([P, E, SEQ])
                                last = nc.vector.tensor_tensor(XG[u][:, c, :, b * SEQ:(b + 1) * SEQ], x, OB[:, :, :], ALU.mult)
                        last.then_inc(s_xg, 1)
                    for u in range(2):
                        dve.wait_ge(s_y, i * 2 + (u + 3))
                        x = X[:, bass.ds(i * 2 + u, 1), :]
                        nc.vector.tensor_tensor(x, out[u][:, 0:DIM].unsqueeze(1), x, ALU.add).then_inc(s_x, 1)


def gated_recurrence(nc, X, XNT, ident, d):
    TC = 512
    NT = TOKENS // TC
    with stage(nc) as (sb, ps, sem):
        W = sb("gr_w", [P, KC, 4 * P])
        WG = sb("gr_wg", [P, KC, DIM])
        B = sb("gr_b", [P, 4])
        BG = sb("gr_bg", [P, 2])
        Z, K, V = (sb("gr_z", [P, 2, TC]), sb("gr_keep", [P, 2, TC]), sb("gr_input", [P, 2, TC]))
        H = sb("gr_h", [P, 2, TC])
        GA = sb("gr_gate", [P, 2, TC])
        O = sb("gr_out", [P, 2, TC])
        psZ = [ps("gr_psz", [P, 512]) for _ in range(2)]
        psH = [ps("gr_psh", [P, 512]) for _ in range(2)]
        psG = [ps("gr_psg", [P, 512]) for _ in range(2)]
        psT = [ps("gr_pst", [P, 2, DIM]) for _ in range(2)]
        s_w, s_p, s_z, s_k, s_zero = sem("weights_loaded"), sem("projected"), sem("z_ready"), sem("keep_ready"), sem("batch_starts_cleared")
        s_h, s_g, s_ga, s_o, s_t, s_x = (sem("h_ready"), sem("gate_projected"), sem("gate_ready"), sem("out_ready"),
                                         sem("out_flipped"), sem("x_updated"))
        with nc.Block() as block:
            @block.sync
            def _(sp):
                sp.dma_start(W[:, :, :], rows_to_sbuf(d["L3_attn_W"])).then_inc(s_w, 16)
                sp.dma_start(WG[:, :, :], rows_to_sbuf(d["L3_attn_W_g"])).then_inc(s_w, 16)
                sp.dma_start(B[:, :], d["L3_attn_b_col"]).then_inc(s_w, 16)
                sp.dma_start(BG[:, :], d["L3_attn_b_g_col"]).then_inc(s_w, 16)

            @block.tensor
            def _(pe):
                pe.wait_ge(s_w, 64)
                pe.sem_inc(s_h, 2)
                pe.sem_inc(s_x, 2)
                with pe.Fori(0, NT) as t:
                    pe.wait_ge(s_h, t * 2 + 2)
                    for n, dst in enumerate(psZ + psH):
                        for c in range(KC):
                            last = nc.tensor.matmul(dst[:, :], W[:, c, n * P:(n + 1) * P], XNT[:, c, bass.ds(t * TC, TC)],
                                                    start=(c == 0), stop=(c == KC - 1))
                    last.then_inc(s_p, 1)
                    pe.wait_ge(s_h, t * 2 + 4)
                    for m in range(2):
                        for c in range(KC):
                            last = nc.tensor.matmul(psG[m][:, :], WG[:, c, m * P:(m + 1) * P], H[:, c, :], start=(c == 0),
                                                    stop=(c == KC - 1))
                    last.then_inc(s_g, 1)
                    pe.wait_ge(s_o, t * 2 + 2)
                    pe.wait_ge(s_x, t * 2 + 2)
                    for j in range(TC // P):
                        for c in range(KC):
                            last = nc.tensor.transpose(psT[j // 2][:, j % 2, c * P:(c + 1) * P], O[:, c, j * P:(j + 1) * P], ident[:, :])
                    last.then_inc(s_t, 1)

            @block.scalar
            def _(act):
                act.wait_ge(s_w, 64)
                with act.Fori(0, NT) as t:
                    act.wait_ge(s_p, t + 1)
                    for m in range(2):
                        nc.scalar.activation(Z[:, m, :], psZ[m][:, :], ACT.Sigmoid, bias=B[:, m:m + 1]).then_inc(s_z, 1)
                    act.wait_ge(s_g, t + 1)
                    for m in range(2):
                        nc.scalar.activation(GA[:, m, :], psG[m][:, :], ACT.Sigmoid, bias=BG[:, m:m + 1]).then_inc(s_ga, 1)

            @block.vector
            def _(dve):
                dve.wait_ge(s_w, 64)
                with dve.Fori(0, NT) as t:
                    for m in range(2):
                        dve.wait_ge(s_z, t * 2 + (m + 1))
                        nc.vector.tensor_scalar(K[:, m, :], Z[:, m, :], -1.0, 1.0, ALU.mult, ALU.add).then_inc(s_k, 1)
                        nc.vector.scalar_tensor_tensor(V[:, m, :], psH[m][:, :], B[:, 2 + m:3 + m], Z[:, m, :], ALU.add,
                                                       ALU.mult).then_inc(s_k, 1)
                        dve.wait_ge(s_k, t * 4 + (2 * m + 2))
                        nc.vector.memset(K[:, m, 0:TC:SEQ], 0.0).then_inc(s_zero, 1)
                        dve.wait_ge(s_zero, t * 2 + (m + 1))
                        nc.vector.tensor_tensor_scan(H[:, m, :], K[:, m, :], V[:, m, :], 0.0, ALU.mult, ALU.add).then_inc(s_h, 1)
                    for m in range(2):
                        dve.wait_ge(s_ga, t * 2 + (m + 1))
                        nc.vector.tensor_tensor(O[:, m, :], GA[:, m, :], H[:, m, :], ALU.mult).then_inc(s_o, 1)
                    dve.wait_ge(s_t, t + 1)
                    for j in range(2):
                        x = X[:, bass.ds(t * 4 + 2 * j, 2), :]
                        nc.vector.tensor_tensor(x, psT[j][:, :, :], x, ALU.add).then_inc(s_x, 1)


def swiglu_quantised(nc, X, XNT, d):
    HID, TC = 768, 512
    NF = HID // P
    NT = TOKENS // TC
    S = 1.0 / 127.0
    TPC = TC // P
    with stage(nc) as (sb, ps, sem):
        WI = [sb("sw_int", [P, KC, HID], I32) for _ in range(2)]
        WDI = sb("sw_down_int", [P, NF, DIM], I32)
        W = [sb("sw_w", [P, KC, HID]) for _ in range(2)]
        WD = sb("sw_down", [P, NF, DIM])
        SI = [sb("sw_silu", [P, TC]) for _ in range(2)]
        HT = [sb("sw_hidden", [P, NF, TC]) for _ in range(2)]
        psG = [ps("sw_psg", [P, 512]) for _ in range(2)]
        psU = [ps("sw_psu", [P, 512]) for _ in range(2)]
        psD = [ps("sw_psd", [P, 512]) for _ in range(2)]
        s_w, s_f = [sem(f"weights{n}_loaded") for n in range(3)], sem("weights_scaled")
        s_up, s_si, s_h, s_dn, s_x = sem("up_projected"), sem("silu_ready"), sem("hidden_ready"), sem("down_projected"), sem("x_updated")
        with nc.Block() as block:
            @block.sync
            def _(sp):
                sp.dma_start(WI[0][:, :, :], rows_to_sbuf(d["L3_ffn_w_gateT"])).then_inc(s_w[0], 16)
                sp.dma_start(WI[1][:, :, :], rows_to_sbuf(d["L3_ffn_w_upT"])).then_inc(s_w[1], 16)
                sp.dma_start(WDI[:, :, :], rows_to_sbuf(d["L3_ffn_w_downT"])).then_inc(s_w[2], 16)

            @block.tensor
            def _(pe):
                pe.wait_ge(s_f, 3)
                pe.sem_inc(s_h, 2)
                pe.sem_inc(s_x, 2)
                with pe.Fori(0, NT // 2) as i:
                    def up(n):
                        for f in range(NF):
                            k = n * NF + f
                            pe.wait_ge(s_h, i * 2 * NF + (k + 1))
                            for w, dst in ((W[0], psG), (W[1], psU)):
                                for c in range(KC):
                                    last = nc.tensor.matmul(dst[k % 2][:, :], w[:, c, f * P:(f + 1) * P],
                                                            XNT[:, c, bass.ds(i * 2 * TC + n * TC, TC)], start=(c == 0), stop=(c == KC - 1))
                            last.then_inc(s_up, 1)

                    def down(n):
                        pe.wait_ge(s_h, i * 2 * NF + ((n + 1) * NF + 2))
                        for j in range(TPC):
                            k = n * TPC + j
                            pe.wait_ge(s_x, i * 2 * TPC + (k + 1))
                            for f in range(NF):
                                last = nc.tensor.matmul(psD[k % 2][:, 0:DIM], HT[n][:, f, j * P:(j + 1) * P], WD[:, f, :],
                                                        start=(f == 0), stop=(f == NF - 1))
                            last.then_inc(s_dn, 1)

                    up(0)
                    up(1)
                    down(0)
                    down(1)

            @block.scalar
            def _(act):
                with act.Fori(0, NT // 2) as i:
                    for k in range(2 * NF):
                        act.wait_ge(s_up, i * 2 * NF + (k + 1))
                        act.wait_ge(s_h, i * 2 * NF + (k + 1))
                        nc.scalar.activation(SI[k % 2][:, :], psG[k % 2][:, :], ACT.Silu).then_inc(s_si, 1)

            @block.vector
            def _(dve):
                for n, (src, dst) in enumerate(((WI[0], W[0]), (WI[1], W[1]), (WDI, WD))):
                    dve.wait_ge(s_w[n], 16)
                    nc.vector.tensor_scalar(dst[:, :, :], src[:, :, :], S, None, ALU.mult).then_inc(s_f, 1)
                dve.sem_inc(s_dn, 2 * TPC)
                with dve.Fori(0, NT // 2) as i:
                    for n in range(2):
                        dve.wait_ge(s_dn, i * 2 * TPC + (n + 1) * TPC)
                        for f in range(NF):
                            k = n * NF + f
                            dve.wait_ge(s_si, i * 2 * NF + (k + 1))
                            nc.vector.tensor_tensor(HT[n][:, f, :], psU[k % 2][:, :], SI[k % 2][:, :], ALU.mult).then_inc(s_h, 1)
                    for k in range(2 * TPC):
                        dve.wait_ge(s_dn, i * 2 * TPC + (2 * TPC + k + 1))
                        x = X[:, bass.ds(i * 2 * TPC + k, 1), :]
                        nc.vector.tensor_tensor(x, psD[k % 2][:, 0:DIM].unsqueeze(1), x, ALU.add).then_inc(s_x, 1)


STAGES = ('L0x', 'L0a', 'L0f', 'L1x', 'L1a', 'L1f', 'L2x', 'L2a', 'L2f', 'L3x', 'L3a', 'L3f')


def perceiver(nc, d, out):
    _stages.clear()
    _names.clear()
    with ExitStack() as ctx:
        X = ctx.enter_context(nc.sbuf_tensor("x_resident", [P, TILES, DIM], F32))
        XNT = ctx.enter_context(nc.sbuf_tensor("x_normed_transposed", [P, KC, TOKENS], F32))
        ident = ctx.enter_context(nc.sbuf_tensor("identity", [P, P], F32))
        ones = ctx.enter_context(nc.sbuf_tensor("ones", [P, P], F32))
        with stage(nc) as (sb, ps, sem):
            s_in, s_one = sem("x_loaded"), sem("ones_set")
            with nc.Block() as block:
                @block.sync
                def _(sp):
                    sp.dma_start(X[:, :, :], d["x"].rearrange("(t b) s d -> (b s) t d", b=2)).then_inc(s_in, 16)
                    sp.dma_start(ident[:, :], d["identity"]).then_inc(s_in, 16)
                    sp.wait_ge(s_in, 32)

                @block.gpsimd
                def _(pool):
                    nc.gpsimd.memset(ones[:, :], 1.0).then_inc(s_one, 1)
                    pool.wait_ge(s_one, 1)

        ctx4 = d["ctxT"].rearrange("(t b) d s -> t b d s", b=2)
        ctxn = d["ctx"].rearrange("(t b) s d -> t b s d", b=2)
        mask4 = d["mask_Bx1x1xS2_fk0"].rearrange("(t b) c e s -> t b (c e s)", b=2)
        if "L0x" in STAGES:
            layernorm_transposed(nc, X, XNT, ident)
            with nc.sbuf_tensor("l0x_qT", [P, KC, TOKENS], F32) as QT:
                project_transposed(nc, XNT, QT, d["L0_xattn_Wq"], d["L0_xattn_bq_col"], KC)
                cross_attention(nc, X, QT, ident, ones, d["spread16"], ctx4, 16, wkv=d["L0_xattn_Wkv"],
                                bk=d["L0_xattn_bk_col"], bv=d["L0_xattn_bv_col"], wo=d["L0_xattn_Wo"], bo=d["L0_xattn_bo"])
        if "L0a" in STAGES:
            layernorm_transposed(nc, X, XNT, ident, passes=2, residual=True,
                                 affine=(d["L0_attn_gamma_col"], d["L0_attn_beta_col"]))
            linear_attention(nc, X, XNT, ident, d)
        if "L0f" in STAGES:
            layernorm_transposed(nc, X, XNT, ident)
            mixed_experts(nc, X, XNT, ident, ones, d)
        if "L1x" in STAGES:
            ctxnT = nc.dram_tensor("ctx_normed_transposed", (BATCH, DIM, NKEY), F32, kind="Internal").ap()
            rows = TILES * P // NKEY
            with nc.sbuf_tensor("context_rows", [P, TILES, DIM], F32) as CX:
                for c in range(BATCH // rows):
                    part = slice(c * rows, (c + 1) * rows)
                    layernorm_transposed(
                        nc, CX, XNT, ident, affine=(d["L1_xattn_ln_c_w_col"], d["L1_xattn_ln_c_b_col"]),
                        load=d["ctx"][part].rearrange("b (t p) d -> p (b t) d", p=P),
                        store=ctxnT[part].rearrange("b (c p) s -> p c b s", p=P))
            layernorm_transposed(nc, X, XNT, ident, passes=2,
                                 affine=(d["L1_xattn_ln_l_w_col"], d["L1_xattn_ln_l_b_col"]))
            with nc.sbuf_tensor("l1x_qT", [P, 8, TOKENS], F32) as QT:
                project_transposed(nc, XNT, QT, d["L1_xattn_Wq"], None, 8)
                cross_attention(nc, X, QT, ident, ones, d["spread64"], ctxnT.rearrange("(t b) d s -> t b d s", b=2), 64,
                                wkv=d["L1_xattn_Wkv"], wo=d["L1_xattn_Wo"], bo=d["L1_xattn_bo"], clip=11.0)
        if "L1a" in STAGES:
            layernorm_transposed(nc, X, XNT, ident)
            self_attention(nc, X, XNT, ident, ones, d, retention=True)
        if "L1f" in STAGES:
            layernorm_transposed(nc, X, XNT, ident)
            routed_experts(nc, X, XNT, ident, ones, d)
        if "L2x" in STAGES:
            layernorm_transposed(nc, X, XNT, ident)
            cross_attention(nc, X, XNT, ident, ones, d["spread16"], ctx4, 16, ctx=ctxn)
        if "L2a" in STAGES:
            layernorm_transposed(nc, X, XNT, ident)
            self_attention(nc, X, XNT, ident, ones, d, retention=False)
        if "L2f" in STAGES:
            layernorm_transposed(nc, X, XNT, ident)
            tiled_experts(nc, X, XNT, ident, ones, d)
        if "L3x" in STAGES:
            layernorm_transposed(nc, X, XNT, ident)
            with nc.sbuf_tensor("l3x_qT", [P, KC, TOKENS], F32) as QT:
                project_transposed(nc, XNT, QT, d["L3_xattn_Wq"], d["L3_xattn_bq_col"], KC)
                cross_attention(nc, X, QT, ident, ones, d["spread16"], ctx4, 16, wkv=d["L3_xattn_Wkv"],
                                bk=d["L3_xattn_bk_col"], bv=d["L3_xattn_bv_col"], wo=d["L3_xattn_Wo"], bo=d["L3_xattn_bo"], mask=mask4)
        if "L3a" in STAGES:
            layernorm_transposed(nc, X, XNT, ident)
            gated_recurrence(nc, X, XNT, ident, d)
        if "L3f" in STAGES:
            layernorm_transposed(nc, X, XNT, ident)
            swiglu_quantised(nc, X, XNT, d)
        with stage(nc) as (sb, ps, sem):
            s_out = sem("x_stored")
            with nc.Block() as block:
                @block.sync
                def _(sp):
                    sp.dma_start(out.rearrange("(t b) s d -> (b s) t d", b=2), X[:, :, :]).then_inc(s_out, 16)
                    sp.wait_ge(s_out, 16)


def kernel(**inputs):
    import numpy as np
    import concourse.bacc as _bacc
    from concourse.bass_utils import run_bass_kernel_spmd as _run

    arrays = {k: np.ascontiguousarray(v) for k, v in inputs.items() if k in DIRECT}
    arrays["ctx"] = np.ascontiguousarray(inputs["ctx_1024"])
    arrays["ctxT"] = np.ascontiguousarray(np.asarray(inputs["ctx_1024"]).transpose(0, 2, 1))
    for n in ("L0", "L3"):
        arrays[f"{n}_xattn_Wkv"] = np.concatenate(
            [np.asarray(inputs[f"{n}_xattn_Wk"]), np.asarray(inputs[f"{n}_xattn_Wv"])], axis=1)
    for k in COLUMNS:
        arrays[k + "_col"] = np.ascontiguousarray(np.asarray(inputs[k]).reshape(-1, 128).T)
    arrays["identity"] = np.eye(128, dtype=np.float32)
    head = np.arange(128) // 16
    arrays["spread16"] = np.where(head[:, None] == np.arange(8)[None], 0.25, 0.0).astype(np.float32)
    more_arrays(arrays, inputs)

    nc = _bacc.Bacc("TRN2", target_bir_lowering=False, num_devices=1)
    d = {k: nc.dram_tensor(f"in_{k}", a.shape, mybir.dt.from_np(a.dtype), kind="ExternalInput").ap()
         for k, a in arrays.items()}
    out = nc.dram_tensor("out_x", (BATCH, SEQ, DIM), F32, kind="ExternalOutput").ap()
    perceiver(nc, d, out)
    r = _run(nc, [{f"in_{k}": a for k, a in arrays.items()}], core_ids=[0])
    return r.results[0]["out_x"]


DIRECT = ("x", "mask_Bx1x1xS2_fk0", "L0_xattn_Wq", "L0_xattn_Wo", "L0_xattn_bo", "L3_xattn_Wq", "L3_xattn_Wo",
          "L3_xattn_bo", "L0_attn_Wqkv", "L0_attn_Wout", "L1_xattn_Wq", "L1_xattn_Wkv", "L1_xattn_Wo", "L1_xattn_bo",
          "L2_attn_bo", "L2_attn_bqkv", "L0_ffn_gb2", "L0_ffn_eb1", "L0_ffn_eb2", "L1_ffn_Wg", "L1_ffn_W_in",
          "L1_ffn_W_out", "L2_ffn_b", "L3_attn_W_g")
COLUMNS = ("L0_xattn_bq", "L0_xattn_bk", "L0_xattn_bv", "L3_xattn_bq", "L3_xattn_bk", "L3_xattn_bv",
           "L0_attn_gamma", "L0_attn_beta", "L1_xattn_ln_c_w", "L1_xattn_ln_c_b", "L1_xattn_ln_l_w", "L1_xattn_ln_l_b",
           "L1_attn_gn_w", "L1_attn_gn_b", "L0_ffn_gb1", "L3_attn_b_g")


def more_arrays(arrays, inputs):
    import numpy as np

    f = np.float32
    part = np.arange(128)
    arrays["spread64"] = np.where((part // 64)[:, None] == np.arange(2)[None], 0.125, 0.0).astype(f)
    arrays["same_head"] = ((part // 16)[:, None] == (part // 16)[None]).astype(f)
    arrays["heads8"] = ((part // 16)[:, None] == np.arange(8)[None]).astype(f)
    arrays["batch_mean"] = np.where((part // 64)[:, None] == (part // 64)[None], 1.0 / (64 * 16), 0.0).astype(f)
    lo, hi = float(np.log(1.0 - 0.999)), float(np.log(1.0 - 0.9))
    gam = (f(1.0) - np.exp(np.linspace(lo, hi, 16, dtype=f))).astype(f)
    dist = (np.arange(64)[:, None] - np.arange(64)[None]).astype(f)
    dec = np.where(dist >= 0, gam[:, None, None] ** np.where(dist >= 0, dist, 0).astype(f), 0).astype(f)
    arrays["decay"] = np.ascontiguousarray(dec.reshape(8, 2, 64, 64).transpose(1, 2, 0, 3).reshape(128, 8, 64))
    g = lambda k: np.asarray(inputs[k])
    arrays["L1_attn_Wqkv"] = np.concatenate([g("L1_attn_wq").T, g("L1_attn_wk").T, g("L1_attn_wv").T], axis=1)
    arrays["L1_attn_WoT"] = np.ascontiguousarray(g("L1_attn_wo").T)
    arrays["L2_attn_WqkvT"] = np.ascontiguousarray(g("L2_attn_Wqkv").T)
    arrays["L2_attn_WoT"] = np.ascontiguousarray(g("L2_attn_Wo").T)
    arrays["L2_attn_wqk_col"] = np.stack([np.tile(g("L2_attn_wq"), 8), np.tile(g("L2_attn_wk"), 8)], axis=1)
    t = lambda k, *axes: np.ascontiguousarray(g(k).transpose(*axes))
    arrays["L0_ffn_gW1T"] = t("L0_ffn_gW1", 1, 0)
    arrays["L0_ffn_gW2T"] = t("L0_ffn_gW2", 1, 0)
    arrays["L0_ffn_eW1T"] = t("L0_ffn_eW1", 0, 2, 1)
    arrays["L0_ffn_eW2T"] = t("L0_ffn_eW2", 0, 2, 1)
    arrays["L2_ffn_tile_sigsT"] = t("L2_ffn_tile_sigs", 1, 0)
    arrays["L2_ffn_WT"] = t("L2_ffn_W", 0, 2, 1)
    for k in ("L3_ffn_w_gate", "L3_ffn_w_up", "L3_ffn_w_down"):
        arrays[k + "T"] = t(k, 1, 0)
    arrays["L3_attn_W"] = np.concatenate([g(f"L3_attn_W_{k}") for k in ("zf", "zs", "hf", "hs")], axis=1)
    arrays["L3_attn_b_col"] = np.stack([g(f"L3_attn_b_{k}") for k in ("zf", "zs", "hf", "hs")], axis=1)
    arrays["expert_order"] = np.broadcast_to(np.arange(8, 0, -1, dtype=f), (128, 8)).copy()
    arrays["before"] = (part[:, None] < part[None]).astype(f)
    pos = (part % 64).astype(f)[:, None]
    div = np.exp(np.arange(0, 32, 2, dtype=f) * f(-np.log(10000.0) / 32))
    ang = (pos * div).astype(f)
    pe = np.zeros((128, 32), f)
    pe[:, 0::2] = np.sin(ang)
    pe[:, 1::2] = np.cos(ang)
    arrays["positionT"] = np.ascontiguousarray(pe.T)
```

```python
from contextlib import ExitStack, contextmanager

import concourse.bass as bass
from concourse import mybir

ALU = mybir.AluOpType
ACT = mybir.ActivationFunctionType
F32 = mybir.dt.float32
I32 = mybir.dt.int32
AX_X = mybir.AxisListType.X

P = 128
BATCH = 32
SEQ = 64
DIM = 256
KC = DIM // P
TOKENS = BATCH * SEQ
TILES = TOKENS // P
NKEY = 256
HEADS = 16
EPS = 1e-5


_stages, _names = [], {}


@contextmanager
def stage(nc):
    sems = []
    _stages.append(len(_stages))
    tag = f"s{len(_stages)}"

    def unique(name):
        _names[name] = _names.get(name, 0) + 1
        return f"{tag}_{name}_{_names[name]}"

    with ExitStack() as ctx:
        def sb(name, shape, dt=F32):
            return ctx.enter_context(nc.sbuf_tensor(unique(name), shape, dt))

        def ps(name, shape, dt=F32):
            return ctx.enter_context(nc.psum_tensor(unique(name), shape, dt))

        def sem(name):
            s = nc.alloc_semaphore(unique(name))
            sems.append(s)
            return s

        yield sb, ps, sem
    nc.clear_and_free_semaphores(sems)
    nc.all_engine_barrier()


class Chain:

    def __init__(self, eng, sem, base=0):
        self.eng, self.sem, self.base, self.n = eng, sem, base, 0

    def __call__(self, ins):
        self.n += 1
        ins.then_inc(self.sem, 1)
        self.eng.wait_ge(self.sem, self.base + self.n)


def rows_to_sbuf(w):
    return w.rearrange("(c p) n -> p c n", p=P)


def row(v):
    return v.rearrange("(a n) -> a n", a=1)


def layernorm_transposed(nc, X, XNT, ident, passes=1, affine=None, residual=False, load=None, store=None):
    with stage(nc) as (sb, ps, sem):
        XN = sb("ln_xn", [P, TILES, DIM])
        stats = sb("ln_stats", [P, TILES, 6])
        diff = sb("ln_diff", [P, TILES])
        mean = sb("ln_mean", [P, TILES])
        var = sb("ln_var", [P, TILES])
        std = sb("ln_std", [P, TILES])
        rstd = sb("ln_rstd", [P, TILES])
        col = sb("ln_col", [P, 2, KC])
        flip = [ps("ln_flip", [P, KC, P]) for _ in range(2)]
        s_var, s_std, s_dve, s_stat = sem("ln_var_ready"), sem("ln_std_ready"), sem("ln_dve_step"), sem("ln_stats_done")
        s_norm, s_flip, s_out, s_col = sem("ln_normed"), sem("ln_flipped"), sem("ln_stored"), sem("ln_columns_loaded")
        s_norm2, s_in, s_dram = sem("ln_pass_normed"), sem("ln_rows_loaded"), sem("ln_dram_stored")
        with nc.Block() as block:
            @block.sync
            def _(sp):
                if load is not None:
                    sp.dma_start(X[:, :, :], load).then_inc(s_in, 16)
                if affine:
                    for n, v in enumerate(affine):
                        sp.dma_start(col[:, n, :], v).then_inc(s_col, 16)
                if store is not None:
                    sp.wait_ge(s_out, TILES)
                    for c in range(KC):
                        sp.dma_start(store[:, c], XNT[:, c, :].rearrange("p (b s) -> p b s", s=NKEY)).then_inc(s_dram, 16)
                    sp.wait_ge(s_dram, 16 * KC)

            @block.vector
            def _(dve):
                link = Chain(dve, s_dve)
                if load is not None:
                    dve.wait_ge(s_in, 16)
                for n in range(passes):
                    src = XN if n else X
                    with dve.Fori(0, TILES // 8) as i:
                        for u in range(8):
                            t = i * 8 + u
                            nc.vector.bn_stats(stats[:, t, :], src[:, t, :]).then_inc(s_stat, 1)
                    dve.wait_ge(s_stat, TILES * (n + 1))
                    link(nc.vector.tensor_tensor(mean[:, :], stats[:, :, 1], stats[:, :, 4], ALU.add))
                    link(nc.vector.tensor_scalar(mean[:, :], mean[:, :], 0.5, None, ALU.mult))
                    link(nc.vector.tensor_tensor(diff[:, :], stats[:, :, 1], stats[:, :, 4], ALU.subtract))
                    link(nc.vector.tensor_tensor(diff[:, :], diff[:, :], diff[:, :], ALU.mult))
                    link(nc.vector.tensor_scalar(diff[:, :], diff[:, :], DIM / 4.0, None, ALU.mult))
                    link(nc.vector.tensor_tensor(var[:, :], stats[:, :, 2], stats[:, :, 5], ALU.add))
                    link(nc.vector.tensor_tensor(var[:, :], var[:, :], diff[:, :], ALU.add))
                    nc.vector.tensor_scalar(var[:, :], var[:, :], 1.0 / DIM, EPS, ALU.mult, ALU.add).then_inc(s_var, 1)
                    dve.wait_ge(s_std, n + 1)
                    link(nc.vector.reciprocal(rstd[:, :], std[:, :]))
                    done = s_norm if n == passes - 1 else s_norm2
                    with dve.Fori(0, TILES // 8) as i:
                        for u in range(8):
                            t = i * 8 + u
                            nc.vector.tensor_scalar(XN[:, t, :], src[:, t, :], mean[:, bass.ds(t, 1)],
                                                    rstd[:, bass.ds(t, 1)], ALU.subtract, ALU.mult).then_inc(done, 1)
                    if n < passes - 1:
                        dve.wait_ge(s_norm2, TILES)
                        if residual:
                            for h in range(2):
                                half = slice(h * TILES // 2, (h + 1) * TILES // 2)
                                link(nc.vector.tensor_tensor(X[:, half, :], X[:, half, :], XN[:, half, :], ALU.add))

            @block.tensor
            def _(pe):
                for t in range(TILES):
                    pe.wait_ge(s_norm, t + 1)
                    if t >= 2:
                        pe.wait_ge(s_out, t - 1)
                    for c in range(KC):
                        last = nc.tensor.transpose(flip[t % 2][:, c, :], XN[:, t, c * P:(c + 1) * P], ident[:, :])
                    last.then_inc(s_flip, 1)

            @block.scalar
            def _(act):
                for n in range(passes):
                    act.wait_ge(s_var, n + 1)
                    nc.scalar.activation(std[:, :], var[:, :], ACT.Sqrt).then_inc(s_std, 1)
                if affine:
                    act.wait_ge(s_col, 32)
                with act.Fori(0, TILES // 8) as i:
                    for u in range(8):
                        act.wait_ge(s_flip, i * 8 + (u + 1))
                        if affine:
                            for c in range(KC):
                                last = nc.scalar.activation(XNT[:, c, bass.ds(i * 8 * P + u * P, P)], flip[u % 2][:, c, :],
                                                            ACT.Identity, bias=col[:, 1, c:c + 1], scale=col[:, 0, c:c + 1])
                        else:
                            last = nc.scalar.copy(XNT[:, :, bass.ds(i * 8 * P + u * P, P)], flip[u % 2][:, :, :])
                        last.then_inc(s_out, 1)


def project_transposed(nc, XNT, dst, w, bias, chunks):
    TC = 512
    with stage(nc) as (sb, ps, sem):
        W = sb("pj_w", [P, KC, chunks * P])
        B = sb("pj_b", [P, chunks])
        out = [ps("pj_out", [P, TC]) for _ in range(4)]
        s_w, s_mm, s_st = sem("pj_w_loaded"), sem("pj_multiplied"), sem("pj_stored")
        jobs = [(m, t) for m in range(chunks) for t in range(TOKENS // TC)]
        with nc.Block() as block:
            @block.sync
            def _(sp):
                sp.dma_start(W[:, :, :], rows_to_sbuf(w)).then_inc(s_w, 16)
                if bias is not None:
                    sp.dma_start(B[:, :], bias).then_inc(s_w, 16)

            @block.tensor
            def _(pe):
                pe.wait_ge(s_w, 16 if bias is None else 32)
                for n, (m, t) in enumerate(jobs):
                    if n >= 4:
                        pe.wait_ge(s_st, n - 3)
                    for c in range(KC):
                        last = nc.tensor.matmul(out[n % 4][:, :], W[:, c, m * P:(m + 1) * P],
                                                XNT[:, c, t * TC:(t + 1) * TC], start=(c == 0), stop=(c == KC - 1))
                    last.then_inc(s_mm, 1)

            @block.vector
            def _(dve):
                if bias is not None:
                    dve.wait_ge(s_w, 32)
                for n, (m, t) in enumerate(jobs):
                    dve.wait_ge(s_mm, n + 1)
                    if bias is not None:
                        last = nc.vector.tensor_scalar(dst[:, m, t * TC:(t + 1) * TC], out[n % 4][:, :], B[:, m:m + 1],
                                                       None, ALU.add)
                    else:
                        last = nc.vector.tensor_copy(dst[:, m, t * TC:(t + 1) * TC], out[n % 4][:, :])
                    last.then_inc(s_st, 1)


def cross_attention(nc, X, QT, ident, ones, spread_mask, ctxT, head, wkv=None, bk=None, bv=None, ctx=None,
                    wo=None, bo=None, mask=None, clip=None):
    inner = HEADS * head
    chunks = inner // P
    PAIR = 2 * head
    HPC = P // head
    STEPS = 4
    MV = bool(clip or mask is not None)
    OWN = wkv is not None
    KB = chunks * NKEY // 512 if OWN else 0
    NAT = (chunks + 3) // 4 if wo is not None else 0
    OP = 4 if PAIR + 1 <= 64 else 2
    OR = 4 // OP
    TAIL = NAT + 1 if wo is not None else 0
    PER_TILE = 4 * KB + TAIL

    def users(n, first, last):
        kind = "KV"[n % 2]
        own = [(kind, k) for k in range(KB)] if not (last and n >= 2) else []
        own += [None] * (4 - len(own))
        tail = n == 0 and not first and wo is not None
        at = [("AT", r) for r in range(NAT)] if tail else []
        return {"pre": at[:1], "u1": own[:1], "mid": at[1:], "u2": own[1:2], "u3": own[2:3],
                "out": [("OUT", 0)] if tail else [], "u4": own[3:4]}

    SLOTS = ("pre", "u1", "mid", "u2", "u3", "out", "u4")

    def index(i, n, user):
        first, last = isinstance(i, int) and i == 0, isinstance(i, int) and i == TILES - 1
        if n < 0:
            return ("K", "V").index(user[0]) * KB + user[1]
        order = [(m, w) for m in range(STEPS) for sl in SLOTS for w in users(m, first, last)[sl] if w]
        before = order.index((n, user))
        if first:
            return 2 * KB + before
        return (i - 1) * PER_TILE + (2 * KB + PER_TILE - TAIL + before)

    def key_ready(i, n, g):
        u = n // 2
        k = KB - 1 if KB == 1 else 2 * g + 1
        if u == 0:
            return (index(0, -1, ("K", k)) if isinstance(i, int) and i == 0 else index(i - 1, 2, ("K", k))) + 1
        return index(i, 0, ("K", k)) + 1

    def value_ready(i, n):
        if n // 2 == 0:
            return (index(0, -1, ("V", KB - 1)) if isinstance(i, int) and i == 0 else index(i - 1, 3, ("V", KB - 1))) + 1
        return index(i, 1, ("V", KB - 1)) + 1

    def last_tail():
        at = (TILES - 2) * PER_TILE + (2 * KB + PER_TILE - TAIL) + PER_TILE - 2 * KB
        return [(at + r, ("AT", r)) for r in range(NAT)] + ([(at + NAT, ("OUT", 0))] if wo is not None else [])

    with stage(nc) as (sb, ps, sem):
        CT = [sb("ca_ctxT", [P, KC, NKEY]) for _ in range(2)]
        KT = [sb("ca_kT", [P, chunks, NKEY]) for _ in range(2)] if OWN else CT
        V = [sb("ca_v", [P, 2, 8, PAIR + 1]) for _ in range(2)]
        CN = [sb("ca_ctx", [P, 2, NKEY]) for _ in range(2)] if not OWN else None
        QB = [sb("ca_q_spread", [P, 4, 2, SEQ]) for _ in range(STEPS)]
        PR = [sb("ca_probs", [P, 4, NKEY]) for _ in range(2)]
        SC = [sb("ca_scores_moved", [P, 4, NKEY]) for _ in range(2)] if MV else None
        PT = [sb("ca_probsT", [P, 8, P]) for _ in range(2)]
        nmax = [sb("ca_neg_max", [P, 4]) for _ in range(2)]
        rsum = [sb("ca_inv_sum", [P, 4]) for _ in range(2)]
        A = sb("ca_attended", [P, inner])
        AT = sb("ca_attendedT", [P, chunks, P])
        SM = sb("ca_spread_mask", [P, HPC])
        if OWN:
            W = sb("ca_wkv", [P, KC, 2 * inner])
        if bk is not None:
            BK = sb("ca_bk", [P, chunks])
            BV = sb("ca_bv", [P, chunks])
        if wo is not None:
            WO = sb("ca_wo", [P, chunks, DIM])
            BO = sb("ca_bo", [1, DIM])
        if mask is not None:
            MFAC = sb("ca_mask_factor", [P, 1])
            MK = [sb("ca_mask", [P, NKEY]) for _ in range(2)]
            MB = [sb("ca_mask_added", [P, NKEY]) for _ in range(2)]
        psS = [ps("ca_scores", [P, 4, NKEY]) for _ in range(2)]
        psT = ps("ca_probs_flipped", [P, 8, P])
        psA = ps("ca_shared", [P, 512])
        psO = ps("ca_out", [P, 512])
        psA2 = psA[:, :].rearrange("p (a b) -> p a b", a=2)

        s_w, s_one = sem("weights_loaded"), sem("v_ones_set")
        s_ct = [sem(f"ctx{u}_loaded") for u in range(2)]
        s_mk = [sem(f"mask{u}_loaded") for u in range(2)]
        s_mb, s_vr = sem("mask_scaled"), sem("context_values_ready")
        psA_filled, psA_emptied = sem("psA_filled"), sem("psA_emptied")
        s_q, s_s, s_mv, s_mx = sem("queries_spread"), sem("scores_ready"), sem("scores_moved"), sem("max_ready")
        s_e, s_t, s_tc = sem("probs_ready"), sem("probs_flipped"), sem("probsT_ready")
        s_pv, s_rs, s_o, s_x = sem("attended"), sem("inv_sum_ready"), sem("attended_stored"), sem("x_updated")
        NW = 16 * (1 + OWN + 2 * (bk is not None) + 2 * (wo is not None))
        CL = 32 if not OWN else 16

        def tiles(eng, body):
            body(0)
            with eng.Fori(1, TILES - 1) as i:
                body(i)
            body(TILES - 1)

        def is_first(i):
            return isinstance(i, int) and i == 0

        def is_last(i):
            return isinstance(i, int) and i == TILES - 1

        with nc.Block() as block:
            @block.sync
            def _(sp):
                sp.dma_start(SM[:, :], spread_mask).then_inc(s_w, 16)
                if OWN:
                    sp.dma_start(W[:, :, :], rows_to_sbuf(wkv)).then_inc(s_w, 16)
                if bk is not None:
                    sp.dma_start(BK[:, :], bk).then_inc(s_w, 16)
                    sp.dma_start(BV[:, :], bv).then_inc(s_w, 16)
                if wo is not None:
                    sp.dma_start(WO[:, :, :], rows_to_sbuf(wo)).then_inc(s_w, 16)
                    sp.dma_start(BO[:, :], row(bo)).then_inc(s_w, 16)
                if mask is not None:
                    sp.sem_inc(s_mb, 2)

                def load(i):
                    for u in range(2):
                        if mask is not None:
                            sp.wait_ge(s_mb, i * 2 + (u + 1))
                            sp.dma_start(MK[u][:, :], mask[i, u].partition_broadcast(P)).then_inc(s_mk[u], 16)
                    for u in range(2):
                        if OWN and not is_first(i):
                            sp.wait_ge(psA_filled, value_ready(i - 1, 2 * u))
                        if not OWN:
                            sp.wait_ge(s_s, i * STEPS + (2 * u + 2))
                        sp.dma_start(CT[u][:, :, :], ctxT[i, u].rearrange("(c p) s -> p c s", p=P)).then_inc(s_ct[u], 16)
                        if not OWN:
                            sp.dma_start(CN[u][:, :, :], ctx[i, u].rearrange("(c p) d -> p c d", p=P)).then_inc(s_ct[u], 16)

                load(0)
                load(1)
                with sp.Fori(2, TILES) as i:
                    load(i)

            @block.gpsimd
            def _(pool):
                for u in range(2):
                    nc.gpsimd.memset(V[u][:, :, :, PAIR:PAIR + 1], 1.0).then_inc(s_one, 1)
                if mask is not None:
                    nc.gpsimd.memset(MFAC[:, :], -1e9).then_inc(s_one, 1)
                    pool.wait_ge(s_one, 3)
                pool.wait_ge(s_w, NW)
                pool.sem_inc(s_s, STEPS)
                if mask is not None:
                    pool.sem_inc(s_mv, STEPS)
                if not OWN:
                    pool.sem_inc(s_pv, STEPS)
                with pool.Fori(0, TILES) as i:
                    for u in range(2):
                        if not OWN:
                            pool.wait_ge(s_ct[u], (i + 1) * CL)
                            pool.wait_ge(s_pv, i * STEPS + (2 * u + 2))
                            for c in range(2):
                                last = nc.gpsimd.tensor_tensor(V[u][:, c, :, 0:PAIR],
                                                               CN[u][:, c, :].rearrange("p (a d) -> p a d", a=8),
                                                               ones[:, 0:1].unsqueeze(2).broadcast_to([P, 8, PAIR]), ALU.mult)
                            last.then_inc(s_vr, 1)
                        if mask is not None:
                            pool.wait_ge(s_mk[u], (i + 1) * 16)
                            pool.wait_ge(s_mv, i * STEPS + (2 * u + 2))
                            nc.gpsimd.tensor_tensor(MB[u][:, :], MK[u][:, :], MFAC[:, :].broadcast_to([P, NKEY]), ALU.mult).then_inc(s_mb, 1)
                        for g in range(2):
                            n = 2 * u + g
                            pool.wait_ge(s_s, i * STEPS + (n + 1))
                            tok = bass.ds(i * P + u * SEQ, SEQ)
                            if chunks == 2:
                                q = QT[:, g, tok].unsqueeze(1).broadcast_to([P, 8, SEQ])
                                m = SM[:, :].unsqueeze(2).broadcast_to([P, 8, SEQ])
                                o = QB[n][:, :, :, :].rearrange("p a b q -> p (a b) q")
                                nc.gpsimd.tensor_tensor(o, q, m, ALU.mult).then_inc(s_q, 1)
                            else:
                                for h in range(2):
                                    q = QT[:, 4 * g:4 * g + 4, tok]
                                    m = SM[:, h:h + 1].unsqueeze(2).broadcast_to([P, 4, SEQ])
                                    last = nc.gpsimd.tensor_tensor(QB[n][:, :, h, :], q, m, ALU.mult)
                                last.then_inc(s_q, 1)

            @block.tensor
            def _(pe):
                def fill(i, n, user, at=None):
                    kind, k = user
                    at = index(i, n, user) if at is None else at
                    if not (isinstance(at, int) and at == 0):
                        pe.wait_ge(psA_emptied, at)
                    if kind in ("K", "V"):
                        u = 0 if n < 0 else 1 - n // 2
                        j = 0 if n < 0 else (i if u else i + 1)
                        pe.wait_ge(s_ct[u], (j + 1) * 16)
                    if kind == "K":
                        for j in range(2):
                            m = 2 * k + j
                            for c in range(KC):
                                last = nc.tensor.matmul(psA2[:, j, :], W[:, c, m * P:(m + 1) * P], CT[u][:, c, :],
                                                        start=(c == 0), stop=(c == KC - 1))
                    elif kind == "V" and chunks == 2:
                        for j in range(2):
                            for c in range(KC):
                                last = nc.tensor.matmul(psA2[:, j, :], CT[u][:, c, j * P:(j + 1) * P],
                                                        W[:, c, inner:2 * inner], start=(c == 0), stop=(c == KC - 1))
                    elif kind == "V":
                        j, hf = k // 2, k % 2
                        for c in range(KC):
                            last = nc.tensor.matmul(psA[:, :], CT[u][:, c, j * P:(j + 1) * P],
                                                    W[:, c, inner + hf * 512:inner + (hf + 1) * 512],
                                                    start=(c == 0), stop=(c == KC - 1))
                    elif kind == "AT":
                        if k == 0:
                            pe.wait_ge(s_o, i * STEPS * OR)
                        for c in range(min(4, chunks)):
                            cc = k * 4 + c
                            last = nc.tensor.transpose(psA[:, c * P:(c + 1) * P], A[:, cc * P:(cc + 1) * P], ident[:, :])
                    else:
                        pe.wait_ge(psA_emptied, at)
                        for c in range(chunks):
                            nc.tensor.matmul(psA[:, 0:DIM], AT[:, c, :], WO[:, c, :], start=(c == 0), stop=False)
                        last = nc.tensor.matmul(psA[:, 0:DIM], ones[0:1, :], BO[:, :], start=False, stop=True)
                    last.then_inc(psA_filled, 1)

                def scores(i, n):
                    u, g = n // 2, n % 2
                    pe.wait_ge(s_q, i * STEPS + (n + 1))
                    if OWN:
                        pe.wait_ge(psA_emptied, key_ready(i, n, g))
                    else:
                        pe.wait_ge(s_ct[u], (i + 1) * CL)
                    for a in range(4):
                        k = KT[u][:, g, :] if chunks == 2 else KT[u][:, 4 * g + a, :]
                        last = nc.tensor.matmul(psS[n % 2][:, a, :], QB[n][:, a, :, :].rearrange("p b q -> p (b q)"), k,
                                                start=True, stop=True)
                    last.then_inc(s_s, 1)

                def flip(i, n):
                    pe.wait_ge(s_e, i * STEPS + (n + 1))
                    for a in range(4):
                        for c in range(2):
                            last = nc.tensor.transpose(psT[:, 2 * a + c, :], PR[n % 2][:, a, c * P:(c + 1) * P], ident[:, :])
                    last.then_inc(s_t, 1)

                def attend(i, n, r):
                    u, g = n // 2, n % 2
                    if r == 0:
                        pe.wait_ge(s_tc, i * STEPS + (n + 1))
                        if g == 0:
                            if OWN:
                                pe.wait_ge(psA_emptied, value_ready(i, n))
                            else:
                                pe.wait_ge(s_vr, i * 2 + (u + 1))
                    if not (is_first(i) and n == 0 and r == 0):
                        pe.wait_ge(s_o, i * STEPS * OR + (n * OR + r))
                    for a in range(OP):
                        pr = r * OP + a
                        for c in range(2):
                            last = nc.tensor.matmul(psO[:, a * (PAIR + 1):(a + 1) * (PAIR + 1)], PT[n % 2][:, 2 * pr + c, :],
                                                    V[u][:, c, 4 * g + pr, :], start=(c == 0), stop=(c == 1))
                    last.then_inc(s_pv, 1)

                def body(i):
                    for n in range(STEPS):
                        us = users(n, is_first(i), is_last(i))

                        def slot(name):
                            for w in us[name]:
                                if w:
                                    fill(i, n, w)

                        def ahead():
                            if not (is_last(i) and n >= 2):
                                scores(i if n < 2 else i + 1, (n + 2) % STEPS)

                        flip(i, n)
                        slot("pre")
                        slot("u1")
                        slot("mid")
                        if not OWN:
                            ahead()
                        attend(i, n, 0)
                        slot("u2")
                        if OR == 2:
                            attend(i, n, 1)
                        slot("u3")
                        slot("out")
                        if OWN:
                            ahead()
                        slot("u4")

                pe.wait_ge(s_w, NW)
                pe.wait_ge(s_one, 2)
                for kind in "KV":
                    for k in range(KB):
                        fill(0, -1, (kind, k))
                scores(0, 0)
                scores(0, 1)
                tiles(pe, body)
                for at, w in last_tail():
                    fill(TILES, 0, w, at)

            @block.scalar
            def _(act):
                def empty(at, w):
                    kind, k = w
                    act.wait_ge(psA_filled, at + 1)
                    if kind == "K" and bk is not None:
                        for j in range(2):
                            last = nc.scalar.activation(KT[key_buffer[0]][:, 2 * k + j, :], psA2[:, j, :], ACT.Identity,
                                                        bias=BK[:, 2 * k + j:2 * k + j + 1])
                    elif kind == "K":
                        last = nc.scalar.copy(KT[key_buffer[0]][:, 2 * k:2 * k + 2, :], psA2)
                    elif bk is not None:
                        for c in range(chunks):
                            last = nc.scalar.activation(AT[:, c, :], psA[:, c * P:(c + 1) * P], ACT.Identity, bias=BV[:, c:c + 1])
                    else:
                        nn = min(4, chunks)
                        last = nc.scalar.copy(AT[:, k * nn:(k + 1) * nn, :].rearrange("p a b -> p (a b)"), psA[:, 0:nn * P])
                    last.then_inc(psA_emptied, 1)

                key_buffer = [0]

                def exponentiate(i, n):
                    if clip:
                        act.wait_ge(s_mv, i * STEPS + (n + 1))
                        nc.scalar.activation(PR[n % 2][:, :, :], SC[n % 2][:, :, :], ACT.Exp).then_inc(s_e, 1)
                        return
                    act.wait_ge(s_mx, i * STEPS + (n + 1))
                    src = SC[n % 2] if MV else psS[n % 2]
                    for a in range(4):
                        last = nc.scalar.activation(PR[n % 2][:, a, :], src[:, a, :], ACT.Exp, bias=nmax[n % 2][:, a:a + 1])
                    last.then_inc(s_e, 1)

                def body(i):
                    for n in range(STEPS):
                        us = users(n, is_first(i), is_last(i))
                        key_buffer[0] = 1 - n // 2

                        def slot(*names):
                            for name in names:
                                for w in us[name]:
                                    if w and w[0] in ("K", "AT"):
                                        empty(index(i, n, w), w)

                        if mask is not None:
                            act.wait_ge(s_t, i * STEPS + (n + 1))
                            nc.scalar.copy(PT[n % 2][:, :, :], psT[:, :, :]).then_inc(s_tc, 1)
                            slot("pre")
                            if not (is_last(i) and n == 3):
                                exponentiate(i if n < 3 else i + 1, (n + 1) % STEPS)
                            slot("u1", "mid", "u2", "u3", "u4")
                            continue
                        slot("pre", "u1", "mid", "u2", "u3")
                        if not (is_last(i) and n >= 2):
                            exponentiate(i if n < 2 else i + 1, (n + 2) % STEPS)
                        slot("u4")

                act.wait_ge(s_w, NW)
                for k in range(KB):
                    empty(index(0, -1, ("K", k)), ("K", k))
                exponentiate(0, 0)
                if mask is None:
                    exponentiate(0, 1)
                tiles(act, body)
                for at, w in last_tail():
                    if w[0] == "AT":
                        empty(at, w)

            @block.vector
            def _(dve):
                PC = 0 if OWN else STEPS
                OFF = STEPS if mask is not None else 0

                def empty(i, at, w, u):
                    kind, k = w
                    dve.wait_ge(psA_filled, at + 1)
                    if kind == "V" and chunks == 2:
                        for c in range(2):
                            last = nc.vector.tensor_copy(V[u][:, c, :, 0:PAIR], psA2[:, c, :].rearrange("p (a d) -> p a d", a=8))
                    elif kind == "V":
                        j, hf = k // 2, k % 2
                        last = nc.vector.tensor_copy(V[u][:, j, 4 * hf:4 * hf + 4, 0:PAIR],
                                                     psA[:, :].rearrange("p (a d) -> p a d", a=4))
                    else:
                        tile = bass.ds(i - 1, 1)
                        last = nc.vector.tensor_tensor(X[:, tile, :], psA[:, 0:DIM].unsqueeze(1), X[:, tile, :], ALU.add)
                    last.then_inc(psA_emptied, 1)

                def take(i, n):
                    dve.wait_ge(s_s, i * STEPS + (n + 1) + STEPS)
                    if clip:
                        nc.vector.tensor_scalar(SC[n % 2][:, :, :], psS[n % 2][:, :, :], -clip, clip, ALU.max,
                                                ALU.min).then_inc(s_mv, 1)
                        return
                    if mask is not None:
                        if n % 2 == 0:
                            dve.wait_ge(s_mb, i * 2 + (n // 2 + 3))
                        nc.vector.tensor_tensor(SC[n % 2][:, :, :], psS[n % 2][:, :, :],
                                                MB[n // 2][:, :].unsqueeze(1).broadcast_to([P, 4, NKEY]), ALU.add).then_inc(s_mv, 1)
                        dve.wait_ge(s_mv, i * STEPS + (n + 1) + OFF)
                    src = SC[n % 2] if MV else psS[n % 2]
                    nc.vector.tensor_reduce(nmax[n % 2][:, :], src[:, :, :], AX_X, ALU.max, negate=True).then_inc(s_mx, 1)

                def store(i, n, r):
                    u, g = n // 2, n % 2
                    at = i * STEPS * OR + (n * OR + r + 1)
                    dve.wait_ge(s_pv, at + PC)
                    O = psO[:, 0:OP * (PAIR + 1)].rearrange("p (a w) -> p a w", a=OP)
                    R = rsum[n % 2][:, r * OP:(r + 1) * OP]
                    nc.vector.reciprocal(R, O[:, :, PAIR]).then_inc(s_rs, 1)
                    dve.wait_ge(s_rs, at)
                    for h in range(2):
                        dst = A[u * SEQ:(u + 1) * SEQ, :].rearrange("p (a b d) -> p a b d", a=8, b=2)[
                            :, 4 * g + r * OP:4 * g + (r + 1) * OP, h, :]
                        last = nc.vector.tensor_tensor(
                            dst, O[h * SEQ:(h + 1) * SEQ, :, h * head:(h + 1) * head],
                            R[h * SEQ:(h + 1) * SEQ, :].unsqueeze(2).broadcast_to([SEQ, OP, head]), ALU.mult)
                    last.then_inc(s_o, 1)

                def body(i):
                    for n in range(STEPS):
                        us = users(n, is_first(i), is_last(i))

                        def slot(*names):
                            for name in names:
                                for w in us[name]:
                                    if w and w[0] in ("V", "OUT"):
                                        empty(i, index(i, n, w), w, 1 - n // 2)

                        def ahead():
                            if not (is_last(i) and n >= 2):
                                take(i if n < 2 else i + 1, (n + 2) % STEPS)

                        if mask is None:
                            dve.wait_ge(s_t, i * STEPS + (n + 1))
                            nc.vector.tensor_copy(PT[n % 2][:, :, :], psT[:, :, :]).then_inc(s_tc, 1)
                        slot("u1")
                        if not OWN:
                            ahead()
                        store(i, n, 0)
                        slot("u2")
                        if OR == 2:
                            store(i, n, 1)
                        slot("u3", "out")
                        if OWN:
                            ahead()
                        slot("u4")
                    if wo is None:
                        dve.wait_ge(s_o, (i + 1) * STEPS * OR)
                        tile = bass.ds(i, 1)
                        nc.vector.tensor_tensor(X[:, tile, :], A[:, :].unsqueeze(1), X[:, tile, :], ALU.add).then_inc(s_x, 1)

                for k in range(KB):
                    empty(0, index(0, -1, ("V", k)), ("V", k), 0)
                take(0, 0)
                take(0, 1)
                tiles(dve, body)
                for at, w in last_tail():
                    if w[0] == "OUT":
                        empty(TILES, at, w, 0)


def linear_attention(nc, X, XNT, ident, d):
    with stage(nc) as (sb, ps, sem):
        W = sb("la_wqkv", [P, KC, 3 * DIM])
        WO = sb("la_wout", [P, KC, DIM])
        SH = sb("la_same_head", [P, P])
        H8 = sb("la_heads", [P, 8])
        XS = sb("la_x", [P, KC, P])
        low = sb("la_below_zero", [P, 2, DIM])
        ex = sb("la_exp", [P, 2, DIM])
        QS = sb("la_qT", [P, KC, P])
        KS = sb("la_k", [P, DIM])
        VS = sb("la_v", [P, 2, P + 1])
        KV = sb("la_kv", [P, 2, 2, P + 8])
        rden = sb("la_inv_denominator", [P, 2, 8])
        A = sb("la_attended", [P, DIM])
        AT = sb("la_attendedT", [P, KC, P])
        psQ, psK = ps("la_psq", [P, 512]), ps("la_pskv", [P, 512])
        psM = [ps("la_psm", [P, 512]) for _ in range(2)]
        psO, psT, psY = ps("la_pso", [P, 512]), ps("la_pst", [P, 512]), ps("la_psy", [P, 512])
        s_w, s_one, s_xs = sem("weights_loaded"), sem("v_ones_set"), sem("x_tile_ready")
        s_p, s_low, s_ex, s_f = sem("qkv_projected"), sem("below_zero_ready"), sem("exp_ready"), sem("features_ready")
        s_m, s_kv, s_o, s_d, s_a = sem("kv_summed"), sem("kv_ready"), sem("out_ready"), sem("dve_step"), sem("attended_ready")
        s_at, s_atc, s_y, s_x = sem("attended_flipped"), sem("attendedT_ready"), sem("out_projected"), sem("x_updated")
        with nc.Block() as block:
            @block.sync
            def _(sp):
                sp.dma_start(W[:, :, :], rows_to_sbuf(d["L0_attn_Wqkv"])).then_inc(s_w, 16)
                sp.dma_start(WO[:, :, :], rows_to_sbuf(d["L0_attn_Wout"])).then_inc(s_w, 16)
                sp.dma_start(SH[:, :], d["same_head"]).then_inc(s_w, 16)
                sp.dma_start(H8[:, :], d["heads8"]).then_inc(s_w, 16)

            @block.gpsimd
            def _(pool):
                nc.gpsimd.memset(VS[:, :, P:P + 1], 1.0).then_inc(s_one, 1)

            @block.tensor
            def _(pe):
                pe.wait_ge(s_w, 64)
                pe.wait_ge(s_one, 1)
                with pe.Fori(0, TILES) as i:
                    pe.wait_ge(s_xs, i + 1)
                    for m in range(KC):
                        for c in range(KC):
                            nc.tensor.matmul(psQ[:, m * P:(m + 1) * P], W[:, c, m * P:(m + 1) * P], XS[:, c, :],
                                             start=(c == 0), stop=(c == KC - 1))
                    for c in range(KC):
                        last = nc.tensor.matmul(psK[:, :], XS[:, c, :], W[:, c, DIM:3 * DIM], start=(c == 0),
                                                stop=(c == KC - 1))
                    last.then_inc(s_p, 1)
                    pe.wait_ge(s_f, i + 1)
                    for b in range(2):
                        r = slice(b * SEQ, (b + 1) * SEQ)
                        for g in range(2):
                            last = nc.tensor.matmul(psM[b][:, g * (P + 1):(g + 1) * (P + 1)], KS[r, g * P:(g + 1) * P],
                                                    VS[r, g, :], start=True, stop=True)
                    last.then_inc(s_m, 1)
                    pe.wait_ge(s_kv, i + 1)
                    for b in range(2):
                        for g in range(2):
                            last = nc.tensor.matmul(psO[b * SEQ:(b + 1) * SEQ, g * (P + 8):(g + 1) * (P + 8)],
                                                    QS[:, g, b * SEQ:(b + 1) * SEQ], KV[:, b, g, :], start=True, stop=True)
                    last.then_inc(s_o, 1)
                    pe.wait_ge(s_a, i + 1)
                    for c in range(KC):
                        last = nc.tensor.transpose(psT[:, c * P:(c + 1) * P], A[:, c * P:(c + 1) * P], ident[:, :])
                    last.then_inc(s_at, 1)
                    pe.wait_ge(s_atc, i + 1)
                    for c in range(KC):
                        last = nc.tensor.matmul(psY[:, 0:DIM], AT[:, c, :], WO[:, c, :], start=(c == 0), stop=(c == KC - 1))
                    last.then_inc(s_y, 1)

            @block.scalar
            def _(act):
                act.sem_inc(s_x, 1)
                with act.Fori(0, TILES) as i:
                    act.wait_ge(s_x, i + 1)
                    nc.scalar.copy(XS[:, :, :], XNT[:, :, bass.ds(i * P, P)]).then_inc(s_xs, 1)
                    act.wait_ge(s_low, i + 1)
                    nc.scalar.activation(ex[:, :, :], low[:, :, :], ACT.Exp).then_inc(s_ex, 1)
                    act.wait_ge(s_at, i + 1)
                    nc.scalar.copy(AT[:, :, :].rearrange("p a b -> p (a b)"), psT[:, 0:DIM]).then_inc(s_atc, 1)

            @block.vector
            def _(dve):
                dve.wait_ge(s_w, 64)
                with dve.Fori(0, TILES) as i:
                    link = Chain(dve, s_d, i * 2)
                    dve.wait_ge(s_p, i + 1)
                    nc.vector.tensor_scalar(low[:, 0, :], psQ[:, 0:DIM], 0.0, None, ALU.min)
                    nc.vector.tensor_scalar(low[:, 1, :], psK[:, 0:DIM], 0.0, None, ALU.min).then_inc(s_low, 1)
                    for g in range(2):
                        nc.vector.tensor_copy(VS[:, g, 0:P], psK[:, DIM + g * P:DIM + (g + 1) * P])
                    dve.wait_ge(s_ex, i + 1)
                    nc.vector.scalar_tensor_tensor(QS[:, :, :].rearrange("p a b -> p (a b)"), psQ[:, 0:DIM], 0.0,
                                                   ex[:, 0, :], ALU.max, ALU.add)
                    nc.vector.scalar_tensor_tensor(KS[:, :], psK[:, 0:DIM], 0.0, ex[:, 1, :], ALU.max,
                                                   ALU.add).then_inc(s_f, 1)
                    dve.wait_ge(s_m, i + 1)
                    for b in range(2):
                        for g in range(2):
                            o = g * (P + 1)
                            nc.vector.tensor_tensor(KV[:, b, g, 0:P], psM[b][:, o:o + P], SH[:, :], ALU.mult)
                            last = nc.vector.tensor_scalar(KV[:, b, g, P:P + 8], H8[:, :], psM[b][:, o + P:o + P + 1], None,
                                                           ALU.mult)
                    last.then_inc(s_kv, 1)
                    dve.wait_ge(s_o, i + 1)
                    O = psO[:, 0:2 * (P + 8)].rearrange("p (g w) -> p g w", g=2)
                    link(nc.vector.tensor_scalar(rden[:, :, :], O[:, :, P:P + 8], 1e-6, None, ALU.add))
                    link(nc.vector.reciprocal(rden[:, :, :], rden[:, :, :]))
                    for g in range(2):
                        last = nc.vector.tensor_tensor(A[:, g * P:(g + 1) * P].rearrange("p (h d) -> p h d", h=8),
                                                       O[:, g, 0:P].rearrange("p (h d) -> p h d", h=8),
                                                       rden[:, g, :].unsqueeze(2).broadcast_to([P, 8, 16]), ALU.mult)
                    last.then_inc(s_a, 1)
                    dve.wait_ge(s_y, i + 1)
                    nc.vector.tensor_tensor(X[:, i, :], psY[:, 0:DIM], X[:, i, :], ALU.add).then_inc(s_x, 1)


def mixed_experts(nc, X, XNT, ident, ones, d):
    E, DFF, TC = 8, 1024, 512
    NM = DFF // P
    NT = TOKENS // TC
    BPC = TC // SEQ
    with ExitStack() as outer:
        def keep(name, shape):
            return outer.enter_context(nc.sbuf_tensor(name, shape, F32))

        GT = keep("me_gateT", [E, P])
        GTOK = keep("me_gate", [P, E])
        GB = keep("me_gate_rows", [P, E, SEQ])
        with stage(nc) as (sb, ps, sem):
            W1 = sb("mg_w1", [P, KC, DIM])
            B1 = sb("mg_b1", [P, KC])
            W2 = sb("mg_w2", [P, KC, E])
            B2 = sb("mg_b2", [1, E])
            hid = [sb("mg_hidden", [P, TC]) for _ in range(2)]
            part = sb("mg_batch_sums", [P, KC, NT, SEQ])
            HM = sb("mg_hidden_mean", [P, KC, 2, SEQ])
            DG = sb("mg_gate_diagonals", [SEQ, E, SEQ])
            psH = [ps("mg_psh", [P, 512]) for _ in range(2)]
            psG, psGT, psB = ps("mg_psg", [P, 512]), ps("mg_psgt", [P, 512]), ps("mg_psb", [P, 512])
            s_w, s_h, s_r, s_p = sem("weights_loaded"), sem("hidden_projected"), sem("hidden_ready"), sem("batch_sums_ready")
            s_d, s_m, s_g, s_gt, s_dg, s_gb = (sem("dve_step"), sem("mean_ready"), sem("gates_projected"), sem("gates_ready"),
                                               sem("diagonals_ready"), sem("gate_rows_projected"))
            jobs = [(m, t) for m in range(KC) for t in range(NT)]
            with nc.Block() as block:
                @block.sync
                def _(sp):
                    sp.dma_start(W1[:, :, :], rows_to_sbuf(d["L0_ffn_gW1T"])).then_inc(s_w, 16)
                    sp.dma_start(B1[:, :], d["L0_ffn_gb1_col"]).then_inc(s_w, 16)
                    sp.dma_start(W2[:, :, :], rows_to_sbuf(d["L0_ffn_gW2T"])).then_inc(s_w, 16)
                    sp.dma_start(B2[:, :], row(d["L0_ffn_gb2"])).then_inc(s_w, 16)

                @block.tensor
                def _(pe):
                    pe.wait_ge(s_w, 64)
                    for n, (m, t) in enumerate(jobs):
                        if n >= 2:
                            pe.wait_ge(s_r, n - 1)
                        for c in range(KC):
                            last = nc.tensor.matmul(psH[n % 2][:, :], W1[:, c, m * P:(m + 1) * P],
                                                    XNT[:, c, t * TC:(t + 1) * TC], start=(c == 0), stop=(c == KC - 1))
                        last.then_inc(s_h, 1)
                    pe.wait_ge(s_m, 1)
                    for c in range(KC):
                        nc.tensor.matmul(psG[:, 0:E], HM[:, c, :, :].rearrange("p a s -> p (a s)"), W2[:, c, :],
                                         start=(c == 0), stop=False)
                    nc.tensor.matmul(psG[:, 0:E], ones[0:1, :], B2[:, :], start=False, stop=True)
                    for c in range(KC):
                        nc.tensor.matmul(psGT[0:E, 0:P], W2[:, c, :], HM[:, c, :, :].rearrange("p a s -> p (a s)"),
                                         start=(c == 0), stop=False)
                    nc.tensor.matmul(psGT[0:E, 0:P], B2[:, :], ones[0:1, :], start=False, stop=True).then_inc(s_g, 1)
                    pe.wait_ge(s_dg, 1)
                    nc.tensor.matmul(psB[:, :], ones[0:SEQ, :], DG[:, :, :].rearrange("p e s -> p (e s)"),
                                     start=True, stop=True).then_inc(s_gb, 1)

                @block.scalar
                def _(act):
                    act.wait_ge(s_w, 64)
                    for n, (m, t) in enumerate(jobs):
                        act.wait_ge(s_h, n + 1)
                        if n >= 2:
                            act.wait_ge(s_p, n - 1)
                        nc.scalar.activation(hid[n % 2][:, :], psH[n % 2][:, :], ACT.Relu, bias=B1[:, m:m + 1]).then_inc(s_r, 1)

                @block.vector
                def _(dve):
                    link = Chain(dve, s_d)
                    for n, (m, t) in enumerate(jobs):
                        dve.wait_ge(s_r, n + 1)
                        nc.vector.tensor_reduce(part[:, m, t, :], hid[n % 2][:, :].rearrange("p (b s) -> p s b", s=SEQ), AX_X,
                                                ALU.add).then_inc(s_p, 1)
                    dve.wait_ge(s_p, len(jobs))
                    for m in range(KC):
                        link(nc.vector.tensor_reduce(HM[:, m, 0, :], part[:, m, :, :].rearrange("p t s -> p s t"), AX_X, ALU.add))
                    link(nc.vector.tensor_scalar(HM[:, :, 1, :], HM[:, :, 0, :], 1.0 / BATCH, None, ALU.mult))
                    nc.vector.tensor_copy(HM[:, :, 0, :], HM[:, :, 1, :]).then_inc(s_m, 1)
                    dve.wait_ge(s_g, 1)
                    nc.vector.tensor_copy(GT[:, :], psGT[0:E, 0:P])
                    link(nc.vector.tensor_copy(GTOK[:, :], psG[:, 0:E]))
                    for e in range(E):
                        last = nc.vector.tensor_scalar(DG[:, e, :], ident[0:SEQ, 0:SEQ], GTOK[0:SEQ, e:e + 1], None, ALU.mult)
                    last.then_inc(s_dg, 1)
                    dve.wait_ge(s_gb, 1)
                    link(nc.vector.tensor_copy(GB[:, :, :].rearrange("p e s -> p (e s)"), psB[:, :]))

        Y1 = keep("me_hidden", [P, NM, TOKENS])
        with stage(nc) as (sb, ps, sem):
            W = sb("m1_w", [P, E, KC, DFF])
            B = sb("m1_b", [E, DFF])
            GTR = sb("m1_gateT", [E, BPC, SEQ])
            XG = sb("m1_x_gated", [P, E, KC, TC])
            out = [ps("m1_ps", [P, 512]) for _ in range(4)]
            s_b, s_gt = sem("biases_loaded"), sem("gateT_ready")
            s_we = [sem(f"expert{e}_loaded") for e in range(E)]
            s_xg, s_mm, s_y = sem("x_gated"), sem("multiplied"), sem("hidden_ready")
            with nc.Block() as block:
                @block.sync
                def _(sp):
                    sp.dma_start(B[:, :], d["L0_ffn_eb1"]).then_inc(s_b, 16)
                    for e in range(E):
                        sp.dma_start(W[:, e, :, :], rows_to_sbuf(d["L0_ffn_eW1T"][e])).then_inc(s_we[e], 16)

                @block.vector
                def _(dve):
                    nc.vector.tensor_copy(GTR[:, :, :], GT[:, 0:SEQ].unsqueeze(1).broadcast_to([E, BPC, SEQ])).then_inc(s_gt, 1)
                    dve.sem_inc(s_mm, NM)
                    with dve.Fori(0, NT) as t:
                        dve.wait_ge(s_mm, t * NM + NM)
                        for e in range(E):
                            for c in range(KC):
                                nc.vector.tensor_tensor(
                                    XG[:, e, c, :].rearrange("p (b s) -> p b s", s=SEQ),
                                    XNT[:, c, bass.ds(t * TC, TC)].rearrange("p (b s) -> p b s", s=SEQ),
                                    GB[:, e, :].unsqueeze(1).broadcast_to([P, BPC, SEQ]), ALU.mult).then_inc(s_xg, 1)

                @block.tensor
                def _(pe):
                    pe.wait_ge(s_b, 16)
                    pe.wait_ge(s_gt, 1)
                    for e in range(E):
                        pe.wait_ge(s_we[e], 16)
                    pe.sem_inc(s_y, 4)
                    with pe.Fori(0, NT) as t:
                        for m in range(NM):
                            pe.wait_ge(s_y, t * NM + (m + 1))
                            dst = out[m % 4][:, :]
                            nc.tensor.matmul(dst, B[:, m * P:(m + 1) * P], GTR[:, :, :].rearrange("p b s -> p (b s)"),
                                             start=True, stop=False)
                            for e in range(E):
                                for c in range(KC):
                                    if m == 0:
                                        pe.wait_ge(s_xg, t * E * KC + (e * KC + c + 1))
                                    last = nc.tensor.matmul(dst, W[:, e, c, m * P:(m + 1) * P], XG[:, e, c, :], start=False,
                                                            stop=(e == E - 1 and c == KC - 1))
                            last.then_inc(s_mm, 1)

                @block.scalar
                def _(act):
                    with act.Fori(0, NT) as t:
                        for m in range(NM):
                            act.wait_ge(s_mm, t * NM + (m + 1 + NM))
                            nc.scalar.activation(Y1[:, m, bass.ds(t * TC, TC)], out[m % 4][:, :], ACT.Relu).then_inc(s_y, 1)

        with stage(nc) as (sb, ps, sem):
            W = sb("m2_w", [P, E // 2, NM, 2, DIM])
            B = sb("m2_b", [E, DIM])
            BT = sb("m2_bias_rows", [P, DIM])
            out = [ps("m2_ps", [P, 2, DIM]) for _ in range(4)]
            psB = ps("m2_psb", [P, 512])
            s_b, s_bm, s_bt, s_bx = sem("bias_loaded"), sem("bias_projected"), sem("bias_rows_ready"), sem("bias_added")
            s_we = [sem(f"experts{e}_loaded") for e in range(E // 2)]
            s_mm, s_h, s_x = sem("multiplied"), sem("first_expert_added"), sem("second_expert_added")
            with nc.Block() as block:
                @block.sync
                def _(sp):
                    sp.dma_start(B[:, :], d["L0_ffn_eb2"]).then_inc(s_b, 16)
                    for j in range(E // 2):
                        for h in range(2):
                            sp.dma_start(W[:, j, :, h, :], rows_to_sbuf(d["L0_ffn_eW2T"][2 * j + h])).then_inc(s_we[j], 16)

                @block.tensor
                def _(pe):
                    pe.wait_ge(s_b, 16)
                    nc.tensor.matmul(psB[:, 0:DIM], GT[:, :], B[:, :], start=True, stop=True).then_inc(s_bm, 1)
                    for j in range(E // 2):
                        pe.wait_ge(s_we[j], 32)
                    pe.sem_inc(s_x, 4)
                    with pe.Fori(0, E // 2) as j:
                        for t in range(TILES):
                            pe.wait_ge(s_x, j * TILES + (t + 1))
                            for m in range(NM):
                                last = nc.tensor.matmul(out[t % 4][:, :, :].rearrange("p a b -> p (a b)"),
                                                        Y1[:, m, t * P:(t + 1) * P],
                                                        W[:, j, m, :, :].rearrange("p a b -> p (a b)"),
                                                        start=(m == 0), stop=(m == NM - 1))
                            last.then_inc(s_mm, 1)

                @block.vector
                def _(dve):
                    dve.wait_ge(s_bm, 1)
                    nc.vector.tensor_copy(BT[:, :], psB[:, 0:DIM]).then_inc(s_bt, 1)
                    dve.wait_ge(s_bt, 1)
                    nc.vector.tensor_tensor(X[:, :, :], X[:, :, :], BT[:, :].unsqueeze(1).broadcast_to([P, TILES, DIM]),
                                            ALU.add).then_inc(s_bx, 1)
                    dve.wait_ge(s_bx, 1)
                    with dve.Fori(0, E // 2) as j:
                        for t in range(TILES):
                            dve.wait_ge(s_mm, j * TILES + (t + 1))
                            nc.vector.scalar_tensor_tensor(X[:, t, :], out[t % 4][:, 0, :], GTOK[:, bass.ds(j * 2, 1)], X[:, t, :],
                                                           ALU.mult, ALU.add).then_inc(s_h, 1)
                            dve.wait_ge(s_h, j * TILES + (t + 1))
                            nc.vector.scalar_tensor_tensor(X[:, t, :], out[t % 4][:, 1, :], GTOK[:, bass.ds(j * 2 + 1, 1)],
                                                           X[:, t, :], ALU.mult, ALU.add).then_inc(s_x, 1)


def first_maximum(nc, link, onehot, top, scratch, values, order, shape):
    link(nc.vector.tensor_reduce(top, values, AX_X, ALU.max))
    link(nc.vector.tensor_tensor(onehot, values, top.unsqueeze(2).broadcast_to(shape), ALU.is_equal))
    link(nc.vector.tensor_tensor(onehot, onehot, order.unsqueeze(1).broadcast_to(shape), ALU.mult))
    link(nc.vector.tensor_reduce(scratch, onehot, AX_X, ALU.max))
    link(nc.vector.tensor_tensor(onehot, onehot, scratch.unsqueeze(2).broadcast_to(shape), ALU.is_equal))


def routed_experts(nc, X, XNT, ident, ones, d):
    E, F, TC = 8, 512, 512
    CAP = -(-2 * TOKENS * 5 // (E * 4))
    NF = F // P
    NT = TOKENS // TC
    with ExitStack() as outer:
        G = outer.enter_context(nc.sbuf_tensor("re_gate", [P, TILES, E], F32))
        with stage(nc) as (sb, ps, sem):
            WG = sb("rt_w", [P, KC, E])
            OR = sb("rt_order", [P, E])
            BE = sb("rt_before", [P, P])
            S = [P, TILES, E]
            L, PRB, P2, KM = sb("rt_logits", S), sb("rt_probs", S), sb("rt_probs_left", S), sb("rt_kept", [P, 2, TILES, E])
            OH = sb("rt_onehot", [P, 2, TILES, E])
            m, sm, v1, v2, sc = (sb("rt_max", [P, TILES]), sb("rt_sum", [P, TILES]), sb("rt_top1", [P, TILES]),
                                 sb("rt_top2", [P, TILES]), sb("rt_scratch", [P, TILES]))
            R = [sb("rt_running", [P, 2 * TILES, E]) for _ in range(2)]
            TOT = sb("rt_totals", [P, 2 * TILES, E])
            psL, psR, psT = ps("rt_psl", [P, 512]), ps("rt_psr", [P, 512]), ps("rt_pst", [P, 512])
            s_w, s_l, s_mx, s_e, s_d, s_oh, s_c = (sem("weights_loaded"), sem("logits_ready"), sem("logits_shifted"),
                                                   sem("exp_ready"), sem("dve_step"), sem("choices_ready"), sem("counts_ready"))
            with nc.Block() as block:
                @block.sync
                def _(sp):
                    sp.dma_start(WG[:, :, :], rows_to_sbuf(d["L1_ffn_Wg"])).then_inc(s_w, 16)
                    sp.dma_start(OR[:, :], d["expert_order"]).then_inc(s_w, 16)
                    sp.dma_start(BE[:, :], d["before"]).then_inc(s_w, 16)

                @block.tensor
                def _(pe):
                    pe.wait_ge(s_w, 48)
                    for t in range(TILES):
                        for c in range(KC):
                            last = nc.tensor.matmul(psL[:, t * E:(t + 1) * E], XNT[:, c, t * P:(t + 1) * P], WG[:, c, :],
                                                    start=(c == 0), stop=(c == KC - 1))
                    last.then_inc(s_l, 1)
                    pe.wait_ge(s_oh, 1)
                    flat = OH[:, :, :, :].rearrange("p k t e -> p (k t e)")
                    nc.tensor.matmul(psR[:, 0:2 * TILES * E], BE[:, :], flat, start=True, stop=True)
                    nc.tensor.matmul(psT[:, 0:2 * TILES * E], ones[:, :], flat, start=True, stop=True).then_inc(s_c, 1)

                @block.scalar
                def _(act):
                    act.wait_ge(s_mx, 1)
                    nc.scalar.activation(PRB[:, :, :], L[:, :, :], ACT.Exp).then_inc(s_e, 1)

                @block.vector
                def _(dve):
                    link = Chain(dve, s_d)
                    dve.wait_ge(s_w, 48)
                    dve.wait_ge(s_l, 1)
                    PL = psL[:, 0:TILES * E].rearrange("p (t e) -> p t e", e=E)
                    link(nc.vector.tensor_reduce(m[:, :], PL, AX_X, ALU.max))
                    nc.vector.tensor_tensor(L[:, :, :], PL, m[:, :].unsqueeze(2).broadcast_to(S), ALU.subtract).then_inc(s_mx, 1)
                    dve.wait_ge(s_e, 1)
                    link(nc.vector.tensor_reduce(sm[:, :], PRB[:, :, :], AX_X, ALU.add))
                    link(nc.vector.reciprocal(sm[:, :], sm[:, :]))
                    link(nc.vector.tensor_tensor(PRB[:, :, :], PRB[:, :, :], sm[:, :].unsqueeze(2).broadcast_to(S), ALU.mult))
                    first_maximum(nc, link, OH[:, 0, :, :], v1[:, :], sc[:, :], PRB[:, :, :], OR[:, :], S)
                    link(nc.vector.scalar_tensor_tensor(P2[:, :, :], OH[:, 0, :, :], -2.0, PRB[:, :, :], ALU.mult, ALU.add))
                    first_maximum(nc, link, OH[:, 1, :, :], v2[:, :], sc[:, :], P2[:, :, :], OR[:, :], S)
                    dve.sem_inc(s_oh, 1)
                    dve.wait_ge(s_c, 1)
                    W2 = 2 * TILES
                    PT = psT[:, 0:W2 * E].rearrange("p (t e) -> p t e", e=E)
                    link(nc.vector.tensor_copy(TOT[:, :, :], PT))
                    src, k, step = TOT, 0, 1
                    while step < W2:
                        dst = R[k % 2]
                        nc.vector.tensor_copy(dst[:, 0:step, :], src[:, 0:step, :])
                        link(nc.vector.tensor_tensor(dst[:, step:W2, :], src[:, step:W2, :], src[:, 0:W2 - step, :], ALU.add))
                        src, k, step = dst, k + 1, step * 2
                    dst = R[k % 2]
                    link(nc.vector.tensor_tensor(dst[:, :, :], src[:, :, :], TOT[:, :, :], ALU.subtract))
                    PR_ = psR[:, 0:W2 * E].rearrange("p (t e) -> p t e", e=E)
                    KF = KM[:, :, :, :].rearrange("p k t e -> p (k t) e")
                    link(nc.vector.tensor_tensor(KF, PR_, dst[:, :, :], ALU.add))
                    link(nc.vector.tensor_scalar(KF, KF, float(CAP), None, ALU.is_lt))
                    link(nc.vector.tensor_tensor(KF, KF, OH[:, :, :, :].rearrange("p k t e -> p (k t) e"), ALU.mult))
                    for n, v in enumerate((v1, v2)):
                        link(nc.vector.tensor_tensor(KM[:, n, :, :], KM[:, n, :, :], v[:, :].unsqueeze(2).broadcast_to(S), ALU.mult))
                    link(nc.vector.tensor_tensor(G[:, :, :], KM[:, 0, :, :], KM[:, 1, :, :], ALU.add))
                    link(nc.vector.tensor_reduce(sm[:, :], G[:, :, :], AX_X, ALU.add))
                    link(nc.vector.tensor_scalar(sm[:, :], sm[:, :], 1e-9, None, ALU.max))
                    link(nc.vector.reciprocal(sm[:, :], sm[:, :]))
                    link(nc.vector.tensor_tensor(G[:, :, :], G[:, :, :], sm[:, :].unsqueeze(2).broadcast_to(S), ALU.mult))

        with stage(nc) as (sb, ps, sem):
            WI = [sb("re_win", [P, KC, 2 * F]) for _ in range(2)]
            WO = [sb("re_wout", [P, NF, DIM]) for _ in range(2)]
            GE = [sb("re_gelu", [P, TC]) for _ in range(2)]
            HT = [sb("re_hidden", [P, NF, TC]) for _ in range(2)]
            psA = [ps("re_psa", [P, 512]) for _ in range(2)]
            psG = [ps("re_psg", [P, 512]) for _ in range(2)]
            psD = [ps("re_psd", [P, 512]) for _ in range(2)]
            s_w = [sem(f"expert{u}_loaded") for u in range(2)]
            s_up, s_ge, s_h, s_dn, s_x = sem("up_projected"), sem("gelu_ready"), sem("hidden_ready"), sem("down_projected"), sem("x_updated")
            NS = 2 * NT
            TPC = TC // P
            with nc.Block() as block:
                @block.sync
                def _(sp):
                    sp.sem_inc(s_dn, NS * TPC)
                    with sp.Fori(0, E // 2) as i:
                        for u in range(2):
                            sp.wait_ge(s_dn, i * NS * TPC + (u + 1) * NT * TPC)
                            sp.dma_start(WI[u][:, :, :], rows_to_sbuf(d["L1_ffn_W_in"].rearrange("(i u) k n -> i u k n", u=2)[i, u])).then_inc(s_w[u], 16)
                            sp.dma_start(WO[u][:, :, :], rows_to_sbuf(d["L1_ffn_W_out"].rearrange("(i u) k n -> i u k n", u=2)[i, u])).then_inc(s_w[u], 16)

                @block.tensor
                def _(pe):
                    pe.sem_inc(s_h, 2)
                    pe.sem_inc(s_x, 2)
                    with pe.Fori(0, E // 2) as i:
                        def up(n):
                            u, t = n // NT, n % NT
                            if t == 0:
                                pe.wait_ge(s_w[u], i * 32 + 32)
                            for f in range(NF):
                                k = n * NF + f
                                pe.wait_ge(s_h, i * NS * NF + (k + 1))
                                for dst, off in ((psA, 0), (psG, F)):
                                    for c in range(KC):
                                        last = nc.tensor.matmul(dst[k % 2][:, :], WI[u][:, c, off + f * P:off + (f + 1) * P],
                                                                XNT[:, c, t * TC:(t + 1) * TC], start=(c == 0), stop=(c == KC - 1))
                                last.then_inc(s_up, 1)

                        def down(n):
                            u, t = n // NT, n % NT
                            pe.wait_ge(s_h, i * NS * NF + ((n + 1) * NF + 2))
                            for j in range(TPC):
                                k = n * TPC + j
                                pe.wait_ge(s_x, i * NS * TPC + (k + 1))
                                for f in range(NF):
                                    last = nc.tensor.matmul(psD[k % 2][:, 0:DIM], HT[n % 2][:, f, j * P:(j + 1) * P], WO[u][:, f, :],
                                                            start=(f == 0), stop=(f == NF - 1))
                                last.then_inc(s_dn, 1)

                        up(0)
                        for n in range(NS):
                            if n + 1 < NS:
                                up(n + 1)
                            down(n)

                @block.scalar
                def _(act):
                    with act.Fori(0, E // 2) as i:
                        for k in range(NS * NF):
                            act.wait_ge(s_up, i * NS * NF + (k + 1))
                            act.wait_ge(s_h, i * NS * NF + (k + 1))
                            nc.scalar.activation(GE[k % 2][:, :], psA[k % 2][:, :], ACT.Gelu).then_inc(s_ge, 1)

                @block.vector
                def _(dve):
                    with dve.Fori(0, E // 2) as i:
                        def hidden(n):
                            for f in range(NF):
                                k = n * NF + f
                                dve.wait_ge(s_ge, i * NS * NF + (k + 1))
                                if f == 0:
                                    dve.wait_ge(s_dn, i * NS * TPC + (NS + n - 1) * TPC)
                                nc.vector.tensor_tensor(HT[n % 2][:, f, :], psG[k % 2][:, :], GE[k % 2][:, :], ALU.mult).then_inc(s_h, 1)

                        def add(n):
                            u, t = n // NT, n % NT
                            for j in range(TPC):
                                k = n * TPC + j
                                dve.wait_ge(s_dn, i * NS * TPC + (NS * TPC + k + 1))
                                tile = t * TPC + j
                                nc.vector.scalar_tensor_tensor(X[:, tile, :], psD[k % 2][:, 0:DIM], G[:, tile, bass.ds(i * 2 + u, 1)],
                                                               X[:, tile, :], ALU.mult, ALU.add).then_inc(s_x, 1)

                        hidden(0)
                        for n in range(NS):
                            if n + 1 < NS:
                                hidden(n + 1)
                            add(n)


def values_by_token(nc, XNT, VA, w, width):
    with stage(nc) as (sb, ps, sem):
        W = sb("vt_w", [P, KC, DIM])
        out = [ps("vt_ps", [P, 512]) for _ in range(4)]
        s_w, s_mm, s_st = sem("weights_loaded"), sem("multiplied"), sem("stored")
        with nc.Block() as block:
            @block.sync
            def _(sp):
                sp.dma_start(W[:, :, :], rows_to_sbuf(w)).then_inc(s_w, 16)

            @block.tensor
            def _(pe):
                pe.wait_ge(s_w, 16)
                for t in range(TILES):
                    if t >= 4:
                        pe.wait_ge(s_st, t - 3)
                    for c in range(KC):
                        last = nc.tensor.matmul(out[t % 4][:, 0:DIM], XNT[:, c, t * P:(t + 1) * P], W[:, c, :],
                                                start=(c == 0), stop=(c == KC - 1))
                    last.then_inc(s_mm, 1)

            @block.vector
            def _(dve):
                with dve.Fori(0, TILES // 4) as i:
                    for u in range(4):
                        dve.wait_ge(s_mm, i * 4 + (u + 1))
                        nc.vector.tensor_copy(VA[:, i * 4 + u, :, 0:32],
                                              out[u][:, 0:DIM].rearrange("p (a w) -> p a w", a=8)).then_inc(s_st, 1)


def normed_heads(nc, XNT, QKT, VA, ident, d):
    with stage(nc) as (sb, ps, sem):
        W = sb("nh_w", [P, KC, 3 * DIM])
        B = sb("nh_bias_rows", [P, 3 * DIM])
        WQK = sb("nh_rms_weights", [P, 2])
        RAW = sb("nh_qk", [P, TILES, 2 * DIM])
        sq = [sb("nh_squares", [P, 2 * DIM]) for _ in range(2)]
        R = sb("nh_rms", [P, TILES, 32])
        psQ = [ps("nh_psq", [P, 512]) for _ in range(2)]
        psV = [ps("nh_psv", [P, 512]) for _ in range(2)]
        psF = [ps("nh_psf", [P, 4, P]) for _ in range(2)]
        s_w, s_one, s_p, s_b, s_v, s_sq, s_r = (sem("weights_loaded"), sem("ones_set"), sem("projected"), sem("qk_ready"),
                                                sem("values_ready"), sem("squares_ready"), sem("squares_summed"))
        s_d, s_rt, s_rt2, s_n, s_f, s_out = (sem("dve_step"), sem("mean_squares_ready"), sem("roots_ready"), sem("normed"),
                                             sem("flipped"), sem("stored"))
        with nc.Block() as block:
            @block.sync
            def _(sp):
                sp.dma_start(W[:, :, :], rows_to_sbuf(d["L2_attn_WqkvT"])).then_inc(s_w, 16)
                sp.dma_start(B[:, :], d["L2_attn_bqkv"].partition_broadcast(P)).then_inc(s_w, 16)
                sp.dma_start(WQK[:, :], d["L2_attn_wqk_col"]).then_inc(s_w, 16)

            @block.gpsimd
            def _(pool):
                nc.gpsimd.memset(VA[:, :, :, 32:33], 1.0).then_inc(s_one, 1)
                pool.wait_ge(s_one, 1)

            @block.tensor
            def _(pe):
                pe.wait_ge(s_w, 48)
                for t in range(TILES):
                    if t >= 2:
                        pe.wait_ge(s_v, t - 1)
                    for dst, lo, hi in ((psQ[t % 2][:, :], 0, 2 * DIM), (psV[t % 2][:, 0:DIM], 2 * DIM, 3 * DIM)):
                        for c in range(KC):
                            last = nc.tensor.matmul(dst, XNT[:, c, t * P:(t + 1) * P], W[:, c, lo:hi], start=(c == 0),
                                                    stop=(c == KC - 1))
                    last.then_inc(s_p, 1)
                for t in range(TILES):
                    pe.wait_ge(s_n, t + 1)
                    if t >= 2:
                        pe.wait_ge(s_out, t - 1)
                    for m in range(4):
                        last = nc.tensor.transpose(psF[t % 2][:, m, :], RAW[:, t, m * P:(m + 1) * P], ident[:, :])
                    last.then_inc(s_f, 1)

            @block.scalar
            def _(act):
                act.wait_ge(s_w, 48)
                act.sem_inc(s_r, 2)
                with act.Fori(0, TILES // 2) as i:
                    for u in range(2):
                        act.wait_ge(s_b, i * 2 + (u + 1))
                        act.wait_ge(s_r, i * 2 + (u + 1))
                        nc.scalar.activation(sq[u][:, :], RAW[:, i * 2 + u, :], ACT.Square).then_inc(s_sq, 1)
                act.wait_ge(s_rt, 1)
                nc.scalar.activation(R[:, :, :], R[:, :, :], ACT.Sqrt).then_inc(s_rt2, 1)
                with act.Fori(0, TILES // 2) as i:
                    for u in range(2):
                        act.wait_ge(s_f, i * 2 + (u + 1))
                        for m in range(2):
                            last = nc.scalar.activation(QKT[:, 2 * m:2 * m + 2, bass.ds(i * 2 * P + u * P, P)],
                                                        psF[u][:, 2 * m:2 * m + 2, :], ACT.Copy, scale=WQK[:, m:m + 1])
                        last.then_inc(s_out, 1)

            @block.vector
            def _(dve):
                link = Chain(dve, s_d)
                dve.wait_ge(s_w, 48)

                def sum_squares(i, u):
                    dve.wait_ge(s_sq, i * 2 + (u + 1))
                    nc.vector.tensor_reduce(R[:, i * 2 + u, :], sq[u][:, :].rearrange("p (h d) -> p h d", d=16), AX_X,
                                            ALU.add).then_inc(s_r, 1)

                with dve.Fori(0, TILES // 2) as i:
                    for u in range(2):
                        dve.wait_ge(s_p, i * 2 + (u + 1))
                        nc.vector.tensor_tensor(RAW[:, i * 2 + u, :], psQ[u][:, :], B[:, 0:2 * DIM], ALU.add).then_inc(s_b, 1)
                        nc.vector.tensor_tensor(VA[:, i * 2 + u, :, 0:32], psV[u][:, 0:DIM].rearrange("p (a w) -> p a w", a=8),
                                                B[:, 2 * DIM:3 * DIM].rearrange("p (a w) -> p a w", a=8), ALU.add).then_inc(s_v, 1)
                        if u:
                            sum_squares(i, 0)
                    sum_squares(i, 1)
                dve.wait_ge(s_r, TILES + 2)
                link(nc.vector.tensor_scalar(R[:, :, :], R[:, :, :], 1.0 / 16, 1e-6, ALU.mult, ALU.add))
                dve.sem_inc(s_rt, 1)
                dve.wait_ge(s_rt2, 1)
                link(nc.vector.reciprocal(R[:, :, :], R[:, :, :]))
                with dve.Fori(0, TILES // 4) as i:
                    for u in range(4):
                        x = RAW[:, i * 4 + u, :].rearrange("p (h d) -> p h d", d=16)
                        nc.vector.tensor_tensor(x, x, R[:, i * 4 + u, :].unsqueeze(2).broadcast_to([P, 32, 16]),
                                                ALU.mult).then_inc(s_n, 1)


def self_attention(nc, X, QKT, VA, ident, ones, d, retention):
    NAME = "L1_attn" if retention else "L2_attn"
    VW = 32 if retention else 33
    with stage(nc) as (sb, ps, sem):
        WO = sb("sa_wo", [P, KC, DIM])
        H8 = sb("sa_heads", [P, 8])
        if retention:
            DEC = sb("sa_decay", [P, 8, SEQ])
            BM = sb("sa_batch_mean", [P, P])
            GN = sb("sa_group_affine", [P, 2, KC])
            st = sb("sa_row_sums", [P, HEADS])
            mu = sb("sa_head_mean", [P, HEADS])
            s2 = sb("sa_square_sums", [P, HEADS])
            A2 = sb("sa_centered", [P, DIM])
            sq = sb("sa_squares", [P, DIM])
            std = sb("sa_head_std", [P, HEADS])
            rs16 = sb("sa_head_rstd", [P, HEADS])
        else:
            BO = sb("sa_bo", [1, DIM])
            nmax = sb("sa_max", [P, 16])
            SC = sb("sa_scores", [P, 8, 2, SEQ])
            rsum = sb("sa_inv_sum", [P, 2, 8])
        VS = sb("sa_v", [P, 8, VW])
        QB = sb("sa_q_spread", [P, 4, 8, SEQ])
        PR = sb("sa_probs", [P, 8, 2, SEQ])
        PT = sb("sa_probsT", [P, 8, P])
        A = sb("sa_attended", [P, DIM])
        AT = sb("sa_attendedT", [P, KC, P])
        psS = ps("sa_pss", [P, 2, 8, SEQ])
        psT = ps("sa_pst", [P, 8, P])
        psO = [ps("sa_pso", [P, 512]) for _ in range(2)]
        psX, psY = ps("sa_psx", [P, 512]), ps("sa_psy", [P, 512])
        s_w, s_q, s_s = sem("weights_loaded"), sem("queries_spread"), sem("scores_ready")
        s_mx, s_mv, s_e, s_t, s_tc, s_pv = (sem("max_ready"), sem("scores_moved"), sem("probs_ready"), sem("probs_flipped"),
                                            sem("probsT_ready"), sem("attended"))
        s_d, s_o, s_a = sem("dve_step"), sem("attended_stored"), sem("attended_final")
        s_gm, s_c2, s_gv, s_gs, s_rt = (sem("head_means_ready"), sem("square_sums_ready"), sem("head_vars_ready"),
                                        sem("variances_ready"), sem("roots_ready"))
        s_at, s_atc, s_y, s_x = sem("attended_flipped"), sem("attendedT_ready"), sem("out_projected"), sem("x_updated")
        NW = 16 * (6 if retention else 3)

        def steps(eng, body):
            body(0)
            with eng.Fori(1, TILES - 1) as i:
                body(i)
            body(TILES - 1)

        def is_first(i):
            return isinstance(i, int) and i == 0

        def is_last(i):
            return isinstance(i, int) and i == TILES - 1

        with nc.Block() as block:
            @block.sync
            def _(sp):
                sp.dma_start(WO[:, :, :], rows_to_sbuf(d[NAME + "_WoT"])).then_inc(s_w, 16)
                sp.dma_start(H8[:, :], d["heads8"]).then_inc(s_w, 16)
                if retention:
                    sp.dma_start(DEC[:, :, :], d["decay"]).then_inc(s_w, 16)
                    sp.dma_start(BM[:, :], d["batch_mean"]).then_inc(s_w, 16)
                    sp.dma_start(GN[:, 0, :], d["L1_attn_gn_w_col"]).then_inc(s_w, 16)
                    sp.dma_start(GN[:, 1, :], d["L1_attn_gn_b_col"]).then_inc(s_w, 16)
                else:
                    sp.dma_start(BO[:, :], row(d["L2_attn_bo"])).then_inc(s_w, 16)

            @block.gpsimd
            def _(pool):
                pool.wait_ge(s_w, NW)
                pool.sem_inc(s_s, 2)
                with pool.Fori(0, TILES) as i:
                    for b in range(2):
                        pool.wait_ge(s_s, i * 2 + (b + 1))
                        for g in range(2):
                            q = QKT[:, g, bass.ds(i * P + b * SEQ, SEQ)].unsqueeze(1).broadcast_to([P, 8, SEQ])
                            m = H8[:, :].unsqueeze(2).broadcast_to([P, 8, SEQ])
                            nc.gpsimd.tensor_tensor(QB[:, 2 * b + g, :, :], q, m, ALU.mult).then_inc(s_q, 1)

            @block.tensor
            def _(pe):
                def scores(i):
                    for b in range(2):
                        for g in range(2):
                            pe.wait_ge(s_q, i * 4 + (2 * b + g + 1))
                            for a in range(4):
                                last = nc.tensor.matmul(psS[:, b, 4 * g + a, :],
                                                        QB[:, 2 * b + g, 2 * a:2 * a + 2, :].rearrange("p b q -> p (b q)"),
                                                        QKT[:, 2 + g, bass.ds(i * P + b * SEQ, SEQ)], start=True, stop=True)
                        last.then_inc(s_s, 1)

                def means(i):
                    pe.wait_ge(s_o, i + 1)
                    nc.tensor.matmul(psX[:, 0:HEADS], BM[:, :], st[:, :], start=True, stop=True).then_inc(s_gm, 1)

                def variances(i):
                    pe.wait_ge(s_c2, i + 1)
                    nc.tensor.matmul(psX[:, 0:HEADS], BM[:, :], s2[:, :], start=True, stop=True).then_inc(s_gv, 1)

                def flip_result(i):
                    pe.wait_ge(s_a if retention else s_o, i + 1)
                    for c in range(KC):
                        last = nc.tensor.transpose(psX[:, c * P:(c + 1) * P], A[:, c * P:(c + 1) * P], ident[:, :])
                    last.then_inc(s_at, 1)

                def output(i):
                    pe.wait_ge(s_atc, i + 1)
                    if not is_first(i):
                        pe.wait_ge(s_x, i)
                    for c in range(KC):
                        last = nc.tensor.matmul(psY[:, 0:DIM], AT[:, c, :], WO[:, c, :], start=(c == 0),
                                                stop=(c == KC - 1 and retention))
                    if not retention:
                        last = nc.tensor.matmul(psY[:, 0:DIM], ones[0:1, :], BO[:, :], start=False, stop=True)
                    last.then_inc(s_y, 1)

                def body(i):
                    before = 0 if isinstance(i, int) and i == 1 else i - 1
                    pe.wait_ge(s_e, (i + 1) * 2 if retention else i + 1)
                    for a in range(8):
                        last = nc.tensor.transpose(psT[:, a, :], PR[:, a, :, :].rearrange("p b j -> p (b j)"), ident[:, :])
                    last.then_inc(s_t, 1)
                    if retention and not is_first(i):
                        means(before)
                    if not is_last(i):
                        scores(i + 1)
                    if not is_first(i):
                        if retention:
                            variances(before)
                        else:
                            flip_result(before)
                    pe.wait_ge(s_tc, i + 1)
                    if not is_first(i) and not retention:
                        pe.wait_ge(s_o, i)
                    for b in range(2):
                        r = slice(b * SEQ, (b + 1) * SEQ)
                        for a in range(8):
                            last = nc.tensor.matmul(psO[b][:, a * VW:(a + 1) * VW], PT[r, a, :], VS[r, a, :], start=True, stop=True)
                    last.then_inc(s_pv, 1)
                    if not is_first(i):
                        if retention:
                            flip_result(before)
                        output(before)

                pe.wait_ge(s_w, NW)
                scores(0)
                steps(pe, body)
                if retention:
                    means(TILES - 1)
                    variances(TILES - 1)
                flip_result(TILES - 1)
                output(TILES - 1)

            @block.scalar
            def _(act):
                def exponentiate(i):
                    act.wait_ge(s_mv, i + 1)
                    nc.scalar.activation(PR[:, :, :, :].rearrange("p a b j -> p (a b j)"),
                                         SC[:, :, :, :].rearrange("p a b j -> p (a b j)"), ACT.Exp).then_inc(s_e, 1)

                def result(i):
                    if retention:
                        act.wait_ge(s_gs, i + 1)
                        nc.scalar.activation(std[:, :], std[:, :], ACT.Sqrt).then_inc(s_rt, 1)
                    act.wait_ge(s_at, i + 1)
                    if retention:
                        for c in range(KC):
                            last = nc.scalar.activation(AT[:, c, :], psX[:, c * P:(c + 1) * P], ACT.Identity,
                                                        bias=GN[:, 1, c:c + 1], scale=GN[:, 0, c:c + 1])
                        last.then_inc(s_atc, 1)
                    else:
                        nc.scalar.copy(AT[:, :, :].rearrange("p a b -> p (a b)"), psX[:, 0:DIM]).then_inc(s_atc, 1)

                def body(i):
                    act.wait_ge(s_t, i + 1)
                    nc.scalar.copy(PT[:, :, :], psT[:, :, :])
                    nc.scalar.copy(VS[:, :, :], VA[:, i, :, :]).then_inc(s_tc, 1)
                    if not is_first(i):
                        result(i - 1)
                    if not retention and not is_last(i):
                        exponentiate(i + 1)

                act.wait_ge(s_w, NW)
                if not retention:
                    exponentiate(0)
                steps(act, body)
                result(TILES - 1)

            @block.vector
            def _(dve):
                NL = 3 if retention else 1
                A3 = A[:, :].rearrange("p (h d) -> p h d", d=16)
                if retention:
                    C3 = A2[:, :].rearrange("p (h d) -> p h d", d=16)

                def take(i):
                    if retention:
                        for b in range(2):
                            dve.wait_ge(s_s, i * 2 + (b + 3))
                            nc.vector.tensor_tensor(PR[:, :, b, :], psS[:, b, :, :], DEC[:, :, :], ALU.mult).then_inc(s_e, 1)
                        return
                    dve.wait_ge(s_s, i * 2 + 4)
                    nc.vector.tensor_reduce(nmax[:, :], psS[:, :, :, :].rearrange("p b a j -> p (b a) j"), AX_X,
                                            ALU.max).then_inc(s_mx, 1)
                    dve.wait_ge(s_mx, i + 1)
                    for b in range(2):
                        last = nc.vector.tensor_tensor(SC[:, :, b, :], psS[:, b, :, :],
                                                       nmax[:, 8 * b:8 * b + 8].unsqueeze(2).broadcast_to([P, 8, SEQ]),
                                                       ALU.subtract)
                    last.then_inc(s_mv, 1)

                def center(i):
                    link = Chain(dve, s_d, i * 5 + 1)
                    dve.wait_ge(s_gm, i + 1)
                    link(nc.vector.tensor_copy(mu[:, :], psX[:, 0:HEADS]))
                    link(nc.vector.tensor_tensor(C3, A3, mu[:, :].unsqueeze(2).broadcast_to([P, HEADS, 16]), ALU.subtract))
                    link(nc.vector.tensor_tensor(sq[:, :], A2[:, :], A2[:, :], ALU.mult))
                    nc.vector.tensor_reduce(s2[:, :], sq[:, :].rearrange("p (h d) -> p h d", d=16), AX_X, ALU.add).then_inc(s_c2, 1)

                def normalise(i):
                    link = Chain(dve, s_d, i * 5 + 4)
                    dve.wait_ge(s_gv, i + 1)
                    nc.vector.tensor_scalar(std[:, :], psX[:, 0:HEADS], 1e-5, None, ALU.add).then_inc(s_gs, 1)
                    dve.wait_ge(s_rt, i + 1)
                    link(nc.vector.reciprocal(rs16[:, :], std[:, :]))
                    nc.vector.tensor_tensor(A3, C3, rs16[:, :].unsqueeze(2).broadcast_to([P, HEADS, 16]), ALU.mult).then_inc(s_a, 1)

                def store(i):
                    dve.wait_ge(s_pv, i + 1)
                    if retention and not is_first(i):
                        dve.wait_ge(s_at, i)
                    if not retention:
                        link = Chain(dve, s_d, i)
                        for b in range(2):
                            O = psO[b][:, 0:8 * VW].rearrange("p (a w) -> p a w", a=8)
                            last = nc.vector.reciprocal(rsum[:, b, :], O[:, :, 32])
                        link(last)
                    for b in range(2):
                        O = psO[b][:, 0:8 * VW].rearrange("p (a w) -> p a w", a=8)
                        for h in range(2):
                            dst = A[b * SEQ:(b + 1) * SEQ, :].rearrange("p (a b d) -> p a b d", a=8, b=2)[:, :, h, :]
                            src = O[h * SEQ:(h + 1) * SEQ, :, 16 * h:16 * h + 16]
                            if retention:
                                last = nc.vector.tensor_copy(dst, src)
                            else:
                                last = nc.vector.tensor_tensor(
                                    dst, src, rsum[h * SEQ:(h + 1) * SEQ, b, :].unsqueeze(2).broadcast_to([SEQ, 8, 16]), ALU.mult)
                    if not retention:
                        last.then_inc(s_o, 1)
                        return
                    Chain(dve, s_d, i * 5)(last)
                    nc.vector.tensor_reduce(st[:, :], A3, AX_X, ALU.add).then_inc(s_o, 1)

                def update(i):
                    dve.wait_ge(s_y, i + 1)
                    x = X[:, bass.ds(i, 1), :]
                    nc.vector.tensor_tensor(x, psY[:, 0:DIM].unsqueeze(1), x, ALU.add).then_inc(s_x, 1)

                def body(i):
                    if retention and not is_first(i):
                        center(i - 1)
                    if not is_last(i):
                        take(i + 1)
                    if retention and not is_first(i):
                        normalise(i - 1)
                    store(i)
                    if not is_first(i):
                        update(i - 1)

                dve.wait_ge(s_w, NW)
                take(0)
                steps(dve, body)
                if retention:
                    center(TILES - 1)
                    normalise(TILES - 1)
                update(TILES - 1)


def tiled_experts(nc, X, XNT, ident, ones, d):
    E = 8
    with stage(nc) as (sb, ps, sem):
        W = sb("te_w", [P, E, KC, DIM])
        B = sb("te_b", [E, DIM])
        PE_ = sb("te_position", [32, P])
        SG = sb("te_signatures", [32, E])
        lt = sb("te_negative", [32, E])
        SN = sb("te_signs", [32, E])
        OR = sb("te_order", [P, E])
        SCR = sb("te_scores", [P, 1, E])
        OH = sb("te_onehot", [P, 1, E])
        top, scr = sb("te_top", [P, 1]), sb("te_scratch", [P, 1])
        OHT = sb("te_onehotT", [E, P])
        DG = sb("te_diagonals", [SEQ, E, SEQ])
        OB = sb("te_onehot_rows", [P, E, SEQ])
        XG = [sb("te_x_picked", [P, KC, E, P]) for _ in range(2)]
        psS, psB, psT = ps("te_pss", [P, 512]), ps("te_psb", [P, 512]), ps("te_pst", [P, 512])
        out = [ps("te_psy", [P, 512]) for _ in range(2)]
        s_w, s_wb, s_sn, s_sc, s_d = sem("small_loaded"), sem("weights_loaded"), sem("signs_ready"), sem("scores_ready"), sem("dve_step")
        s_oh, s_tb, s_ob, s_xg, s_y, s_x = (sem("onehot_ready"), sem("onehot_spread"), sem("onehot_rows_ready"), sem("x_picked"),
                                            sem("multiplied"), sem("x_updated"))
        with nc.Block() as block:
            @block.sync
            def _(sp):
                sp.dma_start(PE_[:, :], d["positionT"]).then_inc(s_w, 16)
                sp.dma_start(SG[:, :], d["L2_ffn_tile_sigsT"]).then_inc(s_w, 16)
                sp.dma_start(OR[:, :], d["expert_order"]).then_inc(s_w, 16)
                sp.dma_start(B[:, :], d["L2_ffn_b"]).then_inc(s_wb, 16)
                for e in range(E):
                    sp.dma_start(W[:, e, :, :], rows_to_sbuf(d["L2_ffn_WT"][e])).then_inc(s_wb, 16)

            @block.tensor
            def _(pe):
                pe.wait_ge(s_sn, 1)
                nc.tensor.matmul(psS[:, 0:E], PE_[:, :], SN[:, :], start=True, stop=True).then_inc(s_sc, 1)
                pe.wait_ge(s_oh, 1)
                nc.tensor.transpose(psT[0:E, 0:P], OH[:, 0, :], ident[:, :])
                nc.tensor.matmul(psB[:, :], ones[0:SEQ, :], DG[:, :, :].rearrange("p e s -> p (e s)"), start=True,
                                 stop=True).then_inc(s_tb, 1)
                pe.wait_ge(s_wb, 16 * (1 + E))
                pe.sem_inc(s_x, 2)
                with pe.Fori(0, TILES // 2) as i:
                    for u in range(2):
                        pe.wait_ge(s_xg, i * 2 + (u + 1))
                        pe.wait_ge(s_x, i * 2 + (u + 1))
                        nc.tensor.matmul(out[u][:, 0:DIM], OHT[:, :], B[:, :], start=True, stop=False)
                        for e in range(E):
                            for c in range(KC):
                                last = nc.tensor.matmul(out[u][:, 0:DIM], XG[u][:, c, e, :], W[:, e, c, :], start=False,
                                                        stop=(e == E - 1 and c == KC - 1))
                        last.then_inc(s_y, 1)

            @block.vector
            def _(dve):
                link = Chain(dve, s_d)
                dve.wait_ge(s_w, 48)
                link(nc.vector.tensor_scalar(lt[:, :], SG[:, :], 0.0, None, ALU.is_lt))
                link(nc.vector.tensor_scalar(SN[:, :], SG[:, :], 0.0, None, ALU.is_gt))
                nc.vector.tensor_tensor(SN[:, :], SN[:, :], lt[:, :], ALU.subtract).then_inc(s_sn, 1)
                dve.wait_ge(s_sc, 1)
                link(nc.vector.tensor_copy(SCR[:, 0, :], psS[:, 0:E]))
                first_maximum(nc, link, OH[:, :, :], top[:, :], scr[:, :], SCR[:, :, :], OR[:, :], [P, 1, E])
                for e in range(E):
                    last = nc.vector.tensor_scalar(DG[:, e, :], ident[0:SEQ, 0:SEQ], OH[0:SEQ, 0, e:e + 1], None, ALU.mult)
                last.then_inc(s_oh, 1)
                dve.wait_ge(s_tb, 1)
                nc.vector.tensor_copy(OHT[:, :], psT[0:E, 0:P])
                nc.vector.tensor_copy(OB[:, :, :].rearrange("p e s -> p (e s)"), psB[:, :]).then_inc(s_ob, 1)
                dve.wait_ge(s_ob, 1)
                dve.sem_inc(s_y, 2)

                with dve.Fori(0, TILES // 2) as i:
                    for u in range(2):
                        dve.wait_ge(s_y, i * 2 + (u + 1))
                        for c in range(KC):
                            for b in range(2):
                                x = XNT[:, c, bass.ds(i * 2 * P + (u * P + b * SEQ), SEQ)].unsqueeze(1).broadcast_to([P, E, SEQ])
                                last = nc.vector.tensor_tensor(XG[u][:, c, :, b * SEQ:(b + 1) * SEQ], x, OB[:, :, :], ALU.mult)
                        last.then_inc(s_xg, 1)
                    for u in range(2):
                        dve.wait_ge(s_y, i * 2 + (u + 3))
                        x = X[:, bass.ds(i * 2 + u, 1), :]
                        nc.vector.tensor_tensor(x, out[u][:, 0:DIM].unsqueeze(1), x, ALU.add).then_inc(s_x, 1)


def gated_recurrence(nc, X, XNT, ident, d):
    TC = 512
    NT = TOKENS // TC
    with stage(nc) as (sb, ps, sem):
        W = sb("gr_w", [P, KC, 4 * P])
        WG = sb("gr_wg", [P, KC, DIM])
        B = sb("gr_b", [P, 4])
        BG = sb("gr_bg", [P, 2])
        Z, K, V = (sb("gr_z", [P, 2, TC]), sb("gr_keep", [P, 2, TC]), sb("gr_input", [P, 2, TC]))
        H = sb("gr_h", [P, 2, TC])
        GA = sb("gr_gate", [P, 2, TC])
        O = sb("gr_out", [P, 2, TC])
        psZ = [ps("gr_psz", [P, 512]) for _ in range(2)]
        psH = [ps("gr_psh", [P, 512]) for _ in range(2)]
        psG = [ps("gr_psg", [P, 512]) for _ in range(2)]
        psT = [ps("gr_pst", [P, 2, DIM]) for _ in range(2)]
        s_w, s_p, s_z, s_k, s_zero = sem("weights_loaded"), sem("projected"), sem("z_ready"), sem("keep_ready"), sem("batch_starts_cleared")
        s_h, s_g, s_ga, s_o, s_t, s_x = (sem("h_ready"), sem("gate_projected"), sem("gate_ready"), sem("out_ready"),
                                         sem("out_flipped"), sem("x_updated"))
        with nc.Block() as block:
            @block.sync
            def _(sp):
                sp.dma_start(W[:, :, :], rows_to_sbuf(d["L3_attn_W"])).then_inc(s_w, 16)
                sp.dma_start(WG[:, :, :], rows_to_sbuf(d["L3_attn_W_g"])).then_inc(s_w, 16)
                sp.dma_start(B[:, :], d["L3_attn_b_col"]).then_inc(s_w, 16)
                sp.dma_start(BG[:, :], d["L3_attn_b_g_col"]).then_inc(s_w, 16)

            @block.tensor
            def _(pe):
                pe.wait_ge(s_w, 64)
                pe.sem_inc(s_h, 2)
                pe.sem_inc(s_x, 2)
                with pe.Fori(0, NT) as t:
                    pe.wait_ge(s_h, t * 2 + 2)
                    for n, dst in enumerate(psZ + psH):
                        for c in range(KC):
                            last = nc.tensor.matmul(dst[:, :], W[:, c, n * P:(n + 1) * P], XNT[:, c, bass.ds(t * TC, TC)],
                                                    start=(c == 0), stop=(c == KC - 1))
                    last.then_inc(s_p, 1)
                    pe.wait_ge(s_h, t * 2 + 4)
                    for m in range(2):
                        for c in range(KC):
                            last = nc.tensor.matmul(psG[m][:, :], WG[:, c, m * P:(m + 1) * P], H[:, c, :], start=(c == 0),
                                                    stop=(c == KC - 1))
                    last.then_inc(s_g, 1)
                    pe.wait_ge(s_o, t * 2 + 2)
                    pe.wait_ge(s_x, t * 2 + 2)
                    for j in range(TC // P):
                        for c in range(KC):
                            last = nc.tensor.transpose(psT[j // 2][:, j % 2, c * P:(c + 1) * P], O[:, c, j * P:(j + 1) * P], ident[:, :])
                    last.then_inc(s_t, 1)

            @block.scalar
            def _(act):
                act.wait_ge(s_w, 64)
                with act.Fori(0, NT) as t:
                    act.wait_ge(s_p, t + 1)
                    for m in range(2):
                        nc.scalar.activation(Z[:, m, :], psZ[m][:, :], ACT.Sigmoid, bias=B[:, m:m + 1]).then_inc(s_z, 1)
                    act.wait_ge(s_g, t + 1)
                    for m in range(2):
                        nc.scalar.activation(GA[:, m, :], psG[m][:, :], ACT.Sigmoid, bias=BG[:, m:m + 1]).then_inc(s_ga, 1)

            @block.vector
            def _(dve):
                dve.wait_ge(s_w, 64)
                with dve.Fori(0, NT) as t:
                    for m in range(2):
                        dve.wait_ge(s_z, t * 2 + (m + 1))
                        nc.vector.tensor_scalar(K[:, m, :], Z[:, m, :], -1.0, 1.0, ALU.mult, ALU.add).then_inc(s_k, 1)
                        nc.vector.scalar_tensor_tensor(V[:, m, :], psH[m][:, :], B[:, 2 + m:3 + m], Z[:, m, :], ALU.add,
                                                       ALU.mult).then_inc(s_k, 1)
                        dve.wait_ge(s_k, t * 4 + (2 * m + 2))
                        nc.vector.memset(K[:, m, 0:TC:SEQ], 0.0).then_inc(s_zero, 1)
                        dve.wait_ge(s_zero, t * 2 + (m + 1))
                        nc.vector.tensor_tensor_scan(H[:, m, :], K[:, m, :], V[:, m, :], 0.0, ALU.mult, ALU.add).then_inc(s_h, 1)
                    for m in range(2):
                        dve.wait_ge(s_ga, t * 2 + (m + 1))
                        nc.vector.tensor_tensor(O[:, m, :], GA[:, m, :], H[:, m, :], ALU.mult).then_inc(s_o, 1)
                    dve.wait_ge(s_t, t + 1)
                    for j in range(2):
                        x = X[:, bass.ds(t * 4 + 2 * j, 2), :]
                        nc.vector.tensor_tensor(x, psT[j][:, :, :], x, ALU.add).then_inc(s_x, 1)


def swiglu_quantised(nc, X, XNT, d):
    HID, TC = 768, 512
    NF = HID // P
    NT = TOKENS // TC
    S = 1.0 / 127.0
    TPC = TC // P
    with stage(nc) as (sb, ps, sem):
        WI = [sb("sw_int", [P, KC, HID], I32) for _ in range(2)]
        WDI = sb("sw_down_int", [P, NF, DIM], I32)
        W = [sb("sw_w", [P, KC, HID]) for _ in range(2)]
        WD = sb("sw_down", [P, NF, DIM])
        SI = [sb("sw_silu", [P, TC]) for _ in range(2)]
        HT = [sb("sw_hidden", [P, NF, TC]) for _ in range(2)]
        psG = [ps("sw_psg", [P, 512]) for _ in range(2)]
        psU = [ps("sw_psu", [P, 512]) for _ in range(2)]
        psD = [ps("sw_psd", [P, 512]) for _ in range(2)]
        s_w, s_f = [sem(f"weights{n}_loaded") for n in range(3)], sem("weights_scaled")
        s_up, s_si, s_h, s_dn, s_x = sem("up_projected"), sem("silu_ready"), sem("hidden_ready"), sem("down_projected"), sem("x_updated")
        with nc.Block() as block:
            @block.sync
            def _(sp):
                sp.dma_start(WI[0][:, :, :], rows_to_sbuf(d["L3_ffn_w_gateT"])).then_inc(s_w[0], 16)
                sp.dma_start(WI[1][:, :, :], rows_to_sbuf(d["L3_ffn_w_upT"])).then_inc(s_w[1], 16)
                sp.dma_start(WDI[:, :, :], rows_to_sbuf(d["L3_ffn_w_downT"])).then_inc(s_w[2], 16)

            @block.tensor
            def _(pe):
                pe.wait_ge(s_f, 3)
                pe.sem_inc(s_h, 2)
                pe.sem_inc(s_x, 2)
                with pe.Fori(0, NT // 2) as i:
                    def up(n):
                        for f in range(NF):
                            k = n * NF + f
                            pe.wait_ge(s_h, i * 2 * NF + (k + 1))
                            for w, dst in ((W[0], psG), (W[1], psU)):
                                for c in range(KC):
                                    last = nc.tensor.matmul(dst[k % 2][:, :], w[:, c, f * P:(f + 1) * P],
                                                            XNT[:, c, bass.ds(i * 2 * TC + n * TC, TC)], start=(c == 0), stop=(c == KC - 1))
                            last.then_inc(s_up, 1)

                    def down(n):
                        pe.wait_ge(s_h, i * 2 * NF + ((n + 1) * NF + 2))
                        for j in range(TPC):
                            k = n * TPC + j
                            pe.wait_ge(s_x, i * 2 * TPC + (k + 1))
                            for f in range(NF):
                                last = nc.tensor.matmul(psD[k % 2][:, 0:DIM], HT[n][:, f, j * P:(j + 1) * P], WD[:, f, :],
                                                        start=(f == 0), stop=(f == NF - 1))
                            last.then_inc(s_dn, 1)

                    up(0)
                    up(1)
                    down(0)
                    down(1)

            @block.scalar
            def _(act):
                with act.Fori(0, NT // 2) as i:
                    for k in range(2 * NF):
                        act.wait_ge(s_up, i * 2 * NF + (k + 1))
                        act.wait_ge(s_h, i * 2 * NF + (k + 1))
                        nc.scalar.activation(SI[k % 2][:, :], psG[k % 2][:, :], ACT.Silu).then_inc(s_si, 1)

            @block.vector
            def _(dve):
                for n, (src, dst) in enumerate(((WI[0], W[0]), (WI[1], W[1]), (WDI, WD))):
                    dve.wait_ge(s_w[n], 16)
                    nc.vector.tensor_scalar(dst[:, :, :], src[:, :, :], S, None, ALU.mult).then_inc(s_f, 1)
                dve.sem_inc(s_dn, 2 * TPC)
                with dve.Fori(0, NT // 2) as i:
                    for n in range(2):
                        dve.wait_ge(s_dn, i * 2 * TPC + (n + 1) * TPC)
                        for f in range(NF):
                            k = n * NF + f
                            dve.wait_ge(s_si, i * 2 * NF + (k + 1))
                            nc.vector.tensor_tensor(HT[n][:, f, :], psU[k % 2][:, :], SI[k % 2][:, :], ALU.mult).then_inc(s_h, 1)
                    for k in range(2 * TPC):
                        dve.wait_ge(s_dn, i * 2 * TPC + (2 * TPC + k + 1))
                        x = X[:, bass.ds(i * 2 * TPC + k, 1), :]
                        nc.vector.tensor_tensor(x, psD[k % 2][:, 0:DIM].unsqueeze(1), x, ALU.add).then_inc(s_x, 1)


STAGES = ('L0x', 'L0a', 'L0f', 'L1x', 'L1a', 'L1f', 'L2x', 'L2a', 'L2f', 'L3x', 'L3a', 'L3f')


def perceiver(nc, d, out):
    _stages.clear()
    _names.clear()
    with ExitStack() as ctx:
        X = ctx.enter_context(nc.sbuf_tensor("x_resident", [P, TILES, DIM], F32))
        XNT = ctx.enter_context(nc.sbuf_tensor("x_normed_transposed", [P, KC, TOKENS], F32))
        ident = ctx.enter_context(nc.sbuf_tensor("identity", [P, P], F32))
        ones = ctx.enter_context(nc.sbuf_tensor("ones", [P, P], F32))
        with stage(nc) as (sb, ps, sem):
            s_in, s_one = sem("x_loaded"), sem("ones_set")
            with nc.Block() as block:
                @block.sync
                def _(sp):
                    sp.dma_start(X[:, :, :], d["x"].rearrange("(t b) s d -> (b s) t d", b=2)).then_inc(s_in, 16)
                    sp.dma_start(ident[:, :], d["identity"]).then_inc(s_in, 16)
                    sp.wait_ge(s_in, 32)

                @block.gpsimd
                def _(pool):
                    nc.gpsimd.memset(ones[:, :], 1.0).then_inc(s_one, 1)
                    pool.wait_ge(s_one, 1)

        ctx4 = d["ctxT"].rearrange("(t b) d s -> t b d s", b=2)
        ctxn = d["ctx"].rearrange("(t b) s d -> t b s d", b=2)
        mask4 = d["mask_Bx1x1xS2_fk0"].rearrange("(t b) c e s -> t b (c e s)", b=2)
        if "L0x" in STAGES:
            layernorm_transposed(nc, X, XNT, ident)
            with nc.sbuf_tensor("l0x_qT", [P, KC, TOKENS], F32) as QT:
                project_transposed(nc, XNT, QT, d["L0_xattn_Wq"], d["L0_xattn_bq_col"], KC)
                cross_attention(nc, X, QT, ident, ones, d["spread16"], ctx4, 16, wkv=d["L0_xattn_Wkv"],
                                bk=d["L0_xattn_bk_col"], bv=d["L0_xattn_bv_col"], wo=d["L0_xattn_Wo"], bo=d["L0_xattn_bo"])
        if "L0a" in STAGES:
            layernorm_transposed(nc, X, XNT, ident, passes=2, residual=True,
                                 affine=(d["L0_attn_gamma_col"], d["L0_attn_beta_col"]))
            linear_attention(nc, X, XNT, ident, d)
        if "L0f" in STAGES:
            layernorm_transposed(nc, X, XNT, ident)
            mixed_experts(nc, X, XNT, ident, ones, d)
        if "L1x" in STAGES:
            ctxnT = nc.dram_tensor("ctx_normed_transposed", (BATCH, DIM, NKEY), F32, kind="Internal").ap()
            rows = TILES * P // NKEY
            with nc.sbuf_tensor("context_rows", [P, TILES, DIM], F32) as CX:
                for c in range(BATCH // rows):
                    part = slice(c * rows, (c + 1) * rows)
                    layernorm_transposed(
                        nc, CX, XNT, ident, affine=(d["L1_xattn_ln_c_w_col"], d["L1_xattn_ln_c_b_col"]),
                        load=d["ctx"][part].rearrange("b (t p) d -> p (b t) d", p=P),
                        store=ctxnT[part].rearrange("b (c p) s -> p c b s", p=P))
            layernorm_transposed(nc, X, XNT, ident, passes=2,
                                 affine=(d["L1_xattn_ln_l_w_col"], d["L1_xattn_ln_l_b_col"]))
            with nc.sbuf_tensor("l1x_qT", [P, 8, TOKENS], F32) as QT:
                project_transposed(nc, XNT, QT, d["L1_xattn_Wq"], None, 8)
                cross_attention(nc, X, QT, ident, ones, d["spread64"], ctxnT.rearrange("(t b) d s -> t b d s", b=2), 64,
                                wkv=d["L1_xattn_Wkv"], wo=d["L1_xattn_Wo"], bo=d["L1_xattn_bo"], clip=11.0)
        if "L1a" in STAGES:
            layernorm_transposed(nc, X, XNT, ident)
            with nc.sbuf_tensor("l1a_qkT", [P, 4, TOKENS], F32) as QKT, \
                    nc.sbuf_tensor("l1a_v", [P, TILES, 8, 32], F32) as VA:
                project_transposed(nc, XNT, QKT, d["L1_attn_Wqk"], None, 4)
                values_by_token(nc, XNT, VA, d["L1_attn_Wv"], 32)
                self_attention(nc, X, QKT, VA, ident, ones, d, retention=True)
        if "L1f" in STAGES:
            layernorm_transposed(nc, X, XNT, ident)
            routed_experts(nc, X, XNT, ident, ones, d)
        if "L2x" in STAGES:
            layernorm_transposed(nc, X, XNT, ident)
            cross_attention(nc, X, XNT, ident, ones, d["spread16"], ctx4, 16, ctx=ctxn)
        if "L2a" in STAGES:
            layernorm_transposed(nc, X, XNT, ident)
            with nc.sbuf_tensor("l2a_qkT", [P, 4, TOKENS], F32) as QKT, \
                    nc.sbuf_tensor("l2a_v", [P, TILES, 8, 33], F32) as VA:
                normed_heads(nc, XNT, QKT, VA, ident, d)
                self_attention(nc, X, QKT, VA, ident, ones, d, retention=False)
        if "L2f" in STAGES:
            layernorm_transposed(nc, X, XNT, ident)
            tiled_experts(nc, X, XNT, ident, ones, d)
        if "L3x" in STAGES:
            layernorm_transposed(nc, X, XNT, ident)
            with nc.sbuf_tensor("l3x_qT", [P, KC, TOKENS], F32) as QT:
                project_transposed(nc, XNT, QT, d["L3_xattn_Wq"], d["L3_xattn_bq_col"], KC)
                cross_attention(nc, X, QT, ident, ones, d["spread16"], ctx4, 16, wkv=d["L3_xattn_Wkv"],
                                bk=d["L3_xattn_bk_col"], bv=d["L3_xattn_bv_col"], wo=d["L3_xattn_Wo"], bo=d["L3_xattn_bo"], mask=mask4)
        if "L3a" in STAGES:
            layernorm_transposed(nc, X, XNT, ident)
            gated_recurrence(nc, X, XNT, ident, d)
        if "L3f" in STAGES:
            layernorm_transposed(nc, X, XNT, ident)
            swiglu_quantised(nc, X, XNT, d)
        with stage(nc) as (sb, ps, sem):
            s_out = sem("x_stored")
            with nc.Block() as block:
                @block.sync
                def _(sp):
                    sp.dma_start(out.rearrange("(t b) s d -> (b s) t d", b=2), X[:, :, :]).then_inc(s_out, 16)
                    sp.wait_ge(s_out, 16)


def kernel(**inputs):
    import numpy as np
    import concourse.bacc as _bacc
    from concourse.bass_utils import run_bass_kernel_spmd as _run

    arrays = {k: np.ascontiguousarray(v) for k, v in inputs.items() if k in DIRECT}
    arrays["ctx"] = np.ascontiguousarray(inputs["ctx_1024"])
    arrays["ctxT"] = np.ascontiguousarray(np.asarray(inputs["ctx_1024"]).transpose(0, 2, 1))
    for n in ("L0", "L3"):
        arrays[f"{n}_xattn_Wkv"] = np.concatenate(
            [np.asarray(inputs[f"{n}_xattn_Wk"]), np.asarray(inputs[f"{n}_xattn_Wv"])], axis=1)
    for k in COLUMNS:
        arrays[k + "_col"] = np.ascontiguousarray(np.asarray(inputs[k]).reshape(-1, 128).T)
    arrays["identity"] = np.eye(128, dtype=np.float32)
    head = np.arange(128) // 16
    arrays["spread16"] = np.where(head[:, None] == np.arange(8)[None], 0.25, 0.0).astype(np.float32)
    more_arrays(arrays, inputs)

    nc = _bacc.Bacc("TRN2", target_bir_lowering=False, num_devices=1)
    d = {k: nc.dram_tensor(f"in_{k}", a.shape, mybir.dt.from_np(a.dtype), kind="ExternalInput").ap()
         for k, a in arrays.items()}
    out = nc.dram_tensor("out_x", (BATCH, SEQ, DIM), F32, kind="ExternalOutput").ap()
    perceiver(nc, d, out)
    r = _run(nc, [{f"in_{k}": a for k, a in arrays.items()}], core_ids=[0])
    return r.results[0]["out_x"]


DIRECT = ("x", "mask_Bx1x1xS2_fk0", "L0_xattn_Wq", "L0_xattn_Wo", "L0_xattn_bo", "L3_xattn_Wq", "L3_xattn_Wo",
          "L3_xattn_bo", "L0_attn_Wqkv", "L0_attn_Wout", "L1_xattn_Wq", "L1_xattn_Wkv", "L1_xattn_Wo", "L1_xattn_bo",
          "L2_attn_bo", "L2_attn_bqkv", "L0_ffn_gb2", "L0_ffn_eb1", "L0_ffn_eb2", "L1_ffn_Wg", "L1_ffn_W_in",
          "L1_ffn_W_out", "L2_ffn_b", "L3_attn_W_g")
COLUMNS = ("L0_xattn_bq", "L0_xattn_bk", "L0_xattn_bv", "L3_xattn_bq", "L3_xattn_bk", "L3_xattn_bv",
           "L0_attn_gamma", "L0_attn_beta", "L1_xattn_ln_c_w", "L1_xattn_ln_c_b", "L1_xattn_ln_l_w", "L1_xattn_ln_l_b",
           "L1_attn_gn_w", "L1_attn_gn_b", "L0_ffn_gb1", "L3_attn_b_g")


def more_arrays(arrays, inputs):
    import numpy as np

    f = np.float32
    part = np.arange(128)
    arrays["spread64"] = np.where((part // 64)[:, None] == np.arange(2)[None], 0.125, 0.0).astype(f)
    arrays["same_head"] = ((part // 16)[:, None] == (part // 16)[None]).astype(f)
    arrays["heads8"] = ((part // 16)[:, None] == np.arange(8)[None]).astype(f)
    arrays["batch_mean"] = np.where((part // 64)[:, None] == (part // 64)[None], 1.0 / (64 * 16), 0.0).astype(f)
    lo, hi = float(np.log(1.0 - 0.999)), float(np.log(1.0 - 0.9))
    gam = (f(1.0) - np.exp(np.linspace(lo, hi, 16, dtype=f))).astype(f)
    dist = (np.arange(64)[:, None] - np.arange(64)[None]).astype(f)
    dec = np.where(dist >= 0, gam[:, None, None] ** np.where(dist >= 0, dist, 0).astype(f), 0).astype(f)
    arrays["decay"] = np.ascontiguousarray(dec.reshape(8, 2, 64, 64).transpose(1, 2, 0, 3).reshape(128, 8, 64))
    g = lambda k: np.asarray(inputs[k])
    arrays["L1_attn_Wqk"] = np.concatenate([g("L1_attn_wq").T, g("L1_attn_wk").T], axis=1)
    arrays["L1_attn_Wv"] = np.ascontiguousarray(g("L1_attn_wv").T)
    arrays["L1_attn_WoT"] = np.ascontiguousarray(g("L1_attn_wo").T)
    arrays["L2_attn_WqkvT"] = np.ascontiguousarray(g("L2_attn_Wqkv").T)
    arrays["L2_attn_WoT"] = np.ascontiguousarray(g("L2_attn_Wo").T)
    arrays["L2_attn_wqk_col"] = np.stack([np.tile(g("L2_attn_wq"), 8), np.tile(g("L2_attn_wk"), 8)], axis=1)
    t = lambda k, *axes: np.ascontiguousarray(g(k).transpose(*axes))
    arrays["L0_ffn_gW1T"] = t("L0_ffn_gW1", 1, 0)
    arrays["L0_ffn_gW2T"] = t("L0_ffn_gW2", 1, 0)
    arrays["L0_ffn_eW1T"] = t("L0_ffn_eW1", 0, 2, 1)
    arrays["L0_ffn_eW2T"] = t("L0_ffn_eW2", 0, 2, 1)
    arrays["L2_ffn_tile_sigsT"] = t("L2_ffn_tile_sigs", 1, 0)
    arrays["L2_ffn_WT"] = t("L2_ffn_W", 0, 2, 1)
    for k in ("L3_ffn_w_gate", "L3_ffn_w_up", "L3_ffn_w_down"):
        arrays[k + "T"] = t(k, 1, 0)
    arrays["L3_attn_W"] = np.concatenate([g(f"L3_attn_W_{k}") for k in ("zf", "zs", "hf", "hs")], axis=1)
    arrays["L3_attn_b_col"] = np.stack([g(f"L3_attn_b_{k}") for k in ("zf", "zs", "hf", "hs")], axis=1)
    arrays["expert_order"] = np.broadcast_to(np.arange(8, 0, -1, dtype=f), (128, 8)).copy()
    arrays["before"] = (part[:, None] < part[None]).astype(f)
    pos = (part % 64).astype(f)[:, None]
    div = np.exp(np.arange(0, 32, 2, dtype=f) * f(-np.log(10000.0) / 32))
    ang = (pos * div).astype(f)
    pe = np.zeros((128, 32), f)
    pe[:, 0::2] = np.sin(ang)
    pe[:, 1::2] = np.cos(ang)
    arrays["positionT"] = np.ascontiguousarray(pe.T)
```

```python
from contextlib import ExitStack, contextmanager

import concourse.bass as bass
from concourse import mybir

ALU = mybir.AluOpType
ACT = mybir.ActivationFunctionType
F32 = mybir.dt.float32
I32 = mybir.dt.int32
R32 = mybir.dt.float32r
AX_X = mybir.AxisListType.X

P = 128
BATCH = 32
SEQ = 64
DIM = 256
KC = DIM // P
TOKENS = BATCH * SEQ
TILES = TOKENS // P
NKEY = 256
HEADS = 16
EPS = 1e-5


_stages, _names = [], {}


@contextmanager
def stage(nc):
    sems = []
    _stages.append(len(_stages))
    tag = f"s{len(_stages)}"

    def unique(name):
        _names[name] = _names.get(name, 0) + 1
        return f"{tag}_{name}_{_names[name]}"

    with ExitStack() as ctx:
        def sb(name, shape, dt=F32):
            return ctx.enter_context(nc.sbuf_tensor(unique(name), shape, dt))

        def ps(name, shape, dt=F32):
            return ctx.enter_context(nc.psum_tensor(unique(name), shape, dt))

        def sem(name):
            s = nc.alloc_semaphore(unique(name))
            sems.append(s)
            return s

        yield sb, ps, sem
    nc.clear_and_free_semaphores(sems)
    nc.all_engine_barrier()


class Chain:

    def __init__(self, eng, sem, base=0):
        self.eng, self.sem, self.base, self.n = eng, sem, base, 0

    def __call__(self, ins):
        self.n += 1
        ins.then_inc(self.sem, 1)
        self.eng.wait_ge(self.sem, self.base + self.n)


def three_passes(nc, dst, lhs, rhs, start, stop):
    nc.tensor.matmul(dst, lhs[0], rhs[1], start=start, stop=False)
    nc.tensor.matmul(dst, lhs[1], rhs[0], start=False, stop=False)
    return nc.tensor.matmul(dst, lhs[0], rhs[0], start=False, stop=stop)


def rows_to_sbuf(w):
    return w.rearrange("(c p) n -> p c n", p=P)


def row(v):
    return v.rearrange("(a n) -> a n", a=1)


def layernorm_transposed(nc, X, XNT, ident, passes=1, affine=None, residual=False, load=None, store=None,
                         rows=None):
    with stage(nc) as (sb, ps, sem):
        XN = sb("ln_xn", [P, TILES, DIM]) if rows is None else rows
        stats = sb("ln_stats", [P, TILES, 6])
        diff = sb("ln_diff", [P, TILES])
        mean = sb("ln_mean", [P, TILES])
        var = sb("ln_var", [P, TILES])
        std = sb("ln_std", [P, TILES])
        rstd = sb("ln_rstd", [P, TILES])
        col = sb("ln_col", [P, 2, KC])
        flip = [ps("ln_flip", [P, KC, P]) for _ in range(4)]
        s_var, s_std, s_dve, s_stat = sem("ln_var_ready"), sem("ln_std_ready"), sem("ln_dve_step"), sem("ln_stats_done")
        s_norm, s_flip, s_out, s_col = sem("ln_normed"), sem("ln_flipped"), sem("ln_stored"), sem("ln_columns_loaded")
        s_norm2, s_in, s_dram = sem("ln_pass_normed"), sem("ln_rows_loaded"), sem("ln_dram_stored")
        with nc.Block() as block:
            @block.sync
            def _(sp):
                if load is not None:
                    sp.dma_start(X[:, :, :], load).then_inc(s_in, 16)
                if affine:
                    for n, v in enumerate(affine):
                        sp.dma_start(col[:, n, :], v).then_inc(s_col, 16)
                if store is not None:
                    sp.wait_ge(s_out, TILES)
                    for c in range(KC):
                        sp.dma_start(store[:, c], XNT[:, c, :].rearrange("p (b s) -> p b s", s=NKEY)).then_inc(s_dram, 16)
                    sp.wait_ge(s_dram, 16 * KC)

            @block.vector
            def _(dve):
                link = Chain(dve, s_dve)
                if load is not None:
                    dve.wait_ge(s_in, 16)
                for n in range(passes):
                    src = XN if n else X
                    with dve.Fori(0, TILES // 8) as i:
                        for u in range(8):
                            t = i * 8 + u
                            nc.vector.bn_stats(stats[:, t, :], src[:, t, :]).then_inc(s_stat, 1)
                    dve.wait_ge(s_stat, TILES * (n + 1))
                    link(nc.vector.tensor_tensor(mean[:, :], stats[:, :, 1], stats[:, :, 4], ALU.add))
                    link(nc.vector.tensor_scalar(mean[:, :], mean[:, :], 0.5, None, ALU.mult))
                    link(nc.vector.tensor_tensor(diff[:, :], stats[:, :, 1], stats[:, :, 4], ALU.subtract))
                    link(nc.vector.tensor_tensor(diff[:, :], diff[:, :], diff[:, :], ALU.mult))
                    link(nc.vector.tensor_scalar(diff[:, :], diff[:, :], DIM / 4.0, None, ALU.mult))
                    link(nc.vector.tensor_tensor(var[:, :], stats[:, :, 2], stats[:, :, 5], ALU.add))
                    link(nc.vector.tensor_tensor(var[:, :], var[:, :], diff[:, :], ALU.add))
                    nc.vector.tensor_scalar(var[:, :], var[:, :], 1.0 / DIM, EPS, ALU.mult, ALU.add).then_inc(s_var, 1)
                    dve.wait_ge(s_std, n + 1)
                    link(nc.vector.reciprocal(rstd[:, :], std[:, :]))
                    done = s_norm if n == passes - 1 else s_norm2
                    with dve.Fori(0, TILES // 8) as i:
                        for u in range(8):
                            t = i * 8 + u
                            nc.vector.tensor_scalar(XN[:, t, :], src[:, t, :], mean[:, bass.ds(t, 1)],
                                                    rstd[:, bass.ds(t, 1)], ALU.subtract, ALU.mult).then_inc(done, 1)
                    if n < passes - 1:
                        dve.wait_ge(s_norm2, TILES)
                        if residual:
                            for h in range(2):
                                half = slice(h * TILES // 2, (h + 1) * TILES // 2)
                                link(nc.vector.tensor_tensor(X[:, half, :], X[:, half, :], XN[:, half, :], ALU.add))

            @block.tensor
            def _(pe):
                for t in range(TILES):
                    pe.wait_ge(s_norm, t + 1)
                    if t >= 4:
                        pe.wait_ge(s_out, t - 3)
                    for c in range(KC):
                        last = nc.tensor.transpose(flip[t % 4][:, c, :], XN[:, t, c * P:(c + 1) * P], ident[:, :])
                    last.then_inc(s_flip, 1)

            @block.scalar
            def _(act):
                for n in range(passes):
                    act.wait_ge(s_var, n + 1)
                    nc.scalar.activation(std[:, :], var[:, :], ACT.Sqrt).then_inc(s_std, 1)
                if affine:
                    act.wait_ge(s_col, 32)
                with act.Fori(0, TILES // 8) as i:
                    for u in range(8):
                        act.wait_ge(s_flip, i * 8 + (u + 1))
                        if affine:
                            for c in range(KC):
                                last = nc.scalar.activation(XNT[:, c, bass.ds(i * 8 * P + u * P, P)], flip[u % 4][:, c, :],
                                                            ACT.Identity, bias=col[:, 1, c:c + 1], scale=col[:, 0, c:c + 1])
                        else:
                            last = nc.scalar.copy(XNT[:, :, bass.ds(i * 8 * P + u * P, P)], flip[u % 4][:, :, :])
                        last.then_inc(s_out, 1)


def project_transposed(nc, XNT, dst, w, bias, chunks):
    TC = 512
    NT = TOKENS // TC
    with stage(nc) as (sb, ps, sem):
        W = sb("pj_w", [P, KC, chunks * P])
        WS = [sb("pj_w_part", [P, KC, chunks * P], R32) for _ in range(2)]
        XS = [sb("pj_x_part", [P, KC, TOKENS], R32) for _ in range(2)]
        B = sb("pj_b", [P, chunks])
        out = [ps("pj_out", [P, TC]) for _ in range(4)]
        s_w, s_mm, s_st = sem("pj_w_loaded"), sem("pj_multiplied"), sem("pj_stored")
        s_b, s_wh, s_wl, s_xh, s_xl = (sem("pj_bias_loaded"), sem("pj_w_high_ready"), sem("pj_w_low_ready"),
                                       sem("pj_x_high_ready"), sem("pj_x_low_ready"))
        jobs = [(t, m) for t in range(NT) for m in range(chunks)]
        with nc.Block() as block:
            @block.sync
            def _(sp):
                sp.dma_start(W[:, :, :], rows_to_sbuf(w)).then_inc(s_w, 16)
                if bias is not None:
                    sp.dma_start(B[:, :], bias).then_inc(s_b, 16)

            @block.scalar
            def _(act):
                for t in range(NT):
                    if t == 1:
                        act.wait_ge(s_w, 16)
                        nc.scalar.copy(WS[0][:, :, :], W[:, :, :]).then_inc(s_wh, 1)
                    nc.scalar.copy(XS[0][:, :, t * TC:(t + 1) * TC], XNT[:, :, t * TC:(t + 1) * TC]).then_inc(s_xh, 1)

            @block.tensor
            def _(pe):
                pe.wait_ge(s_wl, 1)
                for n, (t, m) in enumerate(jobs):
                    if m == 0:
                        pe.wait_ge(s_xl, t + 1)
                    if n >= 4:
                        pe.wait_ge(s_st, n - 3)
                    for c in range(KC):
                        last = three_passes(nc, out[n % 4][:, :], [v[:, c, m * P:(m + 1) * P] for v in WS],
                                            [v[:, c, t * TC:(t + 1) * TC] for v in XS], c == 0, c == KC - 1)
                    last.then_inc(s_mm, 1)

            @block.vector
            def _(dve):
                def low_input(t):
                    dve.wait_ge(s_xh, t + 1)
                    cols = slice(t * TC, (t + 1) * TC)
                    nc.vector.tensor_tensor(XS[1][:, :, cols], XNT[:, :, cols], XS[0][:, :, cols].bitcast(F32), ALU.subtract).then_inc(s_xl, 1)

                low_input(0)
                dve.wait_ge(s_wh, 1)
                nc.vector.tensor_tensor(WS[1][:, :, :], W[:, :, :], WS[0][:, :, :].bitcast(F32), ALU.subtract).then_inc(s_wl, 1)
                if bias is not None:
                    dve.wait_ge(s_b, 16)
                for n, (t, m) in enumerate(jobs):
                    if m == 0 and t + 1 < NT:
                        low_input(t + 1)
                    dve.wait_ge(s_mm, n + 1)
                    if bias is not None:
                        last = nc.vector.tensor_scalar(dst[:, m, t * TC:(t + 1) * TC], out[n % 4][:, :], B[:, m:m + 1],
                                                       None, ALU.add)
                    else:
                        last = nc.vector.tensor_copy(dst[:, m, t * TC:(t + 1) * TC], out[n % 4][:, :])
                    last.then_inc(s_st, 1)


def cross_attention(nc, X, QT, ident, ones, spread_mask, ctxT, head, wkv=None, bk=None, bv=None, ctx=None,
                    wo=None, bo=None, mask=None, clip=None, scratch=None):
    inner = HEADS * head
    chunks = inner // P
    PAIR = 2 * head
    HPC = P // head
    STEPS = 4
    OWN = wkv is not None
    KB = chunks * NKEY // 512 if OWN else 0
    NAT = (chunks + 3) // 4 if wo is not None else 0
    OP = 4 if PAIR + 1 <= 64 else 2
    OR = 4 // OP
    TAIL = NAT + 1 if wo is not None else 0
    PER_TILE = 4 * KB + TAIL

    def users(n, first, last):
        kind = "KV"[n % 2]
        own = [(kind, k) for k in range(KB)] if not (last and n >= 2) else []
        own += [None] * (4 - len(own))
        tail = n == 0 and not first and wo is not None
        at = [("AT", r) for r in range(NAT)] if tail else []
        return {"pre": at[:1], "u1": own[:1], "mid": at[1:], "u2": own[1:2], "u3": own[2:3],
                "out": [("OUT", 0)] if tail else [], "u4": own[3:4]}

    SLOTS = ("pre", "u1", "mid", "u2", "u3", "out", "u4")

    AT_ON_DVE = chunks == 2 and mask is None
    ACT_USERS = ("K",) if AT_ON_DVE else ("K", "AT")
    DVE_USERS = ("V", "OUT", "AT") if AT_ON_DVE else ("V", "OUT")

    def index(i, n, user):
        first, last = isinstance(i, int) and i == 0, isinstance(i, int) and i == TILES - 1
        if n < 0:
            return ("K", "V").index(user[0]) * KB + user[1]
        order = [(m, w) for m in range(STEPS) for sl in SLOTS for w in users(m, first, last)[sl] if w]
        before = order.index((n, user))
        if first:
            return 2 * KB + before
        return (i - 1) * PER_TILE + (2 * KB + PER_TILE - TAIL + before)

    def key_ready(i, n, g):
        u = n // 2
        k = KB - 1 if KB == 1 else 2 * g + 1
        if u == 0:
            return (index(0, -1, ("K", k)) if isinstance(i, int) and i == 0 else index(i - 1, 2, ("K", k))) + 1
        return index(i, 0, ("K", k)) + 1

    def value_ready(i, n):
        if n // 2 == 0:
            return (index(0, -1, ("V", KB - 1)) if isinstance(i, int) and i == 0 else index(i - 1, 3, ("V", KB - 1))) + 1
        return index(i, 1, ("V", KB - 1)) + 1

    def last_tail():
        at = (TILES - 2) * PER_TILE + (2 * KB + PER_TILE - TAIL) + PER_TILE - 2 * KB
        return [(at + r, ("AT", r)) for r in range(NAT)] + ([(at + NAT, ("OUT", 0))] if wo is not None else [])

    with stage(nc) as (sb, ps, sem):
        CT = [sb("ca_ctxT", [P, KC, NKEY]) for _ in range(2)]
        KT = [sb("ca_kT", [P, chunks, NKEY]) for _ in range(2)] if OWN else CT
        V = [sb("ca_v", [P, 2, 8, PAIR + 1]) for _ in range(2)]
        CN = [sb("ca_ctx", [P, 2, NKEY]) for _ in range(2)] if not OWN else None
        QB = [sb("ca_q_spread", [P, 4, 2, SEQ]) for _ in range(STEPS)]
        PR = [sb("ca_probs", [P, 4, NKEY]) for _ in range(2)]
        SC = [sb("ca_scores_moved", [P, 4, NKEY]) for _ in range(2)] if mask is not None else PR if clip else None
        PT = [sb("ca_probsT", [P, 8, P]) for _ in range(2)]
        nmax = [sb("ca_neg_max", [P, 4]) for _ in range(2)]
        rsum = [sb("ca_inv_sum", [P, 4]) for _ in range(2)]
        A = sb("ca_attended", [P, inner])
        AT = sb("ca_attendedT", [P, chunks, P])
        SM = sb("ca_spread_mask", [P, HPC])
        if OWN:
            RAW = [scratch[:, 1, h * inner:(h + 1) * inner] for h in range(2)]
            PIECES = [(c, h) for c in range(KC) for h in range(2)]
            WH, WL = sb("ca_wkv_high", [P, KC, 2 * inner], R32), sb("ca_wkv_low", [P, KC, 2 * inner], R32)
            CH = [sb("ca_ctxT_high", [P, KC, NKEY], R32) for _ in range(2)]
            CL = [sb("ca_ctxT_low", [P, KC, NKEY], R32) for _ in range(2)]
        if bk is not None:
            BK = sb("ca_bk", [P, chunks])
            BV = sb("ca_bv", [P, chunks])
        if wo is not None:
            WO = scratch[:, 0, 0:chunks * DIM].rearrange("p (c n) -> p c n", c=chunks)
            BO = sb("ca_bo", [1, DIM])
        if mask is not None:
            MFAC = sb("ca_mask_factor", [P, 1])
            MK = [sb("ca_mask", [P, NKEY]) for _ in range(2)]
            MB = [sb("ca_mask_added", [P, NKEY]) for _ in range(2)]
        psS = [ps("ca_scores", [P, 4, NKEY]) for _ in range(2)]
        psT = ps("ca_probs_flipped", [P, 8, P])
        psA = ps("ca_shared", [P, 512])
        psO = ps("ca_out", [P, 512])
        psA2 = psA[:, :].rearrange("p (a b) -> p a b", a=2)

        s_w, s_one = sem("weights_loaded"), sem("v_ones_set")
        s_ct = [sem(f"ctx{u}_loaded") for u in range(2)]
        s_mk = [sem(f"mask{u}_loaded") for u in range(2)]
        s_mb, s_vr = sem("mask_scaled"), sem("context_values_ready")
        psA_filled, psA_emptied = sem("psA_filled"), sem("psA_emptied")
        s_q, s_s, s_mv, s_mx = sem("queries_spread"), sem("scores_ready"), sem("scores_moved"), sem("max_ready")
        s_e, s_t, s_tc = sem("probs_ready"), sem("probs_flipped"), sem("probsT_ready")
        s_pv, s_rs, s_o, s_x = sem("attended"), sem("inv_sum_ready"), sem("attended_stored"), sem("x_updated")
        s_raw = [sem(f"raw_weights{h}_loaded") for h in range(2)]
        s_wh, s_wl = sem("w_high_ready"), sem("w_low_ready")
        s_ch, s_cl = sem("ctx_high_ready"), sem("ctx_low_ready")
        NW = 16 * (1 + 2 * (bk is not None) + 2 * (wo is not None))

        def tiles(eng, body):
            body(0)
            with eng.Fori(1, TILES - 1) as i:
                body(i)
            body(TILES - 1)

        def is_first(i):
            return isinstance(i, int) and i == 0

        def is_last(i):
            return isinstance(i, int) and i == TILES - 1

        with nc.Block() as block:
            @block.sync
            def _(sp):
                sp.dma_start(SM[:, :], spread_mask).then_inc(s_w, 16)
                def load_weights(q):
                    c, h = PIECES[q]
                    sp.dma_start(RAW[h], wkv[c * P:(c + 1) * P, h * inner:(h + 1) * inner]).then_inc(s_raw[h], 16)

                if OWN:
                    load_weights(0)
                    load_weights(1)
                if bk is not None:
                    sp.dma_start(BK[:, :], bk).then_inc(s_w, 16)
                    sp.dma_start(BV[:, :], bv).then_inc(s_w, 16)
                if wo is not None:
                    sp.dma_start(WO, rows_to_sbuf(wo)).then_inc(s_w, 16)
                    sp.dma_start(BO[:, :], row(bo)).then_inc(s_w, 16)
                if mask is not None:
                    sp.sem_inc(s_mb, 2)

                def load(i):
                    for u in range(2):
                        if mask is not None:
                            sp.wait_ge(s_mb, i * 2 + (u + 1))
                            sp.dma_start(MK[u][:, :], mask[i, u].partition_broadcast(P)).then_inc(s_mk[u], 16)
                    for u in range(2):
                        if OWN and not is_first(i):
                            sp.wait_ge(s_cl, i * 2 + (u - 1))
                        if not OWN:
                            sp.wait_ge(s_s, i * STEPS + (2 * u + 2))
                            if not is_first(i):
                                sp.wait_ge(s_vr, i * 2 + (u - 1))
                        sp.dma_start(CT[u][:, :, :], ctxT[i, u].rearrange("(c p) s -> p c s", p=P)).then_inc(s_ct[u], 16)
                        if not OWN:
                            sp.dma_start(CN[u][:, :, :], ctx[i, u].rearrange("(c p) d -> p c d", p=P)).then_inc(s_ct[u], 16)

                load(0)
                if OWN:
                    for q in range(2, len(PIECES)):
                        sp.wait_ge(s_wl, q - 1)
                        load_weights(q)
                load(1)
                with sp.Fori(2, TILES) as i:
                    load(i)

            @block.gpsimd
            def _(pool):
                for u in range(2):
                    nc.gpsimd.memset(V[u][:, :, :, PAIR:PAIR + 1], 1.0).then_inc(s_one, 1)
                if mask is not None:
                    nc.gpsimd.memset(MFAC[:, :], -1e9).then_inc(s_one, 1)
                    pool.wait_ge(s_one, 3)
                pool.wait_ge(s_w, NW)
                pool.sem_inc(s_s, STEPS)
                if mask is not None:
                    pool.sem_inc(s_mv, STEPS)
                if not OWN:
                    pool.sem_inc(s_pv, STEPS)
                with pool.Fori(0, TILES) as i:
                    for u in range(2):
                        if mask is not None:
                            pool.wait_ge(s_mk[u], (i + 1) * 16)
                            pool.wait_ge(s_mv, i * STEPS + (2 * u + 2))
                            nc.gpsimd.tensor_tensor(MB[u][:, :], MK[u][:, :], MFAC[:, :].broadcast_to([P, NKEY]), ALU.mult).then_inc(s_mb, 1)
                        for g in range(2):
                            n = 2 * u + g
                            pool.wait_ge(s_s, i * STEPS + (n + 1))
                            tok = bass.ds(i * P + u * SEQ, SEQ)
                            if chunks == 2:
                                q = QT[:, g, tok].unsqueeze(1).broadcast_to([P, 8, SEQ])
                                m = SM[:, :].unsqueeze(2).broadcast_to([P, 8, SEQ])
                                o = QB[n][:, :, :, :].rearrange("p a b q -> p (a b) q")
                                nc.gpsimd.tensor_tensor(o, q, m, ALU.mult).then_inc(s_q, 1)
                            else:
                                for h in range(2):
                                    q = QT[:, 4 * g:4 * g + 4, tok]
                                    m = SM[:, h:h + 1].unsqueeze(2).broadcast_to([P, 4, SEQ])
                                    last = nc.gpsimd.tensor_tensor(QB[n][:, :, h, :], q, m, ALU.mult)
                                last.then_inc(s_q, 1)
                        if not OWN:
                            pool.wait_ge(s_ct[u], (i + 1) * 32)
                            pool.wait_ge(s_pv, i * STEPS + (2 * u + 2))
                            for c in range(2):
                                last = nc.gpsimd.tensor_tensor(V[u][:, c, :, 0:PAIR],
                                                               CN[u][:, c, :].rearrange("p (a d) -> p a d", a=8),
                                                               ones[:, 0:1].unsqueeze(2).broadcast_to([P, 8, PAIR]), ALU.mult)
                            last.then_inc(s_vr, 1)

            @block.tensor
            def _(pe):
                def fill(i, n, user, at=None):
                    kind, k = user
                    at = index(i, n, user) if at is None else at
                    if not (isinstance(at, int) and at == 0):
                        pe.wait_ge(psA_emptied, at)
                    if kind in ("K", "V"):
                        u = 0 if n < 0 else 1 - n // 2
                        j = 0 if n < 0 else (i if u else i + 1)
                        pe.wait_ge(s_cl, j * 2 + (u + 1))
                    if kind == "K":
                        for j in range(2):
                            m = 2 * k + j
                            for c in range(KC):
                                cols = slice(m * P, (m + 1) * P)
                                last = three_passes(nc, psA2[:, j, :], (WH[:, c, cols], WL[:, c, cols]),
                                                    (CH[u][:, c, :], CL[u][:, c, :]), c == 0, c == KC - 1)
                    elif kind == "V" and chunks == 2:
                        for j in range(2):
                            for c in range(KC):
                                keys, cols = slice(j * P, (j + 1) * P), slice(inner, 2 * inner)
                                last = three_passes(nc, psA2[:, j, :], (CH[u][:, c, keys], CL[u][:, c, keys]),
                                                    (WH[:, c, cols], WL[:, c, cols]), c == 0, c == KC - 1)
                    elif kind == "V":
                        j, hf = k // 2, k % 2
                        for c in range(KC):
                            keys, cols = slice(j * P, (j + 1) * P), slice(inner + hf * 512, inner + (hf + 1) * 512)
                            last = three_passes(nc, psA[:, :], (CH[u][:, c, keys], CL[u][:, c, keys]),
                                                (WH[:, c, cols], WL[:, c, cols]), c == 0, c == KC - 1)
                    elif kind == "AT":
                        if k == 0:
                            pe.wait_ge(s_o, i * STEPS * OR)
                        for c in range(min(4, chunks)):
                            cc = k * 4 + c
                            last = nc.tensor.transpose(psA[:, c * P:(c + 1) * P], A[:, cc * P:(cc + 1) * P], ident[:, :])
                    else:
                        pe.wait_ge(psA_emptied, at)
                        for c in range(chunks):
                            nc.tensor.matmul(psA[:, 0:DIM], AT[:, c, :], WO[:, c], start=(c == 0), stop=False)
                        last = nc.tensor.matmul(psA[:, 0:DIM], ones[0:1, :], BO[:, :], start=False, stop=True)
                    last.then_inc(psA_filled, 1)

                def scores(i, n):
                    u, g = n // 2, n % 2
                    pe.wait_ge(s_q, i * STEPS + (n + 1))
                    if OWN:
                        pe.wait_ge(psA_emptied, key_ready(i, n, g))
                    else:
                        pe.wait_ge(s_ct[u], (i + 1) * 32)
                    for a in range(4):
                        k = KT[u][:, g, :] if chunks == 2 else KT[u][:, 4 * g + a, :]
                        last = nc.tensor.matmul(psS[n % 2][:, a, :], QB[n][:, a, :, :].rearrange("p b q -> p (b q)"), k,
                                                start=True, stop=True)
                    last.then_inc(s_s, 1)

                def flip(i, n):
                    pe.wait_ge(s_e, i * STEPS + (n + 1))
                    for a in range(4):
                        for c in range(2):
                            last = nc.tensor.transpose(psT[:, 2 * a + c, :], PR[n % 2][:, a, c * P:(c + 1) * P], ident[:, :])
                    last.then_inc(s_t, 1)

                def attend(i, n, r):
                    u, g = n // 2, n % 2
                    if r == 0:
                        pe.wait_ge(s_tc, i * STEPS + (n + 1))
                        if g == 0:
                            if OWN:
                                pe.wait_ge(psA_emptied, value_ready(i, n))
                            else:
                                pe.wait_ge(s_vr, i * 2 + (u + 1))
                    if not (is_first(i) and n == 0 and r == 0):
                        pe.wait_ge(s_o, i * STEPS * OR + (n * OR + r))
                    for a in range(OP):
                        pr = r * OP + a
                        for c in range(2):
                            last = nc.tensor.matmul(psO[:, a * (PAIR + 1):(a + 1) * (PAIR + 1)], PT[n % 2][:, 2 * pr + c, :],
                                                    V[u][:, c, 4 * g + pr, :], start=(c == 0), stop=(c == 1))
                    last.then_inc(s_pv, 1)

                def body(i):
                    for n in range(STEPS):
                        us = users(n, is_first(i), is_last(i))

                        def slot(name):
                            for w in us[name]:
                                if w:
                                    fill(i, n, w)

                        def ahead():
                            if not (is_last(i) and n >= 2):
                                scores(i if n < 2 else i + 1, (n + 2) % STEPS)

                        flip(i, n)
                        slot("pre")
                        slot("u1")
                        slot("mid")
                        if not OWN:
                            ahead()
                        attend(i, n, 0)
                        slot("u2")
                        if OR == 2:
                            attend(i, n, 1)
                        slot("u3")
                        slot("out")
                        if OWN:
                            ahead()
                        slot("u4")

                pe.wait_ge(s_w, NW)
                pe.wait_ge(s_one, 2)
                if OWN:
                    pe.wait_ge(s_wl, len(PIECES))
                for kind in "KV":
                    for k in range(KB):
                        fill(0, -1, (kind, k))
                scores(0, 0)
                scores(0, 1)
                tiles(pe, body)
                for at, w in last_tail():
                    fill(TILES, 0, w, at)

            @block.scalar
            def _(act):
                def empty(at, w):
                    kind, k = w
                    act.wait_ge(psA_filled, at + 1)
                    if kind == "K" and bk is not None:
                        for j in range(2):
                            last = nc.scalar.activation(KT[key_buffer[0]][:, 2 * k + j, :], psA2[:, j, :], ACT.Identity,
                                                        bias=BK[:, 2 * k + j:2 * k + j + 1])
                    elif kind == "K":
                        last = nc.scalar.copy(KT[key_buffer[0]][:, 2 * k:2 * k + 2, :], psA2)
                    elif bk is not None:
                        for c in range(chunks):
                            last = nc.scalar.activation(AT[:, c, :], psA[:, c * P:(c + 1) * P], ACT.Identity, bias=BV[:, c:c + 1])
                    else:
                        nn = min(4, chunks)
                        last = nc.scalar.copy(AT[:, k * nn:(k + 1) * nn, :].rearrange("p a b -> p (a b)"), psA[:, 0:nn * P])
                    last.then_inc(psA_emptied, 1)

                key_buffer = [0]

                def exponentiate(i, n):
                    if clip:
                        act.wait_ge(s_mv, i * STEPS + (n + 1))
                        nc.scalar.activation(PR[n % 2][:, :, :], SC[n % 2][:, :, :], ACT.Exp).then_inc(s_e, 1)
                        return
                    act.wait_ge(s_mx, i * STEPS + (n + 1))
                    src = SC[n % 2] if mask is not None else psS[n % 2]
                    for a in range(4):
                        last = nc.scalar.activation(PR[n % 2][:, a, :], src[:, a, :], ACT.Exp, bias=nmax[n % 2][:, a:a + 1])
                    last.then_inc(s_e, 1)

                def body(i):
                    for n in range(STEPS):
                        us = users(n, is_first(i), is_last(i))
                        key_buffer[0] = 1 - n // 2

                        def slot(*names):
                            for name in names:
                                for w in us[name]:
                                    if w and w[0] in ACT_USERS:
                                        empty(index(i, n, w), w)

                        if mask is not None:
                            act.wait_ge(s_t, i * STEPS + (n + 1))
                            nc.scalar.copy(PT[n % 2][:, :, :], psT[:, :, :]).then_inc(s_tc, 1)
                            slot("pre")
                            if not (is_last(i) and n == 3):
                                exponentiate(i if n < 3 else i + 1, (n + 1) % STEPS)
                            slot("u1", "mid", "u2", "u3", "u4")
                            if OWN and n % 2 == 0 and not is_last(i):
                                high(i + 1, n // 2)
                            continue
                        slot("pre", "u1", "mid", "u2", "u3")
                        if not (is_last(i) and n >= 2):
                            exponentiate(i if n < 2 else i + 1, (n + 2) % STEPS)
                        slot("u4")
                        if OWN and n % 2 == 0 and not is_last(i):
                            high(i + 1, n // 2)

                def high(i, u):
                    act.wait_ge(s_ct[u], (i + 1) * 16)
                    if not is_first(i):
                        act.wait_ge(psA_filled, value_ready(i - 1, 2 * u))
                    nc.scalar.copy(CH[u][:, :, :], CT[u][:, :, :]).then_inc(s_ch, 1)

                act.wait_ge(s_w, NW)
                if OWN:
                    for c, h in PIECES:
                        act.wait_ge(s_raw[h], 16 * c + 16)
                        nc.scalar.copy(WH[:, c, h * inner:(h + 1) * inner], RAW[h]).then_inc(s_wh, 1)
                    for u in range(2):
                        high(0, u)
                for k in range(KB):
                    empty(index(0, -1, ("K", k)), ("K", k))
                exponentiate(0, 0)
                if mask is None:
                    exponentiate(0, 1)
                tiles(act, body)
                for at, w in last_tail():
                    if w[0] in ACT_USERS:
                        empty(at, w)

            @block.vector
            def _(dve):
                PC = 0 if OWN else STEPS
                OFF = STEPS if mask is not None else 0

                def empty(i, at, w, u):
                    kind, k = w
                    dve.wait_ge(psA_filled, at + 1)
                    if kind == "V" and chunks == 2:
                        for c in range(2):
                            last = nc.vector.tensor_copy(V[u][:, c, :, 0:PAIR], psA2[:, c, :].rearrange("p (a d) -> p a d", a=8))
                    elif kind == "V":
                        j, hf = k // 2, k % 2
                        last = nc.vector.tensor_copy(V[u][:, j, 4 * hf:4 * hf + 4, 0:PAIR],
                                                     psA[:, :].rearrange("p (a d) -> p a d", a=4))
                    elif kind == "AT":
                        for c in range(chunks):
                            last = nc.vector.tensor_scalar(AT[:, c, :], psA[:, c * P:(c + 1) * P], BV[:, c:c + 1], None, ALU.add)
                    else:
                        tile = bass.ds(i - 1, 1)
                        last = nc.vector.tensor_tensor(X[:, tile, :], psA[:, 0:DIM].unsqueeze(1), X[:, tile, :], ALU.add)
                    last.then_inc(psA_emptied, 1)

                def take(i, n):
                    dve.wait_ge(s_s, i * STEPS + (n + 1) + STEPS)
                    if clip:
                        nc.vector.tensor_scalar(SC[n % 2][:, :, :], psS[n % 2][:, :, :], -clip, clip, ALU.max,
                                                ALU.min).then_inc(s_mv, 1)
                        return
                    if mask is not None:
                        if n % 2 == 0:
                            dve.wait_ge(s_mb, i * 2 + (n // 2 + 3))
                        nc.vector.tensor_tensor(SC[n % 2][:, :, :], psS[n % 2][:, :, :],
                                                MB[n // 2][:, :].unsqueeze(1).broadcast_to([P, 4, NKEY]), ALU.add).then_inc(s_mv, 1)
                        dve.wait_ge(s_mv, i * STEPS + (n + 1) + OFF)
                    src = SC[n % 2] if mask is not None else psS[n % 2]
                    nc.vector.tensor_reduce(nmax[n % 2][:, :], src[:, :, :], AX_X, ALU.max, negate=True).then_inc(s_mx, 1)

                def store(i, n, r):
                    u, g = n // 2, n % 2
                    at = i * STEPS * OR + (n * OR + r + 1)
                    dve.wait_ge(s_pv, at + PC)
                    O = psO[:, 0:OP * (PAIR + 1)].rearrange("p (a w) -> p a w", a=OP)
                    R = rsum[n % 2][:, r * OP:(r + 1) * OP]
                    nc.vector.reciprocal(R, O[:, :, PAIR]).then_inc(s_rs, 1)
                    dve.wait_ge(s_rs, at)
                    for h in range(2):
                        dst = A[u * SEQ:(u + 1) * SEQ, :].rearrange("p (a b d) -> p a b d", a=8, b=2)[
                            :, 4 * g + r * OP:4 * g + (r + 1) * OP, h, :]
                        last = nc.vector.tensor_tensor(
                            dst, O[h * SEQ:(h + 1) * SEQ, :, h * head:(h + 1) * head],
                            R[h * SEQ:(h + 1) * SEQ, :].unsqueeze(2).broadcast_to([SEQ, OP, head]), ALU.mult)
                    last.then_inc(s_o, 1)

                def body(i):
                    for n in range(STEPS):
                        us = users(n, is_first(i), is_last(i))

                        def slot(*names):
                            for name in names:
                                for w in us[name]:
                                    if w and w[0] in DVE_USERS:
                                        empty(i, index(i, n, w), w, 1 - n // 2)

                        def ahead():
                            if not (is_last(i) and n >= 2):
                                take(i if n < 2 else i + 1, (n + 2) % STEPS)

                        slot("pre")
                        if mask is None:
                            dve.wait_ge(s_t, i * STEPS + (n + 1))
                            nc.vector.tensor_copy(PT[n % 2][:, :, :], psT[:, :, :]).then_inc(s_tc, 1)
                        if OWN and n % 2 == 1 and not is_last(i):
                            low(i + 1, n // 2)
                        slot("u1")
                        if not OWN:
                            ahead()
                        store(i, n, 0)
                        slot("u2")
                        if OR == 2:
                            store(i, n, 1)
                        slot("u3", "out")
                        if OWN:
                            ahead()
                        slot("u4")
                    if wo is None:
                        dve.wait_ge(s_o, (i + 1) * STEPS * OR)
                        tile = bass.ds(i, 1)
                        nc.vector.tensor_tensor(X[:, tile, :], A[:, :].unsqueeze(1), X[:, tile, :], ALU.add).then_inc(s_x, 1)

                if bk is not None:
                    dve.wait_ge(s_w, NW)

                def low(i, u):
                    dve.wait_ge(s_ch, i * 2 + (u + 1))
                    nc.vector.tensor_tensor(CL[u][:, :, :], CT[u][:, :, :], CH[u][:, :, :].bitcast(F32), ALU.subtract).then_inc(s_cl, 1)

                if OWN:
                    for q, (c, h) in enumerate(PIECES):
                        dve.wait_ge(s_wh, q + 1)
                        cols = slice(h * inner, (h + 1) * inner)
                        nc.vector.tensor_tensor(WL[:, c, cols], RAW[h], WH[:, c, cols].bitcast(F32), ALU.subtract).then_inc(s_wl, 1)
                    for u in range(2):
                        low(0, u)
                for k in range(KB):
                    empty(0, index(0, -1, ("V", k)), ("V", k), 0)
                take(0, 0)
                take(0, 1)
                tiles(dve, body)
                for at, w in last_tail():
                    if w[0] in DVE_USERS:
                        empty(TILES, at, w, 0)


def linear_attention(nc, X, XNT, ident, d):
    LAST = TILES - 1

    def is_first(i):
        return isinstance(i, int) and i == 0

    with stage(nc) as (sb, ps, sem):
        W = sb("la_wqkv", [P, KC, 3 * DIM])
        WO = sb("la_wout", [P, KC, DIM])
        SH = sb("la_same_head", [P, P])
        H8 = sb("la_heads", [P, 8])
        XS = sb("la_x", [P, KC, P])
        low = sb("la_below_zero", [P, 2, DIM])
        ex = sb("la_exp", [P, 2, DIM])
        QS = sb("la_qT", [P, KC, P])
        KS = sb("la_k", [P, DIM])
        VS = sb("la_v", [P, 2, P + 1])
        KV = sb("la_kv", [P, 2, 2, P + 8])
        rden = sb("la_inv_denominator", [P, 2, 8])
        A = sb("la_attended", [P, DIM])
        AT = sb("la_attendedT", [P, KC, P])
        psQ, psK = ps("la_psq", [P, 512]), ps("la_pskv", [P, 512])
        psM = [ps("la_psm", [P, 512]) for _ in range(2)]
        psO, psT, psY = ps("la_pso", [P, 512]), ps("la_pst", [P, 512]), ps("la_psy", [P, 512])
        s_w, s_one, s_xs = sem("weights_loaded"), sem("v_ones_set"), sem("x_tile_ready")
        s_p, s_low, s_ex, s_fk = sem("qkv_projected"), sem("below_zero_ready"), sem("exp_ready"), sem("key_features_ready")
        s_fq = sem("query_features_ready")
        s_m, s_kv, s_o, s_d, s_a = sem("kv_summed"), sem("kv_ready"), sem("out_ready"), sem("dve_step"), sem("attended_ready")
        s_at, s_atc, s_y, s_x = sem("attended_flipped"), sem("attendedT_ready"), sem("out_projected"), sem("x_updated")
        with nc.Block() as block:
            @block.sync
            def _(sp):
                sp.dma_start(W[:, :, :], rows_to_sbuf(d["L0_attn_Wqkv"])).then_inc(s_w, 16)
                sp.dma_start(WO[:, :, :], rows_to_sbuf(d["L0_attn_Wout"])).then_inc(s_w, 16)
                sp.dma_start(SH[:, :], d["same_head"]).then_inc(s_w, 16)
                sp.dma_start(H8[:, :], d["heads8"]).then_inc(s_w, 16)

            @block.gpsimd
            def _(pool):
                nc.gpsimd.memset(VS[:, :, P:P + 1], 1.0).then_inc(s_one, 1)

            @block.tensor
            def _(pe):
                def project(i):
                    pe.wait_ge(s_xs, i + 1)
                    if not is_first(i):
                        pe.wait_ge(s_fq, i)
                    for m in range(KC):
                        for c in range(KC):
                            nc.tensor.matmul(psQ[:, m * P:(m + 1) * P], W[:, c, m * P:(m + 1) * P], XS[:, c, :],
                                             start=(c == 0), stop=(c == KC - 1))
                    for c in range(KC):
                        last = nc.tensor.matmul(psK[:, :], XS[:, c, :], W[:, c, DIM:3 * DIM], start=(c == 0),
                                                stop=(c == KC - 1))
                    last.then_inc(s_p, 1)

                def sum_keys(i):
                    pe.wait_ge(s_fk, i + 1)
                    for b in range(2):
                        r = slice(b * SEQ, (b + 1) * SEQ)
                        for g in range(2):
                            last = nc.tensor.matmul(psM[b][:, g * (P + 1):(g + 1) * (P + 1)], KS[r, g * P:(g + 1) * P],
                                                    VS[r, g, :], start=True, stop=True)
                    last.then_inc(s_m, 1)

                def attend(i):
                    pe.wait_ge(s_kv, i + 1)
                    pe.wait_ge(s_fq, i + 1)
                    for b in range(2):
                        for g in range(2):
                            last = nc.tensor.matmul(psO[b * SEQ:(b + 1) * SEQ, g * (P + 8):(g + 1) * (P + 8)],
                                                    QS[:, g, b * SEQ:(b + 1) * SEQ], KV[:, b, g, :], start=True, stop=True)
                    last.then_inc(s_o, 1)

                def flip(i):
                    pe.wait_ge(s_a, i + 1)
                    for c in range(KC):
                        last = nc.tensor.transpose(psT[:, c * P:(c + 1) * P], A[:, c * P:(c + 1) * P], ident[:, :])
                    last.then_inc(s_at, 1)

                def output(i):
                    pe.wait_ge(s_atc, i + 1)
                    if not is_first(i):
                        pe.wait_ge(s_x, i)
                    for c in range(KC):
                        last = nc.tensor.matmul(psY[:, 0:DIM], AT[:, c, :], WO[:, c, :], start=(c == 0), stop=(c == KC - 1))
                    last.then_inc(s_y, 1)

                def body(i, before):
                    sum_keys(i)
                    flip(before)
                    project(i + 1)
                    output(before)
                    attend(i)

                pe.wait_ge(s_w, 64)
                pe.wait_ge(s_one, 1)
                project(0)
                sum_keys(0)
                project(1)
                attend(0)
                body(1, 0)
                with pe.Fori(2, LAST) as i:
                    body(i, i - 1)
                sum_keys(LAST)
                flip(LAST - 1)
                output(LAST - 1)
                attend(LAST)
                flip(LAST)
                output(LAST)

            @block.scalar
            def _(act):
                def take(i):
                    if not is_first(i):
                        act.wait_ge(s_p, i)
                    nc.scalar.copy(XS[:, :, :], XNT[:, :, bass.ds(i * P, P)]).then_inc(s_xs, 1)

                def exponentiate(i):
                    act.wait_ge(s_low, i + 1)
                    nc.scalar.activation(ex[:, :, :], low[:, :, :], ACT.Exp).then_inc(s_ex, 1)

                def result(i):
                    act.wait_ge(s_at, i + 1)
                    nc.scalar.copy(AT[:, :, :].rearrange("p a b -> p (a b)"), psT[:, 0:DIM]).then_inc(s_atc, 1)

                take(0)
                for i in range(2):
                    take(i + 1)
                    exponentiate(i)
                with act.Fori(1, LAST - 1) as i:
                    result(i - 1)
                    take(i + 2)
                    exponentiate(i + 1)
                result(LAST - 2)
                exponentiate(LAST)
                result(LAST - 1)
                result(LAST)

            @block.vector
            def _(dve):
                def key_features(i):
                    dve.wait_ge(s_p, i + 1)
                    nc.vector.tensor_scalar(low[:, 0, :], psQ[:, 0:DIM], 0.0, None, ALU.min)
                    nc.vector.tensor_scalar(low[:, 1, :], psK[:, 0:DIM], 0.0, None, ALU.min).then_inc(s_low, 1)
                    for g in range(2):
                        nc.vector.tensor_copy(VS[:, g, 0:P], psK[:, DIM + g * P:DIM + (g + 1) * P])
                    dve.wait_ge(s_ex, i + 1)
                    nc.vector.scalar_tensor_tensor(KS[:, :], psK[:, 0:DIM], 0.0, ex[:, 1, :], ALU.max, ALU.add).then_inc(s_fk, 1)

                def query_features(i):
                    nc.vector.scalar_tensor_tensor(QS[:, :, :].rearrange("p a b -> p (a b)"), psQ[:, 0:DIM], 0.0,
                                                   ex[:, 0, :], ALU.max, ALU.add).then_inc(s_fq, 1)

                def mask_sums(i):
                    dve.wait_ge(s_m, i + 1)
                    for b in range(2):
                        for g in range(2):
                            o = g * (P + 1)
                            nc.vector.tensor_tensor(KV[:, b, g, 0:P], psM[b][:, o:o + P], SH[:, :], ALU.mult)
                            last = nc.vector.tensor_scalar(KV[:, b, g, P:P + 8], H8[:, :], psM[b][:, o + P:o + P + 1], None,
                                                           ALU.mult)
                    last.then_inc(s_kv, 1)

                def divide(i):
                    link = Chain(dve, s_d, i * 2)
                    dve.wait_ge(s_o, i + 1)
                    O = psO[:, 0:2 * (P + 8)].rearrange("p (g w) -> p g w", g=2)
                    link(nc.vector.tensor_scalar(rden[:, :, :], O[:, :, P:P + 8], 1e-6, None, ALU.add))
                    link(nc.vector.reciprocal(rden[:, :, :], rden[:, :, :]))
                    for g in range(2):
                        last = nc.vector.tensor_tensor(A[:, g * P:(g + 1) * P].rearrange("p (h d) -> p h d", h=8),
                                                       O[:, g, 0:P].rearrange("p (h d) -> p h d", h=8),
                                                       rden[:, g, :].unsqueeze(2).broadcast_to([P, 8, 16]), ALU.mult)
                    last.then_inc(s_a, 1)

                def update(i):
                    dve.wait_ge(s_y, i + 1)
                    x = X[:, bass.ds(i, 1), :]
                    nc.vector.tensor_tensor(x, psY[:, 0:DIM].unsqueeze(1), x, ALU.add).then_inc(s_x, 1)

                def body(i):
                    mask_sums(i)
                    key_features(i + 1)
                    divide(i)
                    query_features(i + 1)
                    if not is_first(i):
                        update(i - 1)

                dve.wait_ge(s_w, 64)
                key_features(0)
                query_features(0)
                body(0)
                with dve.Fori(1, LAST) as i:
                    body(i)
                mask_sums(LAST)
                divide(LAST)
                update(LAST - 1)
                update(LAST)


def mixed_experts(nc, X, XNT, ident, ones, d):
    E, DFF, TC = 8, 1024, 512
    NM = DFF // P
    NT = TOKENS // TC
    BPC = TC // SEQ
    with ExitStack() as outer:
        def keep(name, shape):
            return outer.enter_context(nc.sbuf_tensor(name, shape, F32))

        GT = keep("me_gateT", [E, P])
        GTOK = keep("me_gate", [P, E])
        with stage(nc) as (sb, ps, sem):
            W1 = sb("mg_w1", [P, KC, DIM])
            B1 = sb("mg_b1", [P, KC])
            W2 = sb("mg_w2", [P, KC, E])
            B2 = sb("mg_b2", [1, E])
            hid = [sb("mg_hidden", [P, TC]) for _ in range(2)]
            part = sb("mg_batch_sums", [P, KC, NT, SEQ])
            HM = sb("mg_hidden_mean", [P, KC, 2, SEQ])
            psH = [ps("mg_psh", [P, 512]) for _ in range(2)]
            psG, psGT = ps("mg_psg", [P, 512]), ps("mg_psgt", [P, 512])
            s_w, s_h, s_r, s_p = sem("weights_loaded"), sem("hidden_projected"), sem("hidden_ready"), sem("batch_sums_ready")
            s_d, s_m, s_g = sem("dve_step"), sem("mean_ready"), sem("gates_projected")
            jobs = [(m, t) for m in range(KC) for t in range(NT)]
            with nc.Block() as block:
                @block.sync
                def _(sp):
                    sp.dma_start(W1[:, :, :], rows_to_sbuf(d["L0_ffn_gW1T"])).then_inc(s_w, 16)
                    sp.dma_start(B1[:, :], d["L0_ffn_gb1_col"]).then_inc(s_w, 16)
                    sp.dma_start(W2[:, :, :], rows_to_sbuf(d["L0_ffn_gW2T"])).then_inc(s_w, 16)
                    sp.dma_start(B2[:, :], row(d["L0_ffn_gb2"])).then_inc(s_w, 16)

                @block.tensor
                def _(pe):
                    pe.wait_ge(s_w, 64)
                    for n, (m, t) in enumerate(jobs):
                        if n >= 2:
                            pe.wait_ge(s_r, n - 1)
                        for c in range(KC):
                            last = nc.tensor.matmul(psH[n % 2][:, :], W1[:, c, m * P:(m + 1) * P],
                                                    XNT[:, c, t * TC:(t + 1) * TC], start=(c == 0), stop=(c == KC - 1))
                        last.then_inc(s_h, 1)
                    pe.wait_ge(s_m, 1)
                    for c in range(KC):
                        nc.tensor.matmul(psG[:, 0:E], HM[:, c, :, :].rearrange("p a s -> p (a s)"), W2[:, c, :],
                                         start=(c == 0), stop=False)
                    nc.tensor.matmul(psG[:, 0:E], ones[0:1, :], B2[:, :], start=False, stop=True)
                    for c in range(KC):
                        nc.tensor.matmul(psGT[0:E, 0:P], W2[:, c, :], HM[:, c, :, :].rearrange("p a s -> p (a s)"),
                                         start=(c == 0), stop=False)
                    nc.tensor.matmul(psGT[0:E, 0:P], B2[:, :], ones[0:1, :], start=False, stop=True).then_inc(s_g, 1)

                @block.scalar
                def _(act):
                    act.wait_ge(s_w, 64)
                    for n, (m, t) in enumerate(jobs):
                        act.wait_ge(s_h, n + 1)
                        if n >= 2:
                            act.wait_ge(s_p, n - 1)
                        nc.scalar.activation(hid[n % 2][:, :], psH[n % 2][:, :], ACT.Relu, bias=B1[:, m:m + 1]).then_inc(s_r, 1)

                @block.vector
                def _(dve):
                    link = Chain(dve, s_d)
                    for n, (m, t) in enumerate(jobs):
                        dve.wait_ge(s_r, n + 1)
                        nc.vector.tensor_reduce(part[:, m, t, :], hid[n % 2][:, :].rearrange("p (b s) -> p s b", s=SEQ), AX_X,
                                                ALU.add).then_inc(s_p, 1)
                    dve.wait_ge(s_p, len(jobs))
                    for m in range(KC):
                        link(nc.vector.tensor_reduce(HM[:, m, 0, :], part[:, m, :, :].rearrange("p t s -> p s t"), AX_X, ALU.add))
                    link(nc.vector.tensor_scalar(HM[:, :, 1, :], HM[:, :, 0, :], 1.0 / BATCH, None, ALU.mult))
                    nc.vector.tensor_copy(HM[:, :, 0, :], HM[:, :, 1, :]).then_inc(s_m, 1)
                    dve.wait_ge(s_g, 1)
                    nc.vector.tensor_copy(GT[:, :], psGT[0:E, 0:P])
                    link(nc.vector.tensor_copy(GTOK[:, :], psG[:, 0:E]))

        for half in range(2):
            mixed_half(nc, X, XNT, ident, d, GT, GTOK, half)


def mixed_half(nc, X, XNT, ident, d, GT, GTOK, half):
    E, DFF, TC = 8, 1024, 512
    NM = DFF // P
    HT = TILES // 2
    NT = HT * P // TC
    T0 = half * HT

    def early(i):
        return isinstance(i, int) and i == 0

    with ExitStack() as outer:
        Y = outer.enter_context(nc.sbuf_tensor(f"me_hidden{half}", [P, HT, DFF], F32))
        with stage(nc) as (sb, ps, sem):
            H = DFF // 512
            NP = HT * H
            W = [sb("m1_w", [P, KC, DFF]) for _ in range(2)]
            WH = [sb("m1_w_high", [P, KC, DFF], R32) for _ in range(2)]
            WL = [sb("m1_w_low", [P, KC, DFF], R32) for _ in range(2)]
            XH, XL = sb("m1_x_high", [P, KC, HT * P], R32), sb("m1_x_low", [P, KC, HT * P], R32)
            B1, B2 = sb("m1_b1", [E, DFF]), sb("m1_b2", [E, DIM])
            R1 = sb("m1_bias_rows", [P, DFF])
            R2 = sb("m2_bias_rows", [P, DIM])
            out = [ps("m1_ps", [P, 512]) for _ in range(4)]
            psB = ps("m1_psb", [P, DFF + 512])
            s_b, s_bm, s_br, s_bx = sem("biases_loaded"), sem("biases_projected"), sem("bias_rows_ready"), sem("bias_added")
            s_w = [sem(f"weights{u}_loaded") for u in range(2)]
            s_wh, s_wl, s_xh, s_xl = sem("w_high_ready"), sem("w_low_ready"), sem("x_high_ready"), sem("x_low_ready")
            s_mm, s_y = sem("multiplied"), sem("expert_added")

            def load_view(i, u):
                return d["L0_ffn_eW1T"].rearrange("(i u) (c p) n -> i u p c n", u=2, p=P)[i, u]

            with nc.Block() as block:
                @block.sync
                def _(sp):
                    def load(i, u):
                        if not early(i):
                            sp.wait_ge(s_wl, i * 2 + (u - 1))
                        sp.dma_start(W[u][:, :, :], load_view(i, u)).then_inc(s_w[u], 16)

                    load(0, 0)
                    sp.dma_start(B1[:, :], d["L0_ffn_eb1"]).then_inc(s_b, 16)
                    sp.dma_start(B2[:, :], d["L0_ffn_eb2"]).then_inc(s_b, 16)
                    load(0, 1)
                    with sp.Fori(1, E // 2) as i:
                        for u in range(2):
                            load(i, u)

                @block.scalar
                def _(act):
                    def high(i, u):
                        act.wait_ge(s_w[u], i * 16 + 16)
                        if not early(i):
                            act.wait_ge(s_mm, (i * 2 + u) * NP - NP)
                        for c in range(KC):
                            last = nc.scalar.copy(WH[u][:, c, :], W[u][:, c, :])
                        last.then_inc(s_wh, 1)

                    for t in range(NT):
                        nc.scalar.copy(XH[:, :, t * TC:(t + 1) * TC], XNT[:, :, T0 * P + t * TC:T0 * P + (t + 1) * TC]).then_inc(s_xh, 1)
                        if t == 0:
                            high(0, 0)
                    high(0, 1)
                    with act.Fori(1, E // 2) as i:
                        for u in range(2):
                            high(i, u)

                @block.tensor
                def _(pe):
                    pe.wait_ge(s_b, 32)
                    for h in range(H):
                        nc.tensor.matmul(psB[:, h * 512:(h + 1) * 512], GT[:, :], B1[:, h * 512:(h + 1) * 512], start=True, stop=True)
                    nc.tensor.matmul(psB[:, DFF:DFF + DIM], GT[:, :], B2[:, :], start=True, stop=True).then_inc(s_bm, 1)
                    pe.sem_inc(s_y, 4)
                    with pe.Fori(0, E // 2) as i:
                        for u in range(2):
                            e = i * 2 + u
                            pe.wait_ge(s_wl, e + 1)
                            for k in range(NP):
                                t, h = k // H, k % H
                                if k % (4 * H) == 0:
                                    pe.wait_ge(s_xl, t // 4 + 1)
                                pe.wait_ge(s_y, e * NP + (k + 1))
                                r, n = slice(t * P, (t + 1) * P), slice(h * 512, (h + 1) * 512)
                                for c in range(KC):
                                    last = three_passes(nc, out[k % 4][:, :], (XH[:, c, r], XL[:, c, r]),
                                                        (WH[u][:, c, n], WL[u][:, c, n]), c == 0, c == KC - 1)
                                last.then_inc(s_mm, 1)

                @block.vector
                def _(dve):
                    def low(i, u):
                        dve.wait_ge(s_wh, i * 2 + (u + 1))
                        nc.vector.tensor_tensor(WL[u][:, :, :], W[u][:, :, :], WH[u][:, :, :].bitcast(F32), ALU.subtract).then_inc(s_wl, 1)

                    def add(i, u):
                        e = i * 2 + u
                        for k in range(NP):
                            t, n = k // H, slice(k % H * 512, (k % H + 1) * 512)
                            dve.wait_ge(s_mm, e * NP + (k + 1))
                            before = R1[:, n] if early(i) and u == 0 else Y[:, t, n]
                            nc.vector.scalar_tensor_tensor(Y[:, t, n], out[k % 4][:, :], GTOK[:, bass.ds(e, 1)], before,
                                                           ALU.mult, ALU.add).then_inc(s_y, 1)

                    for t in range(NT):
                        dve.wait_ge(s_xh, t + 1)
                        r = slice(t * TC, (t + 1) * TC)
                        nc.vector.tensor_tensor(XL[:, :, r], XNT[:, :, T0 * P + t * TC:T0 * P + (t + 1) * TC], XH[:, :, r].bitcast(F32), ALU.subtract).then_inc(s_xl, 1)
                        if t == 0:
                            low(0, 0)
                            dve.wait_ge(s_bm, 1)
                            nc.vector.tensor_copy(R1[:, :], psB[:, 0:DFF])
                            nc.vector.tensor_copy(R2[:, :], psB[:, DFF:DFF + DIM]).then_inc(s_br, 1)
                    low(0, 1)
                    dve.wait_ge(s_br, 1)
                    add(0, 0)
                    low(1, 0)
                    add(0, 1)
                    low(1, 1)
                    with dve.Fori(1, E // 2 - 1) as i:
                        for u in range(2):
                            add(i, u)
                            low(i + 1, u)
                    for u in range(2):
                        add(E // 2 - 1, u)
                    nc.vector.tensor_tensor(X[:, T0:T0 + HT, :], X[:, T0:T0 + HT, :], R2[:, :].unsqueeze(1).broadcast_to([P, HT, DIM]),
                                            ALU.add).then_inc(s_bx, 1)
                    dve.wait_ge(s_bx, 1)

        with stage(nc) as (sb, ps, sem):
            NJ = E // 2
            raw = sb("m2_w", [P, NM, 2, DIM])
            YH, YL = sb("m2_hidden_high", [P, HT, NM, P], R32), sb("m2_hidden_low", [P, HT, NM, P], R32)
            WH, WL = sb("m2_w_high", [P, NM, 2, DIM], R32), sb("m2_w_low", [P, NM, 2, DIM], R32)
            flip = [ps("m2_flip", [P, NM, P]) for _ in range(2)]
            out = [ps("m2_ps", [P, 2, DIM]) for _ in range(4)]
            s_w = [sem(f"chunk{m}_loaded") for m in range(NM)]
            s_wh, s_wl, s_wu = sem("w_high_ready"), sem("w_low_ready"), sem("chunk_used")
            s_f, s_yh, s_yl = sem("hidden_flipped"), sem("hidden_high_ready"), sem("hidden_low_ready")
            s_mm, s_h, s_x = sem("multiplied"), sem("first_expert_added"), sem("second_expert_added")

            with nc.Block() as block:
                @block.sync
                def _(sp):
                    def load(j):
                        for m in range(NM):
                            if not early(j):
                                sp.wait_ge(s_wl, j * NM + (m + 1 - NM))
                            sp.dma_start(raw[:, m, :, :], d["L0_ffn_eW2T"].rearrange("(j h) (m p) n -> j m p h n", h=2, p=P)[j, m]).then_inc(s_w[m], 16)

                    load(0)
                    with sp.Fori(1, NJ) as j:
                        load(j)

                @block.scalar
                def _(act):
                    def high(j):
                        for m in range(NM):
                            act.wait_ge(s_w[m], j * 16 + 16)
                            if not early(j) and m < NM - 1:
                                act.wait_ge(s_wu, j * (NM - 1) + (m + 2 - NM))
                            elif not early(j):
                                act.wait_ge(s_mm, j * HT)
                            nc.scalar.copy(WH[:, m, :, :], raw[:, m, :, :]).then_inc(s_wh, 1)

                    for t in range(HT):
                        act.wait_ge(s_f, t + 1)
                        nc.scalar.activation(YH[:, t, :, :], flip[t % 2][:, :, :], ACT.Relu).then_inc(s_yh, 1)
                        if t == 1:
                            high(0)
                    with act.Fori(1, NJ) as j:
                        high(j)

                @block.tensor
                def _(pe):
                    for t in range(HT):
                        if t >= 2:
                            pe.wait_ge(s_yl, t - 1)
                        for m in range(NM):
                            last = nc.tensor.transpose(flip[t % 2][:, m, :], Y[:, t, m * P:(m + 1) * P], ident[:, :])
                        last.then_inc(s_f, 1)
                    pe.sem_inc(s_x, 4)
                    with pe.Fori(0, NJ) as j:
                        for t in range(HT):
                            pe.wait_ge(s_yl, t + 1)
                            pe.wait_ge(s_x, j * HT + (t + 1))
                            for m in range(NM):
                                if t == 0:
                                    pe.wait_ge(s_wl, j * NM + (m + 1))
                                last = three_passes(nc, out[t % 4][:, :, :].rearrange("p a b -> p (a b)"), (YH[:, t, m, :], YL[:, t, m, :]),
                                                    (WH[:, m, :, :].rearrange("p a b -> p (a b)"),
                                                     WL[:, m, :, :].rearrange("p a b -> p (a b)")), m == 0, m == NM - 1)
                                if t == HT - 1 and m < NM - 1:
                                    last.then_inc(s_wu, 1)
                            last.then_inc(s_mm, 1)

                @block.vector
                def _(dve):
                    def low(j):
                        for m in range(NM):
                            dve.wait_ge(s_wh, j * NM + (m + 1))
                            nc.vector.tensor_tensor(WL[:, m, :, :], raw[:, m, :, :], WH[:, m, :, :].bitcast(F32), ALU.subtract).then_inc(s_wl, 1)

                    def add(j, t):
                        dve.wait_ge(s_mm, j * HT + (t + 1))
                        nc.vector.scalar_tensor_tensor(X[:, T0 + t, :], out[t % 4][:, 0, :], GTOK[:, bass.ds(j * 2, 1)], X[:, T0 + t, :],
                                                       ALU.mult, ALU.add).then_inc(s_h, 1)
                        dve.wait_ge(s_h, j * HT + (t + 1))
                        nc.vector.scalar_tensor_tensor(X[:, T0 + t, :], out[t % 4][:, 1, :], GTOK[:, bass.ds(j * 2 + 1, 1)],
                                                       X[:, T0 + t, :], ALU.mult, ALU.add).then_inc(s_x, 1)

                    for t in range(HT):
                        dve.wait_ge(s_yh, t + 1)
                        nc.vector.scalar_tensor_tensor(YL[:, t, :, :], flip[t % 2][:, :, :], 0.0, YH[:, t, :, :].bitcast(F32),
                                                       ALU.max, ALU.subtract).then_inc(s_yl, 1)
                        if t == 1:
                            low(0)
                    with dve.Fori(0, NJ - 1) as j:
                        for t in range(HT - 1):
                            add(j, t)
                        low(j + 1)
                        add(j, HT - 1)
                    for t in range(HT):
                        add(NJ - 1, t)


def normed_context(nc, ctx, ctxnT, ident, weight, bias):
    W = 8
    GROUPS = BATCH * NKEY // (W * P)
    BPG = W * P // NKEY
    NV = 5
    src = ctx.rearrange("(i u b) (t p) d -> i u p (b t) d", u=2, b=BPG, p=P)
    dst = ctxnT.rearrange("(i u b) (c p) s -> i u c p b s", u=2, b=BPG, p=P)
    with stage(nc) as (sb, ps, sem):
        CX = [sb("nx_rows", [P, W, DIM]) for _ in range(2)]
        XN = [sb("nx_normed", [P, W, DIM]) for _ in range(2)]
        XT = [sb("nx_normedT", [P, KC, W * P]) for _ in range(2)]
        stats = sb("nx_stats", [P, W, 6])
        diff, mean, var = sb("nx_diff", [P, W]), sb("nx_mean", [P, W]), sb("nx_var", [P, W])
        std, rstd, shift = sb("nx_std", [P, W]), sb("nx_rstd", [P, W]), sb("nx_shift", [P, W])
        col = sb("nx_columns", [P, 2, KC])
        flip = [ps("nx_flip", [P, KC, P]) for _ in range(4)]
        s_in = [sem(f"rows{u}_loaded") for u in range(2)]
        s_st = [sem(f"result{u}_stored") for u in range(2)]
        s_w, s_stat, s_d, s_var, s_std, s_sc = (sem("columns_loaded"), sem("statistics_ready"), sem("dve_step"),
                                                sem("variances_ready"), sem("roots_ready"), sem("scales_ready"))
        s_nv, s_na, s_f, s_t = sem("normed_by_vector"), sem("normed_by_scalar"), sem("rows_flipped"), sem("transposed_ready")
        LINKS = 9

        def early(i):
            return isinstance(i, int) and i == 0

        with nc.Block() as block:
            @block.sync
            def _(sp):
                def load(i, u):
                    if not early(i):
                        sp.wait_ge(s_nv, (i * 2 + u) * NV - NV)
                        sp.wait_ge(s_na, (i * 2 + u) * (W - NV) - (W - NV))
                    sp.dma_start(CX[u][:, :, :], src[i, u]).then_inc(s_in[u], 16)

                def store(i, u):
                    sp.wait_ge(s_t, (i * 2 + u) * W + W)
                    for c in range(KC):
                        sp.dma_start(dst[i, u, c], XT[u][:, c, :].rearrange("p (b s) -> p b s", s=NKEY)).then_inc(s_st[u], 16)

                load(0, 0)
                sp.dma_start(col[:, 0, :], weight).then_inc(s_w, 16)
                sp.dma_start(col[:, 1, :], bias).then_inc(s_w, 16)
                load(0, 1)
                with sp.Fori(1, GROUPS // 2) as i:
                    for u in range(2):
                        load(i, u)
                        store(i - 1, u)
                for u in range(2):
                    store(GROUPS // 2 - 1, u)
                for u in range(2):
                    sp.wait_ge(s_st[u], 16 * KC * (GROUPS // 2))

            @block.vector
            def _(dve):
                def group(i, u):
                    g = i * 2 + u
                    link = Chain(dve, s_d, g * LINKS)
                    dve.wait_ge(s_in[u], i * 16 + 16)
                    for t in range(W):
                        nc.vector.bn_stats(stats[:, t, :], CX[u][:, t, :]).then_inc(s_stat, 1)
                    dve.wait_ge(s_stat, g * W + W)
                    link(nc.vector.tensor_tensor(mean[:, :], stats[:, :, 1], stats[:, :, 4], ALU.add))
                    link(nc.vector.tensor_scalar(mean[:, :], mean[:, :], 0.5, None, ALU.mult))
                    link(nc.vector.tensor_tensor(diff[:, :], stats[:, :, 1], stats[:, :, 4], ALU.subtract))
                    link(nc.vector.tensor_tensor(diff[:, :], diff[:, :], diff[:, :], ALU.mult))
                    link(nc.vector.tensor_scalar(diff[:, :], diff[:, :], DIM / 4.0, None, ALU.mult))
                    link(nc.vector.tensor_tensor(var[:, :], stats[:, :, 2], stats[:, :, 5], ALU.add))
                    link(nc.vector.tensor_tensor(var[:, :], var[:, :], diff[:, :], ALU.add))
                    nc.vector.tensor_scalar(var[:, :], var[:, :], 1.0 / DIM, EPS, ALU.mult, ALU.add).then_inc(s_var, 1)
                    dve.wait_ge(s_std, g + 1)
                    link(nc.vector.reciprocal(rstd[:, :], std[:, :]))
                    link(nc.vector.tensor_tensor(shift[:, :], mean[:, :], rstd[:, :], ALU.mult))
                    nc.vector.tensor_scalar(shift[:, :], shift[:, :], -1.0, None, ALU.mult).then_inc(s_sc, 1)
                    if not early(i):
                        dve.wait_ge(s_f, g * W - W)
                    for t in range(NV):
                        nc.vector.tensor_scalar(XN[u][:, t, :], CX[u][:, t, :], mean[:, t:t + 1], rstd[:, t:t + 1],
                                                ALU.subtract, ALU.mult).then_inc(s_nv, 1)
                    dve.wait_ge(s_na, g * (W - NV) + (W - NV))

                for u in range(2):
                    group(0, u)
                with dve.Fori(1, GROUPS // 2) as i:
                    for u in range(2):
                        group(i, u)

            @block.tensor
            def _(pe):
                def group(i, u):
                    g = i * 2 + u
                    for t in range(W):
                        if t < NV:
                            pe.wait_ge(s_nv, g * NV + (t + 1))
                        else:
                            pe.wait_ge(s_na, g * (W - NV) + (t - NV + 1))
                        if not (early(i) and u * W + t < 4):
                            pe.wait_ge(s_t, g * W + (t - 3))
                        for c in range(KC):
                            last = nc.tensor.transpose(flip[t % 4][:, c, :], XN[u][:, t, c * P:(c + 1) * P], ident[:, :])
                        last.then_inc(s_f, 1)

                for u in range(2):
                    group(0, u)
                with pe.Fori(1, GROUPS // 2) as i:
                    for u in range(2):
                        group(i, u)

            @block.scalar
            def _(act):
                def normalise(i, u):
                    g = i * 2 + u
                    act.wait_ge(s_var, g + 1)
                    nc.scalar.activation(std[:, :], var[:, :], ACT.Sqrt).then_inc(s_std, 1)
                    act.wait_ge(s_sc, g + 1)
                    if not early(i):
                        act.wait_ge(s_f, g * W - W)
                    for t in range(NV, W):
                        nc.scalar.activation(XN[u][:, t, :], CX[u][:, t, :], ACT.Identity, bias=shift[:, t:t + 1],
                                             scale=rstd[:, t:t + 1]).then_inc(s_na, 1)

                def copy_out(i, u):
                    g = i * 2 + u
                    if not early(i):
                        act.wait_ge(s_st[u], i * 16 * KC)
                    for t in range(W):
                        act.wait_ge(s_f, g * W + (t + 1))
                        for c in range(KC):
                            last = nc.scalar.activation(XT[u][:, c, t * P:(t + 1) * P], flip[t % 4][:, c, :], ACT.Identity,
                                                        bias=col[:, 1, c:c + 1], scale=col[:, 0, c:c + 1])
                        last.then_inc(s_t, 1)

                act.wait_ge(s_w, 32)
                normalise(0, 0)
                normalise(0, 1)
                copy_out(0, 0)
                with act.Fori(1, GROUPS // 2) as i:
                    normalise(i, 0)
                    copy_out(i - 1, 1)
                    normalise(i, 1)
                    copy_out(i, 0)
                copy_out(GROUPS // 2 - 1, 1)


def first_maximum(nc, link, onehot, top, scratch, values, order, shape):
    link(nc.vector.tensor_reduce(top, values, AX_X, ALU.max))
    link(nc.vector.tensor_tensor(onehot, values, top.unsqueeze(2).broadcast_to(shape), ALU.is_equal))
    link(nc.vector.tensor_tensor(onehot, onehot, order.unsqueeze(1).broadcast_to(shape), ALU.mult))
    link(nc.vector.tensor_reduce(scratch, onehot, AX_X, ALU.max))
    link(nc.vector.tensor_tensor(onehot, onehot, scratch.unsqueeze(2).broadcast_to(shape), ALU.is_equal))


def routed_experts(nc, X, XNT, XN, ident, ones, d):
    E, F = 8, 512
    CAP = -(-2 * TOKENS * 5 // (E * 4))
    NF = F // P
    CHOICES = 2 * TILES
    QT = CAP // P
    HALF = CAP // 2
    queues = nc.dram_tensor("expert_queues", (E * CAP + CHOICES * P, DIM), F32, kind="Internal").ap()
    results = nc.dram_tensor("expert_results", (E * CAP + 1, DIM), F32, kind="Internal").ap()
    with ExitStack() as outer:
        G = outer.enter_context(nc.sbuf_tensor("re_gate", [P, CHOICES], F32))
        TO = outer.enter_context(nc.sbuf_tensor("re_scatter_rows", [P, CHOICES], I32))
        FROM = outer.enter_context(nc.sbuf_tensor("re_gather_rows", [P, CHOICES], I32))
        with stage(nc) as (sb, ps, sem):
            WG = sb("rt_w", [P, KC, E])
            OR = sb("rt_order", [P, E])
            BE = sb("rt_before", [P, P])
            BASE = sb("rt_queue_starts", [P, E])
            SPARE = sb("rt_spare_rows", [P, CHOICES])
            Z = sb("rt_zeros", [P, 8, DIM])
            S = [P, TILES, E]
            C = [P, CHOICES, E]
            L, PRB, P2 = sb("rt_logits", S), sb("rt_probs", S), sb("rt_probs_left", S)
            OH = sb("rt_onehot", [P, 2, TILES, E])
            v = sb("rt_top_probs", [P, 2, TILES])
            m, sm, sc = sb("rt_max", [P, TILES]), sb("rt_sum", [P, TILES]), sb("rt_scratch", [P, TILES])
            R = [sb("rt_running", C) for _ in range(2)]
            TOT, PLACE, KM = sb("rt_totals", C), sb("rt_place", C), sb("rt_kept", C)
            kept, lost, where, to, back = (sb("rt_is_kept", [P, CHOICES]), sb("rt_is_lost", [P, CHOICES]),
                                           sb("rt_queue_row", [P, CHOICES]), sb("rt_to", [P, CHOICES]), sb("rt_back", [P, CHOICES]))
            psL, psR, psT = ps("rt_psl", [P, 512]), ps("rt_psr", [P, 512]), ps("rt_pst", [P, 512])
            s_w, s_l, s_mx, s_e, s_d, s_oh, s_c = (sem("weights_loaded"), sem("logits_ready"), sem("logits_shifted"),
                                                   sem("exp_ready"), sem("dve_step"), sem("choices_ready"), sem("counts_ready"))
            s_z, s_q, s_to, s_sc = sem("zeros_set"), sem("queues_zeroed"), sem("rows_ready"), sem("rows_scattered")
            ZR = 8 * P
            with nc.Block() as block:
                @block.sync
                def _(sp):
                    sp.dma_start(WG[:, :, :], rows_to_sbuf(d["L1_ffn_Wg"])).then_inc(s_w, 16)
                    sp.dma_start(OR[:, :], d["expert_order"]).then_inc(s_w, 16)
                    sp.dma_start(BE[:, :], d["before"]).then_inc(s_w, 16)
                    sp.dma_start(BASE[:, :], d["queue_starts"]).then_inc(s_w, 16)
                    sp.dma_start(SPARE[:, :], d["spare_rows"]).then_inc(s_w, 16)
                    sp.wait_ge(s_z, 1)
                    for r in range(0, E * CAP, ZR):
                        sp.dma_start(queues[r:r + ZR].rearrange("(a p) n -> p a n", p=P), Z[:, :, :]).then_inc(s_q, 16)
                    sp.dma_start(results[E * CAP:E * CAP + 1], Z[0:1, 0, :]).then_inc(s_q, 16)
                    sp.wait_ge(s_q, 16 * (E * CAP // ZR + 1))

                @block.gpsimd
                def _(pool):
                    nc.gpsimd.memset(Z[:, :, :], 0.0).then_inc(s_z, 1)
                    pool.wait_ge(s_q, 16 * (E * CAP // ZR + 1))
                    pool.wait_ge(s_to, 1)
                    for n in range(CHOICES):
                        nc.gpsimd.indirect_dma_start(queues, bass.IndirectOffsetOnAxis(TO[:, n:n + 1], 0),
                                                     XN[:, n % TILES, :], None).then_inc(s_sc, 16)
                    pool.wait_ge(s_sc, 16 * CHOICES)

                @block.tensor
                def _(pe):
                    pe.wait_ge(s_w, 80)
                    for t in range(TILES):
                        for c in range(KC):
                            last = nc.tensor.matmul(psL[:, t * E:(t + 1) * E], XNT[:, c, t * P:(t + 1) * P], WG[:, c, :],
                                                    start=(c == 0), stop=(c == KC - 1))
                    last.then_inc(s_l, 1)
                    pe.wait_ge(s_oh, 1)
                    flat = OH[:, :, :, :].rearrange("p k t e -> p (k t e)")
                    nc.tensor.matmul(psR[:, 0:CHOICES * E], BE[:, :], flat, start=True, stop=True)
                    nc.tensor.matmul(psT[:, 0:CHOICES * E], ones[:, :], flat, start=True, stop=True).then_inc(s_c, 1)

                @block.scalar
                def _(act):
                    act.wait_ge(s_mx, 1)
                    nc.scalar.activation(PRB[:, :, :], L[:, :, :], ACT.Exp).then_inc(s_e, 1)

                @block.vector
                def _(dve):
                    link = Chain(dve, s_d)
                    dve.wait_ge(s_w, 80)
                    dve.wait_ge(s_l, 1)
                    PL = psL[:, 0:TILES * E].rearrange("p (t e) -> p t e", e=E)
                    link(nc.vector.tensor_reduce(m[:, :], PL, AX_X, ALU.max))
                    nc.vector.tensor_tensor(L[:, :, :], PL, m[:, :].unsqueeze(2).broadcast_to(S), ALU.subtract).then_inc(s_mx, 1)
                    dve.wait_ge(s_e, 1)
                    link(nc.vector.tensor_reduce(sm[:, :], PRB[:, :, :], AX_X, ALU.add))
                    link(nc.vector.reciprocal(sm[:, :], sm[:, :]))
                    link(nc.vector.tensor_tensor(PRB[:, :, :], PRB[:, :, :], sm[:, :].unsqueeze(2).broadcast_to(S), ALU.mult))
                    first_maximum(nc, link, OH[:, 0, :, :], v[:, 0, :], sc[:, :], PRB[:, :, :], OR[:, :], S)
                    link(nc.vector.scalar_tensor_tensor(P2[:, :, :], OH[:, 0, :, :], -2.0, PRB[:, :, :], ALU.mult, ALU.add))
                    first_maximum(nc, link, OH[:, 1, :, :], v[:, 1, :], sc[:, :], P2[:, :, :], OR[:, :], S)
                    dve.sem_inc(s_oh, 1)
                    dve.wait_ge(s_c, 1)
                    PT = psT[:, 0:CHOICES * E].rearrange("p (t e) -> p t e", e=E)
                    link(nc.vector.tensor_copy(TOT[:, :, :], PT))
                    src, k, step = TOT, 0, 1
                    while step < CHOICES:
                        dst = R[k % 2]
                        nc.vector.tensor_copy(dst[:, 0:step, :], src[:, 0:step, :])
                        link(nc.vector.tensor_tensor(dst[:, step:CHOICES, :], src[:, step:CHOICES, :],
                                                     src[:, 0:CHOICES - step, :], ALU.add))
                        src, k, step = dst, k + 1, step * 2
                    dst = R[k % 2]
                    link(nc.vector.tensor_tensor(dst[:, :, :], src[:, :, :], TOT[:, :, :], ALU.subtract))
                    PR_ = psR[:, 0:CHOICES * E].rearrange("p (t e) -> p t e", e=E)
                    link(nc.vector.tensor_tensor(PLACE[:, :, :], PR_, dst[:, :, :], ALU.add))
                    link(nc.vector.tensor_scalar(KM[:, :, :], PLACE[:, :, :], float(CAP), None, ALU.is_lt))
                    nc.vector.tensor_tensor(PLACE[:, :, :], PLACE[:, :, :], BASE[:, :].unsqueeze(1).broadcast_to(C), ALU.add)
                    link(nc.vector.tensor_tensor(KM[:, :, :], KM[:, :, :], OH[:, :, :, :].rearrange("p k t e -> p (k t) e"), ALU.mult))
                    nc.vector.tensor_reduce(kept[:, :], KM[:, :, :], AX_X, ALU.add)
                    link(nc.vector.tensor_tensor(PLACE[:, :, :], PLACE[:, :, :], KM[:, :, :], ALU.mult))
                    nc.vector.tensor_scalar(lost[:, :], kept[:, :], -1.0, 1.0, ALU.mult, ALU.add)
                    link(nc.vector.tensor_reduce(where[:, :], PLACE[:, :, :], AX_X, ALU.add))
                    nc.vector.tensor_tensor(to[:, :], lost[:, :], SPARE[:, :], ALU.mult)
                    link(nc.vector.tensor_scalar(back[:, :], lost[:, :], float(E * CAP), None, ALU.mult))
                    nc.vector.tensor_tensor(to[:, :], to[:, :], where[:, :], ALU.add)
                    link(nc.vector.tensor_tensor(back[:, :], back[:, :], where[:, :], ALU.add))
                    nc.vector.tensor_copy(TO[:, :], to[:, :]).then_inc(s_to, 1)
                    nc.vector.tensor_copy(FROM[:, :], back[:, :])
                    GK = G[:, :].rearrange("p (k t) -> p k t", k=2)
                    link(nc.vector.tensor_tensor(GK, v[:, :, :], kept[:, :].rearrange("p (k t) -> p k t", k=2), ALU.mult))
                    link(nc.vector.tensor_tensor(sm[:, :], GK[:, 0, :], GK[:, 1, :], ALU.add))
                    link(nc.vector.tensor_scalar(sm[:, :], sm[:, :], 1e-9, None, ALU.max))
                    link(nc.vector.reciprocal(sm[:, :], sm[:, :]))
                    link(nc.vector.tensor_tensor(GK, GK, sm[:, :].unsqueeze(1).broadcast_to([P, 2, TILES]), ALU.mult))

        with stage(nc) as (sb, ps, sem):
            WI, WO = sb("re_win", [P, KC, 2 * F]), sb("re_wout", [P, NF, DIM])
            WIS = [[sb("re_win_part", [P, KC, 2 * F], R32) for _ in range(2)] for _ in range(2)]
            WOS = [[sb("re_wout_part", [P, NF, DIM], R32) for _ in range(2)] for _ in range(2)]
            XR = [sb("re_rows", [P, QT, DIM]) for _ in range(2)]
            XT = [[sb("re_rowsT_part", [P, KC, CAP], R32) for _ in range(2)] for _ in range(2)]
            GE = [sb("re_gelu", [P, HALF]) for _ in range(2)]
            HF = [sb("re_hidden", [P, HALF]) for _ in range(2)]
            HT = [[sb("re_hidden_part", [P, NF, CAP], R32) for _ in range(2)] for _ in range(2)]
            YR = [sb("re_result", [P, QT, DIM]) for _ in range(2)]
            psF = [ps("re_flip", [P, KC, P]) for _ in range(2)]
            psA = [ps("re_psa", [P, 512]) for _ in range(2)]
            psG = [ps("re_psg", [P, 512]) for _ in range(2)]
            psD = [ps("re_psd", [P, 512]) for _ in range(2)]
            s_r = [sem(f"rows{u}_loaded") for u in range(2)]
            s_wi, s_wo = sem("win_loaded"), sem("wout_loaded")
            s_ih, s_il, s_oh, s_ol = sem("win_high_ready"), sem("win_low_ready"), sem("wout_high_ready"), sem("wout_low_ready")
            s_xh, s_hf, s_hh = sem("rowsT_high_ready"), sem("hidden_product_ready"), sem("hidden_high_ready")
            s_st = [sem(f"result{u}_stored") for u in range(2)]
            s_fl, s_xt, s_up, s_ge = sem("rows_flipped"), sem("rowsT_ready"), sem("up_projected"), sem("gelu_ready")
            s_h, s_dn, s_yr = sem("hidden_ready"), sem("down_projected"), sem("result_ready")
            NU = 2 * NF

            def expert(view, i, u):
                return view.rearrange("(i u) k n -> i u k n", u=2)[i, u]

            def queue(view, i, u):
                return view[0:E * CAP].rearrange("(i u a p) n -> i u p a n", u=2, a=QT, p=P)[i, u]

            def number(i, u):
                return i * 2 + u

            def early(i):
                return isinstance(i, int) and i == 0

            def after(i, u):
                return (i, 1) if u == 0 else (i + 1, 0)

            def weights(i, u, k, split_in, split_out):
                if k in (2, 4) and not (isinstance(i, int) and i == E // 2 - 1 and u == 1):
                    split_in(*after(i, u), k // 2 - 1)
                if k == 6:
                    split_out(i, u)

            def in_order(up, exchange, eng):
                def pair(i):
                    up(i, 1)
                    exchange((i + 1, 0), (i, 0))
                    up(i + 1, 0)
                    exchange((i + 1, 1), (i, 1))

                LAST = E // 2 - 1
                exchange((0, 0), None)
                up(0, 0)
                exchange((0, 1), None)
                pair(0)
                with eng.Fori(1, LAST) as i:
                    pair(i)
                up(LAST, 1)
                exchange(None, (LAST, 0))
                exchange(None, (LAST, 1))

            with nc.Block() as block:
                @block.sync
                def _(sp):
                    def load(i, u):
                        e = number(i, u)
                        if not early(i):
                            sp.wait_ge(s_fl, e * QT - QT)
                        sp.dma_start(XR[u][:, :, :], queue(queues, i, u)).then_inc(s_r[u], 16)
                        if not (early(i) and u == 0):
                            sp.wait_ge(s_il, e * KC)
                        sp.dma_start(WI[:, :, :], rows_to_sbuf(expert(d["L1_ffn_W_in"], i, u))).then_inc(s_wi, 16)
                        if not (early(i) and u == 0):
                            sp.wait_ge(s_ol, e)
                        sp.dma_start(WO[:, :, :], rows_to_sbuf(expert(d["L1_ffn_W_out"], i, u))).then_inc(s_wo, 16)

                    load(0, 0)
                    load(0, 1)
                    with sp.Fori(1, E // 2) as i:
                        for u in range(2):
                            load(i, u)

                @block.gpsimd
                def _(pool):
                    with pool.Fori(0, E // 2) as i:
                        for u in range(2):
                            pool.wait_ge(s_yr, number(i, u) * QT + QT)
                            pool.dma_start(queue(results, i, u), YR[u][:, :, :]).then_inc(s_st[u], 16)
                    for u in range(2):
                        pool.wait_ge(s_st[u], 16 * (E // 2))

                @block.tensor
                def _(pe):
                    def flip(i, u, j):
                        e = number(i, u)
                        if j == 0:
                            pe.wait_ge(s_r[u], i * 16 + 16)
                        if not (early(i) and u * QT + j < 2):
                            pe.wait_ge(s_xt, e * QT + (j - 1))
                        for c in range(KC):
                            last = nc.tensor.transpose(psF[(u * QT + j) % 2][:, c, :], XR[u][:, j, c * P:(c + 1) * P], ident[:, :])
                        last.then_inc(s_fl, 1)

                    def up(i, u):
                        e = number(i, u)
                        pe.wait_ge(s_il, e * KC + KC)
                        pe.wait_ge(s_xt, e * QT + QT)
                        for k in range(NU):
                            f, h = k // 2, k % 2
                            if not (early(i) and u == 0 and k < 2):
                                pe.wait_ge(s_hf, e * NU + (k - 1))
                            for dst, off in ((psA, 0), (psG, F)):
                                for c in range(KC):
                                    cols, rows = slice(off + f * P, off + (f + 1) * P), slice(h * HALF, (h + 1) * HALF)
                                    last = three_passes(nc, dst[k % 2][:, 0:HALF], [w[:, c, cols] for w in WIS[u]],
                                                        [x[:, c, rows] for x in XT[u]], c == 0, c == KC - 1)
                            last.then_inc(s_up, 1)

                    def down(i, u, j):
                        e = number(i, u)
                        if j == 0:
                            pe.wait_ge(s_ol, e + 1)
                            pe.wait_ge(s_h, e * NU + NU)
                        if not (early(i) and u * QT + j < 2):
                            pe.wait_ge(s_yr, e * QT + (j - 1))
                        for f in range(NF):
                            last = three_passes(nc, psD[(u * QT + j) % 2][:, 0:DIM], [h[:, f, j * P:(j + 1) * P] for h in HT[u]],
                                                [w[:, f, :] for w in WOS[u]], f == 0, f == NF - 1)
                        last.then_inc(s_dn, 1)

                    def exchange(rows, done):
                        for j in range(QT):
                            if rows:
                                flip(*rows, j)
                            if done:
                                down(*done, j)

                    in_order(up, exchange, pe)

                @block.scalar
                def _(act):
                    def exchange(rows, done):
                        if rows is None:
                            return
                        i, u = rows
                        e = number(i, u)
                        if not early(i):
                            act.wait_ge(s_up, e * NU - NU)
                        for j in range(QT):
                            act.wait_ge(s_fl, e * QT + (j + 1))
                            nc.scalar.copy(XT[u][0][:, :, j * P:(j + 1) * P], psF[(u * QT + j) % 2][:, :, :]).then_inc(s_xh, 1)

                    def gelu(i, u):
                        e = number(i, u)
                        for k in range(NU):
                            act.wait_ge(s_up, e * NU + (k + 1))
                            if not (early(i) and u == 0 and k < 2):
                                act.wait_ge(s_hf, e * NU + (k - 1))
                            nc.scalar.activation(GE[k % 2][:, :], psA[k % 2][:, 0:HALF], ACT.Gelu).then_inc(s_ge, 1)
                            if k:
                                high_hidden(e, u, k - 1)
                            weights(i, u, k, high_in, high_out)
                        high_hidden(e, u, NU - 1)

                    def high_hidden(e, u, k):
                        f, h = k // 2, k % 2
                        act.wait_ge(s_hf, e * NU + (k + 1))
                        nc.scalar.copy(HT[u][0][:, f, h * HALF:(h + 1) * HALF], HF[k % 2][:, :]).then_inc(s_hh, 1)

                    def high_in(i, u, c):
                        e = number(i, u)
                        act.wait_ge(s_wi, e * 16 + 16)
                        if not early(i):
                            act.wait_ge(s_up, e * NU - NU)
                        nc.scalar.copy(WIS[u][0][:, c, :], WI[:, c, :]).then_inc(s_ih, 1)

                    def high_out(i, u):
                        e = number(i, u)
                        act.wait_ge(s_wo, e * 16 + 16)
                        if not early(i):
                            act.wait_ge(s_dn, e * QT - QT)
                        nc.scalar.copy(WOS[u][0][:, :, :], WO[:, :, :]).then_inc(s_oh, 1)

                    for c in range(KC):
                        high_in(0, 0, c)
                    in_order(gelu, exchange, act)

                @block.vector
                def _(dve):
                    def hidden(i, u):
                        e = number(i, u)
                        if not early(i):
                            dve.wait_ge(s_dn, e * QT - QT)
                        for k in range(NU):
                            dve.wait_ge(s_ge, e * NU + (k + 1))
                            if not (early(i) and u == 0 and k < 2):
                                dve.wait_ge(s_h, e * NU + (k - 1))
                            nc.vector.tensor_tensor(HF[k % 2][:, :], psG[k % 2][:, 0:HALF], GE[k % 2][:, :], ALU.mult).then_inc(s_hf, 1)
                            if k:
                                low_hidden(e, u, k - 1)
                            weights(i, u, k, low_in, low_out)
                        low_hidden(e, u, NU - 1)

                    def low_hidden(e, u, k):
                        f, h = k // 2, k % 2
                        dve.wait_ge(s_hh, e * NU + (k + 1))
                        cols = slice(h * HALF, (h + 1) * HALF)
                        nc.vector.tensor_tensor(HT[u][1][:, f, cols], HF[k % 2][:, :], HT[u][0][:, f, cols].bitcast(F32),
                                                ALU.subtract).then_inc(s_h, 1)

                    def exchange(rows, done):
                        for j in range(QT):
                            if rows:
                                low_rows(*rows, j)
                            if done:
                                result(*done, j)

                    def result(i, u, j):
                        e = number(i, u)
                        if j == 0 and not early(i):
                            dve.wait_ge(s_st[u], i * 16)
                        dve.wait_ge(s_dn, e * QT + (j + 1))
                        nc.vector.tensor_copy(YR[u][:, j, :], psD[(u * QT + j) % 2][:, 0:DIM]).then_inc(s_yr, 1)

                    def low_rows(i, u, j):
                        dve.wait_ge(s_xh, number(i, u) * QT + (j + 1))
                        cols = slice(j * P, (j + 1) * P)
                        nc.vector.tensor_tensor(XT[u][1][:, :, cols], psF[(u * QT + j) % 2][:, :, :],
                                                XT[u][0][:, :, cols].bitcast(F32), ALU.subtract).then_inc(s_xt, 1)

                    def low_in(i, u, c):
                        dve.wait_ge(s_ih, number(i, u) * KC + (c + 1))
                        nc.vector.tensor_tensor(WIS[u][1][:, c, :], WI[:, c, :], WIS[u][0][:, c, :].bitcast(F32), ALU.subtract).then_inc(s_il, 1)

                    def low_out(i, u):
                        dve.wait_ge(s_oh, number(i, u) + 1)
                        nc.vector.tensor_tensor(WOS[u][1][:, :, :], WO[:, :, :], WOS[u][0][:, :, :].bitcast(F32), ALU.subtract).then_inc(s_ol, 1)

                    for c in range(KC):
                        low_in(0, 0, c)
                    in_order(hidden, exchange, dve)

        with stage(nc) as (sb, ps, sem):
            YG = sb("re_gathered", [P, CHOICES, DIM])
            GROUPS = 4
            s_g, s_x = [sem(f"rows{g}_gathered") for g in range(GROUPS)], sem("x_updated")
            with nc.Block() as block:
                @block.gpsimd
                def _(pool):
                    for n in range(CHOICES):
                        k, t = n % 2, n // 2
                        nc.gpsimd.indirect_dma_start(YG[:, k * TILES + t, :], None, results,
                                                     bass.IndirectOffsetOnAxis(FROM[:, k * TILES + t:k * TILES + t + 1], 0)).then_inc(s_g[t * GROUPS // TILES], 16)

                @block.vector
                def _(dve):
                    for g in range(GROUPS):
                        dve.wait_ge(s_g[g], 16 * CHOICES // GROUPS)
                        for k in range(2):
                            for w in range(TILES // GROUPS):
                                t = g * (TILES // GROUPS) + w
                                if k:
                                    dve.wait_ge(s_x, g * (CHOICES // GROUPS) + w + 1)
                                n = k * TILES + t
                                nc.vector.scalar_tensor_tensor(X[:, t, :], YG[:, n, :], G[:, n:n + 1],
                                                               X[:, t, :], ALU.mult, ALU.add).then_inc(s_x, 1)


def values_by_token(nc, XNT, VA, w, width):
    with stage(nc) as (sb, ps, sem):
        W = sb("vt_w", [P, KC, DIM])
        out = [ps("vt_ps", [P, 512]) for _ in range(4)]
        s_w, s_mm, s_st = sem("weights_loaded"), sem("multiplied"), sem("stored")
        with nc.Block() as block:
            @block.sync
            def _(sp):
                sp.dma_start(W[:, :, :], rows_to_sbuf(w)).then_inc(s_w, 16)

            @block.tensor
            def _(pe):
                pe.wait_ge(s_w, 16)
                for t in range(TILES):
                    if t >= 4:
                        pe.wait_ge(s_st, t - 3)
                    for c in range(KC):
                        last = nc.tensor.matmul(out[t % 4][:, 0:DIM], XNT[:, c, t * P:(t + 1) * P], W[:, c, :],
                                                start=(c == 0), stop=(c == KC - 1))
                    last.then_inc(s_mm, 1)

            @block.vector
            def _(dve):
                with dve.Fori(0, TILES // 4) as i:
                    for u in range(4):
                        dve.wait_ge(s_mm, i * 4 + (u + 1))
                        nc.vector.tensor_copy(VA[:, i * 4 + u, :, 0:32],
                                              out[u][:, 0:DIM].rearrange("p (a w) -> p a w", a=8)).then_inc(s_st, 1)


def normed_heads(nc, XNT, QKT, VA, ident, d):
    with stage(nc) as (sb, ps, sem):
        W = sb("nh_w", [P, KC, 3 * DIM])
        B = sb("nh_bias_rows", [P, 3 * DIM])
        WQK = sb("nh_rms_weights", [P, 2])
        RAW = sb("nh_qk", [P, TILES, 2 * DIM])
        sq = [sb("nh_squares", [P, 2 * DIM]) for _ in range(2)]
        R = sb("nh_rms", [P, TILES, 32])
        psQ = [ps("nh_psq", [P, 512]) for _ in range(2)]
        psV = [ps("nh_psv", [P, 512]) for _ in range(2)]
        psF = [ps("nh_psf", [P, 4, P]) for _ in range(2)]
        s_w, s_one, s_p, s_b, s_v, s_sq, s_r = (sem("weights_loaded"), sem("ones_set"), sem("projected"), sem("qk_ready"),
                                                sem("values_ready"), sem("squares_ready"), sem("squares_summed"))
        s_d, s_rt, s_rt2, s_n, s_f, s_out = (sem("dve_step"), sem("mean_squares_ready"), sem("roots_ready"), sem("normed"),
                                             sem("flipped"), sem("stored"))
        with nc.Block() as block:
            @block.sync
            def _(sp):
                sp.dma_start(W[:, :, :], rows_to_sbuf(d["L2_attn_WqkvT"])).then_inc(s_w, 16)
                sp.dma_start(B[:, :], d["L2_attn_bqkv"].partition_broadcast(P)).then_inc(s_w, 16)
                sp.dma_start(WQK[:, :], d["L2_attn_wqk_col"]).then_inc(s_w, 16)

            @block.gpsimd
            def _(pool):
                nc.gpsimd.memset(VA[:, :, :, 32:33], 1.0).then_inc(s_one, 1)
                pool.wait_ge(s_one, 1)

            @block.tensor
            def _(pe):
                pe.wait_ge(s_w, 48)
                for t in range(TILES):
                    if t >= 2:
                        pe.wait_ge(s_v, t - 1)
                    for dst, lo, hi in ((psQ[t % 2][:, :], 0, 2 * DIM), (psV[t % 2][:, 0:DIM], 2 * DIM, 3 * DIM)):
                        for c in range(KC):
                            last = nc.tensor.matmul(dst, XNT[:, c, t * P:(t + 1) * P], W[:, c, lo:hi], start=(c == 0),
                                                    stop=(c == KC - 1))
                    last.then_inc(s_p, 1)
                for t in range(TILES):
                    pe.wait_ge(s_n, t + 1)
                    if t >= 2:
                        pe.wait_ge(s_out, t - 1)
                    for m in range(4):
                        last = nc.tensor.transpose(psF[t % 2][:, m, :], RAW[:, t, m * P:(m + 1) * P], ident[:, :])
                    last.then_inc(s_f, 1)

            @block.scalar
            def _(act):
                act.wait_ge(s_w, 48)
                act.sem_inc(s_r, 2)
                with act.Fori(0, TILES // 2) as i:
                    for u in range(2):
                        act.wait_ge(s_b, i * 2 + (u + 1))
                        act.wait_ge(s_r, i * 2 + (u + 1))
                        nc.scalar.activation(sq[u][:, :], RAW[:, i * 2 + u, :], ACT.Square).then_inc(s_sq, 1)
                act.wait_ge(s_rt, 1)
                nc.scalar.activation(R[:, :, :], R[:, :, :], ACT.Sqrt).then_inc(s_rt2, 1)
                with act.Fori(0, TILES // 2) as i:
                    for u in range(2):
                        act.wait_ge(s_f, i * 2 + (u + 1))
                        for m in range(2):
                            last = nc.scalar.activation(QKT[:, 2 * m:2 * m + 2, bass.ds(i * 2 * P + u * P, P)],
                                                        psF[u][:, 2 * m:2 * m + 2, :], ACT.Copy, scale=WQK[:, m:m + 1])
                        last.then_inc(s_out, 1)

            @block.vector
            def _(dve):
                link = Chain(dve, s_d)
                dve.wait_ge(s_w, 48)

                def sum_squares(i, u):
                    dve.wait_ge(s_sq, i * 2 + (u + 1))
                    nc.vector.tensor_reduce(R[:, i * 2 + u, :], sq[u][:, :].rearrange("p (h d) -> p h d", d=16), AX_X,
                                            ALU.add).then_inc(s_r, 1)

                with dve.Fori(0, TILES // 2) as i:
                    for u in range(2):
                        dve.wait_ge(s_p, i * 2 + (u + 1))
                        nc.vector.tensor_tensor(RAW[:, i * 2 + u, :], psQ[u][:, :], B[:, 0:2 * DIM], ALU.add).then_inc(s_b, 1)
                        nc.vector.tensor_tensor(VA[:, i * 2 + u, :, 0:32], psV[u][:, 0:DIM].rearrange("p (a w) -> p a w", a=8),
                                                B[:, 2 * DIM:3 * DIM].rearrange("p (a w) -> p a w", a=8), ALU.add).then_inc(s_v, 1)
                        if u:
                            sum_squares(i, 0)
                    sum_squares(i, 1)
                dve.wait_ge(s_r, TILES + 2)
                link(nc.vector.tensor_scalar(R[:, :, :], R[:, :, :], 1.0 / 16, 1e-6, ALU.mult, ALU.add))
                dve.sem_inc(s_rt, 1)
                dve.wait_ge(s_rt2, 1)
                link(nc.vector.reciprocal(R[:, :, :], R[:, :, :]))
                with dve.Fori(0, TILES // 4) as i:
                    for u in range(4):
                        x = RAW[:, i * 4 + u, :].rearrange("p (h d) -> p h d", d=16)
                        nc.vector.tensor_tensor(x, x, R[:, i * 4 + u, :].unsqueeze(2).broadcast_to([P, 32, 16]),
                                                ALU.mult).then_inc(s_n, 1)


def self_attention(nc, X, QKT, VA, ident, ones, d, retention):
    NAME = "L1_attn" if retention else "L2_attn"
    VW = 32 if retention else 33
    with stage(nc) as (sb, ps, sem):
        WO = sb("sa_wo", [P, KC, DIM])
        H8 = sb("sa_heads", [P, 8])
        if retention:
            DEC = sb("sa_decay", [P, 2, 8, SEQ])
            KS = sb("sa_k", [P, 2, P])
            BM = sb("sa_batch_mean", [P, P])
            GN = sb("sa_group_affine", [P, 2, KC])
            st = sb("sa_row_sums", [P, HEADS])
            mu = sb("sa_head_mean", [P, HEADS])
            s2 = sb("sa_square_sums", [P, HEADS])
            A2 = sb("sa_centered", [P, DIM])
            sq = sb("sa_squares", [P, DIM])
            std = sb("sa_head_std", [P, HEADS])
            rs16 = sb("sa_head_rstd", [P, HEADS])
        else:
            BO = sb("sa_bo", [1, DIM])
            nmax = sb("sa_max", [P, 16])
            SC = sb("sa_scores", [P, 8, 2, SEQ])
            rsum = sb("sa_inv_sum", [P, 2, 8])
        VS = sb("sa_v", [P, 8, VW])
        QB = sb("sa_q_spread", [P, 4, 8, SEQ])
        if retention:
            PR = [sb("sa_weightsT", [P, 2, 8, SEQ]) for _ in range(2)]
        else:
            PR = sb("sa_probs", [P, 8, 2, SEQ])
            PT = sb("sa_probsT", [P, 8, P])
        A = sb("sa_attended", [P, DIM])
        AT = sb("sa_attendedT", [P, KC, P])
        psS = ps("sa_pss", [P, 2, 8, SEQ])
        psT = ps("sa_pst", [P, 8, P]) if not retention else None
        psO = [ps("sa_pso", [P, 512]) for _ in range(2)]
        psX, psY = ps("sa_psx", [P, 512]), ps("sa_psy", [P, 512])
        s_w, s_q, s_s = sem("weights_loaded"), sem("queries_spread"), sem("scores_ready")
        s_mx, s_mv, s_e, s_t, s_tc, s_pv = (sem("max_ready"), sem("scores_moved"), sem("probs_ready"), sem("probs_flipped"),
                                            sem("probsT_ready"), sem("attended"))
        s_k = sem("keys_ready")
        s_d, s_o, s_a = sem("dve_step"), sem("attended_stored"), sem("attended_final")
        s_gm, s_c2, s_gv, s_gs, s_rt = (sem("head_means_ready"), sem("square_sums_ready"), sem("head_vars_ready"),
                                        sem("variances_ready"), sem("roots_ready"))
        s_at, s_atc, s_y, s_x = sem("attended_flipped"), sem("attendedT_ready"), sem("out_projected"), sem("x_updated")
        NW = 16 * (6 if retention else 3)

        def steps(eng, body):
            body(0, 0)
            with eng.Fori(0, TILES // 2 - 1) as j:
                body(j * 2 + 1, 1)
                body(j * 2 + 2, 0)
            body(TILES - 1, 1)

        def part(x, y):
            return (y, x) if retention else (x, y)

        def is_first(i):
            return isinstance(i, int) and i == 0

        def is_last(i):
            return isinstance(i, int) and i == TILES - 1

        with nc.Block() as block:
            @block.sync
            def _(sp):
                sp.dma_start(WO[:, :, :], rows_to_sbuf(d[NAME + "_WoT"])).then_inc(s_w, 16)
                sp.dma_start(H8[:, :], d["heads8"]).then_inc(s_w, 16)
                if retention:
                    sp.dma_start(DEC[:, :, :, :], d["decay"]).then_inc(s_w, 16)
                    sp.dma_start(BM[:, :], d["batch_mean"]).then_inc(s_w, 16)
                    sp.dma_start(GN[:, 0, :], d["L1_attn_gn_w_col"]).then_inc(s_w, 16)
                    sp.dma_start(GN[:, 1, :], d["L1_attn_gn_b_col"]).then_inc(s_w, 16)
                else:
                    sp.dma_start(BO[:, :], row(d["L2_attn_bo"])).then_inc(s_w, 16)

            @block.gpsimd
            def _(pool):
                pool.wait_ge(s_w, NW)
                pool.sem_inc(s_s, 2)
                with pool.Fori(0, TILES) as i:
                    for x in range(2):
                        pool.wait_ge(s_s, i * 2 + (x + 1))
                        for y in range(2):
                            b, g = part(x, y)
                            q = QKT[:, g, bass.ds(i * P + b * SEQ, SEQ)].unsqueeze(1).broadcast_to([P, 8, SEQ])
                            m = H8[:, :].unsqueeze(2).broadcast_to([P, 8, SEQ])
                            nc.gpsimd.tensor_tensor(QB[:, 2 * x + y, :, :], q, m, ALU.mult).then_inc(s_q, 1)

            @block.tensor
            def _(pe):
                def scores(i):
                    if retention:
                        pe.wait_ge(s_k, i + 1)
                    for x in range(2):
                        for y in range(2):
                            b, g = part(x, y)
                            pe.wait_ge(s_q, i * 4 + (2 * x + y + 1))
                            if retention:
                                last = nc.tensor.matmul(psS[b * SEQ:(b + 1) * SEQ, g, :, :].rearrange("p a q -> p (a q)"),
                                                        KS[:, g, b * SEQ:(b + 1) * SEQ],
                                                        QB[:, 2 * x + y, :, :].rearrange("p a q -> p (a q)"), start=True, stop=True)
                                continue
                            for a in range(4):
                                last = nc.tensor.matmul(psS[:, b, 4 * g + a, :],
                                                        QB[:, 2 * b + g, 2 * a:2 * a + 2, :].rearrange("p b q -> p (b q)"),
                                                        QKT[:, 2 + g, bass.ds(i * P + b * SEQ, SEQ)], start=True, stop=True)
                        last.then_inc(s_s, 1)

                def means(i):
                    pe.wait_ge(s_o, i + 1)
                    nc.tensor.matmul(psX[:, 0:HEADS], BM[:, :], st[:, :], start=True, stop=True).then_inc(s_gm, 1)

                def variances(i):
                    pe.wait_ge(s_c2, i + 1)
                    nc.tensor.matmul(psX[:, 0:HEADS], BM[:, :], s2[:, :], start=True, stop=True).then_inc(s_gv, 1)

                def flip_result(i):
                    pe.wait_ge(s_a if retention else s_o, i + 1)
                    for c in range(KC):
                        last = nc.tensor.transpose(psX[:, c * P:(c + 1) * P], A[:, c * P:(c + 1) * P], ident[:, :])
                    last.then_inc(s_at, 1)

                def output(i):
                    pe.wait_ge(s_atc, i + 1)
                    if not is_first(i):
                        pe.wait_ge(s_x, i)
                    for c in range(KC):
                        last = nc.tensor.matmul(psY[:, 0:DIM], AT[:, c, :], WO[:, c, :], start=(c == 0),
                                                stop=(c == KC - 1 and retention))
                    if not retention:
                        last = nc.tensor.matmul(psY[:, 0:DIM], ones[0:1, :], BO[:, :], start=False, stop=True)
                    last.then_inc(s_y, 1)

                def attend(i, u, b):
                    r = slice(b * SEQ, (b + 1) * SEQ)
                    for a in range(8):
                        if retention:
                            w = PR[u][r, a // 4, 2 * (a % 4):2 * (a % 4) + 2, :].rearrange("p h q -> p (h q)")
                        else:
                            w = PT[r, a, :]
                        last = nc.tensor.matmul(psO[b][:, a * VW:(a + 1) * VW], w, VS[r, a, :], start=True, stop=True)
                    return last

                def body(i, u):
                    before = 0 if isinstance(i, int) and i == 1 else i - 1
                    pe.wait_ge(s_e, (i + 1) * 2 if retention else i + 1)
                    if retention:
                        if not is_first(i):
                            means(before)
                        if not is_last(i):
                            scores(i + 1)
                        if not is_first(i):
                            variances(before)
                        pe.wait_ge(s_tc, i + 1)
                        attend(i, u, 0)
                        if not is_first(i):
                            flip_result(before)
                        attend(i, u, 1).then_inc(s_pv, 1)
                        if not is_first(i):
                            output(before)
                        return
                    for a in range(8):
                        last = nc.tensor.transpose(psT[:, a, :], PR[:, a, :, :].rearrange("p b j -> p (b j)"), ident[:, :])
                    last.then_inc(s_t, 1)
                    if not is_last(i):
                        scores(i + 1)
                    if not is_first(i):
                        flip_result(before)
                    pe.wait_ge(s_tc, i + 1)
                    if not is_first(i):
                        pe.wait_ge(s_o, i)
                    attend(i, u, 0)
                    attend(i, u, 1).then_inc(s_pv, 1)
                    if not is_first(i):
                        output(before)

                pe.wait_ge(s_w, NW)
                scores(0)
                steps(pe, body)
                if retention:
                    means(TILES - 1)
                    variances(TILES - 1)
                flip_result(TILES - 1)
                output(TILES - 1)

            @block.scalar
            def _(act):
                def exponentiate(i):
                    act.wait_ge(s_mv, i + 1)
                    nc.scalar.activation(PR[:, :, :, :].rearrange("p a b j -> p (a b j)"),
                                         SC[:, :, :, :].rearrange("p a b j -> p (a b j)"), ACT.Exp).then_inc(s_e, 1)

                def result(i):
                    if retention:
                        act.wait_ge(s_gs, i + 1)
                        nc.scalar.activation(std[:, :], std[:, :], ACT.Sqrt).then_inc(s_rt, 1)
                    act.wait_ge(s_at, i + 1)
                    if retention:
                        for c in range(KC):
                            last = nc.scalar.activation(AT[:, c, :], psX[:, c * P:(c + 1) * P], ACT.Identity,
                                                        bias=GN[:, 1, c:c + 1], scale=GN[:, 0, c:c + 1])
                        last.then_inc(s_atc, 1)
                    else:
                        nc.scalar.copy(AT[:, :, :].rearrange("p a b -> p (a b)"), psX[:, 0:DIM]).then_inc(s_atc, 1)

                def keys(i):
                    if not is_first(i):
                        act.wait_ge(s_s, i * 2 + 2)
                    nc.scalar.copy(KS[:, :, :], QKT[:, 2:4, bass.ds(i * P, P)]).then_inc(s_k, 1)

                def body(i, u):
                    if not retention:
                        act.wait_ge(s_t, i + 1)
                        nc.scalar.copy(PT[:, :, :], psT[:, :, :])
                    else:
                        if not is_last(i):
                            keys(i + 1)
                        if not is_first(i):
                            act.wait_ge(s_pv, i)
                    nc.scalar.copy(VS[:, :, :], VA[:, i, :, :]).then_inc(s_tc, 1)
                    if not is_first(i):
                        result(i - 1)
                    if not retention and not is_last(i):
                        exponentiate(i + 1)

                act.wait_ge(s_w, NW)
                if retention:
                    keys(0)
                else:
                    exponentiate(0)
                steps(act, body)
                result(TILES - 1)

            @block.vector
            def _(dve):
                NL = 3 if retention else 1
                A3 = A[:, :].rearrange("p (h d) -> p h d", d=16)
                if retention:
                    C3 = A2[:, :].rearrange("p (h d) -> p h d", d=16)

                def take(i, u):
                    if retention:
                        for g in range(2):
                            dve.wait_ge(s_s, i * 2 + (g + 3))
                            nc.vector.tensor_tensor(PR[u][:, g, :, :], psS[:, g, :, :], DEC[:, g, :, :], ALU.mult).then_inc(s_e, 1)
                        return
                    dve.wait_ge(s_s, i * 2 + 4)
                    nc.vector.tensor_reduce(nmax[:, :], psS[:, :, :, :].rearrange("p b a j -> p (b a) j"), AX_X,
                                            ALU.max).then_inc(s_mx, 1)
                    dve.wait_ge(s_mx, i + 1)
                    for b in range(2):
                        last = nc.vector.tensor_tensor(SC[:, :, b, :], psS[:, b, :, :],
                                                       nmax[:, 8 * b:8 * b + 8].unsqueeze(2).broadcast_to([P, 8, SEQ]),
                                                       ALU.subtract)
                    last.then_inc(s_mv, 1)

                def center(i):
                    link = Chain(dve, s_d, i * 5 + 1)
                    dve.wait_ge(s_gm, i + 1)
                    link(nc.vector.tensor_copy(mu[:, :], psX[:, 0:HEADS]))
                    link(nc.vector.tensor_tensor(C3, A3, mu[:, :].unsqueeze(2).broadcast_to([P, HEADS, 16]), ALU.subtract))
                    link(nc.vector.tensor_tensor(sq[:, :], A2[:, :], A2[:, :], ALU.mult))
                    nc.vector.tensor_reduce(s2[:, :], sq[:, :].rearrange("p (h d) -> p h d", d=16), AX_X, ALU.add).then_inc(s_c2, 1)

                def normalise(i):
                    link = Chain(dve, s_d, i * 5 + 4)
                    dve.wait_ge(s_gv, i + 1)
                    nc.vector.tensor_scalar(std[:, :], psX[:, 0:HEADS], 1e-5, None, ALU.add).then_inc(s_gs, 1)
                    dve.wait_ge(s_rt, i + 1)
                    link(nc.vector.reciprocal(rs16[:, :], std[:, :]))
                    nc.vector.tensor_tensor(A3, C3, rs16[:, :].unsqueeze(2).broadcast_to([P, HEADS, 16]), ALU.mult).then_inc(s_a, 1)

                def store(i):
                    dve.wait_ge(s_pv, i + 1)
                    if retention and not is_first(i):
                        dve.wait_ge(s_at, i)
                    if not retention:
                        link = Chain(dve, s_d, i)
                        for b in range(2):
                            O = psO[b][:, 0:8 * VW].rearrange("p (a w) -> p a w", a=8)
                            last = nc.vector.reciprocal(rsum[:, b, :], O[:, :, 32])
                        link(last)
                    for b in range(2):
                        O = psO[b][:, 0:8 * VW].rearrange("p (a w) -> p a w", a=8)
                        for h in range(2):
                            dst = A[b * SEQ:(b + 1) * SEQ, :].rearrange("p (a b d) -> p a b d", a=8, b=2)[:, :, h, :]
                            src = O[h * SEQ:(h + 1) * SEQ, :, 16 * h:16 * h + 16]
                            if retention:
                                last = nc.vector.tensor_copy(dst, src)
                            else:
                                last = nc.vector.tensor_tensor(
                                    dst, src, rsum[h * SEQ:(h + 1) * SEQ, b, :].unsqueeze(2).broadcast_to([SEQ, 8, 16]), ALU.mult)
                    if not retention:
                        last.then_inc(s_o, 1)
                        return
                    Chain(dve, s_d, i * 5)(last)
                    nc.vector.tensor_reduce(st[:, :], A3, AX_X, ALU.add).then_inc(s_o, 1)

                def update(i):
                    dve.wait_ge(s_y, i + 1)
                    x = X[:, bass.ds(i, 1), :]
                    nc.vector.tensor_tensor(x, psY[:, 0:DIM].unsqueeze(1), x, ALU.add).then_inc(s_x, 1)

                def body(i, u):
                    if retention and not is_first(i):
                        center(i - 1)
                    if not is_last(i):
                        take(i + 1, 1 - u)
                    if retention and not is_first(i):
                        normalise(i - 1)
                    store(i)
                    if not is_first(i):
                        update(i - 1)

                dve.wait_ge(s_w, NW)
                take(0, 0)
                steps(dve, body)
                if retention:
                    center(TILES - 1)
                    normalise(TILES - 1)
                update(TILES - 1)


def tiled_experts(nc, X, XNT, ident, ones, d):
    E = 8
    with stage(nc) as (sb, ps, sem):
        W = sb("te_w", [P, E, KC, DIM])
        B = sb("te_b", [E, DIM])
        PE_ = sb("te_position", [32, P])
        SG = sb("te_signatures", [32, E])
        lt = sb("te_negative", [32, E])
        SN = sb("te_signs", [32, E])
        OR = sb("te_order", [P, E])
        SCR = sb("te_scores", [P, 1, E])
        OH = sb("te_onehot", [P, 1, E])
        top, scr = sb("te_top", [P, 1]), sb("te_scratch", [P, 1])
        OHT = sb("te_onehotT", [E, P])
        DG = sb("te_diagonals", [SEQ, E, SEQ])
        OB = sb("te_onehot_rows", [P, E, SEQ])
        XG = [sb("te_x_picked", [P, KC, E, P]) for _ in range(2)]
        psS, psB, psT = ps("te_pss", [P, 512]), ps("te_psb", [P, 512]), ps("te_pst", [P, 512])
        out = [ps("te_psy", [P, 512]) for _ in range(2)]
        s_w, s_wb, s_sn, s_sc, s_d = sem("small_loaded"), sem("weights_loaded"), sem("signs_ready"), sem("scores_ready"), sem("dve_step")
        s_oh, s_tb, s_ob, s_xg, s_y, s_x = (sem("onehot_ready"), sem("onehot_spread"), sem("onehot_rows_ready"), sem("x_picked"),
                                            sem("multiplied"), sem("x_updated"))
        with nc.Block() as block:
            @block.sync
            def _(sp):
                sp.dma_start(PE_[:, :], d["positionT"]).then_inc(s_w, 16)
                sp.dma_start(SG[:, :], d["L2_ffn_tile_sigsT"]).then_inc(s_w, 16)
                sp.dma_start(OR[:, :], d["expert_order"]).then_inc(s_w, 16)
                sp.dma_start(B[:, :], d["L2_ffn_b"]).then_inc(s_wb, 16)
                for e in range(E):
                    sp.dma_start(W[:, e, :, :], rows_to_sbuf(d["L2_ffn_WT"][e])).then_inc(s_wb, 16)

            @block.tensor
            def _(pe):
                pe.wait_ge(s_sn, 1)
                nc.tensor.matmul(psS[:, 0:E], PE_[:, :], SN[:, :], start=True, stop=True).then_inc(s_sc, 1)
                pe.wait_ge(s_oh, 1)
                nc.tensor.transpose(psT[0:E, 0:P], OH[:, 0, :], ident[:, :])
                nc.tensor.matmul(psB[:, :], ones[0:SEQ, :], DG[:, :, :].rearrange("p e s -> p (e s)"), start=True,
                                 stop=True).then_inc(s_tb, 1)
                pe.wait_ge(s_wb, 16 * (1 + E))
                pe.sem_inc(s_x, 2)
                with pe.Fori(0, TILES // 2) as i:
                    for u in range(2):
                        pe.wait_ge(s_xg, i * 2 + (u + 1))
                        pe.wait_ge(s_x, i * 2 + (u + 1))
                        nc.tensor.matmul(out[u][:, 0:DIM], OHT[:, :], B[:, :], start=True, stop=False)
                        for e in range(E):
                            for c in range(KC):
                                last = nc.tensor.matmul(out[u][:, 0:DIM], XG[u][:, c, e, :], W[:, e, c, :], start=False,
                                                        stop=(e == E - 1 and c == KC - 1))
                        last.then_inc(s_y, 1)

            @block.vector
            def _(dve):
                link = Chain(dve, s_d)
                dve.wait_ge(s_w, 48)
                link(nc.vector.tensor_scalar(lt[:, :], SG[:, :], 0.0, None, ALU.is_lt))
                link(nc.vector.tensor_scalar(SN[:, :], SG[:, :], 0.0, None, ALU.is_gt))
                nc.vector.tensor_tensor(SN[:, :], SN[:, :], lt[:, :], ALU.subtract).then_inc(s_sn, 1)
                dve.wait_ge(s_sc, 1)
                link(nc.vector.tensor_copy(SCR[:, 0, :], psS[:, 0:E]))
                first_maximum(nc, link, OH[:, :, :], top[:, :], scr[:, :], SCR[:, :, :], OR[:, :], [P, 1, E])
                for e in range(E):
                    last = nc.vector.tensor_scalar(DG[:, e, :], ident[0:SEQ, 0:SEQ], OH[0:SEQ, 0, e:e + 1], None, ALU.mult)
                last.then_inc(s_oh, 1)
                dve.wait_ge(s_tb, 1)
                nc.vector.tensor_copy(OHT[:, :], psT[0:E, 0:P])
                nc.vector.tensor_copy(OB[:, :, :].rearrange("p e s -> p (e s)"), psB[:, :]).then_inc(s_ob, 1)
                dve.wait_ge(s_ob, 1)
                dve.sem_inc(s_y, 2)

                with dve.Fori(0, TILES // 2) as i:
                    for u in range(2):
                        dve.wait_ge(s_y, i * 2 + (u + 1))
                        for c in range(KC):
                            for b in range(2):
                                x = XNT[:, c, bass.ds(i * 2 * P + (u * P + b * SEQ), SEQ)].unsqueeze(1).broadcast_to([P, E, SEQ])
                                last = nc.vector.tensor_tensor(XG[u][:, c, :, b * SEQ:(b + 1) * SEQ], x, OB[:, :, :], ALU.mult)
                        last.then_inc(s_xg, 1)
                    for u in range(2):
                        dve.wait_ge(s_y, i * 2 + (u + 3))
                        x = X[:, bass.ds(i * 2 + u, 1), :]
                        nc.vector.tensor_tensor(x, out[u][:, 0:DIM].unsqueeze(1), x, ALU.add).then_inc(s_x, 1)


def gated_recurrence(nc, X, XNT, ident, d):
    TC = 512
    NT = TOKENS // TC
    with stage(nc) as (sb, ps, sem):
        W = sb("gr_w", [P, KC, 4 * P])
        WG = sb("gr_wg", [P, KC, DIM])
        B = sb("gr_b", [P, 4])
        BG = sb("gr_bg", [P, 2])
        Z, K, V = (sb("gr_z", [P, 2, TC]), sb("gr_keep", [P, 2, TC]), sb("gr_input", [P, 2, TC]))
        H = sb("gr_h", [P, 2, TC])
        GA = sb("gr_gate", [P, 2, TC])
        O = sb("gr_out", [P, 2, TC])
        psZ = [ps("gr_psz", [P, 512]) for _ in range(2)]
        psH = [ps("gr_psh", [P, 512]) for _ in range(2)]
        psG = [ps("gr_psg", [P, 512]) for _ in range(2)]
        psT = [ps("gr_pst", [P, 2, DIM]) for _ in range(2)]
        s_w, s_p, s_z, s_k, s_zero = sem("weights_loaded"), sem("projected"), sem("z_ready"), sem("keep_ready"), sem("batch_starts_cleared")
        s_h, s_g, s_ga, s_o, s_t, s_x = (sem("h_ready"), sem("gate_projected"), sem("gate_ready"), sem("out_ready"),
                                         sem("out_flipped"), sem("x_updated"))
        with nc.Block() as block:
            @block.sync
            def _(sp):
                sp.dma_start(W[:, :, :], rows_to_sbuf(d["L3_attn_W"])).then_inc(s_w, 16)
                sp.dma_start(WG[:, :, :], rows_to_sbuf(d["L3_attn_W_g"])).then_inc(s_w, 16)
                sp.dma_start(B[:, :], d["L3_attn_b_col"]).then_inc(s_w, 16)
                sp.dma_start(BG[:, :], d["L3_attn_b_g_col"]).then_inc(s_w, 16)

            @block.tensor
            def _(pe):
                pe.wait_ge(s_w, 64)
                pe.sem_inc(s_h, 2)
                pe.sem_inc(s_x, 2)
                with pe.Fori(0, NT) as t:
                    pe.wait_ge(s_h, t * 2 + 2)
                    for n, dst in enumerate(psZ + psH):
                        for c in range(KC):
                            last = nc.tensor.matmul(dst[:, :], W[:, c, n * P:(n + 1) * P], XNT[:, c, bass.ds(t * TC, TC)],
                                                    start=(c == 0), stop=(c == KC - 1))
                    last.then_inc(s_p, 1)
                    pe.wait_ge(s_h, t * 2 + 4)
                    for m in range(2):
                        for c in range(KC):
                            last = nc.tensor.matmul(psG[m][:, :], WG[:, c, m * P:(m + 1) * P], H[:, c, :], start=(c == 0),
                                                    stop=(c == KC - 1))
                    last.then_inc(s_g, 1)
                    pe.wait_ge(s_o, t * 2 + 2)
                    pe.wait_ge(s_x, t * 2 + 2)
                    for j in range(TC // P):
                        for c in range(KC):
                            last = nc.tensor.transpose(psT[j // 2][:, j % 2, c * P:(c + 1) * P], O[:, c, j * P:(j + 1) * P], ident[:, :])
                    last.then_inc(s_t, 1)

            @block.scalar
            def _(act):
                act.wait_ge(s_w, 64)
                with act.Fori(0, NT) as t:
                    act.wait_ge(s_p, t + 1)
                    for m in range(2):
                        nc.scalar.activation(Z[:, m, :], psZ[m][:, :], ACT.Sigmoid, bias=B[:, m:m + 1]).then_inc(s_z, 1)
                    act.wait_ge(s_g, t + 1)
                    for m in range(2):
                        nc.scalar.activation(GA[:, m, :], psG[m][:, :], ACT.Sigmoid, bias=BG[:, m:m + 1]).then_inc(s_ga, 1)

            @block.vector
            def _(dve):
                dve.wait_ge(s_w, 64)
                with dve.Fori(0, NT) as t:
                    for m in range(2):
                        dve.wait_ge(s_z, t * 2 + (m + 1))
                        nc.vector.tensor_scalar(K[:, m, :], Z[:, m, :], -1.0, 1.0, ALU.mult, ALU.add).then_inc(s_k, 1)
                        nc.vector.scalar_tensor_tensor(V[:, m, :], psH[m][:, :], B[:, 2 + m:3 + m], Z[:, m, :], ALU.add,
                                                       ALU.mult).then_inc(s_k, 1)
                        dve.wait_ge(s_k, t * 4 + (2 * m + 2))
                        nc.vector.memset(K[:, m, 0:TC:SEQ], 0.0).then_inc(s_zero, 1)
                        dve.wait_ge(s_zero, t * 2 + (m + 1))
                        nc.vector.tensor_tensor_scan(H[:, m, :], K[:, m, :], V[:, m, :], 0.0, ALU.mult, ALU.add).then_inc(s_h, 1)
                    for m in range(2):
                        dve.wait_ge(s_ga, t * 2 + (m + 1))
                        nc.vector.tensor_tensor(O[:, m, :], GA[:, m, :], H[:, m, :], ALU.mult).then_inc(s_o, 1)
                    dve.wait_ge(s_t, t + 1)
                    for j in range(2):
                        x = X[:, bass.ds(t * 4 + 2 * j, 2), :]
                        nc.vector.tensor_tensor(x, psT[j][:, :, :], x, ALU.add).then_inc(s_x, 1)


def swiglu_quantised(nc, X, XNT, d):
    HID, TC = 768, 512
    NF = HID // P
    NT = TOKENS // TC
    S = 1.0 / 127.0
    TPC = TC // P
    with stage(nc) as (sb, ps, sem):
        WI = [sb("sw_int", [P, KC, HID], I32) for _ in range(2)]
        WDI = sb("sw_down_int", [P, NF, DIM], I32)
        W = [sb("sw_w", [P, KC, HID]) for _ in range(2)]
        WD = sb("sw_down", [P, NF, DIM])
        SI = [sb("sw_silu", [P, TC]) for _ in range(2)]
        HF = [sb("sw_hidden", [P, TC]) for _ in range(2)]
        WS = [[sb("sw_w_part", [P, KC, HID], R32) for _ in range(2)] for _ in range(2)]
        WDS = [sb("sw_down_part", [P, NF, DIM], R32) for _ in range(2)]
        XS = [sb("sw_x_part", [P, KC, TOKENS], R32) for _ in range(2)]
        HT = [[sb("sw_hidden_part", [P, NF, TC], R32) for _ in range(2)] for _ in range(2)]
        psG = [ps("sw_psg", [P, 512]) for _ in range(2)]
        psU = [ps("sw_psu", [P, 512]) for _ in range(2)]
        psD = [ps("sw_psd", [P, 512]) for _ in range(2)]
        s_w, s_f = [sem(f"weights{n}_loaded") for n in range(3)], sem("weights_scaled")
        s_wh, s_wl, s_xh, s_xl = sem("w_high_ready"), sem("w_low_ready"), sem("x_high_ready"), sem("x_low_ready")
        s_hf, s_hh = sem("hidden_product_ready"), sem("hidden_high_ready")
        s_up, s_si, s_h, s_dn, s_x = sem("up_projected"), sem("silu_ready"), sem("hidden_ready"), sem("down_projected"), sem("x_updated")
        with nc.Block() as block:
            @block.sync
            def _(sp):
                sp.dma_start(WI[0][:, :, :], rows_to_sbuf(d["L3_ffn_w_gateT"])).then_inc(s_w[0], 16)
                sp.dma_start(WI[1][:, :, :], rows_to_sbuf(d["L3_ffn_w_upT"])).then_inc(s_w[1], 16)
                sp.dma_start(WDI[:, :, :], rows_to_sbuf(d["L3_ffn_w_downT"])).then_inc(s_w[2], 16)

            @block.tensor
            def _(pe):
                pe.wait_ge(s_wl, 3)
                pe.wait_ge(s_xl, NT)
                pe.sem_inc(s_hf, 2)
                pe.sem_inc(s_x, 2)
                with pe.Fori(0, NT // 2) as i:
                    def up(n):
                        for f in range(NF):
                            k = n * NF + f
                            pe.wait_ge(s_hf, i * 2 * NF + (k + 1))
                            for ws, dst in ((WS[0], psG), (WS[1], psU)):
                                for c in range(KC):
                                    last = three_passes(nc, dst[k % 2][:, :], [w[:, c, f * P:(f + 1) * P] for w in ws],
                                                        [x[:, c, bass.ds(i * 2 * TC + n * TC, TC)] for x in XS], c == 0, c == KC - 1)
                            last.then_inc(s_up, 1)

                    def down(n):
                        pe.wait_ge(s_h, i * 2 * NF + (n + 1) * NF)
                        for j in range(TPC):
                            k = n * TPC + j
                            pe.wait_ge(s_x, i * 2 * TPC + (k + 1))
                            for f in range(NF):
                                last = three_passes(nc, psD[k % 2][:, 0:DIM], [h[:, f, j * P:(j + 1) * P] for h in HT[n]],
                                                    [w[:, f, :] for w in WDS], f == 0, f == NF - 1)
                            last.then_inc(s_dn, 1)

                    up(0)
                    up(1)
                    down(0)
                    down(1)

            @block.scalar
            def _(act):
                for t in range(NT):
                    nc.scalar.copy(XS[0][:, :, t * TC:(t + 1) * TC], XNT[:, :, t * TC:(t + 1) * TC]).then_inc(s_xh, 1)
                for n, (src, dst) in enumerate(((W[0], WS[0]), (W[1], WS[1]), (WD, WDS))):
                    act.wait_ge(s_f, n + 1)
                    nc.scalar.copy(dst[0][:, :, :], src[:, :, :]).then_inc(s_wh, 1)
                with act.Fori(0, NT // 2) as i:
                    def high(k):
                        act.wait_ge(s_hf, i * 2 * NF + (k + 3))
                        if k % NF == 0:
                            act.wait_ge(s_dn, i * 2 * TPC + (k // NF + 1) * TPC)
                        nc.scalar.copy(HT[k // NF][0][:, k % NF, :], HF[k % 2][:, :]).then_inc(s_hh, 1)

                    for k in range(2 * NF):
                        act.wait_ge(s_up, i * 2 * NF + (k + 1))
                        act.wait_ge(s_hf, i * 2 * NF + (k + 1))
                        nc.scalar.activation(SI[k % 2][:, :], psG[k % 2][:, :], ACT.Silu).then_inc(s_si, 1)
                        if k:
                            high(k - 1)
                    high(2 * NF - 1)

            @block.vector
            def _(dve):
                for t in range(NT):
                    dve.wait_ge(s_xh, t + 1)
                    r = slice(t * TC, (t + 1) * TC)
                    nc.vector.tensor_tensor(XS[1][:, :, r], XNT[:, :, r], XS[0][:, :, r].bitcast(F32), ALU.subtract).then_inc(s_xl, 1)
                for n, (src, dst) in enumerate(((WI[0], W[0]), (WI[1], W[1]), (WDI, WD))):
                    dve.wait_ge(s_w[n], 16)
                    nc.vector.tensor_scalar(dst[:, :, :], src[:, :, :], S, None, ALU.mult).then_inc(s_f, 1)
                for n, (src, dst) in enumerate(((W[0], WS[0]), (W[1], WS[1]), (WD, WDS))):
                    dve.wait_ge(s_wh, n + 1)
                    nc.vector.tensor_tensor(dst[1][:, :, :], src[:, :, :], dst[0][:, :, :].bitcast(F32), ALU.subtract).then_inc(s_wl, 1)
                dve.sem_inc(s_dn, 2 * TPC)
                with dve.Fori(0, NT // 2) as i:
                    def low(k):
                        dve.wait_ge(s_hh, i * 2 * NF + (k + 1))
                        nc.vector.tensor_tensor(HT[k // NF][1][:, k % NF, :], HF[k % 2][:, :],
                                                HT[k // NF][0][:, k % NF, :].bitcast(F32), ALU.subtract).then_inc(s_h, 1)

                    for k in range(2 * NF):
                        dve.wait_ge(s_si, i * 2 * NF + (k + 1))
                        if k >= 2:
                            dve.wait_ge(s_h, i * 2 * NF + (k - 1))
                        nc.vector.tensor_tensor(HF[k % 2][:, :], psU[k % 2][:, :], SI[k % 2][:, :], ALU.mult).then_inc(s_hf, 1)
                        if k:
                            low(k - 1)
                    low(2 * NF - 1)
                    for k in range(2 * TPC):
                        dve.wait_ge(s_dn, i * 2 * TPC + (2 * TPC + k + 1))
                        x = X[:, bass.ds(i * 2 * TPC + k, 1), :]
                        nc.vector.tensor_tensor(x, psD[k % 2][:, 0:DIM].unsqueeze(1), x, ALU.add).then_inc(s_x, 1)


STAGES = ('L0x', 'L0a', 'L0f', 'L1x', 'L1a', 'L1f', 'L2x', 'L2a', 'L2f', 'L3x', 'L3a', 'L3f')


def perceiver(nc, d, out):
    _stages.clear()
    _names.clear()
    with ExitStack() as ctx:
        X = ctx.enter_context(nc.sbuf_tensor("x_resident", [P, TILES, DIM], F32))
        XNT = ctx.enter_context(nc.sbuf_tensor("x_normed_transposed", [P, KC, TOKENS], F32))
        ident = ctx.enter_context(nc.sbuf_tensor("identity", [P, P], F32))
        ones = ctx.enter_context(nc.sbuf_tensor("ones", [P, P], F32))
        with stage(nc) as (sb, ps, sem):
            s_in, s_one = sem("x_loaded"), sem("ones_set")
            with nc.Block() as block:
                @block.sync
                def _(sp):
                    sp.dma_start(X[:, :, :], d["x"].rearrange("(t b) s d -> (b s) t d", b=2)).then_inc(s_in, 16)
                    sp.dma_start(ident[:, :], d["identity"]).then_inc(s_in, 16)
                    sp.wait_ge(s_in, 32)

                @block.gpsimd
                def _(pool):
                    nc.gpsimd.memset(ones[:, :], 1.0).then_inc(s_one, 1)
                    pool.wait_ge(s_one, 1)

        ctx4 = d["ctxT"].rearrange("(t b) d s -> t b d s", b=2)
        ctxn = d["ctx"].rearrange("(t b) s d -> t b s d", b=2)
        mask4 = d["mask_Bx1x1xS2_fk0"].rearrange("(t b) c e s -> t b (c e s)", b=2)
        if "L0x" in STAGES:
            layernorm_transposed(nc, X, XNT, ident)
            with nc.sbuf_tensor("l0x_qT", [P, KC, TOKENS], F32) as QT:
                project_transposed(nc, XNT, QT, d["L0_xattn_Wq"], d["L0_xattn_bq_col"], KC)
                cross_attention(nc, X, QT, ident, ones, d["spread16"], ctx4, 16, wkv=d["L0_xattn_Wkv"],
                                bk=d["L0_xattn_bk_col"], bv=d["L0_xattn_bv_col"], wo=d["L0_xattn_Wo"], bo=d["L0_xattn_bo"], scratch=XNT)
        if "L0a" in STAGES:
            layernorm_transposed(nc, X, XNT, ident, passes=2, residual=True,
                                 affine=(d["L0_attn_gamma_col"], d["L0_attn_beta_col"]))
            linear_attention(nc, X, XNT, ident, d)
        if "L0f" in STAGES:
            layernorm_transposed(nc, X, XNT, ident)
            mixed_experts(nc, X, XNT, ident, ones, d)
        if "L1x" in STAGES:
            ctxnT = nc.dram_tensor("ctx_normed_transposed", (BATCH, DIM, NKEY), F32, kind="Internal").ap()
            normed_context(nc, d["ctx"], ctxnT, ident, d["L1_xattn_ln_c_w_col"], d["L1_xattn_ln_c_b_col"])
            layernorm_transposed(nc, X, XNT, ident, passes=2,
                                 affine=(d["L1_xattn_ln_l_w_col"], d["L1_xattn_ln_l_b_col"]))
            with nc.sbuf_tensor("l1x_qT", [P, 8, TOKENS], F32) as QT:
                project_transposed(nc, XNT, QT, d["L1_xattn_Wq"], None, 8)
                cross_attention(nc, X, QT, ident, ones, d["spread64"], ctxnT.rearrange("(t b) d s -> t b d s", b=2), 64,
                                wkv=d["L1_xattn_Wkv"], wo=d["L1_xattn_Wo"], bo=d["L1_xattn_bo"], clip=11.0, scratch=XNT)
        if "L1a" in STAGES:
            layernorm_transposed(nc, X, XNT, ident)
            with nc.sbuf_tensor("l1a_qkT", [P, 4, TOKENS], F32) as QKT, \
                    nc.sbuf_tensor("l1a_v", [P, TILES, 8, 32], F32) as VA:
                project_transposed(nc, XNT, QKT, d["L1_attn_Wqk"], None, 4)
                values_by_token(nc, XNT, VA, d["L1_attn_Wv"], 32)
                self_attention(nc, X, QKT, VA, ident, ones, d, retention=True)
        if "L1f" in STAGES:
            with nc.sbuf_tensor("x_normed", [P, TILES, DIM], F32) as XN:
                layernorm_transposed(nc, X, XNT, ident, rows=XN)
                routed_experts(nc, X, XNT, XN, ident, ones, d)
        if "L2x" in STAGES:
            layernorm_transposed(nc, X, XNT, ident)
            cross_attention(nc, X, XNT, ident, ones, d["spread16"], ctx4, 16, ctx=ctxn)
        if "L2a" in STAGES:
            layernorm_transposed(nc, X, XNT, ident)
            with nc.sbuf_tensor("l2a_qkT", [P, 4, TOKENS], F32) as QKT, \
                    nc.sbuf_tensor("l2a_v", [P, TILES, 8, 33], F32) as VA:
                normed_heads(nc, XNT, QKT, VA, ident, d)
                self_attention(nc, X, QKT, VA, ident, ones, d, retention=False)
        if "L2f" in STAGES:
            layernorm_transposed(nc, X, XNT, ident)
            tiled_experts(nc, X, XNT, ident, ones, d)
        if "L3x" in STAGES:
            layernorm_transposed(nc, X, XNT, ident)
            with nc.sbuf_tensor("l3x_qT", [P, KC, TOKENS], F32) as QT:
                project_transposed(nc, XNT, QT, d["L3_xattn_Wq"], d["L3_xattn_bq_col"], KC)
                cross_attention(nc, X, QT, ident, ones, d["spread16"], ctx4, 16, wkv=d["L3_xattn_Wkv"],
                                bk=d["L3_xattn_bk_col"], bv=d["L3_xattn_bv_col"], wo=d["L3_xattn_Wo"], bo=d["L3_xattn_bo"], mask=mask4,
                                scratch=XNT)
        if "L3a" in STAGES:
            layernorm_transposed(nc, X, XNT, ident)
            gated_recurrence(nc, X, XNT, ident, d)
        if "L3f" in STAGES:
            layernorm_transposed(nc, X, XNT, ident)
            swiglu_quantised(nc, X, XNT, d)
        with stage(nc) as (sb, ps, sem):
            s_out = sem("x_stored")
            with nc.Block() as block:
                @block.sync
                def _(sp):
                    sp.dma_start(out.rearrange("(t b) s d -> (b s) t d", b=2), X[:, :, :]).then_inc(s_out, 16)
                    sp.wait_ge(s_out, 16)


def kernel(**inputs):
    import numpy as np
    import concourse.bacc as _bacc
    from concourse.bass_utils import run_bass_kernel_spmd as _run

    arrays = {k: np.ascontiguousarray(v) for k, v in inputs.items() if k in DIRECT}
    arrays["ctx"] = np.ascontiguousarray(inputs["ctx_1024"])
    arrays["ctxT"] = np.ascontiguousarray(np.asarray(inputs["ctx_1024"]).transpose(0, 2, 1))
    for n in ("L0", "L3"):
        arrays[f"{n}_xattn_Wkv"] = np.concatenate(
            [np.asarray(inputs[f"{n}_xattn_Wk"]), np.asarray(inputs[f"{n}_xattn_Wv"])], axis=1)
    for k in COLUMNS:
        arrays[k + "_col"] = np.ascontiguousarray(np.asarray(inputs[k]).reshape(-1, 128).T)
    arrays["identity"] = np.eye(128, dtype=np.float32)
    head = np.arange(128) // 16
    arrays["spread16"] = np.where(head[:, None] == np.arange(8)[None], 0.25, 0.0).astype(np.float32)
    more_arrays(arrays, inputs)

    nc = _bacc.Bacc("TRN2", target_bir_lowering=False, num_devices=1)
    d = {k: nc.dram_tensor(f"in_{k}", a.shape, mybir.dt.from_np(a.dtype), kind="ExternalInput").ap()
         for k, a in arrays.items()}
    out = nc.dram_tensor("out_x", (BATCH, SEQ, DIM), F32, kind="ExternalOutput").ap()
    perceiver(nc, d, out)
    r = _run(nc, [{f"in_{k}": a for k, a in arrays.items()}], core_ids=[0])
    return r.results[0]["out_x"]


DIRECT = ("x", "mask_Bx1x1xS2_fk0", "L0_xattn_Wq", "L0_xattn_Wo", "L0_xattn_bo", "L3_xattn_Wq", "L3_xattn_Wo",
          "L3_xattn_bo", "L0_attn_Wqkv", "L0_attn_Wout", "L1_xattn_Wq", "L1_xattn_Wkv", "L1_xattn_Wo", "L1_xattn_bo",
          "L2_attn_bo", "L2_attn_bqkv", "L0_ffn_gb2", "L0_ffn_eb1", "L0_ffn_eb2", "L1_ffn_Wg", "L1_ffn_W_in",
          "L1_ffn_W_out", "L2_ffn_b", "L3_attn_W_g")
COLUMNS = ("L0_xattn_bq", "L0_xattn_bk", "L0_xattn_bv", "L3_xattn_bq", "L3_xattn_bk", "L3_xattn_bv",
           "L0_attn_gamma", "L0_attn_beta", "L1_xattn_ln_c_w", "L1_xattn_ln_c_b", "L1_xattn_ln_l_w", "L1_xattn_ln_l_b",
           "L1_attn_gn_w", "L1_attn_gn_b", "L0_ffn_gb1", "L3_attn_b_g")


def more_arrays(arrays, inputs):
    import numpy as np

    f = np.float32
    part = np.arange(128)
    arrays["spread64"] = np.where((part // 64)[:, None] == np.arange(2)[None], 0.125, 0.0).astype(f)
    arrays["same_head"] = ((part // 16)[:, None] == (part // 16)[None]).astype(f)
    arrays["heads8"] = ((part // 16)[:, None] == np.arange(8)[None]).astype(f)
    arrays["batch_mean"] = np.where((part // 64)[:, None] == (part // 64)[None], 1.0 / (64 * 16), 0.0).astype(f)
    lo, hi = float(np.log(1.0 - 0.999)), float(np.log(1.0 - 0.9))
    gam = (f(1.0) - np.exp(np.linspace(lo, hi, 16, dtype=f))).astype(f)
    dist = (np.arange(64)[:, None] - np.arange(64)[None]).astype(f)
    dec = np.where(dist >= 0, gam[:, None, None] ** np.where(dist >= 0, dist, 0).astype(f), 0).astype(f)
    arrays["decay"] = np.ascontiguousarray(np.tile(dec.transpose(2, 0, 1).reshape(64, 2, 8, 64), (2, 1, 1, 1)))
    g = lambda k: np.asarray(inputs[k])
    arrays["L1_attn_Wqk"] = np.concatenate([g("L1_attn_wq").T, g("L1_attn_wk").T], axis=1)
    arrays["L1_attn_Wv"] = np.ascontiguousarray(g("L1_attn_wv").T)
    arrays["L1_attn_WoT"] = np.ascontiguousarray(g("L1_attn_wo").T)
    arrays["L2_attn_WqkvT"] = np.ascontiguousarray(g("L2_attn_Wqkv").T)
    arrays["L2_attn_WoT"] = np.ascontiguousarray(g("L2_attn_Wo").T)
    arrays["L2_attn_wqk_col"] = np.stack([np.tile(g("L2_attn_wq"), 8), np.tile(g("L2_attn_wk"), 8)], axis=1)
    t = lambda k, *axes: np.ascontiguousarray(g(k).transpose(*axes))
    arrays["L0_ffn_gW1T"] = t("L0_ffn_gW1", 1, 0)
    arrays["L0_ffn_gW2T"] = t("L0_ffn_gW2", 1, 0)
    arrays["L0_ffn_eW1T"] = t("L0_ffn_eW1", 0, 2, 1)
    arrays["L0_ffn_eW2T"] = t("L0_ffn_eW2", 0, 2, 1)
    arrays["L2_ffn_tile_sigsT"] = t("L2_ffn_tile_sigs", 1, 0)
    arrays["L2_ffn_WT"] = t("L2_ffn_W", 0, 2, 1)
    for k in ("L3_ffn_w_gate", "L3_ffn_w_up", "L3_ffn_w_down"):
        arrays[k + "T"] = t(k, 1, 0)
    arrays["L3_attn_W"] = np.concatenate([g(f"L3_attn_W_{k}") for k in ("zf", "zs", "hf", "hs")], axis=1)
    arrays["L3_attn_b_col"] = np.stack([g(f"L3_attn_b_{k}") for k in ("zf", "zs", "hf", "hs")], axis=1)
    arrays["expert_order"] = np.broadcast_to(np.arange(8, 0, -1, dtype=f), (128, 8)).copy()
    arrays["queue_starts"] = np.broadcast_to(np.arange(8, dtype=f) * 640, (128, 8)).copy()
    arrays["spare_rows"] = (8 * 640 + np.arange(32)[None] * 128 + part[:, None]).astype(f)
    arrays["before"] = (part[:, None] < part[None]).astype(f)
    pos = (part % 64).astype(f)[:, None]
    div = np.exp(np.arange(0, 32, 2, dtype=f) * f(-np.log(10000.0) / 32))
    ang = (pos * div).astype(f)
    pe = np.zeros((128, 32), f)
    pe[:, 0::2] = np.sin(ang)
    pe[:, 1::2] = np.cos(ang)
    arrays["positionT"] = np.ascontiguousarray(pe.T)
```
